# Optimizing a Trainium2 kernel written in Bass

```python
import numpy as np
import jax
import jax.numpy as jnp

def _softmax(x, axis=-1):
    return jax.nn.softmax(x, axis=axis)

def _gelu(x):
    return jax.nn.gelu(x, approximate=True)

def _silu(x):
    return jax.nn.silu(x)

def _sigmoid(x):
    return jax.nn.sigmoid(x)

def _layernorm(x, axis=-1, eps=1e-05):
    m = jnp.mean(x, axis=axis, keepdims=True)
    v = jnp.var(x, axis=axis, keepdims=True)
    return (x - m) / jnp.sqrt(v + eps)

def _scatter_add(tgt, idx, src, axis=0):
    return tgt.at[idx].add(src)

def _segment_sum(src, seg, n):
    return jax.ops.segment_sum(src, seg, n)
kernel_name = 'mk_xattn_seq_d4_seqx_r8_68c3e7'

def setup_inputs(seed: int=0):
    np.random.seed(seed)
    _w = jnp.asarray

    def _rec_inputs():
        import jax
        import jax.numpy as jnp
        _rk = jax.random.key(seed)
        x = -0.0002928 + 1 * jax.random.normal(jax.random.fold_in(_rk, 1), (32, 64, 256), jnp.float32)
        _lenS = 64 - jax.random.randint(jax.random.fold_in(_rk, 7), (32,), 0, max(1, 64 // 4) + 1, jnp.int32)
        _lenS2 = 64 - jax.random.randint(jax.random.fold_in(_rk, 8), (32,), 0, max(1, 64 // 4) + 1, jnp.int32)
        _ctx_2048P = jax.random.normal(jax.random.fold_in(_rk, 11), (32, 16, 256), jnp.float32)
        _ctx_2048c = jax.random.dirichlet(jax.random.fold_in(_rk, 511), 0.3 * jnp.ones((16,), jnp.float32), (32, 64))
        _ctx_2048t = jnp.einsum('bsk,bkd->bsd', _ctx_2048c, _ctx_2048P)
        _ctx_2048t = _ctx_2048t * jax.lax.rsqrt(jnp.mean(jnp.square(_ctx_2048t)) + 1e-12) * 0.953939
        ctx_2048 = -1.39393e-06 + 0.999914 * (_ctx_2048t + 0.3 * jax.random.normal(jax.random.fold_in(_rk, 611), (32, 64, 256), jnp.float32))
        _validS = jnp.arange(64)[None, :] < _lenS[:, None]
        _validS2 = jnp.arange(64)[None, :] < _lenS2[:, None]
        _causal = jnp.tril(jnp.ones((64, 64), dtype=bool))
        mask_1x1xSxS2_fc1 = jnp.where(jnp.broadcast_to(_validS2[0:1, None, None, :], (1, 1, 64, 64)), 1.0, 0.0).astype(jnp.float32)
        mask_Bx1xSxS2_ff1 = jnp.where(jnp.ones((32, 1, 64, 64), dtype=bool), 1.0, 0.0).astype(jnp.float32)
        mask_BxS2_ik0 = jnp.where(jnp.broadcast_to(_validS2[:, :], (32, 64)), 0, 1).astype(jnp.int32)
        return (x, ctx_2048, mask_1x1xSxS2_fc1, mask_Bx1xSxS2_ff1, mask_BxS2_ik0)
    x, ctx_2048, mask_1x1xSxS2_fc1, mask_Bx1xSxS2_ff1, mask_BxS2_ik0 = _rec_inputs()

    def _L0_xattn_setup():
        import jax, jax.numpy as jnp
        import numpy as np
        H = 256
        NH = 16
        HD = H // NH
        EPS = 1e-05

        def gelu(x):
            return 0.5 * x * (1.0 + jnp.tanh(0.7978845608028654 * x * (1.0 + 0.044715 * x * x)))

        def layernorm(x, scale, bias):
            m = jnp.mean(x, axis=-1, keepdims=True)
            v = jnp.mean(jnp.square(x - m), axis=-1, keepdims=True)
            return (x - m) * jax.lax.rsqrt(v + EPS) * scale + bias

        def split_heads(x):
            b, s, _ = x.shape
            return x.reshape(b, s, NH, HD).transpose(0, 2, 1, 3)

        def merge_heads(x):
            b, nh, s, hd = x.shape
            return x.transpose(0, 2, 1, 3).reshape(b, s, nh * hd)

        def attention(q, k, v, mask):
            scores = jnp.einsum('bhqd,bhkd->bhqk', q, k) / jnp.sqrt(jnp.float32(HD))
            scores = scores * mask - 10000.0 * (1.0 - mask)
            probs = jax.nn.softmax(scores, axis=-1)
            return jnp.einsum('bhqk,bhkd->bhqd', probs, v)
        key = jax.random.key(seed)
        ks = jax.random.split(key, 16)
        b, s, t = (2, 128, 128)
        w = lambda k, i, o: jax.random.normal(k, (i, o), jnp.float32) * 0.02
        inp = {'hidden_states': jax.random.normal(ks[0], (b, s, H), jnp.float32), 'encoder_states': jax.random.normal(ks[1], (b, t, H), jnp.float32), 'ltor_mask': jnp.tril(jnp.ones((1, 1, s, s), jnp.float32)), 'cross_mask': jnp.ones((b, 1, s, t), jnp.float32), 'ln1_s': jnp.ones((H,), jnp.float32), 'ln1_b': jnp.zeros((H,), jnp.float32), 'w_qkv': w(ks[2], H, 3 * H), 'b_qkv': jnp.zeros((3 * H,), jnp.float32), 'w_ao': w(ks[3], H, H), 'b_ao': jnp.zeros((H,), jnp.float32), 'ln2_s': jnp.ones((H,), jnp.float32), 'ln2_b': jnp.zeros((H,), jnp.float32), 'w_q': w(ks[4], H, H), 'b_q': jnp.zeros((H,), jnp.float32), 'w_kv': w(ks[5], H, 2 * H), 'b_kv': jnp.zeros((2 * H,), jnp.float32), 'w_co': w(ks[6], H, H), 'b_co': jnp.zeros((H,), jnp.float32), 'ln3_s': jnp.ones((H,), jnp.float32), 'ln3_b': jnp.zeros((H,), jnp.float32), 'w1': w(ks[7], H, 4 * H), 'b1': jnp.zeros((4 * H,), jnp.float32), 'w2': w(ks[8], 4 * H, H), 'b2': jnp.zeros((H,), jnp.float32)}
        return inp
    _L0_xattn_all = _L0_xattn_setup()
    _L0_xattn_in = {k: v for k, v in _L0_xattn_all.items() if k in ('ln1_s', 'ln1_b', 'w_qkv', 'b_qkv', 'w_ao', 'b_ao', 'ln2_s', 'ln2_b', 'w_q', 'b_q', 'w_kv', 'b_kv', 'w_co', 'b_co', 'ln3_s', 'ln3_b', 'w1', 'b1', 'w2', 'b2')}
    del _L0_xattn_all

    def _L1_xattn_setup():
        import jax, jax.numpy as jnp
        import numpy as np
        B, P, K, H, NH = (4, 256, 32, 256, 16)
        DH = H // NH
        EPS = 1e-06

        def rmsnorm(x, w):
            var = jnp.mean(jnp.square(x), axis=-1, keepdims=True)
            return x * jax.lax.rsqrt(var + EPS) * w
        key = jax.random.key(seed)
        ks = jax.random.split(key, 12)
        s = 0.02
        return {'x': jax.random.normal(ks[0], (B, P, H), jnp.float32), 'latents': jax.random.normal(ks[1], (B, K, H), jnp.float32), 'attention_mask': jax.random.randint(ks[2], (B, P), 0, 2, jnp.int32), 'q_w': s * jax.random.normal(ks[3], (H, H), jnp.float32), 'q_b': jnp.zeros((H,), jnp.float32), 'kv_w': s * jax.random.normal(ks[4], (H, 2 * H), jnp.float32), 'kv_b': jnp.zeros((2 * H,), jnp.float32), 'out_w': s * jax.random.normal(ks[5], (H, H), jnp.float32), 'out_b': jnp.zeros((H,), jnp.float32), 'postnorm_w': jnp.ones((H,), jnp.float32), 'mlp_w1': s * jax.random.normal(ks[6], (H, 4 * H), jnp.float32), 'mlp_b1': jnp.zeros((4 * H,), jnp.float32), 'mlp_w2': s * jax.random.normal(ks[7], (4 * H, H), jnp.float32), 'mlp_b2': jnp.zeros((H,), jnp.float32)}
    _L1_xattn_all = _L1_xattn_setup()
    _L1_xattn_in = {k: v for k, v in _L1_xattn_all.items() if k in ('q_w', 'q_b', 'kv_w', 'kv_b', 'out_w', 'out_b', 'postnorm_w', 'mlp_w1', 'mlp_b1', 'mlp_w2', 'mlp_b2')}
    del _L1_xattn_all

    def _L2_xattn_setup():
        import jax, jax.numpy as jnp
        import numpy as np
        B, Q, S1, S2 = (4, 32, 256, 256)
        D, H, K, F = (256, 16, 128, 1024)
        LN_EPS = 1e-05

        def _layer_norm(x, scale, offset):
            mu = jnp.mean(x, axis=-1, keepdims=True)
            var = jnp.var(x, axis=-1, keepdims=True)
            return (x - mu) * jax.lax.rsqrt(var + LN_EPS) * scale + offset

        def _cross_attention(q_in, kv_in, wq, bq, wk, bk, wv, bv, wo, bo, bias_k, bias_v):
            b, q_len, _ = q_in.shape
            t = kv_in.shape[1]
            qh = (q_in @ wq + bq).reshape(b, q_len, H, K)
            kh = (kv_in @ wk + bk).reshape(b, t, H, K)
            vh = (kv_in @ wv + bv).reshape(b, t, H, K)
            kh = jnp.concatenate([kh, jnp.broadcast_to(bias_k, (b, 1, H, K))], axis=1)
            vh = jnp.concatenate([vh, jnp.broadcast_to(bias_v, (b, 1, H, K))], axis=1)
            scale = jnp.sqrt(jnp.asarray(K, q_in.dtype))
            logits = jnp.einsum('bqhk,bthk->bhqt', qh, kh) / scale
            weights = jax.nn.softmax(logits, axis=-1)
            ctx = jnp.einsum('bhqt,bthk->bqhk', weights, vh).reshape(b, q_len, H * K)
            return ctx @ wo + bo

        def _forward(x, xf_1, xf_2, ln1_scale, ln1_offset, wq1, bq1, wk1, bk1, wv1, bv1, wo1, bo1, bias_k1, bias_v1, ln2_scale, ln2_offset, wq2, bq2, wk2, bk2, wv2, bv2, wo2, bo2, bias_k2, bias_v2, ln_mlp_scale, ln_mlp_offset, w_fc1, b_fc1, w_fc2, b_fc2):
            res = x
            h = _layer_norm(x, ln1_scale, ln1_offset)
            x = res + _cross_attention(h, xf_1, wq1, bq1, wk1, bk1, wv1, bv1, wo1, bo1, bias_k1, bias_v1)
            res = x
            h = _layer_norm(x, ln2_scale, ln2_offset)
            x = res + _cross_attention(h, xf_2, wq2, bq2, wk2, bk2, wv2, bv2, wo2, bo2, bias_k2, bias_v2)
            h = _layer_norm(x, ln_mlp_scale, ln_mlp_offset)
            h = jax.nn.gelu(h @ w_fc1 + b_fc1, approximate=False) @ w_fc2 + b_fc2
            return x + h
        key = jax.random.key(seed)
        ks = iter(jax.random.split(key, 64))

        def rn(shape, s=0.02):
            return jax.random.normal(next(ks), shape, jnp.float32) * s
        inp = {'x': rn((B, Q, D), 1.0), 'xf_1': rn((B, S1, D), 1.0), 'xf_2': rn((B, S2, D), 1.0)}
        for i in (1, 2):
            inp[f'ln{i}_scale'] = jnp.ones((D,), jnp.float32)
            inp[f'ln{i}_offset'] = jnp.zeros((D,), jnp.float32)
            inp[f'wq{i}'] = rn((D, H * K))
            inp[f'bq{i}'] = jnp.zeros((H * K,), jnp.float32)
            inp[f'wk{i}'] = rn((D, H * K))
            inp[f'bk{i}'] = jnp.zeros((H * K,), jnp.float32)
            inp[f'wv{i}'] = rn((D, H * K))
            inp[f'bv{i}'] = jnp.zeros((H * K,), jnp.float32)
            inp[f'wo{i}'] = rn((H * K, D))
            inp[f'bo{i}'] = jnp.zeros((D,), jnp.float32)
            inp[f'bias_k{i}'] = rn((1, 1, H, K))
            inp[f'bias_v{i}'] = rn((1, 1, H, K))
        inp['ln_mlp_scale'] = jnp.ones((D,), jnp.float32)
        inp['ln_mlp_offset'] = jnp.zeros((D,), jnp.float32)
        inp['w_fc1'] = rn((D, F))
        inp['b_fc1'] = jnp.zeros((F,), jnp.float32)
        inp['w_fc2'] = rn((F, D))
        inp['b_fc2'] = jnp.zeros((D,), jnp.float32)
        return inp
    _L2_xattn_all = _L2_xattn_setup()
    _L2_xattn_in = {k: v for k, v in _L2_xattn_all.items() if k in ('ln1_scale', 'ln1_offset', 'wq1', 'bq1', 'wk1', 'bk1', 'wv1', 'bv1', 'wo1', 'bo1', 'bias_k1', 'bias_v1', 'ln2_scale', 'ln2_offset', 'wq2', 'bq2', 'wk2', 'bk2', 'wv2', 'bv2', 'wo2', 'bo2', 'bias_k2', 'bias_v2', 'ln_mlp_scale', 'ln_mlp_offset', 'w_fc1', 'b_fc1', 'w_fc2', 'b_fc2')}
    del _L2_xattn_all

    def _L3_xattn_setup():
        import jax, jax.numpy as jnp
        import numpy as np
        B, L, E, H = (4, 64, 256, 32)
        S = E // H
        EXTRA_MAA, EXTRA_DECAY = (32, 64)
        EPS = 1e-05

        def _ln(x, w, b):
            m = jnp.mean(x, axis=-1, keepdims=True)
            v = jnp.mean((x - m) ** 2, axis=-1, keepdims=True)
            return (x - m) * jax.lax.rsqrt(v + EPS) * w + b

        def _token_shift(xn, prev_row):
            first = (prev_row - xn[:, 0])[:, None]
            rest = xn[:, :-1] - xn[:, 1:]
            return jnp.concatenate([first, rest], axis=1)
        key = jax.random.key(seed)
        ks = jax.random.split(key, 24)
        rn = lambda k, shp, s=1.0: jax.random.normal(k, shp, dtype=jnp.float32) * s
        return dict(x=rn(ks[0], (B, L, E)), state=rn(ks[1], (B, 2 + S, E), 0.1), ln1_w=jnp.ones((E,), jnp.float32), ln1_b=jnp.zeros((E,), jnp.float32), ln2_w=jnp.ones((E,), jnp.float32), ln2_b=jnp.zeros((E,), jnp.float32), maa_x=rn(ks[2], (E,), 0.02), maa_w1=rn(ks[3], (E, 5 * EXTRA_MAA), 0.02), maa_w2=rn(ks[4], (5, EXTRA_MAA, E), 0.02), maa_stack=rn(ks[5], (5, E), 0.02), time_decay=rn(ks[6], (E,), 0.5), decay_w1=rn(ks[7], (E, EXTRA_DECAY), 0.02), decay_w2=rn(ks[8], (EXTRA_DECAY, E), 0.02), faaaa=rn(ks[9], (H, S), 0.1), Wr=rn(ks[10], (E, E), 0.02), Wk=rn(ks[11], (E, E), 0.02), Wv=rn(ks[12], (E, E), 0.02), Wg=rn(ks[13], (E, E), 0.02), Wo=rn(ks[14], (E, E), 0.02), gn_w=jnp.ones((E,), jnp.float32), gn_b=jnp.zeros((E,), jnp.float32), ffn_maa_k=rn(ks[15], (E,), 0.02), ffn_maa_r=rn(ks[16], (E,), 0.02), ffn_Wk=rn(ks[17], (E, E), 0.02), ffn_Wr=rn(ks[18], (E, E), 0.02), ffn_Wv=rn(ks[19], (E, E), 0.02), i=0)
    _L3_xattn_all = _L3_xattn_setup()
    _L3_xattn_in = {k: v for k, v in _L3_xattn_all.items() if k in ('ln1_w', 'ln1_b', 'ln2_w', 'ln2_b', 'maa_x', 'maa_w1', 'maa_w2', 'maa_stack', 'time_decay', 'decay_w1', 'decay_w2', 'faaaa', 'Wr', 'Wk', 'Wv', 'Wg', 'Wo', 'gn_w', 'gn_b', 'ffn_maa_k', 'ffn_maa_r', 'ffn_Wk', 'ffn_Wr', 'ffn_Wv')}
    del _L3_xattn_all
    return {'x': x, 'ctx_2048': ctx_2048, 'mask_1x1xSxS2_fc1': mask_1x1xSxS2_fc1, 'mask_Bx1xSxS2_ff1': mask_Bx1xSxS2_ff1, 'mask_BxS2_ik0': mask_BxS2_ik0, 'L0_xattn_ln1_s': _L0_xattn_in['ln1_s'], 'L0_xattn_ln1_b': _L0_xattn_in['ln1_b'], 'L0_xattn_w_qkv': _L0_xattn_in['w_qkv'], 'L0_xattn_b_qkv': _L0_xattn_in['b_qkv'], 'L0_xattn_w_ao': _L0_xattn_in['w_ao'], 'L0_xattn_b_ao': _L0_xattn_in['b_ao'], 'L0_xattn_ln2_s': _L0_xattn_in['ln2_s'], 'L0_xattn_ln2_b': _L0_xattn_in['ln2_b'], 'L0_xattn_w_q': _L0_xattn_in['w_q'], 'L0_xattn_b_q': _L0_xattn_in['b_q'], 'L0_xattn_w_kv': _L0_xattn_in['w_kv'], 'L0_xattn_b_kv': _L0_xattn_in['b_kv'], 'L0_xattn_w_co': _L0_xattn_in['w_co'], 'L0_xattn_b_co': _L0_xattn_in['b_co'], 'L0_xattn_ln3_s': _L0_xattn_in['ln3_s'], 'L0_xattn_ln3_b': _L0_xattn_in['ln3_b'], 'L0_xattn_w1': _L0_xattn_in['w1'], 'L0_xattn_b1': _L0_xattn_in['b1'], 'L0_xattn_w2': _L0_xattn_in['w2'], 'L0_xattn_b2': _L0_xattn_in['b2'], 'L1_xattn_q_w': _L1_xattn_in['q_w'], 'L1_xattn_q_b': _L1_xattn_in['q_b'], 'L1_xattn_kv_w': _L1_xattn_in['kv_w'], 'L1_xattn_kv_b': _L1_xattn_in['kv_b'], 'L1_xattn_out_w': _L1_xattn_in['out_w'], 'L1_xattn_out_b': _L1_xattn_in['out_b'], 'L1_xattn_postnorm_w': _L1_xattn_in['postnorm_w'], 'L1_xattn_mlp_w1': _L1_xattn_in['mlp_w1'], 'L1_xattn_mlp_b1': _L1_xattn_in['mlp_b1'], 'L1_xattn_mlp_w2': _L1_xattn_in['mlp_w2'], 'L1_xattn_mlp_b2': _L1_xattn_in['mlp_b2'], 'L2_xattn_ln1_scale': _L2_xattn_in['ln1_scale'], 'L2_xattn_ln1_offset': _L2_xattn_in['ln1_offset'], 'L2_xattn_wq1': _L2_xattn_in['wq1'], 'L2_xattn_bq1': _L2_xattn_in['bq1'], 'L2_xattn_wk1': _L2_xattn_in['wk1'], 'L2_xattn_bk1': _L2_xattn_in['bk1'], 'L2_xattn_wv1': _L2_xattn_in['wv1'], 'L2_xattn_bv1': _L2_xattn_in['bv1'], 'L2_xattn_wo1': _L2_xattn_in['wo1'], 'L2_xattn_bo1': _L2_xattn_in['bo1'], 'L2_xattn_bias_k1': _L2_xattn_in['bias_k1'], 'L2_xattn_bias_v1': _L2_xattn_in['bias_v1'], 'L2_xattn_ln2_scale': _L2_xattn_in['ln2_scale'], 'L2_xattn_ln2_offset': _L2_xattn_in['ln2_offset'], 'L2_xattn_wq2': _L2_xattn_in['wq2'], 'L2_xattn_bq2': _L2_xattn_in['bq2'], 'L2_xattn_wk2': _L2_xattn_in['wk2'], 'L2_xattn_bk2': _L2_xattn_in['bk2'], 'L2_xattn_wv2': _L2_xattn_in['wv2'], 'L2_xattn_bv2': _L2_xattn_in['bv2'], 'L2_xattn_wo2': _L2_xattn_in['wo2'], 'L2_xattn_bo2': _L2_xattn_in['bo2'], 'L2_xattn_bias_k2': _L2_xattn_in['bias_k2'], 'L2_xattn_bias_v2': _L2_xattn_in['bias_v2'], 'L2_xattn_ln_mlp_scale': _L2_xattn_in['ln_mlp_scale'], 'L2_xattn_ln_mlp_offset': _L2_xattn_in['ln_mlp_offset'], 'L2_xattn_w_fc1': _L2_xattn_in['w_fc1'], 'L2_xattn_b_fc1': _L2_xattn_in['b_fc1'], 'L2_xattn_w_fc2': _L2_xattn_in['w_fc2'], 'L2_xattn_b_fc2': _L2_xattn_in['b_fc2'], 'L3_xattn_ln1_w': _L3_xattn_in['ln1_w'], 'L3_xattn_ln1_b': _L3_xattn_in['ln1_b'], 'L3_xattn_ln2_w': _L3_xattn_in['ln2_w'], 'L3_xattn_ln2_b': _L3_xattn_in['ln2_b'], 'L3_xattn_maa_x': _L3_xattn_in['maa_x'], 'L3_xattn_maa_w1': _L3_xattn_in['maa_w1'], 'L3_xattn_maa_w2': _L3_xattn_in['maa_w2'], 'L3_xattn_maa_stack': _L3_xattn_in['maa_stack'], 'L3_xattn_time_decay': _L3_xattn_in['time_decay'], 'L3_xattn_decay_w1': _L3_xattn_in['decay_w1'], 'L3_xattn_decay_w2': _L3_xattn_in['decay_w2'], 'L3_xattn_faaaa': _L3_xattn_in['faaaa'], 'L3_xattn_Wr': _L3_xattn_in['Wr'], 'L3_xattn_Wk': _L3_xattn_in['Wk'], 'L3_xattn_Wv': _L3_xattn_in['Wv'], 'L3_xattn_Wg': _L3_xattn_in['Wg'], 'L3_xattn_Wo': _L3_xattn_in['Wo'], 'L3_xattn_gn_w': _L3_xattn_in['gn_w'], 'L3_xattn_gn_b': _L3_xattn_in['gn_b'], 'L3_xattn_ffn_maa_k': _L3_xattn_in['ffn_maa_k'], 'L3_xattn_ffn_maa_r': _L3_xattn_in['ffn_maa_r'], 'L3_xattn_ffn_Wk': _L3_xattn_in['ffn_Wk'], 'L3_xattn_ffn_Wr': _L3_xattn_in['ffn_Wr'], 'L3_xattn_ffn_Wv': _L3_xattn_in['ffn_Wv']}

def reference(x, ctx_2048, mask_1x1xSxS2_fc1, mask_Bx1xSxS2_ff1, mask_BxS2_ik0, L0_xattn_ln1_s, L0_xattn_ln1_b, L0_xattn_w_qkv, L0_xattn_b_qkv, L0_xattn_w_ao, L0_xattn_b_ao, L0_xattn_ln2_s, L0_xattn_ln2_b, L0_xattn_w_q, L0_xattn_b_q, L0_xattn_w_kv, L0_xattn_b_kv, L0_xattn_w_co, L0_xattn_b_co, L0_xattn_ln3_s, L0_xattn_ln3_b, L0_xattn_w1, L0_xattn_b1, L0_xattn_w2, L0_xattn_b2, L1_xattn_q_w, L1_xattn_q_b, L1_xattn_kv_w, L1_xattn_kv_b, L1_xattn_out_w, L1_xattn_out_b, L1_xattn_postnorm_w, L1_xattn_mlp_w1, L1_xattn_mlp_b1, L1_xattn_mlp_w2, L1_xattn_mlp_b2, L2_xattn_ln1_scale, L2_xattn_ln1_offset, L2_xattn_wq1, L2_xattn_bq1, L2_xattn_wk1, L2_xattn_bk1, L2_xattn_wv1, L2_xattn_bv1, L2_xattn_wo1, L2_xattn_bo1, L2_xattn_bias_k1, L2_xattn_bias_v1, L2_xattn_ln2_scale, L2_xattn_ln2_offset, L2_xattn_wq2, L2_xattn_bq2, L2_xattn_wk2, L2_xattn_bk2, L2_xattn_wv2, L2_xattn_bv2, L2_xattn_wo2, L2_xattn_bo2, L2_xattn_bias_k2, L2_xattn_bias_v2, L2_xattn_ln_mlp_scale, L2_xattn_ln_mlp_offset, L2_xattn_w_fc1, L2_xattn_b_fc1, L2_xattn_w_fc2, L2_xattn_b_fc2, L3_xattn_ln1_w, L3_xattn_ln1_b, L3_xattn_ln2_w, L3_xattn_ln2_b, L3_xattn_maa_x, L3_xattn_maa_w1, L3_xattn_maa_w2, L3_xattn_maa_stack, L3_xattn_time_decay, L3_xattn_decay_w1, L3_xattn_decay_w2, L3_xattn_faaaa, L3_xattn_Wr, L3_xattn_Wk, L3_xattn_Wv, L3_xattn_Wg, L3_xattn_Wo, L3_xattn_gn_w, L3_xattn_gn_b, L3_xattn_ffn_maa_k, L3_xattn_ffn_maa_r, L3_xattn_ffn_Wk, L3_xattn_ffn_Wr, L3_xattn_ffn_Wv):
    import jax
    import jax.numpy as jnp

    def _L0_xattn_ref(hidden_states, encoder_states, ltor_mask, cross_mask, ln1_s, ln1_b, w_qkv, b_qkv, w_ao, b_ao, ln2_s, ln2_b, w_q, b_q, w_kv, b_kv, w_co, b_co, ln3_s, ln3_b, w1, b1, w2, b2):
        import jax, jax.numpy as jnp
        import numpy as np
        H = 256
        NH = 16
        HD = H // NH
        EPS = 1e-05

        def gelu(x):
            return 0.5 * x * (1.0 + jnp.tanh(0.7978845608028654 * x * (1.0 + 0.044715 * x * x)))

        def layernorm(x, scale, bias):
            m = jnp.mean(x, axis=-1, keepdims=True)
            v = jnp.mean(jnp.square(x - m), axis=-1, keepdims=True)
            return (x - m) * jax.lax.rsqrt(v + EPS) * scale + bias

        def split_heads(x):
            b, s, _ = x.shape
            return x.reshape(b, s, NH, HD).transpose(0, 2, 1, 3)

        def merge_heads(x):
            b, nh, s, hd = x.shape
            return x.transpose(0, 2, 1, 3).reshape(b, s, nh * hd)

        def attention(q, k, v, mask):
            scores = jnp.einsum('bhqd,bhkd->bhqk', q, k) / jnp.sqrt(jnp.float32(HD))
            scores = scores * mask - 10000.0 * (1.0 - mask)
            probs = jax.nn.softmax(scores, axis=-1)
            return jnp.einsum('bhqk,bhkd->bhqd', probs, v)
        ln_out = layernorm(hidden_states, ln1_s, ln1_b)
        qkv = ln_out @ w_qkv + b_qkv
        q, k, v = jnp.split(qkv, 3, axis=-1)
        ctx = merge_heads(attention(split_heads(q), split_heads(k), split_heads(v), ltor_mask))
        attn_out = ctx @ w_ao + b_ao
        x = hidden_states + attn_out
        ln_out = layernorm(x, ln2_s, ln2_b)
        q = ln_out @ w_q + b_q
        kv = encoder_states @ w_kv + b_kv
        k, v = jnp.split(kv, 2, axis=-1)
        ctx = merge_heads(attention(split_heads(q), split_heads(k), split_heads(v), cross_mask))
        cross_out = ctx @ w_co + b_co
        x = x + cross_out
        ln_out = layernorm(x, ln3_s, ln3_b)
        mlp_out = gelu(ln_out @ w1 + b1) @ w2 + b2
        return x + mlp_out

    def _L1_xattn_ref(x, latents, attention_mask, q_w, q_b, kv_w, kv_b, out_w, out_b, postnorm_w, mlp_w1, mlp_b1, mlp_w2, mlp_b2):
        import jax, jax.numpy as jnp
        import numpy as np
        B, P, K, H, NH = (4, 256, 32, 256, 16)
        DH = H // NH
        EPS = 1e-06

        def rmsnorm(x, w):
            var = jnp.mean(jnp.square(x), axis=-1, keepdims=True)
            return x * jax.lax.rsqrt(var + EPS) * w
        b, p, _ = x.shape
        k_len = latents.shape[1]
        residual = latents
        h = jnp.concatenate([x, latents], axis=1)
        q = (latents @ q_w + q_b).reshape(b, k_len, NH, DH)
        kv = (h @ kv_w + kv_b).reshape(b, p + k_len, NH, DH, 2)
        kmat, v = (kv[..., 0], kv[..., 1])
        attn = jnp.einsum('bkhd,bnhd->bhkn', q, kmat) / DH
        full_mask = jnp.concatenate([attention_mask.astype(bool), jnp.ones((b, k_len), bool)], axis=-1)
        attn = jnp.where(full_mask[:, None, None, :], attn, -jnp.inf)
        attn = jax.nn.softmax(attn.astype(jnp.float32), axis=-1).astype(q.dtype)
        attn_out = jnp.einsum('bhkn,bnhd->bkhd', attn, v).reshape(b, k_len, H)
        attn_out = attn_out @ out_w + out_b + residual
        out = rmsnorm(attn_out, postnorm_w)
        out = jax.nn.gelu(out @ mlp_w1 + mlp_b1) @ mlp_w2 + mlp_b2
        return out + residual

    def _L2_xattn_ref(x, xf_1, xf_2, ln1_scale, ln1_offset, wq1, bq1, wk1, bk1, wv1, bv1, wo1, bo1, bias_k1, bias_v1, ln2_scale, ln2_offset, wq2, bq2, wk2, bk2, wv2, bv2, wo2, bo2, bias_k2, bias_v2, ln_mlp_scale, ln_mlp_offset, w_fc1, b_fc1, w_fc2, b_fc2):
        import jax, jax.numpy as jnp
        import numpy as np
        B, Q, S1, S2 = (4, 32, 256, 256)
        D, H, K, F = (256, 16, 128, 1024)
        LN_EPS = 1e-05

        def _layer_norm(x, scale, offset):
            mu = jnp.mean(x, axis=-1, keepdims=True)
            var = jnp.var(x, axis=-1, keepdims=True)
            return (x - mu) * jax.lax.rsqrt(var + LN_EPS) * scale + offset

        def _cross_attention(q_in, kv_in, wq, bq, wk, bk, wv, bv, wo, bo, bias_k, bias_v):
            b, q_len, _ = q_in.shape
            t = kv_in.shape[1]
            qh = (q_in @ wq + bq).reshape(b, q_len, H, K)
            kh = (kv_in @ wk + bk).reshape(b, t, H, K)
            vh = (kv_in @ wv + bv).reshape(b, t, H, K)
            kh = jnp.concatenate([kh, jnp.broadcast_to(bias_k, (b, 1, H, K))], axis=1)
            vh = jnp.concatenate([vh, jnp.broadcast_to(bias_v, (b, 1, H, K))], axis=1)
            scale = jnp.sqrt(jnp.asarray(K, q_in.dtype))
            logits = jnp.einsum('bqhk,bthk->bhqt', qh, kh) / scale
            weights = jax.nn.softmax(logits, axis=-1)
            ctx = jnp.einsum('bhqt,bthk->bqhk', weights, vh).reshape(b, q_len, H * K)
            return ctx @ wo + bo

        def _forward(x, xf_1, xf_2, ln1_scale, ln1_offset, wq1, bq1, wk1, bk1, wv1, bv1, wo1, bo1, bias_k1, bias_v1, ln2_scale, ln2_offset, wq2, bq2, wk2, bk2, wv2, bv2, wo2, bo2, bias_k2, bias_v2, ln_mlp_scale, ln_mlp_offset, w_fc1, b_fc1, w_fc2, b_fc2):
            res = x
            h = _layer_norm(x, ln1_scale, ln1_offset)
            x = res + _cross_attention(h, xf_1, wq1, bq1, wk1, bk1, wv1, bv1, wo1, bo1, bias_k1, bias_v1)
            res = x
            h = _layer_norm(x, ln2_scale, ln2_offset)
            x = res + _cross_attention(h, xf_2, wq2, bq2, wk2, bk2, wv2, bv2, wo2, bo2, bias_k2, bias_v2)
            h = _layer_norm(x, ln_mlp_scale, ln_mlp_offset)
            h = jax.nn.gelu(h @ w_fc1 + b_fc1, approximate=False) @ w_fc2 + b_fc2
            return x + h
        return _forward(x, xf_1, xf_2, ln1_scale, ln1_offset, wq1, bq1, wk1, bk1, wv1, bv1, wo1, bo1, bias_k1, bias_v1, ln2_scale, ln2_offset, wq2, bq2, wk2, bk2, wv2, bv2, wo2, bo2, bias_k2, bias_v2, ln_mlp_scale, ln_mlp_offset, w_fc1, b_fc1, w_fc2, b_fc2)

    def _L3_xattn_ref(x, state, ln1_w, ln1_b, ln2_w, ln2_b, maa_x, maa_w1, maa_w2, maa_stack, time_decay, decay_w1, decay_w2, faaaa, Wr, Wk, Wv, Wg, Wo, gn_w, gn_b, ffn_maa_k, ffn_maa_r, ffn_Wk, ffn_Wr, ffn_Wv, i):
        import jax, jax.numpy as jnp
        import numpy as np
        B, L, E, H = (4, 64, 256, 32)
        S = E // H
        EXTRA_MAA, EXTRA_DECAY = (32, 64)
        EPS = 1e-05

        def _ln(x, w, b):
            m = jnp.mean(x, axis=-1, keepdims=True)
            v = jnp.mean((x - m) ** 2, axis=-1, keepdims=True)
            return (x - m) * jax.lax.rsqrt(v + EPS) * w + b

        def _token_shift(xn, prev_row):
            first = (prev_row - xn[:, 0])[:, None]
            rest = xn[:, :-1] - xn[:, 1:]
            return jnp.concatenate([first, rest], axis=1)
        b, l = (x.shape[0], x.shape[1])
        i0 = (2 + S) * i + 0
        i1 = (2 + S) * i + 1
        xn = _ln(x, ln1_w, ln1_b)
        sx = _token_shift(xn, state[:, i1])
        xxx = jnp.tanh((xn + sx * maa_x) @ maa_w1).reshape(b, l, 5, 1, EXTRA_MAA)
        xxx = jnp.matmul(xxx, maa_w2).reshape(b, l, 5, E)
        x5 = xn[:, :, None] + sx[:, :, None] * (maa_stack + xxx)
        w = jnp.exp(-jnp.exp(time_decay + jnp.tanh(x5[:, :, 1] @ decay_w1) @ decay_w2))
        w = w.reshape(b, l, H, S)
        r = (x5[:, :, 3] @ Wr.T).reshape(b, l, H, S)
        k = (x5[:, :, 0] @ Wk.T).reshape(b, l, H, S)
        v = (x5[:, :, 2] @ Wv.T).reshape(b, l, H, S)
        g = jax.nn.silu(x5[:, :, 4] @ Wg.T)
        s0 = state[:, (2 + S) * i + 2:(2 + S) * (i + 1)].reshape(b, H, S, S)
        u = faaaa[None, :, :, None]

        def step(s, rkvw):
            r_t, k_t, v_t, w_t = rkvw
            a = k_t[:, :, :, None] * v_t[:, :, None, :]
            out = jnp.einsum('bhk,bhkd->bhd', r_t, u * a + s)
            return (a + w_t[:, :, :, None] * s, out)
        xs = tuple((jnp.moveaxis(t, 1, 0) for t in (r, k, v, w)))
        _, outs = jax.lax.scan(step, s0, xs)
        att = jnp.moveaxis(outs, 0, 1).reshape(b, l, E)
        a4 = att.reshape(b, l, H, S)
        m = jnp.mean(a4, axis=-1, keepdims=True)
        var = jnp.mean((a4 - m) ** 2, axis=-1, keepdims=True)
        att = ((a4 - m) * jax.lax.rsqrt(var + EPS)).reshape(b, l, E) * gn_w + gn_b
        x = x + att * g @ Wo.T
        xn2 = _ln(x, ln2_w, ln2_b)
        sx2 = _token_shift(xn2, state[:, i0])
        xk = xn2 + sx2 * ffn_maa_k
        xr = xn2 + sx2 * ffn_maa_r
        rr = jax.nn.sigmoid(xr @ ffn_Wr.T)
        kk = jnp.square(jax.nn.relu(xk @ ffn_Wk.T))
        x = x + rr * (kk @ ffn_Wv.T)
        return x
    x = _L0_xattn_ref(x, ctx_2048, mask_1x1xSxS2_fc1, mask_Bx1xSxS2_ff1, L0_xattn_ln1_s, L0_xattn_ln1_b, L0_xattn_w_qkv, L0_xattn_b_qkv, L0_xattn_w_ao, L0_xattn_b_ao, L0_xattn_ln2_s, L0_xattn_ln2_b, L0_xattn_w_q, L0_xattn_b_q, L0_xattn_w_kv, L0_xattn_b_kv, L0_xattn_w_co, L0_xattn_b_co, L0_xattn_ln3_s, L0_xattn_ln3_b, L0_xattn_w1, L0_xattn_b1, L0_xattn_w2, L0_xattn_b2)
    x = _L1_xattn_ref(ctx_2048, x, mask_BxS2_ik0, L1_xattn_q_w, L1_xattn_q_b, L1_xattn_kv_w, L1_xattn_kv_b, L1_xattn_out_w, L1_xattn_out_b, L1_xattn_postnorm_w, L1_xattn_mlp_w1, L1_xattn_mlp_b1, L1_xattn_mlp_w2, L1_xattn_mlp_b2)
    x = _L2_xattn_ref(x, ctx_2048, ctx_2048, L2_xattn_ln1_scale, L2_xattn_ln1_offset, L2_xattn_wq1, L2_xattn_bq1, L2_xattn_wk1, L2_xattn_bk1, L2_xattn_wv1, L2_xattn_bv1, L2_xattn_wo1, L2_xattn_bo1, L2_xattn_bias_k1, L2_xattn_bias_v1, L2_xattn_ln2_scale, L2_xattn_ln2_offset, L2_xattn_wq2, L2_xattn_bq2, L2_xattn_wk2, L2_xattn_bk2, L2_xattn_wv2, L2_xattn_bv2, L2_xattn_wo2, L2_xattn_bo2, L2_xattn_bias_k2, L2_xattn_bias_v2, L2_xattn_ln_mlp_scale, L2_xattn_ln_mlp_offset, L2_xattn_w_fc1, L2_xattn_b_fc1, L2_xattn_w_fc2, L2_xattn_b_fc2)
    x = _L3_xattn_ref(x, ctx_2048, L3_xattn_ln1_w, L3_xattn_ln1_b, L3_xattn_ln2_w, L3_xattn_ln2_b, L3_xattn_maa_x, L3_xattn_maa_w1, L3_xattn_maa_w2, L3_xattn_maa_stack, L3_xattn_time_decay, L3_xattn_decay_w1, L3_xattn_decay_w2, L3_xattn_faaaa, L3_xattn_Wr, L3_xattn_Wk, L3_xattn_Wv, L3_xattn_Wg, L3_xattn_Wo, L3_xattn_gn_w, L3_xattn_gn_b, L3_xattn_ffn_maa_k, L3_xattn_ffn_maa_r, L3_xattn_ffn_Wk, L3_xattn_ffn_Wr, L3_xattn_ffn_Wv, 0)
    return x

_drawn_inputs = setup_inputs


def setup_inputs(seed=0):
    import zlib

    import numpy as np

    out = dict(_drawn_inputs(seed))
    spreads = {'L0_xattn_ln1_s': (1.0, 0.6),
     'L0_xattn_ln1_b': (0.0, 0.789),
     'L0_xattn_b_qkv': (0.0, 0.283),
     'L0_xattn_b_ao': (0.0, 0.1),
     'L0_xattn_ln2_s': (1.0, 0.6),
     'L0_xattn_ln2_b': (0.0, 2.0),
     'L0_xattn_b_q': (0.0, 2.0),
     'L0_xattn_b_kv': (0.0, 0.291),
     'L0_xattn_b_co': (0.0, 0.1),
     'L0_xattn_ln3_s': (1.0, 0.6),
     'L0_xattn_ln3_b': (0.0, 0.685),
     'L0_xattn_b1': (0.0, 0.1),
     'L0_xattn_b2': (0.0, 0.1),
     'L1_xattn_q_b': (0.0, 0.8),
     'L1_xattn_kv_b': (0.0, 0.8),
     'L1_xattn_out_b': (0.0, 0.8),
     'L1_xattn_postnorm_w': (1.0, 0.6),
     'L1_xattn_mlp_b1': (0.0, 0.1),
     'L1_xattn_mlp_b2': (0.0, 0.1),
     'L2_xattn_ln1_scale': (1.0, 0.6),
     'L2_xattn_ln1_offset': (0.0, 0.8),
     'L2_xattn_bq1': (0.0, 0.8),
     'L2_xattn_bk1': (0.0, 2.0),
     'L2_xattn_bv1': (0.0, 0.1),
     'L2_xattn_bo1': (0.0, 0.1),
     'L2_xattn_ln2_scale': (1.0, 0.6),
     'L2_xattn_ln2_offset': (0.0, 0.8),
     'L2_xattn_bq2': (0.0, 0.8),
     'L2_xattn_bk2': (0.0, 2.0),
     'L2_xattn_bv2': (0.0, 0.1),
     'L2_xattn_bo2': (0.0, 0.1),
     'L2_xattn_ln_mlp_scale': (1.0, 0.6),
     'L2_xattn_ln_mlp_offset': (0.0, 0.8),
     'L2_xattn_b_fc1': (0.0, 0.1),
     'L2_xattn_b_fc2': (0.0, 0.1),
     'L3_xattn_ln1_w': (1.0, 0.559),
     'L3_xattn_ln1_b': (0.0, 0.545),
     'L3_xattn_ln2_w': (1.0, 0.6),
     'L3_xattn_ln2_b': (0.0, 0.8),
     'L3_xattn_gn_w': (1.0, 0.6),
     'L3_xattn_gn_b': (0.0, 0.8)}
    factors = {'L0_xattn_w_qkv': 3.224,
     'L0_xattn_w_q': 8.0,
     'L1_xattn_q_w': 8.0,
     'L1_xattn_kv_w': 8.0,
     'L1_xattn_out_w': 8.0,
     'L2_xattn_wq1': 8.0,
     'L2_xattn_wk1': 8.0,
     'L2_xattn_bias_k1': 64.0,
     'L2_xattn_bias_v1': 52.321,
     'L2_xattn_wq2': 8.0,
     'L2_xattn_wk2': 8.0,
     'L2_xattn_bias_k2': 64.0,
     'L2_xattn_bias_v2': 63.794,
     'L3_xattn_maa_x': 8.0,
     'L3_xattn_maa_w1': 8.0,
     'L3_xattn_maa_w2': 8.0,
     'L3_xattn_maa_stack': 8.0,
     'L3_xattn_time_decay': 2.76,
     'L3_xattn_decay_w1': 8.0,
     'L3_xattn_decay_w2': 8.0,
     'L3_xattn_faaaa': 5.884,
     'L3_xattn_ffn_maa_k': 8.0,
     'L3_xattn_ffn_maa_r': 8.0,
     'L3_xattn_ffn_Wk': 2.957,
     'L3_xattn_ffn_Wr': 8.0,
     'L3_xattn_ffn_Wv': 2.725}
    for name, (base, spread) in spreads.items():
        noise = np.random.default_rng([zlib.crc32(name.encode()), seed]).standard_normal(out[name].shape)
        drawn = base * np.exp(spread * noise) if base else spread * noise
        out[name] = jnp.asarray(drawn.astype(out[name].dtype))
    for name, factor in factors.items():
        out[name] = (out[name] * factor).astype(out[name].dtype)
    return out
```

```python
import numpy as np
from contextlib import ExitStack

import concourse.bass as bass
from concourse import mybir

F32 = mybir.dt.float32
I32 = mybir.dt.int32
ALU = mybir.AluOpType
ACT = mybir.ActivationFunctionType
AX = mybir.AxisListType

BATCH, SEQ, DIM = 32, 64, 256
P = 128
PER_TILE = P // SEQ
TILES = BATCH // PER_TILE
ROUNDS = TILES // 2
DC = DIM // P
HIDDEN = 4 * DIM
HC = HIDDEN // P
HEADS, HEAD = 16, 16
PAIRS = HEADS // 2
MASKED = 10000.0
MINUS_INF = -1.0e30
BANK = 512


class Links:

    def __init__(self, sem, engine, per_round):
        self.sem, self.engine, self.per_round, self.n = sem, engine, per_round, 0

    def mark(self, instruction):
        self.n += 1
        return instruction.then_inc(self.sem, 1)

    def wait(self, i):
        self.engine.wait_ge(self.sem, i * self.per_round + self.n)

    def check(self):
        assert self.n == self.per_round, f"links per round: {self.n}, stated {self.per_round}"


def count(i, per_round, k):
    return i * per_round + k + 1


def cleared(nc, semaphores):
    with nc.Block() as block:
        @block.sync
        def _(sp):
            for sem in semaphores:
                sp.sem_clear(sem)

LN_EPS = 1e-5

L0_WEIGHTS = {"l0_w_qkv": (DIM, 3 * DIM), "l0_w_ao": (DIM, DIM), "l0_w_q": (DIM, DIM), "l0_w_kv": (DIM, 2 * DIM),
              "l0_w_co": (DIM, DIM), "l0_w1": (DIM, HIDDEN), "l0_w2": (HIDDEN, DIM)}

COLS = {}
for _n in (1, 2, 3):
    COLS[f"l0_ln{_n}_s"] = (f"L0_xattn_ln{_n}_s", 0, DIM)
    COLS[f"l0_ln{_n}_b"] = (f"L0_xattn_ln{_n}_b", 0, DIM)
COLS["l0_bq0"] = ("L0_xattn_b_qkv", 0, DIM)
COLS["l0_bk0"] = ("L0_xattn_b_qkv", DIM, DIM)
COLS["l0_bv0"] = ("L0_xattn_b_qkv", 2 * DIM, DIM)
COLS["l0_bq1"] = ("L0_xattn_b_q", 0, DIM)
COLS["l0_bk1"] = ("L0_xattn_b_kv", 0, DIM)
COLS["l0_bv1"] = ("L0_xattn_b_kv", DIM, DIM)
COLS["l0_b1"] = ("L0_xattn_b1", 0, HIDDEN)
ROWS = {"l0_b_ao": "L0_xattn_b_ao", "l0_b_co": "L0_xattn_b_co", "l0_b2": "L0_xattn_b2"}
RMS_EPS = 1e-6
L1_WEIGHTS = {"l1_q_w": (DIM, DIM), "l1_k_w": (DIM, DIM), "l1_v_w": (DIM, DIM), "l1_out_w": (DIM, DIM),
              "l1_mlp_w1": (DIM, HIDDEN), "l1_mlp_w2": (HIDDEN, DIM)}
COLS["l1_bq"] = ("L1_xattn_q_b", 0, DIM)
COLS["l1_bk"] = ("l1_k_b", 0, DIM)
COLS["l1_bv"] = ("l1_v_b", 0, DIM)
COLS["l1_postnorm_w"] = ("L1_xattn_postnorm_w", 0, DIM)
COLS["l1_b1"] = ("L1_xattn_mlp_b1", 0, HIDDEN)
ROWS["l1_out_b"] = "L1_xattn_out_b"
ROWS["l1_mlp_b2"] = "L1_xattn_mlp_b2"
WIDE = 128
L2_VECTOR_LINKS = 12 + 2 * HEADS * 4
L2_WEIGHTS = {}
for _a in (1, 2):
    L2_WEIGHTS |= {f"l2_wo{_a}": (HEADS * WIDE, DIM)}
for _a in (1, 2):
    L2_WEIGHTS |= {f"l2_wv{_a}": (DIM, HEADS * WIDE), f"l2_wq{_a}": (DIM, HEADS * WIDE), f"l2_wk{_a}": (DIM, HEADS * WIDE)}
    COLS[f"l2_bq{_a}"] = (f"L2_xattn_bq{_a}", 0, HEADS * WIDE)
    COLS[f"l2_bk{_a}"] = (f"L2_xattn_bk{_a}", 0, HEADS * WIDE)
    COLS[f"l2_bv{_a}"] = (f"L2_xattn_bv{_a}", 0, HEADS * WIDE)
    COLS[f"l2_bias_k{_a}"] = (f"L2_xattn_bias_k{_a}", 0, HEADS * WIDE)
    COLS[f"l2_bias_v{_a}"] = (f"L2_xattn_bias_v{_a}", 0, HEADS * WIDE)
    ROWS[f"l2_bo{_a}"] = f"L2_xattn_bo{_a}"
L2_WEIGHTS |= {"l2_w_fc1": (DIM, HIDDEN), "l2_w_fc2": (HIDDEN, DIM)}
for _n, _name in enumerate(("ln1", "ln2", "ln_mlp")):
    COLS[f"l2_ln{_n}_s"] = (f"L2_xattn_{_name}_scale", 0, DIM)
    COLS[f"l2_ln{_n}_b"] = (f"L2_xattn_{_name}_offset", 0, DIM)
COLS["l2_b_fc1"] = ("L2_xattn_b_fc1", 0, HIDDEN)
ROWS["l2_b_fc2"] = "L2_xattn_b_fc2"
HEAD8 = 8
LORA, DECAY = 32, 64
L3_VECTOR_LINKS = 23
L3_SCALAR_LINKS = 1
L3_WEIGHTS = {"l3_maa_w1": (DIM, 5 * LORA), "l3_maa_w2": (DIM, DIM), "l3_decay_w1": (DIM, DECAY), "l3_decay_w2": (P, DIM)}
L3_WEIGHTS |= {f"l3_{_n}": (DIM, DIM) for _n in ("Wk", "Wv", "Wr", "Wg", "Wo", "ffn_Wk", "ffn_Wr", "ffn_Wv")}
for _n in (1, 2):
    COLS[f"l3_ln{_n}_w"] = (f"L3_xattn_ln{_n}_w", 0, DIM)
    COLS[f"l3_ln{_n}_b"] = (f"L3_xattn_ln{_n}_b", 0, DIM)
for _n in ("maa_x", "time_decay", "faaaa", "gn_w", "gn_b", "ffn_maa_k", "ffn_maa_r"):
    COLS[f"l3_{_n}"] = (f"L3_xattn_{_n}", 0, DIM)
COLS["l3_maa_stack"] = ("L3_xattn_maa_stack", 0, 5 * DIM)
COL_AT, NCOLS = {}, 0
for _n, (_, _, _length) in COLS.items():
    COL_AT[_n] = NCOLS
    NCOLS += _length // P
ROW_NAMES = list(ROWS)
NROWS = len(ROWS)


def decoder_layer(nc, x_in, ctx, self_mask, cross_mask, x_out, w, col, row, ident, parity):
    with ExitStack() as held:
        semaphores, running = [], ExitStack()

        def sb(name, shape, dtype=F32):
            return held.enter_context(nc.sbuf_tensor("l0_" + name, shape, dtype))

        def sem(name):
            semaphores.append(held.enter_context(nc.semaphore("l0_" + name)))
            return semaphores[-1]

        x_tile = [sb(f"x_tile{s}", [P, DIM]) for s in range(2)]
        c_tile = [sb(f"c_tile{s}", [P, DIM]) for s in range(2)]
        mask1 = sb("mask1", [P, SEQ])
        mask2 = [sb(f"mask2_{s}", [P, SEQ]) for s in range(2)]
        bias1 = sb("bias1", [P, SEQ])
        bias2 = [sb(f"bias2_{s}", [P, SEQ]) for s in range(2)]
        stats = [sb(f"stats{s}", [P, 6]) for s in range(2)]
        mean_var = [sb(f"mean_var{s}", [P, 2]) for s in range(2)]
        var_eps = [sb(f"var_eps{s}", [P, 1]) for s in range(2)]
        rstd = [sb(f"rstd{s}", [P, 1]) for s in range(2)]
        pad = [sb(f"pad{s}", [P, 1]) for s in range(2)]
        minus_half = sb("minus_half", [P, 1])
        xn = [sb(f"xn{s}", [P, DIM]) for s in range(2)]
        hT = [sb(f"hT{s}", [P, DC, P]) for s in range(2)]
        cT = [sb(f"cT{s}", [P, DC, P]) for s in range(2)]
        qT = [sb(f"qT{s}", [P, DC, P]) for s in range(2)]
        kT = [sb(f"kT{s}", [P, DC, 2, P]) for s in range(2)]
        vp = [sb(f"vp{s}", [P, PER_TILE, PAIRS, 2, HEAD + 1]) for s in range(2)]
        probs = [sb(f"probs{s}", [P, 4, 2 * DC, SEQ]) for s in range(2)]
        row_max = [sb(f"row_max{s}", [P, HEADS]) for s in range(2)]
        pT = [sb(f"pT{s}", [P, PAIRS, P]) for s in range(2)]
        inv_sum = [sb(f"inv_sum{s}", [P, HEADS]) for s in range(2)]
        att = [sb(f"att{s}", [P, DIM]) for s in range(2)]
        aT = [sb(f"aT{s}", [P, DC, P]) for s in range(2)]
        res = [sb(f"res{s}", [P, DIM]) for s in range(2)]
        res_b = [sb(f"res_b{s}", [P, DIM]) for s in range(2)]
        hidT = [sb(f"hidT{s}", [P, HC, P]) for s in range(2)]
        y_out = [sb(f"y_out{s}", [P, DIM]) for s in range(2)]
        ps_s = held.enter_context(nc.psum_tensor("l0_ps_s", [P, 4, BANK], F32))
        ps_a = [held.enter_context(nc.psum_tensor(f"l0_ps_a{s}", [P, BANK], F32)) for s in range(2)]
        ps_b = [held.enter_context(nc.psum_tensor(f"l0_ps_b{s}", [P, BANK], F32)) for s in range(2)]

        x_loaded = [sem(f"x_loaded{s}") for s in range(2)]
        c_loaded = [sem(f"c_loaded{s}") for s in range(2)]
        mask2_loaded = [sem(f"mask2_loaded{s}") for s in range(2)]
        mask1_loaded = sem("mask1_loaded")
        stored = [sem(f"stored{s}") for s in range(2)]
        set_up = sem("set_up")
        vector_set_up = sem("vector_set_up")
        vector_step = sem("vector_step")
        var_ready = sem("var_ready")
        rstd_ready = sem("rstd_ready")
        xn_ready = sem("xn_ready")
        xT_ready = sem("xT_ready")
        hT_ready = sem("hT_ready")
        cT_in_psum = sem("cT_in_psum")
        cT_ready = sem("cT_ready")
        k_in_psum = sem("k_in_psum")
        qv_in_psum = sem("qv_in_psum")
        q_ready = sem("q_ready")
        k_ready = sem("k_ready")
        v_ready = sem("v_ready")
        s_in_psum = sem("s_in_psum")
        s_masked = sem("s_masked")
        shifted = sem("shifted")
        p_ready = sem("p_ready")
        pT_in_psum = sem("pT_in_psum")
        pT_lo_ready = sem("pT_lo_ready")
        pT_hi_ready = sem("pT_hi_ready")
        o_in_psum = sem("o_in_psum")
        att_ready = sem("att_ready")
        aT_in_psum = sem("aT_in_psum")
        aT_ready = sem("aT_ready")
        y_in_psum = sem("y_in_psum")
        res_ready = sem("res_ready")
        res_b_ready = sem("res_b_ready")
        y_ready = sem("y_ready")
        hid_in_psum = sem("hid_in_psum")
        hid_ready = sem("hid_ready")

        wq = [w["l0_w_qkv"][:, :, 0:DIM], w["l0_w_q"][:, :, :]]
        wk = [w["l0_w_qkv"][:, :, DIM:2 * DIM], w["l0_w_kv"][:, :, 0:DIM]]
        wv = [w["l0_w_qkv"][:, :, 2 * DIM:3 * DIM], w["l0_w_kv"][:, :, DIM:2 * DIM]]
        wo = [w["l0_w_ao"], w["l0_w_co"]]
        w1, w2 = w["l0_w1"], w["l0_w2"]
        scale = HEAD ** -0.5
        VECTOR_LINKS = 26

        block = running.enter_context(nc.Block())

        @block.sync
        def _(sp):
            for b in range(PER_TILE):
                sp.dma_start(mask1[b * SEQ:(b + 1) * SEQ, :], self_mask).then_inc(mask1_loaded, 16)
            for s in range(2):
                sp.dma_start(x_tile[s][:], x_in[bass.ts(s, P), :]).then_inc(x_loaded[s], 16)
                sp.dma_start(c_tile[s][:], ctx[bass.ts(s, P), :]).then_inc(c_loaded[s], 16)
                sp.dma_start(mask2[s][:], cross_mask[bass.ts(s, P), :]).then_inc(mask2_loaded[s], 16)
                sp.sem_inc(stored[s], 16)

            def store(i, s):
                sp.wait_ge(y_ready, count(i, 2, s))
                sp.nop()
                sp.dma_start(x_out[bass.ds(i * 2 * P + s * P, P), :], y_out[s][:]).then_inc(stored[s], 16)

            with sp.Fori(0, ROUNDS - 1) as i:
                for s in range(2):
                    sp.wait_ge(res_b_ready, count(i, 6, s))
                    sp.wait_ge(xn_ready, count(i, 6, s))
                    sp.nop()
                    sp.dma_start(x_tile[s][:], x_in[bass.ds(i * 2 * P + (s + 2) * P, P), :]).then_inc(x_loaded[s], 16)
                    sp.wait_ge(cT_in_psum, count(i, 2, s))
                    sp.nop()
                    sp.dma_start(c_tile[s][:], ctx[bass.ds(i * 2 * P + (s + 2) * P, P), :]).then_inc(c_loaded[s], 16)
                for s in range(2):
                    sp.wait_ge(s_masked, count(i, 4, 2 + s))
                    sp.nop()
                    sp.dma_start(mask2[s][:], cross_mask[bass.ds(i * 2 * P + (s + 2) * P, P), :]).then_inc(mask2_loaded[s], 16)
                for s in range(2):
                    store(i, s)
            for s in range(2):
                store(ROUNDS - 1, s)
            for s in range(2):
                sp.wait_ge(stored[s], 16 * (ROUNDS + 1))

        @block.gpsimd
        def _(pool):
            nc.gpsimd.memset(minus_half[:], -0.5).then_inc(set_up, 1)
            for s in range(2):
                nc.gpsimd.memset(vp[s][:], 0.0).then_inc(set_up, 1)
            pool.wait_ge(set_up, 3)
            for s in range(2):
                for e in range(2):
                    nc.gpsimd.memset(vp[s][e * SEQ:(e + 1) * SEQ, :, :, e, HEAD:HEAD + 1], 1.0).then_inc(set_up, 1)

            def inverse_deviation(i, n, s):
                pool.wait_ge(var_ready, count(i, 6, 2 * n + s))
                nc.gpsimd.tensor_tensor(rstd[s][:], var_eps[s][:], minus_half[:], ALU.pow).then_inc(rstd_ready, 1)

            def residual_with_bias(n, s, source, bias):
                nc.gpsimd.tensor_tensor(res_b[s][:], source[:], row[bias], ALU.add).then_inc(res_b_ready, 1)

            pool.wait_ge(set_up, 7)

            with pool.Fori(0, ROUNDS) as i:
                for s in range(2):
                    inverse_deviation(i, 0, s)
                for s in range(2):
                    residual_with_bias(0, s, x_tile[s], "l0_b_ao")
                for n, bias in ((1, "l0_b_co"), (2, "l0_b2")):
                    for s in range(2):
                        inverse_deviation(i, n, s)
                        residual_with_bias(n, s, res[s], bias)

        @block.scalar
        def _(act):
            def normed_transposed(i, n, s):
                act.wait_ge(xT_ready, count(i, 6, 2 * n + s))
                for c in range(DC):
                    last = nc.scalar.activation(hT[s][:, c, :], ps_a[s][:, c * P:(c + 1) * P], ACT.Identity,
                                                bias=col(f"l0_ln{n + 1}_b", c), scale=col(f"l0_ln{n + 1}_s", c))
                last.then_inc(hT_ready, 1)

            def queries(i, a, s):
                act.wait_ge(qv_in_psum, count(i, 4, 2 * a + s))
                for c in range(DC):
                    last = nc.scalar.activation(qT[s][:, c, :], ps_b[s][:, c * P:(c + 1) * P], ACT.Identity,
                                                bias=col(f"l0_bq{a}", c), scale=1.0)
                last.then_inc(q_ready, 1)

            def values(i, a, s):
                for e in range(2):
                    half = slice(e * SEQ, (e + 1) * SEQ)
                    last = nc.scalar.activation(
                        vp[s][half, :, :, e, 0:HEAD],
                        ps_b[s][half, DIM:2 * DIM].rearrange("k (b h d) -> k b h d", b=PER_TILE, h=PAIRS), ACT.Copy)
                last.then_inc(v_ready, 1)

            def exponentials(i, a, s):
                act.wait_ge(shifted, count(i, 4, 2 * a + s))
                nc.scalar.activation(probs[s][:], probs[s][:], ACT.Exp).then_inc(p_ready, 1)

            def probs_transposed(i, a, s):
                act.wait_ge(pT_in_psum, count(i, 8, 4 * a + 2 * s))
                nc.scalar.activation(pT[s][:, 0:PAIRS // 2, :], ps_a[s][:].rearrange("k (h q) -> k h q", q=P),
                                     ACT.Copy).then_inc(pT_lo_ready, 1)

            def attended_transposed(i, a, s):
                act.wait_ge(aT_in_psum, count(i, 4, 2 * a + s))
                for c in range(DC):
                    last = nc.scalar.activation(aT[s][:, c, :], ps_b[s][:, c * P:(c + 1) * P], ACT.Identity,
                                                bias=col(f"l0_bv{a}", c), scale=1.0)
                last.then_inc(aT_ready, 1)

            def hidden(i, s):
                for half, bank in enumerate((ps_a[s], ps_b[s])):
                    act.wait_ge(hid_in_psum, count(i, 4, 2 * s + half))
                    for c in range(HC // 2):
                        h = half * (HC // 2) + c
                        last = nc.scalar.activation(hidT[s][:, h, :], bank[:, c * P:(c + 1) * P], ACT.Gelu_apprx_tanh,
                                                    bias=col("l0_b1", h), scale=1.0)
                    last.then_inc(hid_ready, 1)

            act.wait_ge(set_up, 7)
            with act.Fori(0, ROUNDS) as i:
                for a in range(2):
                    for s in range(2):
                        normed_transposed(i, a, s)
                    for s in range(2):
                        queries(i, a, s)
                        values(i, a, s)
                    for s in range(2):
                        exponentials(i, a, s)
                    for s in range(2):
                        probs_transposed(i, a, s)
                    for s in range(2):
                        attended_transposed(i, a, s)
                for s in range(2):
                    normed_transposed(i, 2, s)
                for s in range(2):
                    hidden(i, s)

        @block.vector
        def _(dve):
            links = Links(vector_step, dve, VECTOR_LINKS)

            def layer_norm(i, n, s, source):
                links.mark(nc.vector.bn_stats(stats[s][:], source[:]))
                links.wait(i)
                nc.vector.memset(pad[s][:], 0.0)
                links.mark(nc.vector.bn_aggr(mean_var[s][:], stats[s][:]))
                links.wait(i)
                nc.vector.tensor_scalar(var_eps[s][:], mean_var[s][:, 1:2], LN_EPS, None, ALU.add).then_inc(var_ready, 1)
                dve.wait_ge(rstd_ready, count(i, 6, 2 * n + s))
                nc.vector.tensor_scalar(xn[s][:], source[:], mean_var[s][:, 0:1], rstd[s][:], ALU.subtract, ALU.mult
                                        ).then_inc(xn_ready, 1)

            def context_transposed(i, s):
                dve.wait_ge(cT_in_psum, count(i, 2, s))
                nc.vector.tensor_copy(cT[s][:], ps_b[s][:, 0:DIM].rearrange("f (c t) -> f c t", c=DC)
                                      ).then_inc(cT_ready, 1)

            def keys(i, a, s):
                dve.wait_ge(k_in_psum, count(i, 4, 2 * a + s))
                for c in range(DC):
                    for e in range(2):
                        last = nc.vector.tensor_scalar(kT[s][:, c, e, :], ps_a[s][:, c * P:(c + 1) * P],
                                                       col(f"l0_bk{a}", c), parity[:, e:e + 1], ALU.add, ALU.mult)
                last.then_inc(k_ready, 1)

            def mask_scores(i, a, s):
                mask, bias = (mask1, bias1) if a == 0 else (mask2[s], bias2[s])
                if a == 1:
                    dve.wait_ge(mask2_loaded[s], count(i, 1, 0) * 16)
                    links.mark(nc.vector.tensor_scalar(bias[:], mask[:], 1.0, MASKED, ALU.subtract, ALU.mult))
                dve.wait_ge(s_in_psum, count(i, 4, 2 * a + s))
                for g in range(4):
                    last = nc.vector.scalar_tensor_tensor(
                        out=probs[s][:, g, :, :], in0=ps_s[:, g, 0:2 * DC * SEQ].rearrange("q (h k) -> q h k", k=SEQ),
                        scalar=scale, in1=mask[:].unsqueeze(1).to_broadcast([P, 2 * DC, SEQ]),
                        op0=ALU.mult, op1=ALU.mult)
                last.then_inc(s_masked, 1)

            def shift_scores(i, a, s):
                bias = bias1 if a == 0 else bias2[s]
                dve.wait_ge(s_masked, count(i, 4, 2 * a + s))
                flat = probs[s][:].rearrange("q g h k -> q (g h) k")
                links.wait(i)
                links.mark(nc.vector.tensor_tensor(flat, flat, bias[:].unsqueeze(1).to_broadcast([P, HEADS, SEQ]), ALU.add))
                links.wait(i)
                links.mark(nc.vector.tensor_reduce(row_max[s][:], flat, AX.X, ALU.max))
                links.wait(i)
                nc.vector.tensor_tensor(flat, flat, row_max[s][:].unsqueeze(2).to_broadcast([P, HEADS, SEQ]),
                                        ALU.subtract).then_inc(shifted, 1)

            def probs_transposed(i, a, s):
                dve.wait_ge(pT_in_psum, count(i, 8, 4 * a + 2 * s + 1))
                nc.vector.tensor_copy(pT[s][:, PAIRS // 2:, :], ps_b[s][:].rearrange("k (h q) -> k h q", q=P)
                                      ).then_inc(pT_hi_ready, 1)

            def normalise(i, a, s):
                dve.wait_ge(o_in_psum, count(i, 4, 2 * a + s))
                o = ps_a[s][:, 0:HEADS * (HEAD + 1)].rearrange("q (h d) -> q h d", d=HEAD + 1)
                links.mark(nc.vector.reciprocal(inv_sum[s][:].unsqueeze(2), o[:, :, HEAD:HEAD + 1]))
                links.wait(i)
                nc.vector.tensor_tensor(att[s][:].rearrange("q (h d) -> q h d", d=HEAD), o[:, :, 0:HEAD],
                                        inv_sum[s][:].unsqueeze(2).to_broadcast([P, HEADS, HEAD]), ALU.mult
                                        ).then_inc(att_ready, 1)

            def add_residual(i, n, s):
                dve.wait_ge(y_in_psum, count(i, 6, 2 * n + s))
                dve.wait_ge(res_b_ready, count(i, 6, 2 * n + s))
                y = ps_a[s][:, 0:DIM]
                if n < 2:
                    nc.vector.tensor_tensor(res[s][:], y, res_b[s][:], ALU.add).then_inc(res_ready, 1)
                    dve.wait_ge(res_ready, count(i, 4, 2 * n + s))
                else:
                    dve.wait_ge(stored[s], (i + 1) * 16)
                    nc.vector.tensor_tensor(y_out[s][:], y, res_b[s][:], ALU.add).then_inc(y_ready, 1)

            for b in range(1):
                dve.wait_ge(mask1_loaded, 16 * PER_TILE)
                nc.vector.tensor_scalar(bias1[:], mask1[:], 1.0, MASKED, ALU.subtract, ALU.mult).then_inc(vector_set_up, 1)
                dve.wait_ge(vector_set_up, 1)
            with dve.Fori(0, ROUNDS) as i:
                for a in range(2):
                    for s in range(2):
                        if a == 0:
                            dve.wait_ge(x_loaded[s], count(i, 1, 0) * 16)
                            layer_norm(i, 0, s, x_tile[s])
                        else:
                            layer_norm(i, 1, s, res[s])
                    if a == 0:
                        for s in range(2):
                            context_transposed(i, s)
                    for s in range(2):
                        keys(i, a, s)
                    for s in range(2):
                        mask_scores(i, a, s)
                        shift_scores(i, a, s)
                    for s in range(2):
                        probs_transposed(i, a, s)
                    for s in range(2):
                        normalise(i, a, s)
                    for s in range(2):
                        add_residual(i, a, s)
                for s in range(2):
                    layer_norm(i, 2, s, res[s])
                for s in range(2):
                    add_residual(i, 2, s)
            links.check()

        @block.tensor
        def _(pe):
            def normed(i, n, s):
                pe.wait_ge(xn_ready, count(i, 6, 2 * n + s))
                for c in range(DC):
                    last = nc.tensor.transpose(ps_a[s][:, c * P:(c + 1) * P], xn[s][:, c * P:(c + 1) * P], ident)
                last.then_inc(xT_ready, 1)

            def context(i, s):
                pe.wait_ge(c_loaded[s], count(i, 1, 0) * 16)
                for c in range(DC):
                    last = nc.tensor.transpose(ps_b[s][:, c * P:(c + 1) * P], c_tile[s][:, c * P:(c + 1) * P], ident)
                last.then_inc(cT_in_psum, 1)

            def project(i, a, s):
                def transposed(bank, weights, moving):
                    for c in range(DC):
                        for k in range(DC):
                            last = nc.tensor.matmul(bank[:, c * P:(c + 1) * P], weights[:, k, c * P:(c + 1) * P],
                                                    moving[:, k, :], start=(k == 0), stop=(k == DC - 1))
                    return last

                source = hT[s] if a == 0 else cT[s]
                pe.wait_ge(hT_ready, count(i, 6, 2 * a + s))
                transposed(ps_a[s], wk[a], source).then_inc(k_in_psum, 1)
                if a == 0:
                    pe.wait_ge(cT_ready, count(i, 2, s))
                transposed(ps_b[s], wq[a], hT[s])
                for b in range(PER_TILE):
                    for e in range(2):
                        for k in range(DC):
                            last = nc.tensor.matmul(
                                ps_b[s][e * SEQ:(e + 1) * SEQ, DIM + b * P:DIM + (b + 1) * P],
                                source[:, k, b * SEQ:(b + 1) * SEQ],
                                wv[a][:, k, :].rearrange("f (h e d) -> f h e d", e=2, d=HEAD)[:, :, e, :],
                                start=(k == 0), stop=(k == DC - 1))
                last.then_inc(qv_in_psum, 1)

            def scores(i, a, s):
                pe.wait_ge(q_ready, count(i, 4, 2 * a + s))
                pe.wait_ge(k_ready, count(i, 4, 2 * a + s))
                if a == 0 and s == 0:
                    pass
                else:
                    pe.wait_ge(s_masked, count(i, 4, 2 * a + s - 1))
                for g in range(4):
                    rows = slice(32 * g, 32 * g + 32)
                    for c in range(DC):
                        for b in range(PER_TILE):
                            last = nc.tensor.matmul(ps_s[b * SEQ:(b + 1) * SEQ, g, c * P:(c + 1) * P],
                                                    qT[s][rows, c, b * SEQ:(b + 1) * SEQ],
                                                    kT[s][rows, c, :, b * SEQ:(b + 1) * SEQ], start=True, stop=True)
                last.then_inc(s_in_psum, 1)

            def transpose_probs(i, a, s):
                pe.wait_ge(p_ready, count(i, 4, 2 * a + s))
                pe.wait_ge(v_ready, count(i, 4, 2 * a + s))
                for half, bank in enumerate((ps_a[s], ps_b[s])):
                    for j in range(PAIRS // 2):
                        g, c = divmod(half * (PAIRS // 2) + j, DC)
                        last = nc.tensor.transpose(bank[:, j * P:(j + 1) * P],
                                                   probs[s][:, g, 2 * c:2 * c + 2, :], ident)
                    last.then_inc(pT_in_psum, 1)

            def attend(i, a, s):
                pe.wait_ge(pT_lo_ready, count(i, 4, 2 * a + s))
                pe.wait_ge(pT_hi_ready, count(i, 4, 2 * a + s))
                wide = 2 * (HEAD + 1)
                for j in range(PAIRS):
                    g, c = divmod(j, DC)
                    pair = 4 * c + g
                    for b in range(PER_TILE):
                        last = nc.tensor.matmul(ps_a[s][b * SEQ:(b + 1) * SEQ, pair * wide:(pair + 1) * wide],
                                                pT[s][:, j, b * SEQ:(b + 1) * SEQ], vp[s][:, b, pair, :, :],
                                                start=True, stop=True)
                last.then_inc(o_in_psum, 1)

            def transpose_attended(i, a, s):
                pe.wait_ge(att_ready, count(i, 4, 2 * a + s))
                for c in range(DC):
                    last = nc.tensor.transpose(ps_b[s][:, c * P:(c + 1) * P], att[s][:, c * P:(c + 1) * P], ident)
                last.then_inc(aT_in_psum, 1)

            def project_out(i, a, s):
                pe.wait_ge(aT_ready, count(i, 4, 2 * a + s))
                for k in range(DC):
                    last = nc.tensor.matmul(ps_a[s][:, 0:DIM], aT[s][:, k, :], wo[a][:, k, :],
                                            start=(k == 0), stop=(k == DC - 1))
                last.then_inc(y_in_psum, 1)

            def mlp_up(i, s):
                pe.wait_ge(hT_ready, count(i, 6, 4 + s))
                for half, bank in enumerate((ps_a[s], ps_b[s])):
                    for c in range(HC // 2):
                        h = half * (HC // 2) + c
                        for k in range(DC):
                            last = nc.tensor.matmul(bank[:, c * P:(c + 1) * P], w1[:, k, h * P:(h + 1) * P], hT[s][:, k, :],
                                                    start=(k == 0), stop=(k == DC - 1))
                    last.then_inc(hid_in_psum, 1)

            def mlp_down(i, s):
                for half in range(2):
                    pe.wait_ge(hid_ready, count(i, 4, 2 * s + half))
                    for c in range(HC // 2):
                        h = half * (HC // 2) + c
                        last = nc.tensor.matmul(ps_a[s][:, 0:DIM], hidT[s][:, h, :], w2[:, h, :],
                                                start=(h == 0), stop=(h == HC - 1))
                last.then_inc(y_in_psum, 1)

            pe.wait_ge(set_up, 7)
            with pe.Fori(0, ROUNDS) as i:
                for a in range(2):
                    for s in range(2):
                        normed(i, a, s)
                        if a == 0:
                            context(i, s)
                    for stage in (project, scores, transpose_probs, attend, transpose_attended, project_out):
                        for s in range(2):
                            stage(i, a, s)
                for s in range(2):
                    normed(i, 2, s)
                for s in range(2):
                    mlp_up(i, s)
                for s in range(2):
                    mlp_down(i, s)

        running.close()
        cleared(nc, semaphores)


def resampler_layer(nc, x_in, ctx, key_mask, x_out, w, col, row, ident, parity):
    with ExitStack() as held:
        semaphores, running = [], ExitStack()

        def sb(name, shape, dtype=F32):
            return held.enter_context(nc.sbuf_tensor("l1_" + name, shape, dtype))

        def sem(name):
            semaphores.append(held.enter_context(nc.semaphore("l1_" + name)))
            return semaphores[-1]

        x_tile = [sb(f"x_tile{s}", [P, DIM]) for s in range(2)]
        c_tile = [sb(f"c_tile{s}", [P, DIM]) for s in range(2)]
        mask = [sb(f"mask{s}", [P, SEQ], I32) for s in range(2)]
        bias = [sb(f"bias{s}", [P, 2 * SEQ]) for s in range(2)]
        stats = [sb(f"stats{s}", [P, 6]) for s in range(2)]
        mean_var = [sb(f"mean_var{s}", [P, 2]) for s in range(2)]
        var_eps = [sb(f"var_eps{s}", [P, 1]) for s in range(2)]
        rstd = [sb(f"rstd{s}", [P, 1]) for s in range(2)]
        pad = [sb(f"pad{s}", [P, 1]) for s in range(2)]
        minus_half = sb("minus_half", [P, 1])
        xn = [sb(f"xn{s}", [P, DIM]) for s in range(2)]
        mean_square = [sb(f"mean_square{s}", [P, 1]) for s in range(2)]
        hT = [sb(f"hT{s}", [P, DC, P]) for s in range(2)]
        srcT = [sb(f"srcT{s}", [P, DC, PER_TILE, 2, SEQ]) for s in range(2)]
        qT = [sb(f"qT{s}", [P, DC, P]) for s in range(2)]
        kT = [sb(f"kT{s}", [P, DC, 2, 2 * P]) for s in range(2)]
        v = [sb(f"v{s}", [P, PER_TILE, HEADS, HEAD + 1]) for s in range(2)]
        probs = [sb(f"probs{s}", [P, 4, 2 * DC, 2 * SEQ]) for s in range(2)]
        row_max = [sb(f"row_max{s}", [P, HEADS]) for s in range(2)]
        pT = [sb(f"pT{s}", [P, HEADS, P]) for s in range(2)]
        inv_sum = [sb(f"inv_sum{s}", [P, HEADS]) for s in range(2)]
        att = [sb(f"att{s}", [P, DIM]) for s in range(2)]
        aT = [sb(f"aT{s}", [P, DC, P]) for s in range(2)]
        res = [sb(f"res{s}", [P, DIM]) for s in range(2)]
        res_b = [sb(f"res_b{s}", [P, DIM]) for s in range(2)]
        final_b = [sb(f"final_b{s}", [P, DIM]) for s in range(2)]
        hidT = [sb(f"hidT{s}", [P, HC, P]) for s in range(2)]
        y_out = [sb(f"y_out{s}", [P, DIM]) for s in range(2)]
        ps_s = held.enter_context(nc.psum_tensor("l1_ps_s", [P, 4, BANK], F32))
        ps_a = [held.enter_context(nc.psum_tensor(f"l1_ps_a{s}", [P, BANK], F32)) for s in range(2)]
        ps_b = [held.enter_context(nc.psum_tensor(f"l1_ps_b{s}", [P, BANK], F32)) for s in range(2)]

        x_loaded = [sem(f"x_loaded{s}") for s in range(2)]
        c_loaded = [sem(f"c_loaded{s}") for s in range(2)]
        mask_loaded = [sem(f"mask_loaded{s}") for s in range(2)]
        stored = [sem(f"stored{s}") for s in range(2)]
        set_up = sem("set_up")
        vector_step = sem("vector_step")
        var_ready = sem("var_ready")
        rstd_ready = sem("rstd_ready")
        xn_ready = sem("xn_ready")
        xT_ready = sem("xT_ready")
        hT_ready = sem("hT_ready")
        lT_in_psum = sem("lT_in_psum")
        lT_ready = sem("lT_ready")
        cT_in_psum = sem("cT_in_psum")
        cT_ready = sem("cT_ready")
        k_in_psum = sem("k_in_psum")
        q_in_psum = sem("q_in_psum")
        v_in_psum = sem("v_in_psum")
        q_ready = sem("q_ready")
        k_ready = sem("k_ready")
        v_ready = sem("v_ready")
        s_in_psum = sem("s_in_psum")
        bias_ready = sem("bias_ready")
        s_masked = sem("s_masked")
        shifted = sem("shifted")
        p_ready = sem("p_ready")
        pT_in_psum = sem("pT_in_psum")
        pT_lo_ready = sem("pT_lo_ready")
        pT_hi_ready = sem("pT_hi_ready")
        o_in_psum = sem("o_in_psum")
        att_ready = sem("att_ready")
        aT_in_psum = sem("aT_in_psum")
        aT_ready = sem("aT_ready")
        y_in_psum = sem("y_in_psum")
        res_ready = sem("res_ready")
        res_b_ready = sem("res_b_ready")
        final_b_ready = sem("final_b_ready")
        y_ready = sem("y_ready")
        hid_in_psum = sem("hid_in_psum")
        hid_ready = sem("hid_ready")

        wq, wk, wv, wo = w["l1_q_w"], w["l1_k_w"], w["l1_v_w"], w["l1_out_w"]
        w1, w2 = w["l1_mlp_w1"], w["l1_mlp_w2"]
        scale = 1.0 / HEAD
        VECTOR_LINKS = 10

        block = running.enter_context(nc.Block())

        @block.sync
        def _(sp):
            def load_mask(i, t, s):
                for b in range(PER_TILE):
                    sp.dma_start(mask[s][b * SEQ:(b + 1) * SEQ, :],
                                 key_mask[bass.ds(i * 2 * PER_TILE + t * PER_TILE + b, 1), :].partition_broadcast(SEQ)
                                 ).then_inc(mask_loaded[s], 16)

            for s in range(2):
                sp.dma_start(x_tile[s][:], x_in[bass.ts(s, P), :]).then_inc(x_loaded[s], 16)
                sp.dma_start(c_tile[s][:], ctx[bass.ts(s, P), :]).then_inc(c_loaded[s], 16)
                load_mask(0, s, s)
                sp.sem_inc(stored[s], 16)

            def store(i, s):
                sp.wait_ge(y_ready, count(i, 2, s))
                sp.nop()
                sp.dma_start(x_out[bass.ds(i * 2 * P + s * P, P), :], y_out[s][:]).then_inc(stored[s], 16)

            with sp.Fori(0, ROUNDS - 1) as i:
                for s in range(2):
                    sp.wait_ge(final_b_ready, count(i, 2, s))
                    sp.wait_ge(lT_in_psum, count(i, 2, s))
                    sp.nop()
                    sp.dma_start(x_tile[s][:], x_in[bass.ds(i * 2 * P + (s + 2) * P, P), :]).then_inc(x_loaded[s], 16)
                    sp.wait_ge(cT_in_psum, count(i, 2, s))
                    sp.nop()
                    sp.dma_start(c_tile[s][:], ctx[bass.ds(i * 2 * P + (s + 2) * P, P), :]).then_inc(c_loaded[s], 16)
                for s in range(2):
                    sp.wait_ge(s_masked, count(i, 2, s))
                    sp.nop()
                    load_mask(i, s + 2, s)
                for s in range(2):
                    store(i, s)
            for s in range(2):
                store(ROUNDS - 1, s)
            for s in range(2):
                sp.wait_ge(stored[s], 16 * (ROUNDS + 1))

        @block.gpsimd
        def _(pool):
            nc.gpsimd.memset(minus_half[:], -0.5).then_inc(set_up, 1)
            for s in range(2):
                nc.gpsimd.memset(v[s][:, :, :, HEAD:HEAD + 1], 1.0).then_inc(set_up, 1)
                nc.gpsimd.memset(bias[s][:, SEQ:], 0.0).then_inc(set_up, 1)

            pool.wait_ge(set_up, 5)

            with pool.Fori(0, ROUNDS) as i:
                for s in range(2):
                    pool.wait_ge(bias_ready, count(i, 2, s))
                    pool.wait_ge(x_loaded[s], count(i, 1, 0) * 16)
                    nc.gpsimd.tensor_tensor(res_b[s][:], x_tile[s][:], row["l1_out_b"], ALU.add).then_inc(res_b_ready, 1)
                    nc.gpsimd.tensor_tensor(final_b[s][:], x_tile[s][:], row["l1_mlp_b2"], ALU.add).then_inc(final_b_ready, 1)
                for s in range(2):
                    pool.wait_ge(var_ready, count(i, 2, s))
                    nc.gpsimd.tensor_tensor(rstd[s][:], var_eps[s][:], minus_half[:], ALU.pow).then_inc(rstd_ready, 1)

        @block.scalar
        def _(act):
            def latents_transposed(i, s):
                act.wait_ge(lT_in_psum, count(i, 2, s))
                nc.scalar.activation(srcT[s][:, :, :, 1, :].rearrange("f c b t -> f (c b) t"),
                                     ps_a[s][:, 0:DIM].rearrange("f (m t) -> f m t", t=SEQ), ACT.Copy).then_inc(lT_ready, 1)

            def normed_transposed(i, s):
                act.wait_ge(xT_ready, count(i, 2, s))
                for c in range(DC):
                    last = nc.scalar.activation(hT[s][:, c, :], ps_a[s][:, c * P:(c + 1) * P], ACT.Identity,
                                                bias=0.0, scale=col("l1_postnorm_w", c))
                last.then_inc(hT_ready, 1)

            def queries(i, s):
                act.wait_ge(q_in_psum, count(i, 2, s))
                for c in range(DC):
                    last = nc.scalar.activation(qT[s][:, c, :], ps_b[s][:, c * P:(c + 1) * P], ACT.Identity,
                                                bias=col("l1_bq", c), scale=1.0)
                last.then_inc(q_ready, 1)

            def values(i, s):
                act.wait_ge(v_in_psum, count(i, 2, s))
                nc.scalar.activation(v[s][:, :, :, 0:HEAD].rearrange("k b h d -> k (b h) d"),
                                     ps_s[:, 2 + s, :].rearrange("k (m d) -> k m d", d=HEAD), ACT.Copy).then_inc(v_ready, 1)

            def exponentials(i, s):
                act.wait_ge(shifted, count(i, 2, s))
                nc.scalar.activation(probs[s][:], probs[s][:], ACT.Exp).then_inc(p_ready, 1)

            def probs_transposed(i, s):
                for half in range(2):
                    act.wait_ge(pT_in_psum, count(i, 8, 4 * s + 2 * half))
                    nc.scalar.activation(pT[s][:, 8 * half:8 * half + 4, :], ps_a[s][:].rearrange("k (h q) -> k h q", q=P),
                                         ACT.Copy).then_inc(pT_lo_ready, 1)

            def attended_transposed(i, s):
                act.wait_ge(aT_in_psum, count(i, 2, s))
                for c in range(DC):
                    last = nc.scalar.activation(aT[s][:, c, :], ps_b[s][:, c * P:(c + 1) * P], ACT.Identity,
                                                bias=col("l1_bv", c), scale=1.0)
                last.then_inc(aT_ready, 1)

            def hidden(i, s):
                for half, bank in enumerate((ps_a[s], ps_b[s])):
                    act.wait_ge(hid_in_psum, count(i, 4, 2 * s + half))
                    for c in range(HC // 2):
                        h = half * (HC // 2) + c
                        last = nc.scalar.activation(hidT[s][:, h, :], bank[:, c * P:(c + 1) * P], ACT.Gelu_apprx_tanh,
                                                    bias=col("l1_b1", h), scale=1.0)
                    last.then_inc(hid_ready, 1)

            act.wait_ge(set_up, 5)
            with act.Fori(0, ROUNDS) as i:
                for s in range(2):
                    latents_transposed(i, s)
                for s in range(2):
                    queries(i, s)
                    values(i, s)
                for s in range(2):
                    exponentials(i, s)
                for s in range(2):
                    probs_transposed(i, s)
                for s in range(2):
                    attended_transposed(i, s)
                for s in range(2):
                    normed_transposed(i, s)
                for s in range(2):
                    hidden(i, s)

        @block.vector
        def _(dve):
            links = Links(vector_step, dve, VECTOR_LINKS)

            def rms_norm(i, s):
                links.mark(nc.vector.bn_stats(stats[s][:], res[s][:]))
                links.wait(i)
                nc.vector.memset(pad[s][:], 0.0)
                links.mark(nc.vector.bn_aggr(mean_var[s][:], stats[s][:]))
                links.wait(i)
                links.mark(nc.vector.scalar_tensor_tensor(out=mean_square[s][:], in0=mean_var[s][:, 0:1],
                                                          scalar=mean_var[s][:, 0:1], in1=mean_var[s][:, 1:2],
                                                          op0=ALU.mult, op1=ALU.add))
                links.wait(i)
                nc.vector.tensor_scalar(var_eps[s][:], mean_square[s][:], RMS_EPS, None, ALU.add).then_inc(var_ready, 1)
                dve.wait_ge(rstd_ready, count(i, 2, s))
                nc.vector.tensor_scalar(xn[s][:], res[s][:], rstd[s][:], None, ALU.mult).then_inc(xn_ready, 1)

            def context_transposed(i, s):
                dve.wait_ge(cT_in_psum, count(i, 2, s))
                nc.vector.tensor_copy(srcT[s][:, :, :, 0, :].rearrange("f c b t -> f (c b) t"),
                                      ps_b[s][:, 0:DIM].rearrange("f (m t) -> f m t", t=SEQ)).then_inc(cT_ready, 1)

            def keys(i, s):
                dve.wait_ge(k_in_psum, count(i, 2, s))
                for c in range(DC):
                    for e in range(2):
                        last = nc.vector.tensor_scalar(kT[s][:, c, e, :], ps_a[s][:, c * 2 * P:(c + 1) * 2 * P],
                                                       col("l1_bk", c), parity[:, e:e + 1], ALU.add, ALU.mult)
                last.then_inc(k_ready, 1)

            def mask_bias(i, s):
                dve.wait_ge(mask_loaded[s], count(i, 1, 0) * 16 * PER_TILE)
                nc.vector.tensor_scalar(bias[s][:, 0:SEQ], mask[s][:], 0.0, MINUS_INF, ALU.is_equal, ALU.mult).then_inc(bias_ready, 1)

            def mask_scores(i, s):
                dve.wait_ge(bias_ready, count(i, 2, s))
                dve.wait_ge(s_in_psum, count(i, 2, s))
                for g in range(4):
                    last = nc.vector.scalar_tensor_tensor(
                        out=probs[s][:, g, :, :], in0=ps_s[:, g, :].rearrange("q (h k) -> q h k", k=2 * SEQ),
                        scalar=scale, in1=bias[s][:].unsqueeze(1).to_broadcast([P, 2 * DC, 2 * SEQ]),
                        op0=ALU.mult, op1=ALU.add)
                last.then_inc(s_masked, 1)

            def shift_scores(i, s):
                dve.wait_ge(s_masked, count(i, 2, s))
                flat = probs[s][:].rearrange("q g h k -> q (g h) k")
                links.mark(nc.vector.tensor_reduce(row_max[s][:], flat, AX.X, ALU.max))
                links.wait(i)
                nc.vector.tensor_tensor(flat, flat, row_max[s][:].unsqueeze(2).to_broadcast([P, HEADS, 2 * SEQ]),
                                        ALU.subtract).then_inc(shifted, 1)

            def probs_transposed(i, s):
                for half in range(2):
                    dve.wait_ge(pT_in_psum, count(i, 8, 4 * s + 2 * half + 1))
                    nc.vector.tensor_copy(pT[s][:, 8 * half + 4:8 * half + 8, :], ps_b[s][:].rearrange("k (h q) -> k h q", q=P)
                                          ).then_inc(pT_hi_ready, 1)

            def normalise(i, s):
                dve.wait_ge(o_in_psum, count(i, 2, s))
                o = ps_a[s][:, 0:HEADS * (HEAD + 1)].rearrange("q (h d) -> q h d", d=HEAD + 1)
                links.mark(nc.vector.reciprocal(inv_sum[s][:].unsqueeze(2), o[:, :, HEAD:HEAD + 1]))
                links.wait(i)
                nc.vector.tensor_tensor(att[s][:].rearrange("q (h d) -> q h d", d=HEAD), o[:, :, 0:HEAD],
                                        inv_sum[s][:].unsqueeze(2).to_broadcast([P, HEADS, HEAD]), ALU.mult
                                        ).then_inc(att_ready, 1)

            def add_residual(i, n, s):
                dve.wait_ge(y_in_psum, count(i, 4, 2 * n + s))
                y = ps_a[s][:, 0:DIM]
                if n == 0:
                    dve.wait_ge(res_b_ready, count(i, 2, s))
                    nc.vector.tensor_tensor(res[s][:], y, res_b[s][:], ALU.add).then_inc(res_ready, 1)
                    dve.wait_ge(res_ready, count(i, 2, s))
                else:
                    dve.wait_ge(final_b_ready, count(i, 2, s))
                    dve.wait_ge(stored[s], (i + 1) * 16)
                    nc.vector.tensor_tensor(y_out[s][:], y, final_b[s][:], ALU.add).then_inc(y_ready, 1)

            dve.wait_ge(set_up, 5)
            with dve.Fori(0, ROUNDS) as i:
                for s in range(2):
                    mask_bias(i, s)
                for s in range(2):
                    context_transposed(i, s)
                for s in range(2):
                    keys(i, s)
                for s in range(2):
                    mask_scores(i, s)
                    shift_scores(i, s)
                for s in range(2):
                    probs_transposed(i, s)
                for s in range(2):
                    normalise(i, s)
                for s in range(2):
                    add_residual(i, 0, s)
                for s in range(2):
                    rms_norm(i, s)
                for s in range(2):
                    add_residual(i, 1, s)
            links.check()

        @block.tensor
        def _(pe):
            def latents(i, s):
                pe.wait_ge(bias_ready, count(i, 2, s))
                pe.wait_ge(x_loaded[s], count(i, 1, 0) * 16)
                for c in range(DC):
                    last = nc.tensor.transpose(ps_a[s][:, c * P:(c + 1) * P], x_tile[s][:, c * P:(c + 1) * P], ident)
                last.then_inc(lT_in_psum, 1)

            def normed(i, s):
                pe.wait_ge(xn_ready, count(i, 2, s))
                for c in range(DC):
                    last = nc.tensor.transpose(ps_a[s][:, c * P:(c + 1) * P], xn[s][:, c * P:(c + 1) * P], ident)
                last.then_inc(xT_ready, 1)

            def context(i, s):
                pe.wait_ge(c_loaded[s], count(i, 1, 0) * 16)
                for c in range(DC):
                    last = nc.tensor.transpose(ps_b[s][:, c * P:(c + 1) * P], c_tile[s][:, c * P:(c + 1) * P], ident)
                last.then_inc(cT_in_psum, 1)

            def project(i, s):
                pe.wait_ge(cT_ready, count(i, 2, s))
                pe.wait_ge(lT_ready, count(i, 2, s))
                for c in range(DC):
                    for k in range(DC):
                        last = nc.tensor.matmul(ps_a[s][:, c * 2 * P:(c + 1) * 2 * P], wk[:, k, c * P:(c + 1) * P],
                                                srcT[s][:, k].rearrange("f b m t -> f (b m t)"),
                                                start=(k == 0), stop=(k == DC - 1))
                last.then_inc(k_in_psum, 1)
                for c in range(DC):
                    for k in range(DC):
                        last = nc.tensor.matmul(ps_b[s][:, c * P:(c + 1) * P], wq[:, k, c * P:(c + 1) * P],
                                                srcT[s][:, k, :, 1, :], start=(k == 0), stop=(k == DC - 1))
                last.then_inc(q_in_psum, 1)
                for b in range(PER_TILE):
                    for k in range(DC):
                        last = nc.tensor.matmul(ps_s[:, 2 + s, b * DIM:(b + 1) * DIM],
                                                srcT[s][:, k, b].rearrange("f m t -> f (m t)"), wv[:, k, :],
                                                start=(k == 0), stop=(k == DC - 1))
                last.then_inc(v_in_psum, 1)

            def scores(i, s):
                pe.wait_ge(q_ready, count(i, 2, s))
                pe.wait_ge(k_ready, count(i, 2, s))
                if s == 0:
                    for r in range(2):
                        pe.wait_ge(v_ready, count(i, 2, r))
                else:
                    pe.wait_ge(s_masked, count(i, 2, 0))
                for g in range(4):
                    rows = slice(32 * g, 32 * g + 32)
                    for c in range(DC):
                        for b in range(PER_TILE):
                            last = nc.tensor.matmul(ps_s[b * SEQ:(b + 1) * SEQ, g, c * 2 * P:(c + 1) * 2 * P],
                                                    qT[s][rows, c, b * SEQ:(b + 1) * SEQ],
                                                    kT[s][rows, c, :, b * 2 * SEQ:(b + 1) * 2 * SEQ], start=True, stop=True)
                last.then_inc(s_in_psum, 1)

            def transpose_probs(i, s):
                pe.wait_ge(p_ready, count(i, 2, s))
                for quarter in range(4):
                    bank = (ps_a, ps_b)[quarter % 2][s]
                    if quarter >= 2:
                        pe.wait_ge((pT_lo_ready, pT_hi_ready)[quarter % 2], count(i, 4, 2 * s))
                    for j in range(4):
                        last = nc.tensor.transpose(bank[:, j * P:(j + 1) * P], probs[s][:, quarter, j, :], ident)
                    last.then_inc(pT_in_psum, 1)

            def attend(i, s):
                pe.wait_ge(pT_lo_ready, count(i, 4, 2 * s + 1))
                pe.wait_ge(pT_hi_ready, count(i, 4, 2 * s + 1))
                wide = HEAD + 1
                for g in range(4):
                    for j in range(2 * DC):
                        head = (j // 2) * PAIRS + 2 * g + j % 2
                        for b in range(PER_TILE):
                            last = nc.tensor.matmul(ps_a[s][b * SEQ:(b + 1) * SEQ, head * wide:(head + 1) * wide],
                                                    pT[s][:, 4 * g + j, b * SEQ:(b + 1) * SEQ], v[s][:, b, head, :],
                                                    start=True, stop=True)
                last.then_inc(o_in_psum, 1)

            def transpose_attended(i, s):
                pe.wait_ge(att_ready, count(i, 2, s))
                for c in range(DC):
                    last = nc.tensor.transpose(ps_b[s][:, c * P:(c + 1) * P], att[s][:, c * P:(c + 1) * P], ident)
                last.then_inc(aT_in_psum, 1)

            def project_out(i, s):
                pe.wait_ge(aT_ready, count(i, 2, s))
                for k in range(DC):
                    last = nc.tensor.matmul(ps_a[s][:, 0:DIM], aT[s][:, k, :], wo[:, k, :],
                                            start=(k == 0), stop=(k == DC - 1))
                last.then_inc(y_in_psum, 1)

            def mlp_up(i, s):
                pe.wait_ge(hT_ready, count(i, 2, s))
                for half, bank in enumerate((ps_a[s], ps_b[s])):
                    for c in range(HC // 2):
                        h = half * (HC // 2) + c
                        for k in range(DC):
                            last = nc.tensor.matmul(bank[:, c * P:(c + 1) * P], w1[:, k, h * P:(h + 1) * P], hT[s][:, k, :],
                                                    start=(k == 0), stop=(k == DC - 1))
                    last.then_inc(hid_in_psum, 1)

            def mlp_down(i, s):
                for half in range(2):
                    pe.wait_ge(hid_ready, count(i, 4, 2 * s + half))
                    for c in range(HC // 2):
                        h = half * (HC // 2) + c
                        last = nc.tensor.matmul(ps_a[s][:, 0:DIM], hidT[s][:, h, :], w2[:, h, :],
                                                start=(h == 0), stop=(h == HC - 1))
                last.then_inc(y_in_psum, 1)

            pe.wait_ge(set_up, 5)
            with pe.Fori(0, ROUNDS) as i:
                for s in range(2):
                    latents(i, s)
                    context(i, s)
                for stage in (project, scores, transpose_probs, attend, transpose_attended, project_out, normed):
                    for s in range(2):
                        stage(i, s)
                for s in range(2):
                    mlp_up(i, s)
                for s in range(2):
                    mlp_down(i, s)

        running.close()
        cleared(nc, semaphores)


def wide_attention_layer(nc, x_in, ctx, x_out, w, col, row, ident):
    with ExitStack() as held:
        semaphores, running = [], ExitStack()

        def sb(name, shape, dtype=F32):
            return held.enter_context(nc.sbuf_tensor("l2_" + name, shape, dtype))

        def sem(name):
            semaphores.append(held.enter_context(nc.semaphore("l2_" + name)))
            return semaphores[-1]

        def bank(name):
            return held.enter_context(nc.psum_tensor("l2_ps_" + name, [P, BANK], F32))

        ROUND = 2 * P
        KEYS = P + 1
        scale = WIDE ** -0.5

        x_tile = sb("x_tile", [P, 2, DIM])
        c_tile = sb("c_tile", [P, 2, DIM])
        stats = [sb(f"stats{u}", [P, 6]) for u in range(2)]
        pad = [sb(f"pad{u}", [P, 1]) for u in range(2)]
        mean_var = [sb(f"mean_var{u}", [P, 2]) for u in range(2)]
        var_eps = [sb(f"var_eps{u}", [P, 1]) for u in range(2)]
        rstd = [sb(f"rstd{u}", [P, 1]) for u in range(2)]
        minus_half = sb("minus_half", [P, 1])
        one = sb("one", [P, 1])
        xn = sb("xn", [P, 2, DIM])
        hT = sb("hT", [P, DC, ROUND])
        cT = sb("cT", [P, DC, ROUND])
        qT = sb("qT", [P, ROUND])
        kT = sb("kT", [P, 2, KEYS])
        v = [[sb(f"v{g}{u}", [P, 4 * WIDE]) for u in range(2)] for g in range(2)]
        other_sequence = sb("other_sequence", [P, KEYS])
        probs = [sb(f"probs{u}", [P, KEYS]) for u in range(2)]
        row_max = [sb(f"row_max{u}", [P, 1]) for u in range(2)]
        shift = [sb(f"shift{u}", [P, 1]) for u in range(2)]
        row_sum = [sb(f"row_sum{u}", [P, 1]) for u in range(2)]
        inv_sum = [sb(f"inv_sum{u}", [P, 1]) for u in range(2)]
        learned = [sb(f"learned{u}", [P, P]) for u in range(2)]
        learnedT = sb("learnedT", [P, 2, P])
        pT = sb("pT", [P, 2, P])
        oT = sb("oT", [P, 2, P])
        res = sb("res", [P, 2, DIM])
        res_b = sb("res_b", [P, 2, DIM])
        hidT = sb("hidT", [P, HC, ROUND])
        y_out = sb("y_out", [P, 2, DIM])
        value_gap = sb("value_gap", [P, HEADS, HEADS])
        gap_out = [sb(f"gap_out{a}", [HEADS, DIM]) for a in range(2)]
        out_bias = [sb(f"out_bias{a}", [P, DIM]) for a in range(2)]
        ps_q, ps_k, ps_v, ps_s, ps_p, ps_o, ps_y, ps_x = (bank(n) for n in "qkvspoyx")

        x_loaded, c_loaded, stored = sem("x_loaded"), sem("c_loaded"), sem("stored")
        set_up = sem("set_up")
        gap_ready = sem("gap_ready")
        folded_in_psum = sem("folded_in_psum")
        folded_ready = sem("folded_ready")
        vector_step = sem("vector_step")
        var_ready = sem("var_ready")
        rstd_ready = sem("rstd_ready")
        xn_ready = sem("xn_ready")
        xT_in_psum = sem("xT_in_psum")
        hT_ready = sem("hT_ready")
        cT_in_psum = sem("cT_in_psum")
        cT_ready = sem("cT_ready")
        q_in_psum, q_ready = sem("q_in_psum"), sem("q_ready")
        k_in_psum, k_ready = sem("k_in_psum"), sem("k_ready")
        learned_key_ready = sem("learned_key_ready")
        v_in_psum, v_ready = sem("v_in_psum"), sem("v_ready")
        s_in_psum = sem("s_in_psum")
        shift_ready = sem("shift_ready")
        exp_ready = sem("exp_ready")
        p_ready = sem("p_ready")
        learned_ready = sem("learned_ready")
        pT_in_psum, pT_ready = sem("pT_in_psum"), sem("pT_ready")
        o_in_psum, o_ready = sem("o_in_psum"), sem("o_ready")
        learnedT_in_psum, learnedT_ready = sem("learnedT_in_psum"), sem("learnedT_ready")
        y_in_psum = sem("y_in_psum")
        res_ready = sem("res_ready")
        res_b_ready = sem("res_b_ready")
        hid_in_psum, hid_ready = sem("hid_in_psum"), sem("hid_ready")
        y_ready = sem("y_ready")

        wq = [w["l2_wq1"], w["l2_wq2"]]
        wk = [w["l2_wk1"], w["l2_wk2"]]
        wv = [w["l2_wv1"], w["l2_wv2"]]
        wo = [w["l2_wo1"], w["l2_wo2"]]

        def rows_of(dram, first):
            return dram[bass.ds(first, ROUND), :].rearrange("(u p) d -> p u d", p=P)

        def per_head(i, a, h):
            return count(i, 2 * HEADS, a * HEADS + h)

        def per_head_tile(i, a, h, u):
            return count(i, 4 * HEADS, (a * HEADS + h) * 2 + u)

        def value_event(i, a, g, u):
            return count(i, 16, a * 8 + g * 2 + u)

        block = running.enter_context(nc.Block())

        @block.sync
        def _(sp):
            sp.dma_start(x_tile[:], rows_of(x_in, 0)).then_inc(x_loaded, 16)
            sp.dma_start(c_tile[:], rows_of(ctx, 0)).then_inc(c_loaded, 16)
            sp.sem_inc(stored, 16)
            with sp.Fori(0, ROUNDS - 1) as i:
                sp.wait_ge(cT_in_psum, count(i, 1, 0))
                sp.nop()
                sp.dma_start(c_tile[:], rows_of(ctx, i * ROUND + ROUND)).then_inc(c_loaded, 16)
                sp.wait_ge(res_b_ready, count(i, 6, 1))
                sp.wait_ge(xn_ready, count(i, 6, 1))
                sp.nop()
                sp.dma_start(x_tile[:], rows_of(x_in, i * ROUND + ROUND)).then_inc(x_loaded, 16)
                sp.wait_ge(y_ready, count(i, 2, 1))
                sp.nop()
                sp.dma_start(rows_of(x_out, i * ROUND), y_out[:]).then_inc(stored, 16)
            sp.wait_ge(y_ready, 2 * ROUNDS)
            sp.dma_start(rows_of(x_out, (ROUNDS - 1) * ROUND), y_out[:]).then_inc(stored, 16)
            sp.wait_ge(stored, 16 * (ROUNDS + 1))

        @block.gpsimd
        def _(pool):
            nc.gpsimd.memset(minus_half[:], -0.5).then_inc(set_up, 1)
            nc.gpsimd.memset(one[:], 1.0).then_inc(set_up, 1)
            nc.gpsimd.memset(other_sequence[:], 0.0).then_inc(set_up, 1)
            nc.gpsimd.memset(value_gap[:], 0.0).then_inc(set_up, 1)
            for u in range(2):
                nc.gpsimd.memset(learned[u][:], 0.0).then_inc(set_up, 1)
            pool.wait_ge(set_up, 6)
            for b in range(2):
                nc.gpsimd.memset(other_sequence[b * SEQ:(b + 1) * SEQ, (1 - b) * SEQ:(2 - b) * SEQ], MINUS_INF).then_inc(set_up, 1)
            pool.wait_ge(set_up, 8)
            pool.wait_ge(folded_ready, 4)

            def inverse_deviation(i, n, u):
                pool.wait_ge(var_ready, count(i, 6, 2 * n + u))
                nc.gpsimd.tensor_tensor(rstd[u][:], var_eps[u][:], minus_half[:], ALU.pow).then_inc(rstd_ready, 1)

            def residual_with_bias(n, u, source, bias):
                nc.gpsimd.tensor_tensor(res_b[:, u, :], source[:, u, :], bias, ALU.add).then_inc(res_b_ready, 1)

            def learned_key(i, a, h):
                pool.wait_ge(k_in_psum, per_head(i, a, h))
                nc.gpsimd.tensor_tensor(kT[:, :, P:KEYS], col(f"l2_bias_k{a + 1}", h).unsqueeze(1).to_broadcast([P, 2, 1]),
                                        one[:].unsqueeze(1).to_broadcast([P, 2, 1]), ALU.mult).then_inc(learned_key_ready, 1)

            def learned_probability(i, a, h):
                for u in range(2):
                    pool.wait_ge(p_ready, per_head_tile(i, a, h, u))
                    nc.gpsimd.tensor_tensor(learned[u][:, h:h + 1], probs[u][:, P:KEYS], one[:], ALU.mult).then_inc(learned_ready, 1)

            with pool.Fori(0, ROUNDS) as i:
                for n in range(3):
                    source = x_tile if n == 0 else res
                    bias = (out_bias[0][:], out_bias[1][:], row["l2_b_fc2"])[n]
                    for u in range(2):
                        inverse_deviation(i, n, u)
                    for u in range(2):
                        residual_with_bias(n, u, source, bias)
                    if n < 2:
                        for h in range(HEADS + 1):
                            if h < HEADS:
                                learned_key(i, n, h)
                            if h > 0:
                                learned_probability(i, n, h - 1)

        @block.scalar
        def _(act):
            def normed_transposed(i, n):
                act.wait_ge(xT_in_psum, count(i, 3, n))
                for c in range(DC):
                    last = nc.scalar.activation(hT[:, c, :], ps_x[:, c * ROUND:(c + 1) * ROUND], ACT.Identity,
                                                bias=col(f"l2_ln{n}_b", c), scale=col(f"l2_ln{n}_s", c))
                last.then_inc(hT_ready, 1)

            def queries(i, a, h):
                act.wait_ge(q_in_psum, per_head(i, a, h))
                nc.scalar.activation(qT[:], ps_q[:, 0:ROUND], ACT.Identity, bias=col(f"l2_bq{a + 1}", h), scale=1.0
                                     ).then_inc(q_ready, 1)

            def values(i, a, g, u):
                act.wait_ge(v_in_psum, value_event(i, a, g, u))
                nc.scalar.activation(v[g % 2][u][:], ps_v[:], ACT.Copy).then_inc(v_ready, 1)

            def exponentials(i, a, h):
                for u in range(2):
                    act.wait_ge(shift_ready, per_head_tile(i, a, h, u))
                    nc.scalar.activation(probs[u][:], probs[u][:], ACT.Exp, bias=shift[u][:], scale=scale,
                                         accum_out=row_sum[u][:]).then_inc(exp_ready, 1)

            def attended(i, a, h):
                act.wait_ge(o_in_psum, per_head(i, a, h))
                nc.scalar.activation(oT[:].rearrange("d u q -> d (u q)"), ps_o[:, 0:ROUND], ACT.Copy).then_inc(o_ready, 1)

            def learned_transposed(i, a):
                act.wait_ge(learnedT_in_psum, count(i, 2, a))
                nc.scalar.activation(learnedT[:].rearrange("h u q -> h (u q)"), ps_x[:, 0:ROUND], ACT.Copy
                                     ).then_inc(learnedT_ready, 1)

            def hidden(i):
                for j, ps in enumerate((ps_q, ps_k, ps_v, ps_o)):
                    act.wait_ge(hid_in_psum, count(i, 4, j))
                    for c in range(2):
                        last = nc.scalar.activation(hidT[:, 2 * j + c, :], ps[:, c * ROUND:(c + 1) * ROUND], ACT.Gelu,
                                                    bias=col("l2_b_fc1", 2 * j + c), scale=1.0)
                    last.then_inc(hid_ready, 1)

            act.wait_ge(folded_ready, 4)
            with act.Fori(0, ROUNDS) as i:
                for a in range(2):
                    for u in range(2):
                        values(i, a, 0, u)
                    normed_transposed(i, a)
                    for h in range(HEADS + 1):
                        if h > 0:
                            exponentials(i, a, h - 1)
                        if h < HEADS:
                            queries(i, a, h)
                            g, r = divmod(h, 4)
                            if r % 2 and g < 3:
                                values(i, a, g + 1, r // 2)
                        if h > 0:
                            attended(i, a, h - 1)
                    learned_transposed(i, a)
                normed_transposed(i, 2)
                hidden(i)

        @block.vector
        def _(dve):
            links = Links(vector_step, dve, L2_VECTOR_LINKS)

            def layer_norm(i, n, u, source):
                links.mark(nc.vector.bn_stats(stats[u][:], source[:, u, :]))
                links.wait(i)
                nc.vector.memset(pad[u][:], 0.0)
                links.mark(nc.vector.bn_aggr(mean_var[u][:], stats[u][:]))
                links.wait(i)
                nc.vector.tensor_scalar(var_eps[u][:], mean_var[u][:, 1:2], LN_EPS, None, ALU.add).then_inc(var_ready, 1)
                dve.wait_ge(rstd_ready, count(i, 6, 2 * n + u))
                nc.vector.tensor_scalar(xn[:, u, :], source[:, u, :], mean_var[u][:, 0:1], rstd[u][:], ALU.subtract, ALU.mult
                                        ).then_inc(xn_ready, 1)

            def keys(i, a, h):
                dve.wait_ge(k_in_psum, per_head(i, a, h))
                nc.vector.tensor_scalar(kT[:, :, 0:P], ps_k[:, 0:ROUND].rearrange("d (u k) -> d u k", u=2),
                                        col(f"l2_bk{a + 1}", h), None, ALU.add).then_inc(k_ready, 1)

            def maxima(i, a, h):
                dve.wait_ge(s_in_psum, per_head(i, a, h))
                if h > 0:
                    dve.wait_ge(learned_ready, per_head_tile(i, a, h - 1, 1))
                for u in range(2):
                    nc.vector.memset(pad[u][:], 0.0)
                    links.mark(nc.vector.tensor_tensor_reduce(
                        out=probs[u][:], in0=ps_s[:, u * KEYS:(u + 1) * KEYS], in1=other_sequence[:], scale=1.0,
                        scalar=MINUS_INF, op0=ALU.add, op1=ALU.max, accum_out=row_max[u][:]))
                for u in range(2):
                    if u == 0:
                        links.wait(i)
                    nc.vector.tensor_scalar(shift[u][:], row_max[u][:], -scale, None, ALU.mult).then_inc(shift_ready, 1)

            def normalise(i, a, h):
                for u in range(2):
                    dve.wait_ge(exp_ready, per_head_tile(i, a, h, u))
                    links.mark(nc.vector.reciprocal(inv_sum[u][:], row_sum[u][:]))
                    links.wait(i)
                    nc.vector.tensor_scalar(probs[u][:], probs[u][:], inv_sum[u][:], None, ALU.mult).then_inc(p_ready, 1)

            def probs_transposed(i, a, h):
                dve.wait_ge(pT_in_psum, per_head(i, a, h))
                nc.vector.tensor_copy(pT[:].rearrange("k u q -> k (u q)"), ps_p[:, 0:ROUND]).then_inc(pT_ready, 1)

            def add_residual(i, n):
                dve.wait_ge(y_in_psum, count(i, 3, n))
                for u in range(2):
                    dve.wait_ge(res_b_ready, count(i, 6, 2 * n + u))
                    y = ps_y[:, u * DIM:(u + 1) * DIM]
                    if n < 2:
                        nc.vector.tensor_tensor(res[:, u, :], y, res_b[:, u, :], ALU.add).then_inc(res_ready, 1)
                    else:
                        dve.wait_ge(stored, (i + 1) * 16)
                        nc.vector.tensor_tensor(y_out[:, u, :], y, res_b[:, u, :], ALU.add).then_inc(y_ready, 1)
                if n < 2:
                    dve.wait_ge(res_ready, count(i, 4, 2 * n + 1))

            dve.wait_ge(set_up, 8)
            bv_wide = hidT[:].rearrange("p c t -> p (c t)").rearrange("p (h m) -> p h m", m=P)
            for a in range(2):
                if a:
                    dve.wait_ge(folded_in_psum, a)
                bias_v, bv = (col(f"l2_bias_v{a + 1}", 0, HEADS), col(f"l2_bv{a + 1}", 0, HEADS))
                nc.vector.tensor_tensor(value_gap[:].rearrange("p h m -> p (h m)")[:, 0:HEADS * HEADS:HEADS + 1],
                                        bias_v, bv, ALU.subtract)
                nc.vector.tensor_copy(bv_wide, bv.unsqueeze(2).to_broadcast([P, HEADS, P])).then_inc(gap_ready, 1)
                dve.wait_ge(folded_in_psum, a + 1)
                nc.vector.tensor_tensor(out_bias[a][:], ps_y[:, 0:DIM], row[f"l2_bo{a + 1}"], ALU.add).then_inc(folded_ready, 1)
                nc.vector.tensor_copy(gap_out[a][:], ps_x[0:HEADS, 0:DIM]).then_inc(folded_ready, 1)

            with dve.Fori(0, ROUNDS) as i:
                dve.wait_ge(cT_in_psum, count(i, 1, 0))
                nc.vector.tensor_copy(cT[:].rearrange("f c t -> f (c t)"), ps_x[:]).then_inc(cT_ready, 1)
                for a in range(2):
                    if a == 0:
                        dve.wait_ge(x_loaded, count(i, 1, 0) * 16)
                    for u in range(2):
                        layer_norm(i, a, u, res if a else x_tile)
                    for h in range(HEADS + 1):
                        if h > 0:
                            maxima(i, a, h - 1)
                            normalise(i, a, h - 1)
                        if h < HEADS:
                            keys(i, a, h)
                        if h > 0:
                            probs_transposed(i, a, h - 1)
                    add_residual(i, a)
                for u in range(2):
                    layer_norm(i, 2, u, res)
                add_residual(i, 2)
            links.check()

        @block.tensor
        def _(pe):
            def context(i):
                pe.wait_ge(c_loaded, count(i, 1, 0) * 16)
                for c in range(DC):
                    for u in range(2):
                        last = nc.tensor.transpose(ps_x[:, c * ROUND + u * P:c * ROUND + (u + 1) * P],
                                                   c_tile[:, u, c * P:(c + 1) * P], ident)
                last.then_inc(cT_in_psum, 1)
                pe.wait_ge(cT_ready, count(i, 1, 0))

            def normed(i, n):
                for u in range(2):
                    pe.wait_ge(xn_ready, count(i, 6, 2 * n + u))
                    for c in range(DC):
                        last = nc.tensor.transpose(ps_x[:, c * ROUND + u * P:c * ROUND + (u + 1) * P],
                                                   xn[:, u, c * P:(c + 1) * P], ident)
                last.then_inc(xT_in_psum, 1)

            def project(ps, weights, h, moving, ready):
                for k in range(DC):
                    last = nc.tensor.matmul(ps[:, 0:ROUND], weights[:, k, h * WIDE:(h + 1) * WIDE], moving[:, k, :],
                                            start=(k == 0), stop=(k == DC - 1))
                last.then_inc(ready, 1)

            def values(i, a, g, u):
                if g or u:
                    pe.wait_ge(v_ready, value_event(i, a, g, u) - 1)
                for k in range(DC):
                    last = nc.tensor.matmul(ps_v[:], cT[:, k, u * P:(u + 1) * P],
                                            wv[a][:, k, g * 4 * WIDE:(g + 1) * 4 * WIDE],
                                            start=(k == 0), stop=(k == DC - 1))
                last.then_inc(v_in_psum, 1)

            def scores(i, a, h):
                pe.wait_ge(q_ready, per_head(i, a, h))
                pe.wait_ge(k_ready, per_head(i, a, h))
                pe.wait_ge(learned_key_ready, per_head(i, a, h))
                for u in range(2):
                    last = nc.tensor.matmul(ps_s[:, u * KEYS:(u + 1) * KEYS], qT[:, u * P:(u + 1) * P], kT[:, u, :],
                                            start=True, stop=True)
                last.then_inc(s_in_psum, 1)

            def transpose_probs(i, a, h):
                for u in range(2):
                    pe.wait_ge(p_ready, per_head_tile(i, a, h, u))
                    last = nc.tensor.transpose(ps_p[:, u * P:(u + 1) * P], probs[u][:, 0:P], ident)
                last.then_inc(pT_in_psum, 1)

            def attend(i, a, h):
                g, r = divmod(h, 4)
                pe.wait_ge(pT_ready, per_head(i, a, h))
                if r == 0:
                    pe.wait_ge(v_ready, value_event(i, a, g, 1))
                for u in range(2):
                    last = nc.tensor.matmul(ps_o[:, u * P:(u + 1) * P], v[g % 2][u][:, r * WIDE:(r + 1) * WIDE],
                                            pT[:, u, :], start=True, stop=True)
                last.then_inc(o_in_psum, 1)

            def project_out(i, a, h):
                pe.wait_ge(o_ready, per_head(i, a, h))
                for u in range(2):
                    nc.tensor.matmul(ps_y[:, u * DIM:(u + 1) * DIM], oT[:, u, :], wo[a][:, h, :],
                                     start=(h == 0 and u == 0), stop=False, skip_group_check=True)

            def learned_value(i, a):
                pe.wait_ge(learned_ready, per_head_tile(i, a, HEADS - 1, 1))
                for u in range(2):
                    last = nc.tensor.transpose(ps_x[:, u * P:(u + 1) * P], learned[u][:], ident)
                last.then_inc(learnedT_in_psum, 1)

            def add_learned_value(i, a):
                pe.wait_ge(learnedT_ready, count(i, 2, a))
                for u in range(2):
                    last = nc.tensor.matmul(ps_y[:, u * DIM:(u + 1) * DIM], learnedT[0:HEADS, u, :], gap_out[a][:],
                                            start=False, stop=True, skip_group_check=True)
                last.then_inc(y_in_psum, 1)

            def mlp(i):
                pe.wait_ge(hT_ready, count(i, 3, 2))
                for j, ps in enumerate((ps_q, ps_k, ps_v, ps_o)):
                    for c in range(2):
                        h = 2 * j + c
                        for k in range(DC):
                            last = nc.tensor.matmul(ps[:, c * ROUND:(c + 1) * ROUND], w["l2_w_fc1"][:, k, h * P:(h + 1) * P],
                                                    hT[:, k, :], start=(k == 0), stop=(k == DC - 1))
                    last.then_inc(hid_in_psum, 1)
                for j in range(4):
                    pe.wait_ge(hid_ready, count(i, 4, j))
                    for h in (2 * j, 2 * j + 1):
                        for u in range(2):
                            last = nc.tensor.matmul(ps_y[:, u * DIM:(u + 1) * DIM], hidT[:, h, u * P:(u + 1) * P],
                                                    w["l2_w_fc2"][:, h, :], start=(h == 0 and u == 0),
                                                    stop=(h == HC - 1), skip_group_check=True)
                last.then_inc(y_in_psum, 1)

            bv_wide = hidT[:].rearrange("p c t -> p (c t)").rearrange("p (h m) -> p h m", m=P)
            for a in range(2):
                pe.wait_ge(gap_ready, a + 1)
                if a:
                    pe.wait_ge(folded_ready, 2 * a)
                for h in range(HEADS):
                    nc.tensor.matmul(ps_y[:, 0:DIM], bv_wide[:, h, :], wo[a][:, h, :], start=(h == 0), stop=(h == HEADS - 1))
                for h in range(HEADS):
                    last = nc.tensor.matmul(ps_x[0:HEADS, 0:DIM], value_gap[:, h, :], wo[a][:, h, :],
                                            start=(h == 0), stop=(h == HEADS - 1))
                last.then_inc(folded_in_psum, 1)
            pe.wait_ge(folded_ready, 4)

            with pe.Fori(0, ROUNDS) as i:
                context(i)
                for a in range(2):
                    for u in range(2):
                        values(i, a, 0, u)
                    normed(i, a)
                    pe.wait_ge(hT_ready, count(i, 3, a))
                    for h in range(HEADS + 2):
                        if h < HEADS:
                            project(ps_q, wq[a], h, hT, q_in_psum)
                            project(ps_k, wk[a], h, cT, k_in_psum)
                        if h >= 2:
                            project_out(i, a, h - 2)
                        if 1 <= h <= HEADS:
                            transpose_probs(i, a, h - 1)
                        if h == HEADS:
                            learned_value(i, a)
                        if h < HEADS:
                            g, r = divmod(h, 4)
                            if r % 2 and g < 3:
                                values(i, a, g + 1, r // 2)
                            scores(i, a, h)
                        if 1 <= h <= HEADS:
                            attend(i, a, h - 1)
                    add_learned_value(i, a)
                normed(i, 2)
                mlp(i)

        running.close()
        cleared(nc, semaphores)


def recurrent_layer(nc, x_in, ctx, x_out, w, col, ident, select, head_of):
    with ExitStack() as held:
        semaphores, running = [], ExitStack()

        def sb(name, shape, dtype=F32):
            return held.enter_context(nc.sbuf_tensor("l3_" + name, shape, dtype))

        def sem(name):
            semaphores.append(held.enter_context(nc.semaphore("l3_" + name)))
            return semaphores[-1]

        ROUND = 2 * P
        NB = ROUND // SEQ
        ORDER = (0, 2, 1, 3, 4)

        x_tile = sb("x_tile", [P, 2, DIM])
        first_rows = sb("first_rows", [2 * NB, DIM])
        state = sb("state", [P, DC, NB, HEAD8])
        stats = [sb(f"stats{u}", [P, 6]) for u in range(2)]
        pad = [sb(f"pad{u}", [P, 1]) for u in range(2)]
        mean_var = [sb(f"mean_var{u}", [P, 2]) for u in range(2)]
        var_eps = [sb(f"var_eps{u}", [P, 1]) for u in range(2)]
        rstd = [sb(f"rstd{u}", [P, 1]) for u in range(2)]
        minus_half = sb("minus_half", [P, 1])
        one_column = sb("one_column", [P, 1])
        xn = sb("xn", [P, 2, DIM])
        xnT = [sb(f"xnT{n}", [P, DC, NB, 1 + SEQ]) for n in range(2)]
        sxT = sb("sxT", [P, DC, NB, SEQ])
        mixed = sb("mixed", [P, DC, NB, SEQ])
        loraT = sb("loraT", [P, 2, ROUND])
        part = [sb(f"part{j}", [P, DC, NB, SEQ]) for j in range(5)]
        x5 = [sb(f"x5_{j}", [P, DC, ROUND]) for j in range(5)]
        decayT = sb("decayT", [DECAY, ROUND])
        rate = sb("rate", [P, DC, ROUND])
        wT = sb("wT", [P, DC, NB, SEQ])
        kT, vT, rT, gT = (sb(n, [P, DC, ROUND]) for n in ("kT", "vT", "rT", "gT"))
        gate = sb("gate", [P, DC, ROUND])
        rukT = sb("rukT", [P, DC, ROUND])
        s = [sb(f"s{c}", [P, HEAD8, NB, SEQ]) for c in range(DC)]
        ruk = sb("ruk", [P, 2, DC, P // HEAD8])
        att = sb("att", [P, 2, DIM])
        square = sb("square", [P, 2, DIM])
        group = [sb(f"group{n}", [P, 4 * P // HEAD8]) for n in range(4)]
        gated = sb("gated", [P, DC, ROUND])
        res = sb("res", [P, 2, DIM])
        xkT, xrT = sb("xkT", [P, DC, ROUND]), sb("xrT", [P, DC, ROUND])
        kk, kk2 = sb("kk", [P, DC, ROUND]), sb("kk2", [P, DC, ROUND])
        receptance = sb("receptance", [P, 2, DIM])
        part_y = sb("part_y", [P, 2, DIM])
        y_out = sb("y_out", [P, 2, DIM])
        ps_j = [held.enter_context(nc.psum_tensor(f"l3_ps_j{j}", [P, BANK], F32)) for j in range(5)]
        ps_m = [held.enter_context(nc.psum_tensor(f"l3_ps_m{j}", [P, BANK], F32)) for j in range(3)]

        x_loaded, rows_loaded, state_loaded, stored = (sem(n) for n in ("x_loaded", "rows_loaded", "state_loaded", "stored"))
        set_up = sem("set_up")
        vector_step = sem("vector_step")
        scalar_step = sem("scalar_step")
        var_ready, rstd_ready = sem("var_ready"), sem("rstd_ready")
        xn_ready = sem("xn_ready")
        xT_in_psum, xnT_ready = sem("xT_in_psum"), sem("xnT_ready")
        rows_in_psum, rows_ready = sem("rows_in_psum"), sem("rows_ready")
        sx_ready = sem("sx_ready")
        mixed_ready = sem("mixed_ready")
        lora_in_psum, lora_ready = sem("lora_in_psum"), sem("lora_ready")
        mix_in_psum = sem("mix_in_psum")
        part_ready, x5_ready = sem("part_ready"), sem("x5_ready")
        k_in_psum, k_ready = sem("k_in_psum"), sem("k_ready")
        v_in_psum, v_ready = sem("v_in_psum"), sem("v_ready")
        decay_in_psum, decay_ready = sem("decay_in_psum"), sem("decay_ready")
        rate_in_psum, w_ready = sem("rate_in_psum"), sem("w_ready")
        r_in_psum, r_ready = sem("r_in_psum"), sem("r_ready")
        g_in_psum, g_ready = sem("g_in_psum"), sem("g_ready")
        gate_ready = sem("gate_ready")
        start_ready = sem("start_ready")
        spread_in_psum = sem("spread_in_psum")
        addend_ready = sem("addend_ready")
        out_ready = sem("out_ready")
        ruk_ready = sem("ruk_ready")
        att_in_psum = sem("att_in_psum")
        deviation_ready, root_ready = sem("deviation_ready"), sem("root_ready")
        att_ready = sem("att_ready")
        attT_in_psum, attT_ready = sem("attT_in_psum"), sem("attT_ready")
        gated_ready = sem("gated_ready")
        y_in_psum = sem("y_in_psum")
        channel_ready = sem("channel_ready")
        kk_in_psum, kk_ready = sem("kk_in_psum"), sem("kk_ready")
        kk2_ready = sem("kk2_ready")
        rr_in_psum, rr_ready = sem("rr_in_psum"), sem("rr_ready")
        kv_in_psum = sem("kv_in_psum")
        y_ready = sem("y_ready")

        one = lambda i: count(i, 1, 0)

        def rows_of(dram, first):
            return dram[bass.ds(first, ROUND), :].rearrange("(u p) d -> p u d", p=P)

        def flat(t):
            return t.rearrange("p c b t -> p c (b t)")

        ctx_rows = ctx.rearrange("(b r) d -> b (r d)", r=SEQ)

        block = running.enter_context(nc.Block())

        @block.sync
        def _(sp):
            def load_x(b0):
                sp.dma_start(x_tile[:], rows_of(x_in, b0 * SEQ)).then_inc(x_loaded, 16)

            def load_rows(b0):
                for r in range(2):
                    sp.dma_start(first_rows[r * NB:(r + 1) * NB, :], ctx_rows[bass.ds(b0, NB), r * DIM:(r + 1) * DIM]
                                 ).then_inc(rows_loaded, 16)

            def load_state(b0):
                for c in range(DC):
                    first = 2 * DIM + c * P * HEAD8
                    sp.dma_start(state[:, c, :, :], ctx_rows[bass.ds(b0, NB), first:first + P * HEAD8].rearrange(
                        "b (p d) -> p b d", d=HEAD8)).then_inc(state_loaded, 16)

            load_x(0)
            load_rows(0)
            load_state(0)
            sp.sem_inc(stored, 16)
            with sp.Fori(0, ROUNDS - 1) as i:
                sp.wait_ge(rows_in_psum, one(i))
                sp.nop()
                load_rows(i * NB + NB)
                sp.wait_ge(start_ready, one(i))
                sp.nop()
                load_state(i * NB + NB)
                sp.wait_ge(xn_ready, count(i, 4, 2))
                sp.nop()
                load_x(i * NB + NB)
                sp.wait_ge(y_ready, one(i))
                sp.nop()
                sp.dma_start(rows_of(x_out, i * ROUND), y_out[:]).then_inc(stored, 16)
            sp.wait_ge(y_ready, ROUNDS)
            sp.dma_start(rows_of(x_out, (ROUNDS - 1) * ROUND), y_out[:]).then_inc(stored, 16)
            sp.wait_ge(stored, 16 * (ROUNDS + 1))

        @block.gpsimd
        def _(pool):
            nc.gpsimd.memset(minus_half[:], -0.5).then_inc(set_up, 1)
            nc.gpsimd.memset(one_column[:], 1.0).then_inc(set_up, 1)
            nc.gpsimd.memset(wT[:], 0.0).then_inc(set_up, 1)
            pool.wait_ge(set_up, 3)

            def inverse_deviation(i, n, u):
                pool.wait_ge(var_ready, count(i, 4, 2 * n + u))
                nc.gpsimd.tensor_tensor(rstd[u][:], var_eps[u][:], minus_half[:], ALU.pow).then_inc(rstd_ready, 1)

            with pool.Fori(0, ROUNDS) as i:
                for u in range(2):
                    inverse_deviation(i, 0, u)
                pool.wait_ge(state_loaded, one(i) * 16 * DC)
                for c in range(DC):
                    last = nc.gpsimd.tensor_tensor(s[c][:, :, :, 0], state[:, c, :, :].rearrange("p b d -> p d b"),
                                                   one_column[:].unsqueeze(1).to_broadcast([P, HEAD8, NB]), ALU.mult)
                last.then_inc(start_ready, 1)
                for n, j in enumerate(ORDER):
                    pool.wait_ge(part_ready, count(i, 5, n))
                    for c in range(DC):
                        last = nc.gpsimd.tensor_tensor(x5[j][:, c, :].rearrange("p (b t) -> p b t", t=SEQ),
                                                       part[j][:, c, :, :], xnT[0][:, c, :, 1:], ALU.add)
                    last.then_inc(x5_ready, 1)
                for u in range(2):
                    inverse_deviation(i, 1, u)
                pool.wait_ge(kk_ready, one(i))
                nc.gpsimd.tensor_tensor(kk2[:], kk[:], kk[:], ALU.mult).then_inc(kk2_ready, 1)

        @block.scalar
        def _(act):
            links = Links(scalar_step, act, L3_SCALAR_LINKS)

            def normed_transposed(i, n, ps):
                act.wait_ge(xT_in_psum, count(i, 2, n))
                for c in range(DC):
                    last = nc.scalar.activation(xnT[n][:, c, :, 1:], ps[:, c * ROUND:(c + 1) * ROUND].rearrange(
                        "f (b t) -> f b t", t=SEQ), ACT.Identity, bias=col(f"l3_ln{n + 1}_b", c), scale=col(f"l3_ln{n + 1}_w", c))
                last.then_inc(xnT_ready, 1)

            def copied(i, ready, out, ps, done):
                act.wait_ge(ready, one(i))
                nc.scalar.activation(out[:].rearrange("p c t -> p (c t)"), ps[:], ACT.Copy).then_inc(done, 1)

            with act.Fori(0, ROUNDS) as i:
                act.wait_ge(rows_in_psum, one(i))
                for n in range(2):
                    last = nc.scalar.activation(xnT[n][:, :, :, 0], ps_m[1][:, 0:2 * DC * NB].rearrange(
                        "f (c r b) -> f c r b", r=2, b=NB)[:, :, 1 - n, :], ACT.Copy)
                last.then_inc(rows_ready, 1)
                normed_transposed(i, 0, ps_m[0])
                act.wait_ge(lora_in_psum, one(i))
                nc.scalar.activation(loraT[:, 0, :], ps_m[1][:, 0:ROUND], ACT.Tanh)
                nc.scalar.activation(loraT[0:LORA, 1, :], ps_m[1][0:LORA, ROUND:2 * ROUND], ACT.Tanh).then_inc(lora_ready, 1)
                copied(i, k_in_psum, kT, ps_j[0], k_ready)
                copied(i, v_in_psum, vT, ps_j[2], v_ready)
                act.wait_ge(decay_in_psum, one(i))
                nc.scalar.activation(decayT[:], ps_j[1][0:DECAY, 0:ROUND], ACT.Tanh).then_inc(decay_ready, 1)
                copied(i, r_in_psum, rT, ps_j[3], r_ready)
                act.wait_ge(rate_in_psum, one(i))
                for c in range(DC):
                    last = nc.scalar.activation(rate[:, c, :], ps_j[1][:, c * ROUND:(c + 1) * ROUND], ACT.Exp,
                                                bias=col("l3_time_decay", c), scale=1.0)
                links.mark(last)
                links.wait(i)
                for c in range(DC):
                    last = nc.scalar.activation(wT[:, c, :, 1:], rate[:, c, :].rearrange("p (b t) -> p b t", t=SEQ)[:, :, 0:SEQ - 1],
                                                ACT.Exp, scale=-1.0)
                last.then_inc(w_ready, 1)
                act.wait_ge(g_in_psum, one(i))
                nc.scalar.activation(gT[:].rearrange("p c t -> p (c t)"), ps_j[4][:], ACT.Tanh, scale=0.5).then_inc(g_ready, 1)
                act.wait_ge(deviation_ready, one(i))
                nc.scalar.activation(group[3][:], group[2][:], ACT.Sqrt).then_inc(root_ready, 1)
                act.wait_ge(attT_in_psum, one(i))
                for c in range(DC):
                    last = nc.scalar.activation(kk[:, c, :], ps_m[0][:, c * ROUND:(c + 1) * ROUND], ACT.Identity,
                                                bias=col("l3_gn_b", c), scale=col("l3_gn_w", c))
                last.then_inc(attT_ready, 1)
                normed_transposed(i, 1, ps_m[2])
                act.wait_ge(kk_in_psum, one(i))
                nc.scalar.activation(kk[:].rearrange("p c t -> p (c t)"), ps_j[0][:], ACT.Relu).then_inc(kk_ready, 1)
                act.wait_ge(rr_in_psum, one(i))
                nc.scalar.activation(receptance[:].rearrange("p u d -> p (u d)"), ps_j[1][:], ACT.Tanh, scale=0.5).then_inc(rr_ready, 1)
            links.check()

        @block.vector
        def _(dve):
            links = Links(vector_step, dve, L3_VECTOR_LINKS)

            def layer_norm(i, n, u, source):
                links.mark(nc.vector.bn_stats(stats[u][:], source[:, u, :]))
                links.wait(i)
                nc.vector.memset(pad[u][:], 0.0)
                links.mark(nc.vector.bn_aggr(mean_var[u][:], stats[u][:]))
                links.wait(i)
                nc.vector.tensor_scalar(var_eps[u][:], mean_var[u][:, 1:2], LN_EPS, None, ALU.add).then_inc(var_ready, 1)
                dve.wait_ge(rstd_ready, count(i, 4, 2 * n + u))
                nc.vector.tensor_scalar(xn[:, u, :], source[:, u, :], mean_var[u][:, 0:1], rstd[u][:], ALU.subtract, ALU.mult
                                        ).then_inc(xn_ready, 1)

            def shifted(i, n):
                dve.wait_ge(xnT_ready, count(i, 2, n))
                for c in range(DC):
                    last = nc.vector.tensor_tensor(sxT[:, c], xnT[n][:, c, :, 0:SEQ], xnT[n][:, c, :, 1:], ALU.subtract)
                links.mark(last)
                links.wait(i)

            def mix(out, n, amount):
                for c in range(DC):
                    last = nc.vector.scalar_tensor_tensor(out=out[:, c], in0=sxT[:, c], scalar=col(amount, c),
                                                          in1=xnT[n][:, c, :, 1:], op0=ALU.mult, op1=ALU.add)
                return last

            def by_token(t):
                return t.rearrange("p c (b t) -> p c b t", t=SEQ)

            dve.wait_ge(set_up, 3)
            with dve.Fori(0, ROUNDS) as i:
                dve.wait_ge(x_loaded, one(i) * 16)
                for u in range(2):
                    layer_norm(i, 0, u, x_tile)
                shifted(i, 0)
                mix(mixed[:], 0, "l3_maa_x").then_inc(mixed_ready, 1)
                for n, j in enumerate(ORDER):
                    dve.wait_ge(mix_in_psum, count(i, 5, n))
                    for c in range(DC):
                        last = nc.vector.scalar_tensor_tensor(
                            out=part[j][:, c].rearrange("p b t -> p (b t)"), in0=ps_j[j][:, c * ROUND:(c + 1) * ROUND],
                            scalar=col("l3_maa_stack", j * DC + c), in1=sxT[:, c].rearrange("p b t -> p (b t)"),
                            op0=ALU.add, op1=ALU.mult)
                    last.then_inc(part_ready, 1)
                dve.wait_ge(k_ready, one(i))
                dve.wait_ge(r_ready, one(i))
                for c in range(DC):
                    last = nc.vector.scalar_tensor_tensor(out=rukT[:, c, :], in0=rT[:, c, :], scalar=col("l3_faaaa", c),
                                                          in1=kT[:, c, :], op0=ALU.mult, op1=ALU.mult)
                last.then_inc(ruk_ready, 1)
                dve.wait_ge(g_ready, one(i))
                nc.vector.scalar_tensor_tensor(out=gate[:].rearrange("p c t -> p (c t)"), in0=gT[:].rearrange("p c t -> p (c t)"),
                                               scalar=1.0, in1=ps_j[4][:], op0=ALU.add, op1=ALU.mult).then_inc(gate_ready, 1)
                dve.wait_ge(start_ready, one(i))
                dve.wait_ge(w_ready, one(i))
                for c in range(DC):
                    for q in range(HEAD8 // 2):
                        n = c * (HEAD8 // 2) + q
                        dve.wait_ge(spread_in_psum, count(i, 8, n))
                        spread = ps_m[n % 3][:].rearrange("p (d b t) -> p d b t", d=2, t=SEQ)
                        for d in range(2):
                            last = nc.vector.tensor_tensor(s[c][:, 2 * q + d, :, 1:], spread[:, d, :, 0:SEQ - 1],
                                                           by_token(kT[:])[:, c, :, 0:SEQ - 1], ALU.mult)
                        last.then_inc(addend_ready, 1)
                        dve.wait_ge(addend_ready, count(i, 8, n))
                        for d in range(2):
                            run = s[c][:, 2 * q + d].rearrange("p b t -> p (b t)")
                            last = nc.vector.tensor_tensor_scan(run, wT[:, c].rearrange("p b t -> p (b t)"), run, 0.0,
                                                                ALU.mult, ALU.add)
                    links.mark(last)
                    links.wait(i)
                    run = s[c][:].rearrange("p d b t -> p d (b t)")
                    nc.vector.tensor_tensor(run, run, rT[:, c, :].unsqueeze(1).to_broadcast([P, HEAD8, ROUND]), ALU.mult
                                            ).then_inc(out_ready, 1)
                heads = 2 * DIM // HEAD8

                def grouped(t):
                    return t.rearrange("p (h d) -> p h d", d=HEAD8)

                def spread_over_head(t):
                    return t.unsqueeze(2).to_broadcast([P, heads, HEAD8])

                att_flat, sq_flat = (t[:].rearrange("p u d -> p (u d)") for t in (att, square))
                dve.wait_ge(att_in_psum, one(i))
                links.mark(nc.vector.tensor_copy(ruk[:].rearrange("p u c h -> p (u c h)"), ps_j[0][:, 0:heads]))
                links.wait(i)
                links.mark(nc.vector.tensor_tensor(grouped(sq_flat), grouped(ps_j[2][:]),
                                                   spread_over_head(ruk[:].rearrange("p u c h -> p (u c h)")), ALU.mult))
                links.wait(i)
                links.mark(nc.vector.tensor_tensor(att_flat, ps_j[1][:], sq_flat, ALU.add))
                links.wait(i)
                links.mark(nc.vector.tensor_reduce(group[0][:], grouped(att_flat), AX.X, ALU.add))
                links.wait(i)
                links.mark(nc.vector.tensor_scalar(group[1][:], group[0][:], 1.0 / HEAD8, None, ALU.mult))
                links.wait(i)
                links.mark(nc.vector.tensor_tensor(grouped(att_flat), grouped(att_flat), spread_over_head(group[1][:]), ALU.subtract))
                links.wait(i)
                links.mark(nc.vector.tensor_tensor(sq_flat, att_flat, att_flat, ALU.mult))
                links.wait(i)
                links.mark(nc.vector.tensor_reduce(group[0][:], grouped(sq_flat), AX.X, ALU.add))
                links.wait(i)
                nc.vector.tensor_scalar(group[2][:], group[0][:], 1.0 / HEAD8, LN_EPS, ALU.mult, ALU.add).then_inc(deviation_ready, 1)
                dve.wait_ge(root_ready, one(i))
                links.mark(nc.vector.reciprocal(group[1][:], group[3][:]))
                links.wait(i)
                nc.vector.tensor_tensor(grouped(att_flat), grouped(att_flat), spread_over_head(group[1][:]), ALU.mult
                                        ).then_inc(att_ready, 1)
                dve.wait_ge(attT_ready, one(i))
                nc.vector.scalar_tensor_tensor(out=gated[:], in0=kk[:], scalar=0.5, in1=gate[:], op0=ALU.mult, op1=ALU.mult
                                               ).then_inc(gated_ready, 1)
                dve.wait_ge(y_in_psum, one(i))
                links.mark(nc.vector.tensor_tensor(res[:].rearrange("p u d -> p (u d)"), ps_m[1][:],
                                                   x_tile[:].rearrange("p u d -> p (u d)"), ALU.add))
                links.wait(i)
                for u in range(2):
                    layer_norm(i, 1, u, res)
                shifted(i, 1)
                mix(by_token(xkT[:]), 1, "l3_ffn_maa_k").then_inc(channel_ready, 1)
                mix(by_token(xrT[:]), 1, "l3_ffn_maa_r").then_inc(channel_ready, 1)
                dve.wait_ge(rr_ready, one(i))
                dve.wait_ge(kv_in_psum, one(i))
                links.mark(nc.vector.scalar_tensor_tensor(
                    out=part_y[:].rearrange("p u d -> p (u d)"), in0=receptance[:].rearrange("p u d -> p (u d)"), scalar=1.0,
                    in1=ps_j[2][:], op0=ALU.add, op1=ALU.mult))
                links.wait(i)
                dve.wait_ge(stored, one(i) * 16)
                nc.vector.scalar_tensor_tensor(out=y_out[:], in0=part_y[:], scalar=0.5, in1=res[:], op0=ALU.mult, op1=ALU.add
                                               ).then_inc(y_ready, 1)
            links.check()

        @block.tensor
        def _(pe):
            def transposed(ps, tokens, u):
                for c in range(DC):
                    last = nc.tensor.transpose(ps[:, c * ROUND + u * P:c * ROUND + (u + 1) * P], tokens[:, u, c * P:(c + 1) * P], ident)
                return last

            def features_out(ps, weights, moving):
                for c in range(DC):
                    for k in range(DC):
                        last = nc.tensor.matmul(ps[:, c * ROUND:(c + 1) * ROUND], weights[:, k, c * P:(c + 1) * P], moving[:, k, :],
                                                start=(k == 0), stop=(k == DC - 1))
                return last

            def tokens_out(ps, weights, stationary):
                for u in range(2):
                    for k in range(DC):
                        last = nc.tensor.matmul(ps[:, u * DIM:(u + 1) * DIM], stationary[:, k, u * P:(u + 1) * P], weights[:, k, :],
                                                start=(k == 0), stop=(k == DC - 1))
                return last

            with pe.Fori(0, ROUNDS) as i:
                pe.wait_ge(rows_loaded, one(i) * 32)
                for u in range(2):
                    pe.wait_ge(xn_ready, count(i, 4, u))
                    last = transposed(ps_m[0], xn, u)
                last.then_inc(xT_in_psum, 1)
                for c in range(DC):
                    last = nc.tensor.transpose(ps_m[1][:, c * 2 * NB:(c + 1) * 2 * NB], first_rows[:, c * P:(c + 1) * P],
                                               ident[0:2 * NB, 0:2 * NB])
                last.then_inc(rows_in_psum, 1)
                pe.wait_ge(mixed_ready, one(i))
                pe.wait_ge(rows_ready, one(i))
                for k in range(DC):
                    nc.tensor.matmul(ps_m[1][:, 0:ROUND], w["l3_maa_w1"][:, k, 0:P], mixed[:, k].rearrange("p b t -> p (b t)"),
                                     start=(k == 0), stop=(k == DC - 1))
                for k in range(DC):
                    last = nc.tensor.matmul(ps_m[1][0:LORA, ROUND:2 * ROUND], w["l3_maa_w1"][:, k, P:P + LORA],
                                            mixed[:, k].rearrange("p b t -> p (b t)"), start=(k == 0), stop=(k == DC - 1))
                last.then_inc(lora_in_psum, 1)
                pe.wait_ge(lora_ready, one(i))
                for j in ORDER:
                    rows, half = (slice(LORA * j, LORA * (j + 1)), 0) if j < 4 else (slice(0, LORA), 1)
                    for c in range(DC):
                        last = nc.tensor.matmul(ps_j[j][:, c * ROUND:(c + 1) * ROUND], w["l3_maa_w2"][rows, half, c * P:(c + 1) * P],
                                                loraT[rows, half, :], start=True, stop=True)
                    last.then_inc(mix_in_psum, 1)
                x5_at = {j: n for n, j in enumerate(ORDER)}
                for j in (0, 2, 1):
                    pe.wait_ge(x5_ready, count(i, 5, x5_at[j]))
                    if j == 0:
                        features_out(ps_j[0], w["l3_Wk"], x5[0]).then_inc(k_in_psum, 1)
                    if j == 2:
                        features_out(ps_j[2], w["l3_Wv"], x5[2]).then_inc(v_in_psum, 1)
                    if j == 1:
                        for k in range(DC):
                            last = nc.tensor.matmul(ps_j[1][0:DECAY, 0:ROUND], w["l3_decay_w1"][:, k, :], x5[1][:, k, :],
                                                    start=(k == 0), stop=(k == DC - 1))
                        last.then_inc(decay_in_psum, 1)
                pe.wait_ge(x5_ready, count(i, 5, x5_at[3]))
                features_out(ps_j[3], w["l3_Wr"], x5[3]).then_inc(r_in_psum, 1)
                pe.wait_ge(decay_ready, one(i))
                for c in range(DC):
                    last = nc.tensor.matmul(ps_j[1][:, c * ROUND:(c + 1) * ROUND], w["l3_decay_w2"][0:DECAY, 0, c * P:(c + 1) * P],
                                            decayT[:], start=True, stop=True)
                last.then_inc(rate_in_psum, 1)
                pe.wait_ge(x5_ready, count(i, 5, x5_at[4]))
                features_out(ps_j[4], w["l3_Wg"], x5[4]).then_inc(g_in_psum, 1)
                pe.wait_ge(v_ready, one(i))
                for c in range(DC):
                    for q in range(HEAD8 // 2):
                        n = c * (HEAD8 // 2) + q
                        if n >= 3:
                            pe.wait_ge(addend_ready, count(i, 8, n - 3))
                        for d in range(2):
                            last = nc.tensor.matmul(ps_m[n % 3][:, d * ROUND:(d + 1) * ROUND], select[:, 2 * q + d, :],
                                                    vT[:, c, :], start=True, stop=True)
                        last.then_inc(spread_in_psum, 1)
                pe.wait_ge(k_ready, one(i))
                pe.wait_ge(ruk_ready, one(i))
                pe.wait_ge(w_ready, one(i))
                for u in range(2):
                    for c in range(DC):
                        nc.tensor.transpose(ps_j[2][:, u * DIM + c * P:u * DIM + (c + 1) * P], vT[:, c, u * P:(u + 1) * P], ident)
                per_chunk = P // HEAD8
                for u in range(2):
                    for c in range(DC):
                        at = (u * DC + c) * per_chunk
                        nc.tensor.matmul(ps_j[0][:, at:at + per_chunk], rukT[:, c, u * P:(u + 1) * P], head_of, start=True, stop=True)
                for c in range(DC):
                    pe.wait_ge(out_ready, count(i, 2, c))
                    for u in range(2):
                        for d in range(HEAD8):
                            first = u * DIM + c * P + d
                            last = nc.tensor.matmul(ps_j[1][:, first:u * DIM + (c + 1) * P:HEAD8],
                                                    s[c][:, d].rearrange("p b t -> p (b t)")[:, u * P:(u + 1) * P], head_of,
                                                    start=True, stop=True)
                last.then_inc(att_in_psum, 1)
                pe.wait_ge(att_ready, one(i))
                for u in range(2):
                    last = transposed(ps_m[0], att, u)
                last.then_inc(attT_in_psum, 1)
                pe.wait_ge(gated_ready, one(i))
                tokens_out(ps_m[1], w["l3_Wo"], gated).then_inc(y_in_psum, 1)
                for u in range(2):
                    pe.wait_ge(xn_ready, count(i, 4, 2 + u))
                    last = transposed(ps_m[2], xn, u)
                last.then_inc(xT_in_psum, 1)
                pe.wait_ge(channel_ready, count(i, 2, 0))
                features_out(ps_j[0], w["l3_ffn_Wk"], xkT).then_inc(kk_in_psum, 1)
                pe.wait_ge(channel_ready, count(i, 2, 1))
                tokens_out(ps_j[1], w["l3_ffn_Wr"], xrT).then_inc(rr_in_psum, 1)
                pe.wait_ge(kk2_ready, one(i))
                tokens_out(ps_j[2], w["l3_ffn_Wv"], kk2).then_inc(kv_in_psum, 1)

        running.close()
        cleared(nc, semaphores)


LAYER_WEIGHTS = (L0_WEIGHTS, L1_WEIGHTS, L2_WEIGHTS, L3_WEIGHTS)


def program(nc, dram, x_out, layers=(0, 1, 2, 3)):
    with ExitStack() as held:
        def sb(name, shape):
            return held.enter_context(nc.sbuf_tensor(name, shape, F32))

        cols = sb("cols", [P, NCOLS])
        rows = sb("rows", [P, NROWS * DIM])
        ident = sb("ident", [P, P])
        parity = sb("parity", [P, 2])
        select = sb("select", [P, HEAD8, P])
        head_of = sb("head_of", [P, P // HEAD8])
        col = lambda name, c, n=1: cols[:, COL_AT[name] + c:COL_AT[name] + c + n]
        row = {n: rows[:, k * DIM:(k + 1) * DIM] for k, n in enumerate(ROW_NAMES)}
        between = [nc.dram_tensor(f"between{n}", (BATCH * SEQ, DIM), F32).ap() for n in range(3)]
        loaded = held.enter_context(nc.semaphore("loaded"))
        x, expected = dram["x"], 0
        for layer in layers:
            with ExitStack() as layer_held:
                w = {n: layer_held.enter_context(nc.sbuf_tensor(n, [P, k // P, m], F32))
                     for n, (k, m) in LAYER_WEIGHTS[layer].items()}
                constants = ((cols, "cols"), (ident, "ident"), (parity, "parity"), (select, "select"), (head_of, "head_of"))
                expected += len(w) + (len(constants) + 1 if layer == layers[0] else 0)
                with nc.Block() as block:
                    @block.sync
                    def _(sp):
                        if layer == layers[0]:
                            for tile, name in constants:
                                sp.dma_start(tile[:], dram[name]).then_inc(loaded, 16)
                            sp.dma_start(rows[:], dram["rows"].partition_broadcast(P)).then_inc(loaded, 16)
                        for n in w:
                            sp.dma_start(w[n][:], dram[n].rearrange("(k p) m -> p k m", p=P)).then_inc(loaded, 16)
                        sp.wait_ge(loaded, 16 * expected)
                y = x_out if layer == layers[-1] else between[layer]
                if layer == 0:
                    decoder_layer(nc, x, dram["ctx"], dram["self_mask"], dram["cross_mask"], y, w, col, row, ident[:], parity)
                if layer == 1:
                    resampler_layer(nc, x, dram["ctx"], dram["key_mask"], y, w, col, row, ident[:], parity)
                if layer == 2:
                    wide_attention_layer(nc, x, dram["ctx"], y, w, col, row, ident[:])
                if layer == 3:
                    recurrent_layer(nc, x, dram["ctx"], y, w, col, ident[:], select, head_of[:])
                x = y


def laid_out(inputs):
    a = {n: np.asarray(x) for n, x in inputs.items()}
    out = {"x": a["x"].reshape(-1, DIM), "ctx": a["ctx_2048"].reshape(-1, DIM),
           "self_mask": a["mask_1x1xSxS2_fc1"].reshape(SEQ, SEQ),
           "cross_mask": a["mask_Bx1xSxS2_ff1"].reshape(-1, SEQ), "key_mask": a["mask_BxS2_ik0"]}
    a["l1_k_b"], a["l1_v_b"] = a["L1_xattn_kv_b"][0::2], a["L1_xattn_kv_b"][1::2]
    out["l1_k_w"], out["l1_v_w"] = a["L1_xattn_kv_w"][:, 0::2], a["L1_xattn_kv_w"][:, 1::2]
    for name in ("Wk", "Wv", "Wr", "Wg", "Wo", "ffn_Wk", "ffn_Wr", "ffn_Wv"):
        out["l3_" + name] = a["L3_xattn_" + name].T
    out["l3_maa_w2"] = np.zeros((2 * P, DIM), np.float32)
    out["l3_maa_w2"][:5 * LORA] = a["L3_xattn_maa_w2"].reshape(5 * LORA, DIM)
    out["l3_decay_w2"] = np.zeros((P, DIM), np.float32)
    out["l3_decay_w2"][:DECAY] = a["L3_xattn_decay_w2"]
    head, within = np.arange(P) // HEAD8, np.arange(P) % HEAD8
    out["select"] = ((head[:, None, None] == head[None, None, :])
                     & (within[:, None, None] == np.arange(HEAD8)[None, :, None])).astype(np.float32)
    out["head_of"] = (head[:, None] == np.arange(P // HEAD8)[None]).astype(np.float32)
    for weights in LAYER_WEIGHTS:
        for name in weights:
            if name not in out:
                out[name] = a["L" + name[1] + "_xattn_" + name[3:]]
    out["cols"] = np.concatenate([a[name].reshape(-1)[first:first + n].reshape(-1, P).T for name, first, n in COLS.values()], 1)
    out["rows"] = np.concatenate([a[name].reshape(-1) for name in ROWS.values()])[None]
    out["ident"] = np.eye(P, dtype=np.float32)
    out["parity"] = (np.arange(P)[:, None] // HEAD % 2 == np.arange(2)[None]).astype(np.float32)
    return {n: np.ascontiguousarray(x) for n, x in out.items()}


def kernel(**inputs):
    import concourse.bacc as bacc
    from concourse.bass_utils import run_bass_kernel_spmd

    nc = bacc.Bacc("TRN2", target_bir_lowering=False, num_devices=1)
    arrays = {f"in_{n}": a for n, a in laid_out(inputs).items()}
    dram = {n[3:]: nc.dram_tensor(n, a.shape, mybir.dt.from_np(a.dtype), kind="ExternalInput").ap() for n, a in arrays.items()}
    out = nc.dram_tensor("out", (BATCH * SEQ, DIM), F32, kind="ExternalOutput").ap()
    program(nc, dram, out)
    result = run_bass_kernel_spmd(nc, [arrays], core_ids=[0])
    return result.results[0]["out"].reshape(BATCH, SEQ, DIM)
```

```python
import numpy as np
from contextlib import ExitStack

import concourse.bass as bass
from concourse import mybir

F32 = mybir.dt.float32
I32 = mybir.dt.int32
ALU = mybir.AluOpType
ACT = mybir.ActivationFunctionType
AX = mybir.AxisListType

BATCH, SEQ, DIM = 32, 64, 256
P = 128
PER_TILE = P // SEQ
TILES = BATCH // PER_TILE
ROUNDS = TILES // 2
DC = DIM // P
HIDDEN = 4 * DIM
HC = HIDDEN // P
HEADS, HEAD = 16, 16
PAIRS = HEADS // 2
MASKED = 10000.0
MINUS_INF = -1.0e30
BANK = 512


class Links:

    def __init__(self, sem, engine, per_round):
        self.sem, self.engine, self.per_round, self.n = sem, engine, per_round, 0
        self.loop_pass = None

    def begin(self, n=0):
        self.n = n

    def mark(self, instruction):
        self.n += 1
        return instruction.then_inc(self.sem, 1)

    def wait(self, i):
        through = i if self.loop_pass is None else self.loop_pass
        self.engine.wait_ge(self.sem, through * self.per_round + self.n)

    def check(self, ahead=0):
        n = self.n - ahead
        assert n == self.per_round, f"links per round: {n}, stated {self.per_round}"


def count(i, per_round, k):
    return i * per_round + k + 1


def skewed(engine, lag, *stages, links=None):
    n = len(stages)

    def in_pass(i):
        if links:
            links.loop_pass = i

    def run(k, i, s):
        for step in stages[k]:
            step(i, s)

    in_pass(0)
    for k in range(lag):
        run(k, 0, 0)
    ahead = links.n if links else 0
    with engine.Fori(0, ROUNDS - 1) as i:
        in_pass(i)
        for k in range(n):
            if k + lag < n:
                run(k + lag, i, 0)
            else:
                run(k + lag - n, i + 1, 0)
            run(k, i, 1)
    if links:
        links.check(ahead)
        links.begin(ahead)
    in_pass(ROUNDS - 1)
    for k in range(n):
        if k + lag < n:
            run(k + lag, ROUNDS - 1, 0)
        run(k, ROUNDS - 1, 1)


def cleared(nc, semaphores):
    with nc.Block() as block:
        @block.sync
        def _(sp):
            for sem in semaphores:
                sp.sem_clear(sem)

LN_EPS = 1e-5

L0_WEIGHTS = {"l0_w_qkv": (DIM, 3 * DIM), "l0_w_ao": (DIM, DIM), "l0_w_q": (DIM, DIM), "l0_w_kv": (DIM, 2 * DIM),
              "l0_w_co": (DIM, DIM), "l0_w1": (DIM, HIDDEN), "l0_w2": (HIDDEN, DIM)}

COLS = {}
for _n in (1, 2, 3):
    COLS[f"l0_ln{_n}_s"] = (f"L0_xattn_ln{_n}_s", 0, DIM)
    COLS[f"l0_ln{_n}_b"] = (f"L0_xattn_ln{_n}_b", 0, DIM)
COLS["l0_bq0"] = ("L0_xattn_b_qkv", 0, DIM)
COLS["l0_bk0"] = ("L0_xattn_b_qkv", DIM, DIM)
COLS["l0_bv0"] = ("L0_xattn_b_qkv", 2 * DIM, DIM)
COLS["l0_bq1"] = ("L0_xattn_b_q", 0, DIM)
COLS["l0_bk1"] = ("L0_xattn_b_kv", 0, DIM)
COLS["l0_bv1"] = ("L0_xattn_b_kv", DIM, DIM)
COLS["l0_b1"] = ("L0_xattn_b1", 0, HIDDEN)
ROWS = {"l0_b_ao": "L0_xattn_b_ao", "l0_b_co": "L0_xattn_b_co", "l0_b2": "L0_xattn_b2"}
RMS_EPS = 1e-6
L1_WEIGHTS = {"l1_q_w": (DIM, DIM), "l1_k_w": (DIM, DIM), "l1_v_w": (DIM, DIM), "l1_out_w": (DIM, DIM),
              "l1_mlp_w1": (DIM, HIDDEN), "l1_mlp_w2": (HIDDEN, DIM)}
COLS["l1_bq"] = ("L1_xattn_q_b", 0, DIM)
COLS["l1_bk"] = ("l1_k_b", 0, DIM)
COLS["l1_bv"] = ("l1_v_b", 0, DIM)
COLS["l1_postnorm_w"] = ("L1_xattn_postnorm_w", 0, DIM)
COLS["l1_b1"] = ("L1_xattn_mlp_b1", 0, HIDDEN)
ROWS["l1_out_b"] = "L1_xattn_out_b"
ROWS["l1_mlp_b2"] = "L1_xattn_mlp_b2"
WIDE = 128
L2_VECTOR_LINKS = HEADS * 4
L2_WEIGHTS = {}
for _a in (1, 2):
    L2_WEIGHTS |= {f"l2_wo{_a}": (HEADS * WIDE, DIM)}
for _a in (1, 2):
    L2_WEIGHTS |= {f"l2_wv{_a}": (DIM, HEADS * WIDE), f"l2_wq{_a}": (DIM, HEADS * WIDE), f"l2_wk{_a}": (DIM, HEADS * WIDE)}
    COLS[f"l2_bq{_a}"] = (f"L2_xattn_bq{_a}", 0, HEADS * WIDE)
    COLS[f"l2_bk{_a}"] = (f"L2_xattn_bk{_a}", 0, HEADS * WIDE)
    COLS[f"l2_bv{_a}"] = (f"L2_xattn_bv{_a}", 0, HEADS * WIDE)
    COLS[f"l2_bias_k{_a}"] = (f"L2_xattn_bias_k{_a}", 0, HEADS * WIDE)
    COLS[f"l2_bias_v{_a}"] = (f"L2_xattn_bias_v{_a}", 0, HEADS * WIDE)
    ROWS[f"l2_bo{_a}"] = f"L2_xattn_bo{_a}"
L2_WEIGHTS |= {"l2_w_fc1": (DIM, HIDDEN), "l2_w_fc2": (HIDDEN, DIM)}
for _n, _name in enumerate(("ln1", "ln2", "ln_mlp")):
    COLS[f"l2_ln{_n}_s"] = (f"L2_xattn_{_name}_scale", 0, DIM)
    COLS[f"l2_ln{_n}_b"] = (f"L2_xattn_{_name}_offset", 0, DIM)
COLS["l2_b_fc1"] = ("L2_xattn_b_fc1", 0, HIDDEN)
ROWS["l2_b_fc2"] = "L2_xattn_b_fc2"
HEAD8 = 8
LORA, DECAY = 32, 64
L3_VECTOR_LINKS = 23
L3_SCALAR_LINKS = 1
L3_WEIGHTS = {"l3_maa_w1": (DIM, 5 * LORA), "l3_maa_w2": (DIM, DIM), "l3_decay_w1": (DIM, DECAY), "l3_decay_w2": (P, DIM)}
L3_WEIGHTS |= {f"l3_{_n}": (DIM, DIM) for _n in ("Wk", "Wv", "Wr", "Wg", "Wo", "ffn_Wk", "ffn_Wr", "ffn_Wv")}
for _n in (1, 2):
    COLS[f"l3_ln{_n}_w"] = (f"L3_xattn_ln{_n}_w", 0, DIM)
    COLS[f"l3_ln{_n}_b"] = (f"L3_xattn_ln{_n}_b", 0, DIM)
for _n in ("maa_x", "time_decay", "faaaa", "gn_w", "gn_b", "ffn_maa_k", "ffn_maa_r"):
    COLS[f"l3_{_n}"] = (f"L3_xattn_{_n}", 0, DIM)
COLS["l3_maa_stack"] = ("L3_xattn_maa_stack", 0, 5 * DIM)
COL_AT, NCOLS = {}, 0
for _n, (_, _, _length) in COLS.items():
    COL_AT[_n] = NCOLS
    NCOLS += _length // P
ROW_NAMES = list(ROWS)
NROWS = len(ROWS)


def decoder_layer(nc, x_in, ctx, self_mask, cross_mask, x_out, w, weights_in, prefetch, col, row, ident, parity):
    with ExitStack() as held:
        semaphores, running = [], ExitStack()

        def sb(name, shape, dtype=F32):
            return held.enter_context(nc.sbuf_tensor("l0_" + name, shape, dtype))

        def sem(name):
            semaphores.append(held.enter_context(nc.semaphore("l0_" + name)))
            return semaphores[-1]

        x_tile = [sb(f"x_tile{s}", [P, DIM]) for s in range(2)]
        c_tile = [sb(f"c_tile{s}", [P, DIM]) for s in range(2)]
        mask1 = sb("mask1", [P, SEQ])
        mask2 = [sb(f"mask2_{s}", [P, SEQ]) for s in range(2)]
        bias1 = sb("bias1", [P, SEQ])
        bias2 = [sb(f"bias2_{s}", [P, SEQ]) for s in range(2)]
        stats = [sb(f"stats{s}", [P, 6]) for s in range(2)]
        mean_var = [sb(f"mean_var{s}", [P, 2]) for s in range(2)]
        var_eps = [sb(f"var_eps{s}", [P, 1]) for s in range(2)]
        rstd = [sb(f"rstd{s}", [P, 1]) for s in range(2)]
        pad = [sb(f"pad{s}", [P, 1]) for s in range(2)]
        minus_half = sb("minus_half", [P, 1])
        xn = [sb(f"xn{s}", [P, DIM]) for s in range(2)]
        hT = [sb(f"hT{s}", [P, DC, P]) for s in range(2)]
        cT = [sb(f"cT{s}", [P, DC, P]) for s in range(2)]
        qT = [sb(f"qT{s}", [P, DC, P]) for s in range(2)]
        kT = [sb(f"kT{s}", [P, DC, 2, P]) for s in range(2)]
        vp = [sb(f"vp{s}", [P, PER_TILE, PAIRS, 2, HEAD + 1]) for s in range(2)]
        probs = [sb(f"probs{s}", [P, 4, 2 * DC, SEQ]) for s in range(2)]
        row_max = [sb(f"row_max{s}", [P, HEADS]) for s in range(2)]
        pT = [sb(f"pT{s}", [P, PAIRS, P]) for s in range(2)]
        inv_sum = [sb(f"inv_sum{s}", [P, HEADS]) for s in range(2)]
        att = [sb(f"att{s}", [P, DIM]) for s in range(2)]
        aT = [sb(f"aT{s}", [P, DC, P]) for s in range(2)]
        res = [sb(f"res{s}", [P, DIM]) for s in range(2)]
        res_b = [sb(f"res_b{s}", [P, DIM]) for s in range(2)]
        hidT = [sb(f"hidT{s}", [P, HC, P]) for s in range(2)]
        y_out = [sb(f"y_out{s}", [P, DIM]) for s in range(2)]
        ps_s = held.enter_context(nc.psum_tensor("l0_ps_s", [P, 4, BANK], F32))
        ps_a = [held.enter_context(nc.psum_tensor(f"l0_ps_a{s}", [P, BANK], F32)) for s in range(2)]
        ps_b = [held.enter_context(nc.psum_tensor(f"l0_ps_b{s}", [P, BANK], F32)) for s in range(2)]

        x_loaded = [sem(f"x_loaded{s}") for s in range(2)]
        c_loaded = [sem(f"c_loaded{s}") for s in range(2)]
        mask2_loaded = [sem(f"mask2_loaded{s}") for s in range(2)]
        mask1_loaded = sem("mask1_loaded")
        stored = [sem(f"stored{s}") for s in range(2)]
        set_up = sem("set_up")
        scores_read = sem("scores_read")
        vector_set_up = sem("vector_set_up")
        vector_step = sem("vector_step")
        var_ready = [sem(f"var_ready{s}") for s in range(2)]
        rstd_ready = [sem(f"rstd_ready{s}") for s in range(2)]
        xn_ready = [sem(f"xn_ready{s}") for s in range(2)]
        xT_ready = [sem(f"xT_ready{s}") for s in range(2)]
        hT_ready = [sem(f"hT_ready{s}") for s in range(2)]
        cT_in_psum = [sem(f"cT_in_psum{s}") for s in range(2)]
        cT_ready = [sem(f"cT_ready{s}") for s in range(2)]
        k_in_psum = [sem(f"k_in_psum{s}") for s in range(2)]
        v_in_psum = [sem(f"v_in_psum{s}") for s in range(2)]
        q_in_psum = [sem(f"q_in_psum{s}") for s in range(2)]
        q_ready = [sem(f"q_ready{s}") for s in range(2)]
        k_ready = [sem(f"k_ready{s}") for s in range(2)]
        v_ready = [sem(f"v_ready{s}") for s in range(2)]
        s_in_psum = [sem(f"s_in_psum{s}") for s in range(2)]
        s_masked = [sem(f"s_masked{s}") for s in range(2)]
        shifted = [sem(f"shifted{s}") for s in range(2)]
        p_ready = [sem(f"p_ready{s}") for s in range(2)]
        pT_in_psum = [sem(f"pT_in_psum{s}") for s in range(2)]
        pT_lo_ready = [sem(f"pT_lo_ready{s}") for s in range(2)]
        pT_hi_ready = [sem(f"pT_hi_ready{s}") for s in range(2)]
        o_in_psum = [sem(f"o_in_psum{s}") for s in range(2)]
        att_ready = [sem(f"att_ready{s}") for s in range(2)]
        aT_in_psum = [sem(f"aT_in_psum{s}") for s in range(2)]
        aT_ready = [sem(f"aT_ready{s}") for s in range(2)]
        y_in_psum = [sem(f"y_in_psum{s}") for s in range(2)]
        res_ready = [sem(f"res_ready{s}") for s in range(2)]
        res_b_ready = [sem(f"res_b_ready{s}") for s in range(2)]
        y_ready = [sem(f"y_ready{s}") for s in range(2)]
        hid_in_psum = [sem(f"hid_in_psum{s}") for s in range(2)]
        hid_ready = [sem(f"hid_ready{s}") for s in range(2)]

        wq = [w["l0_w_qkv"][:, :, 0:DIM], w["l0_w_q"][:, :, :]]
        wk = [w["l0_w_qkv"][:, :, DIM:2 * DIM], w["l0_w_kv"][:, :, 0:DIM]]
        wv = [w["l0_w_qkv"][:, :, 2 * DIM:3 * DIM], w["l0_w_kv"][:, :, DIM:2 * DIM]]
        wo = [w["l0_w_ao"], w["l0_w_co"]]
        w1, w2 = w["l0_w1"], w["l0_w2"]
        scale = HEAD ** -0.5
        VECTOR_LINKS = 26
        LAG = 6

        block = running.enter_context(nc.Block())

        @block.sync
        def _(sp):
            for b in range(PER_TILE):
                sp.dma_start(mask1[b * SEQ:(b + 1) * SEQ, :], self_mask).then_inc(mask1_loaded, 16)
            for s in range(2):
                sp.dma_start(x_tile[s][:], x_in[bass.ts(s, P), :]).then_inc(x_loaded[s], 16)
                sp.dma_start(c_tile[s][:], ctx[bass.ts(s, P), :]).then_inc(c_loaded[s], 16)
                sp.dma_start(mask2[s][:], cross_mask[bass.ts(s, P), :]).then_inc(mask2_loaded[s], 16)
                sp.sem_inc(stored[s], 16)
            prefetch(sp)

            def store(i, s):
                sp.wait_ge(y_ready[s], count(i, 1, 0))
                sp.nop()
                sp.dma_start(x_out[bass.ds(i * 2 * P + s * P, P), :], y_out[s][:]).then_inc(stored[s], 16)

            with sp.Fori(0, ROUNDS - 1) as i:
                for s in range(2):
                    sp.wait_ge(res_b_ready[s], count(i, 3, 0))
                    sp.wait_ge(xn_ready[s], count(i, 3, 0))
                    sp.nop()
                    sp.dma_start(x_tile[s][:], x_in[bass.ds(i * 2 * P + (s + 2) * P, P), :]).then_inc(x_loaded[s], 16)
                    sp.wait_ge(cT_in_psum[s], count(i, 1, 0))
                    sp.nop()
                    sp.dma_start(c_tile[s][:], ctx[bass.ds(i * 2 * P + (s + 2) * P, P), :]).then_inc(c_loaded[s], 16)
                    sp.wait_ge(s_masked[s], count(i, 2, 1))
                    sp.nop()
                    sp.dma_start(mask2[s][:], cross_mask[bass.ds(i * 2 * P + (s + 2) * P, P), :]).then_inc(mask2_loaded[s], 16)
                    store(i, s)
            for s in range(2):
                store(ROUNDS - 1, s)
            for s in range(2):
                sp.wait_ge(stored[s], 16 * (ROUNDS + 1))

        @block.gpsimd
        def _(pool):
            nc.gpsimd.memset(minus_half[:], -0.5).then_inc(set_up, 1)
            for s in range(2):
                nc.gpsimd.memset(vp[s][:], 0.0).then_inc(set_up, 1)
            pool.wait_ge(set_up, 3)
            for s in range(2):
                for e in range(2):
                    nc.gpsimd.memset(vp[s][e * SEQ:(e + 1) * SEQ, :, :, e, HEAD:HEAD + 1], 1.0).then_inc(set_up, 1)

            def inverse_deviation(i, n, s):
                pool.wait_ge(var_ready[s], count(i, 3, n))
                nc.gpsimd.tensor_tensor(rstd[s][:], var_eps[s][:], minus_half[:], ALU.pow).then_inc(rstd_ready[s], 1)

            def residual_with_bias(n, s, source, bias):
                nc.gpsimd.tensor_tensor(res_b[s][:], source[:], row[bias], ALU.add).then_inc(res_b_ready[s], 1)

            pool.wait_ge(set_up, 7)

            def norm_step(n):
                return lambda i, s: inverse_deviation(i, n, s)

            def residual(n):
                return lambda i, s: residual_with_bias(n, s, x_tile[s] if n == 0 else res[s], ("l0_b_ao", "l0_b_co", "l0_b2")[n])

            skewed(pool, LAG,
                   (norm_step(0),), (residual(0),), (), (), (), (), (), (norm_step(1), residual(1)),
                   (), (), (), (), (), (), (norm_step(2), residual(2)), (), (), ())

        @block.scalar
        def _(act):
            def normed_transposed(i, n, s):
                act.wait_ge(xT_ready[s], count(i, 3, n))
                for c in range(DC):
                    last = nc.scalar.activation(hT[s][:, c, :], ps_a[s][:, c * P:(c + 1) * P], ACT.Identity,
                                                bias=col(f"l0_ln{n + 1}_b", c), scale=col(f"l0_ln{n + 1}_s", c))
                last.then_inc(hT_ready[s], 1)

            def queries(i, a, s):
                act.wait_ge(q_in_psum[s], count(i, 2, a))
                for c in range(DC):
                    last = nc.scalar.activation(qT[s][:, c, :], ps_b[s][:, c * P:(c + 1) * P], ACT.Identity,
                                                bias=col(f"l0_bq{a}", c), scale=1.0)
                last.then_inc(q_ready[s], 1)

            def values(i, a, s):
                act.wait_ge(v_in_psum[s], count(i, 2, a))
                for e in range(2):
                    half = slice(e * SEQ, (e + 1) * SEQ)
                    last = nc.scalar.activation(
                        vp[s][half, :, :, e, 0:HEAD],
                        ps_b[s][half, DIM:2 * DIM].rearrange("k (b h d) -> k b h d", b=PER_TILE, h=PAIRS), ACT.Copy)
                last.then_inc(v_ready[s], 1)

            def exponentials(i, a, s):
                act.wait_ge(shifted[s], count(i, 2, a))
                nc.scalar.activation(probs[s][:], probs[s][:], ACT.Exp).then_inc(p_ready[s], 1)

            def probs_transposed(i, a, s):
                act.wait_ge(pT_in_psum[s], count(i, 4, 2 * a))
                nc.scalar.activation(pT[s][:, 0:PAIRS // 2, :], ps_a[s][:].rearrange("k (h q) -> k h q", q=P),
                                     ACT.Copy).then_inc(pT_lo_ready[s], 1)

            def attended_transposed(i, a, s):
                act.wait_ge(aT_in_psum[s], count(i, 2, a))
                for c in range(DC):
                    last = nc.scalar.activation(aT[s][:, c, :], ps_b[s][:, c * P:(c + 1) * P], ACT.Identity,
                                                bias=col(f"l0_bv{a}", c), scale=1.0)
                last.then_inc(aT_ready[s], 1)

            def hidden(i, s):
                for half, bank in enumerate((ps_a[s], ps_b[s])):
                    act.wait_ge(hid_in_psum[s], count(i, 2, half))
                    for c in range(HC // 2):
                        h = half * (HC // 2) + c
                        last = nc.scalar.activation(hidT[s][:, h, :], bank[:, c * P:(c + 1) * P], ACT.Gelu_apprx_tanh,
                                                    bias=col("l0_b1", h), scale=1.0)
                    last.then_inc(hid_ready[s], 1)

            act.wait_ge(set_up, 7)

            def attention(a):
                of = lambda step: lambda i, s: step(i, a, s)
                return (tuple(map(of, steps)) for steps in (
                    (normed_transposed,), (queries,), (values, exponentials), (probs_transposed,), (), (attended_transposed,), ()))

            skewed(act, LAG,
                   (), *attention(0), *attention(1), (lambda i, s: normed_transposed(i, 2, s),), (hidden,), ())

        @block.vector
        def _(dve):
            links = Links(vector_step, dve, VECTOR_LINKS)

            def layer_norm(i, n, s, source):
                links.mark(nc.vector.bn_stats(stats[s][:], source[:]))
                links.wait(i)
                nc.vector.memset(pad[s][:], 0.0)
                links.mark(nc.vector.bn_aggr(mean_var[s][:], stats[s][:]))
                links.wait(i)
                nc.vector.tensor_scalar(var_eps[s][:], mean_var[s][:, 1:2], LN_EPS, None, ALU.add).then_inc(var_ready[s], 1)
                dve.wait_ge(rstd_ready[s], count(i, 3, n))
                nc.vector.tensor_scalar(xn[s][:], source[:], mean_var[s][:, 0:1], rstd[s][:], ALU.subtract, ALU.mult
                                        ).then_inc(xn_ready[s], 1)

            def context_transposed(i, s):
                dve.wait_ge(cT_in_psum[s], count(i, 1, 0))
                nc.vector.tensor_copy(cT[s][:], ps_b[s][:, 0:DIM].rearrange("f (c t) -> f c t", c=DC)
                                      ).then_inc(cT_ready[s], 1)

            def keys(i, a, s):
                dve.wait_ge(k_in_psum[s], count(i, 2, a))
                for c in range(DC):
                    for e in range(2):
                        last = nc.vector.tensor_scalar(kT[s][:, c, e, :], ps_a[s][:, c * P:(c + 1) * P],
                                                       col(f"l0_bk{a}", c), parity[:, e:e + 1], ALU.add, ALU.mult)
                last.then_inc(k_ready[s], 1)

            def mask_scores(i, a, s):
                mask, bias = (mask1, bias1) if a == 0 else (mask2[s], bias2[s])
                if a == 1:
                    dve.wait_ge(mask2_loaded[s], count(i, 1, 0) * 16)
                    links.mark(nc.vector.tensor_scalar(bias[:], mask[:], 1.0, MASKED, ALU.subtract, ALU.mult))
                dve.wait_ge(s_in_psum[s], count(i, 2, a))
                for g in range(4):
                    last = nc.vector.scalar_tensor_tensor(
                        out=probs[s][:, g, :, :], in0=ps_s[:, g, 0:2 * DC * SEQ].rearrange("q (h k) -> q h k", k=SEQ),
                        scalar=scale, in1=mask[:].unsqueeze(1).to_broadcast([P, 2 * DC, SEQ]),
                        op0=ALU.mult, op1=ALU.mult)
                last.then_inc(s_masked[s], 1)
                dve.wait_ge(s_masked[s], count(i, 2, a))
                dve.sem_inc(scores_read, 1)

            def shift_scores(i, a, s):
                bias = bias1 if a == 0 else bias2[s]
                dve.wait_ge(s_masked[s], count(i, 2, a))
                flat = probs[s][:].rearrange("q g h k -> q (g h) k")
                links.wait(i)
                links.mark(nc.vector.tensor_tensor(flat, flat, bias[:].unsqueeze(1).to_broadcast([P, HEADS, SEQ]), ALU.add))
                links.wait(i)
                links.mark(nc.vector.tensor_reduce(row_max[s][:], flat, AX.X, ALU.max))
                links.wait(i)
                nc.vector.tensor_tensor(flat, flat, row_max[s][:].unsqueeze(2).to_broadcast([P, HEADS, SEQ]),
                                        ALU.subtract).then_inc(shifted[s], 1)

            def probs_transposed(i, a, s):
                dve.wait_ge(pT_in_psum[s], count(i, 4, 2 * a + 1))
                nc.vector.tensor_copy(pT[s][:, PAIRS // 2:, :], ps_b[s][:].rearrange("k (h q) -> k h q", q=P)
                                      ).then_inc(pT_hi_ready[s], 1)

            def normalise(i, a, s):
                dve.wait_ge(o_in_psum[s], count(i, 2, a))
                o = ps_a[s][:, 0:HEADS * (HEAD + 1)].rearrange("q (h d) -> q h d", d=HEAD + 1)
                links.mark(nc.vector.reciprocal(inv_sum[s][:].unsqueeze(2), o[:, :, HEAD:HEAD + 1]))
                links.wait(i)
                nc.vector.tensor_tensor(att[s][:].rearrange("q (h d) -> q h d", d=HEAD), o[:, :, 0:HEAD],
                                        inv_sum[s][:].unsqueeze(2).to_broadcast([P, HEADS, HEAD]), ALU.mult
                                        ).then_inc(att_ready[s], 1)

            def add_residual(i, n, s):
                dve.wait_ge(y_in_psum[s], count(i, 3, n))
                dve.wait_ge(res_b_ready[s], count(i, 3, n))
                y = ps_a[s][:, 0:DIM]
                if n < 2:
                    nc.vector.tensor_tensor(res[s][:], y, res_b[s][:], ALU.add).then_inc(res_ready[s], 1)
                    dve.wait_ge(res_ready[s], count(i, 2, n))
                else:
                    dve.wait_ge(stored[s], (i + 1) * 16)
                    nc.vector.tensor_tensor(y_out[s][:], y, res_b[s][:], ALU.add).then_inc(y_ready[s], 1)

            for b in range(1):
                dve.wait_ge(mask1_loaded, 16 * PER_TILE)
                nc.vector.tensor_scalar(bias1[:], mask1[:], 1.0, MASKED, ALU.subtract, ALU.mult).then_inc(vector_set_up, 1)
                dve.wait_ge(vector_set_up, 1)

            def first_norm(i, s):
                dve.wait_ge(x_loaded[s], count(i, 1, 0) * 16)
                layer_norm(i, 0, s, x_tile[s])

            def attention(a):
                def residual_and_norm(i, a, s):
                    add_residual(i, a, s)
                    layer_norm(i, a + 1, s, res[s])

                of = lambda step: lambda i, s: step(i, a, s)
                return (tuple(map(of, steps)) for steps in (
                    (keys,), (mask_scores, shift_scores), (probs_transposed,), (normalise,), (), (residual_and_norm,)))

            skewed(dve, LAG,
                   (first_norm,), (context_transposed,), *attention(0), (), *attention(1),
                   (), (), (lambda i, s: add_residual(i, 2, s),), links=links)

        @block.tensor
        def _(pe):
            def normed(i, n, s):
                pe.wait_ge(xn_ready[s], count(i, 3, n))
                for c in range(DC):
                    last = nc.tensor.transpose(ps_a[s][:, c * P:(c + 1) * P], xn[s][:, c * P:(c + 1) * P], ident)
                last.then_inc(xT_ready[s], 1)

            def context(i, s):
                pe.wait_ge(c_loaded[s], count(i, 1, 0) * 16)
                for c in range(DC):
                    last = nc.tensor.transpose(ps_b[s][:, c * P:(c + 1) * P], c_tile[s][:, c * P:(c + 1) * P], ident)
                last.then_inc(cT_in_psum[s], 1)

            def project(i, a, s):
                def transposed(bank, weights, moving):
                    for c in range(DC):
                        for k in range(DC):
                            last = nc.tensor.matmul(bank[:, c * P:(c + 1) * P], weights[:, k, c * P:(c + 1) * P],
                                                    moving[:, k, :], start=(k == 0), stop=(k == DC - 1))
                    return last

                source = hT[s] if a == 0 else cT[s]
                pe.wait_ge(hT_ready[s], count(i, 3, a))
                transposed(ps_a[s], wk[a], source).then_inc(k_in_psum[s], 1)
                if a == 0:
                    pe.wait_ge(cT_ready[s], count(i, 1, 0))
                transposed(ps_b[s], wq[a], hT[s]).then_inc(q_in_psum[s], 1)

            def values(i, a, s):
                source = hT[s] if a == 0 else cT[s]
                for b in range(PER_TILE):
                    for e in range(2):
                        for k in range(DC):
                            last = nc.tensor.matmul(
                                ps_b[s][e * SEQ:(e + 1) * SEQ, DIM + b * P:DIM + (b + 1) * P],
                                source[:, k, b * SEQ:(b + 1) * SEQ],
                                wv[a][:, k, :].rearrange("f (h e d) -> f h e d", e=2, d=HEAD)[:, :, e, :],
                                start=(k == 0), stop=(k == DC - 1))
                last.then_inc(v_in_psum[s], 1)

            def scores(i, a, s):
                pe.wait_ge(q_ready[s], count(i, 2, a))
                pe.wait_ge(k_ready[s], count(i, 2, a))
                if scores_done.n:
                    scores_done.wait(i)
                scores_done.n += 1
                for g in range(4):
                    rows = slice(32 * g, 32 * g + 32)
                    for c in range(DC):
                        for b in range(PER_TILE):
                            last = nc.tensor.matmul(ps_s[b * SEQ:(b + 1) * SEQ, g, c * P:(c + 1) * P],
                                                    qT[s][rows, c, b * SEQ:(b + 1) * SEQ],
                                                    kT[s][rows, c, :, b * SEQ:(b + 1) * SEQ], start=True, stop=True)
                last.then_inc(s_in_psum[s], 1)

            def transpose_probs(i, a, s):
                pe.wait_ge(p_ready[s], count(i, 2, a))
                pe.wait_ge(v_ready[s], count(i, 2, a))
                for half, bank in enumerate((ps_a[s], ps_b[s])):
                    for j in range(PAIRS // 2):
                        g, c = divmod(half * (PAIRS // 2) + j, DC)
                        last = nc.tensor.transpose(bank[:, j * P:(j + 1) * P],
                                                   probs[s][:, g, 2 * c:2 * c + 2, :], ident)
                    last.then_inc(pT_in_psum[s], 1)

            def attend(i, a, s):
                pe.wait_ge(pT_lo_ready[s], count(i, 2, a))
                pe.wait_ge(pT_hi_ready[s], count(i, 2, a))
                wide = 2 * (HEAD + 1)
                for j in range(PAIRS):
                    g, c = divmod(j, DC)
                    pair = 4 * c + g
                    for b in range(PER_TILE):
                        last = nc.tensor.matmul(ps_a[s][b * SEQ:(b + 1) * SEQ, pair * wide:(pair + 1) * wide],
                                                pT[s][:, j, b * SEQ:(b + 1) * SEQ], vp[s][:, b, pair, :, :],
                                                start=True, stop=True)
                last.then_inc(o_in_psum[s], 1)

            def transpose_attended(i, a, s):
                pe.wait_ge(att_ready[s], count(i, 2, a))
                for c in range(DC):
                    last = nc.tensor.transpose(ps_b[s][:, c * P:(c + 1) * P], att[s][:, c * P:(c + 1) * P], ident)
                last.then_inc(aT_in_psum[s], 1)

            def project_out(i, a, s):
                pe.wait_ge(*weights_in)
                pe.wait_ge(aT_ready[s], count(i, 2, a))
                for k in range(DC):
                    last = nc.tensor.matmul(ps_a[s][:, 0:DIM], aT[s][:, k, :], wo[a][:, k, :],
                                            start=(k == 0), stop=(k == DC - 1))
                last.then_inc(y_in_psum[s], 1)

            def mlp_up(i, s):
                pe.wait_ge(hT_ready[s], count(i, 3, 2))
                for half, bank in enumerate((ps_a[s], ps_b[s])):
                    for c in range(HC // 2):
                        h = half * (HC // 2) + c
                        for k in range(DC):
                            last = nc.tensor.matmul(bank[:, c * P:(c + 1) * P], w1[:, k, h * P:(h + 1) * P], hT[s][:, k, :],
                                                    start=(k == 0), stop=(k == DC - 1))
                    last.then_inc(hid_in_psum[s], 1)

            def mlp_down(i, s):
                for half in range(2):
                    pe.wait_ge(hid_ready[s], count(i, 2, half))
                    for c in range(HC // 2):
                        h = half * (HC // 2) + c
                        last = nc.tensor.matmul(ps_a[s][:, 0:DIM], hidT[s][:, h, :], w2[:, h, :],
                                                start=(h == 0), stop=(h == HC - 1))
                last.then_inc(y_in_psum[s], 1)

            scores_done = Links(scores_read, pe, 4)
            pe.wait_ge(set_up, 7)

            def attention(a):
                of = lambda step: lambda i, s: step(i, a, s)
                return (tuple(map(of, steps)) for steps in (
                    (project,), (scores, values), (transpose_probs,), (attend,), (transpose_attended,), (project_out,)))

            skewed(pe, LAG,
                   (), (lambda i, s: normed(i, 0, s), context), *attention(0), (lambda i, s: normed(i, 1, s),), *attention(1),
                   (lambda i, s: normed(i, 2, s),), (mlp_up,), (mlp_down,), links=scores_done)

        running.close()
        cleared(nc, semaphores)


def resampler_layer(nc, x_in, ctx, key_mask, x_out, w, col, row, ident, parity):
    with ExitStack() as held:
        semaphores, running = [], ExitStack()

        def sb(name, shape, dtype=F32):
            return held.enter_context(nc.sbuf_tensor("l1_" + name, shape, dtype))

        def sem(name):
            semaphores.append(held.enter_context(nc.semaphore("l1_" + name)))
            return semaphores[-1]

        x_tile = [sb(f"x_tile{s}", [P, DIM]) for s in range(2)]
        c_tile = [sb(f"c_tile{s}", [P, DIM]) for s in range(2)]
        mask = [sb(f"mask{s}", [P, SEQ], I32) for s in range(2)]
        bias = [sb(f"bias{s}", [P, 2 * SEQ]) for s in range(2)]
        stats = [sb(f"stats{s}", [P, 6]) for s in range(2)]
        mean_var = [sb(f"mean_var{s}", [P, 2]) for s in range(2)]
        var_eps = [sb(f"var_eps{s}", [P, 1]) for s in range(2)]
        rstd = [sb(f"rstd{s}", [P, 1]) for s in range(2)]
        pad = [sb(f"pad{s}", [P, 1]) for s in range(2)]
        minus_half = sb("minus_half", [P, 1])
        xn = [sb(f"xn{s}", [P, DIM]) for s in range(2)]
        mean_square = [sb(f"mean_square{s}", [P, 1]) for s in range(2)]
        hT = [sb(f"hT{s}", [P, DC, P]) for s in range(2)]
        srcT = [sb(f"srcT{s}", [P, DC, PER_TILE, 2, SEQ]) for s in range(2)]
        qT = [sb(f"qT{s}", [P, DC, P]) for s in range(2)]
        kT = [sb(f"kT{s}", [P, DC, 2, 2 * P]) for s in range(2)]
        v = [sb(f"v{s}", [P, PER_TILE, HEADS, HEAD + 1]) for s in range(2)]
        probs = [sb(f"probs{s}", [P, 4, 2 * DC, 2 * SEQ]) for s in range(2)]
        row_max = [sb(f"row_max{s}", [P, HEADS]) for s in range(2)]
        pT = [sb(f"pT{s}", [P, HEADS, P]) for s in range(2)]
        inv_sum = [sb(f"inv_sum{s}", [P, HEADS]) for s in range(2)]
        att = [sb(f"att{s}", [P, DIM]) for s in range(2)]
        aT = [sb(f"aT{s}", [P, DC, P]) for s in range(2)]
        res = [sb(f"res{s}", [P, DIM]) for s in range(2)]
        res_b = [sb(f"res_b{s}", [P, DIM]) for s in range(2)]
        final_b = [sb(f"final_b{s}", [P, DIM]) for s in range(2)]
        hidT = [sb(f"hidT{s}", [P, HC, P]) for s in range(2)]
        y_out = [sb(f"y_out{s}", [P, DIM]) for s in range(2)]
        ps_s = held.enter_context(nc.psum_tensor("l1_ps_s", [P, 4, BANK], F32))
        ps_a = [held.enter_context(nc.psum_tensor(f"l1_ps_a{s}", [P, BANK], F32)) for s in range(2)]
        ps_b = [held.enter_context(nc.psum_tensor(f"l1_ps_b{s}", [P, BANK], F32)) for s in range(2)]

        x_loaded = [sem(f"x_loaded{s}") for s in range(2)]
        c_loaded = [sem(f"c_loaded{s}") for s in range(2)]
        mask_loaded = [sem(f"mask_loaded{s}") for s in range(2)]
        stored = [sem(f"stored{s}") for s in range(2)]
        set_up = sem("set_up")
        scores_read = sem("scores_read")
        vector_step = sem("vector_step")
        var_ready = [sem(f"var_ready{s}") for s in range(2)]
        rstd_ready = [sem(f"rstd_ready{s}") for s in range(2)]
        xn_ready = [sem(f"xn_ready{s}") for s in range(2)]
        xT_ready = [sem(f"xT_ready{s}") for s in range(2)]
        hT_ready = [sem(f"hT_ready{s}") for s in range(2)]
        lT_in_psum = [sem(f"lT_in_psum{s}") for s in range(2)]
        lT_ready = [sem(f"lT_ready{s}") for s in range(2)]
        cT_in_psum = [sem(f"cT_in_psum{s}") for s in range(2)]
        cT_ready = [sem(f"cT_ready{s}") for s in range(2)]
        k_in_psum = [sem(f"k_in_psum{s}") for s in range(2)]
        q_in_psum = [sem(f"q_in_psum{s}") for s in range(2)]
        v_in_psum = [sem(f"v_in_psum{s}") for s in range(2)]
        q_ready = [sem(f"q_ready{s}") for s in range(2)]
        k_ready = [sem(f"k_ready{s}") for s in range(2)]
        v_ready = [sem(f"v_ready{s}") for s in range(2)]
        s_in_psum = [sem(f"s_in_psum{s}") for s in range(2)]
        bias_ready = [sem(f"bias_ready{s}") for s in range(2)]
        s_masked = [sem(f"s_masked{s}") for s in range(2)]
        shifted = [sem(f"shifted{s}") for s in range(2)]
        p_ready = [sem(f"p_ready{s}") for s in range(2)]
        pT_in_psum = [sem(f"pT_in_psum{s}") for s in range(2)]
        pT_lo_ready = [sem(f"pT_lo_ready{s}") for s in range(2)]
        pT_hi_ready = [sem(f"pT_hi_ready{s}") for s in range(2)]
        o_in_psum = [sem(f"o_in_psum{s}") for s in range(2)]
        att_ready = [sem(f"att_ready{s}") for s in range(2)]
        aT_in_psum = [sem(f"aT_in_psum{s}") for s in range(2)]
        aT_ready = [sem(f"aT_ready{s}") for s in range(2)]
        y_in_psum = [sem(f"y_in_psum{s}") for s in range(2)]
        res_ready = [sem(f"res_ready{s}") for s in range(2)]
        res_b_ready = [sem(f"res_b_ready{s}") for s in range(2)]
        final_b_ready = [sem(f"final_b_ready{s}") for s in range(2)]
        y_ready = [sem(f"y_ready{s}") for s in range(2)]
        hid_in_psum = [sem(f"hid_in_psum{s}") for s in range(2)]
        hid_ready = [sem(f"hid_ready{s}") for s in range(2)]

        wq, wk, wv, wo = w["l1_q_w"], w["l1_k_w"], w["l1_v_w"], w["l1_out_w"]
        w1, w2 = w["l1_mlp_w1"], w["l1_mlp_w2"]
        scale = 1.0 / HEAD
        VECTOR_LINKS = 10
        LAG = 2

        block = running.enter_context(nc.Block())

        @block.sync
        def _(sp):
            def load_mask(i, t, s):
                for b in range(PER_TILE):
                    sp.dma_start(mask[s][b * SEQ:(b + 1) * SEQ, :],
                                 key_mask[bass.ds(i * 2 * PER_TILE + t * PER_TILE + b, 1), :].partition_broadcast(SEQ)
                                 ).then_inc(mask_loaded[s], 16)

            for s in range(2):
                sp.dma_start(x_tile[s][:], x_in[bass.ts(s, P), :]).then_inc(x_loaded[s], 16)
                sp.dma_start(c_tile[s][:], ctx[bass.ts(s, P), :]).then_inc(c_loaded[s], 16)
                load_mask(0, s, s)
                sp.sem_inc(stored[s], 16)

            def store(i, s):
                sp.wait_ge(y_ready[s], count(i, 1, 0))
                sp.nop()
                sp.dma_start(x_out[bass.ds(i * 2 * P + s * P, P), :], y_out[s][:]).then_inc(stored[s], 16)

            with sp.Fori(0, ROUNDS - 1) as i:
                for s in range(2):
                    sp.wait_ge(final_b_ready[s], count(i, 1, 0))
                    sp.wait_ge(lT_in_psum[s], count(i, 1, 0))
                    sp.nop()
                    sp.dma_start(x_tile[s][:], x_in[bass.ds(i * 2 * P + (s + 2) * P, P), :]).then_inc(x_loaded[s], 16)
                    sp.wait_ge(cT_in_psum[s], count(i, 1, 0))
                    sp.nop()
                    sp.dma_start(c_tile[s][:], ctx[bass.ds(i * 2 * P + (s + 2) * P, P), :]).then_inc(c_loaded[s], 16)
                    sp.wait_ge(s_masked[s], count(i, 1, 0))
                    sp.nop()
                    load_mask(i, s + 2, s)
                    store(i, s)
            for s in range(2):
                store(ROUNDS - 1, s)
            for s in range(2):
                sp.wait_ge(stored[s], 16 * (ROUNDS + 1))

        @block.gpsimd
        def _(pool):
            nc.gpsimd.memset(minus_half[:], -0.5).then_inc(set_up, 1)
            for s in range(2):
                nc.gpsimd.memset(v[s][:, :, :, HEAD:HEAD + 1], 1.0).then_inc(set_up, 1)
                nc.gpsimd.memset(bias[s][:, SEQ:], 0.0).then_inc(set_up, 1)

            pool.wait_ge(set_up, 5)

            def residuals(i, s):
                pool.wait_ge(bias_ready[s], count(i, 1, 0))
                pool.wait_ge(x_loaded[s], count(i, 1, 0) * 16)
                nc.gpsimd.tensor_tensor(res_b[s][:], x_tile[s][:], row["l1_out_b"], ALU.add).then_inc(res_b_ready[s], 1)
                nc.gpsimd.tensor_tensor(final_b[s][:], x_tile[s][:], row["l1_mlp_b2"], ALU.add).then_inc(final_b_ready[s], 1)

            def inverse_root(i, s):
                pool.wait_ge(var_ready[s], count(i, 1, 0))
                nc.gpsimd.tensor_tensor(rstd[s][:], var_eps[s][:], minus_half[:], ALU.pow).then_inc(rstd_ready[s], 1)

            skewed(pool, LAG, (residuals,), (), (), (), (), (), (inverse_root,), (), (), ())

        @block.scalar
        def _(act):
            def latents_transposed(i, s):
                act.wait_ge(lT_in_psum[s], count(i, 1, 0))
                nc.scalar.activation(srcT[s][:, :, :, 1, :].rearrange("f c b t -> f (c b) t"),
                                     ps_a[s][:, 0:DIM].rearrange("f (m t) -> f m t", t=SEQ), ACT.Copy).then_inc(lT_ready[s], 1)

            def normed_transposed(i, s):
                act.wait_ge(xT_ready[s], count(i, 1, 0))
                for c in range(DC):
                    last = nc.scalar.activation(hT[s][:, c, :], ps_a[s][:, c * P:(c + 1) * P], ACT.Identity,
                                                bias=0.0, scale=col("l1_postnorm_w", c))
                last.then_inc(hT_ready[s], 1)

            def queries(i, s):
                act.wait_ge(q_in_psum[s], count(i, 1, 0))
                for c in range(DC):
                    last = nc.scalar.activation(qT[s][:, c, :], ps_b[s][:, c * P:(c + 1) * P], ACT.Identity,
                                                bias=col("l1_bq", c), scale=1.0)
                last.then_inc(q_ready[s], 1)

            def values(i, s):
                act.wait_ge(v_in_psum[s], count(i, 1, 0))
                nc.scalar.activation(v[s][:, :, :, 0:HEAD].rearrange("k b h d -> k (b h) d"),
                                     ps_b[s][:].rearrange("k (m d) -> k m d", d=HEAD), ACT.Copy).then_inc(v_ready[s], 1)

            def exponentials(i, s):
                act.wait_ge(shifted[s], count(i, 1, 0))
                nc.scalar.activation(probs[s][:], probs[s][:], ACT.Exp).then_inc(p_ready[s], 1)

            def probs_transposed(i, s):
                for half in range(2):
                    act.wait_ge(pT_in_psum[s], count(i, 4, 2 * half))
                    nc.scalar.activation(pT[s][:, 8 * half:8 * half + 4, :], ps_a[s][:].rearrange("k (h q) -> k h q", q=P),
                                         ACT.Copy).then_inc(pT_lo_ready[s], 1)

            def attended_transposed(i, s):
                act.wait_ge(aT_in_psum[s], count(i, 1, 0))
                for c in range(DC):
                    last = nc.scalar.activation(aT[s][:, c, :], ps_b[s][:, c * P:(c + 1) * P], ACT.Identity,
                                                bias=col("l1_bv", c), scale=1.0)
                last.then_inc(aT_ready[s], 1)

            def hidden(i, s):
                for half, bank in enumerate((ps_a[s], ps_b[s])):
                    act.wait_ge(hid_in_psum[s], count(i, 2, half))
                    for c in range(HC // 2):
                        h = half * (HC // 2) + c
                        last = nc.scalar.activation(hidT[s][:, h, :], bank[:, c * P:(c + 1) * P], ACT.Gelu_apprx_tanh,
                                                    bias=col("l1_b1", h), scale=1.0)
                    last.then_inc(hid_ready[s], 1)

            act.wait_ge(set_up, 5)
            skewed(act, LAG, (latents_transposed,), (queries,), (values, exponentials), (probs_transposed,), (),
                   (attended_transposed,), (), (normed_transposed,), (hidden,), ())

        @block.vector
        def _(dve):
            links = Links(vector_step, dve, VECTOR_LINKS)

            def rms_norm(i, s):
                links.mark(nc.vector.bn_stats(stats[s][:], res[s][:]))
                links.wait(i)
                nc.vector.memset(pad[s][:], 0.0)
                links.mark(nc.vector.bn_aggr(mean_var[s][:], stats[s][:]))
                links.wait(i)
                links.mark(nc.vector.scalar_tensor_tensor(out=mean_square[s][:], in0=mean_var[s][:, 0:1],
                                                          scalar=mean_var[s][:, 0:1], in1=mean_var[s][:, 1:2],
                                                          op0=ALU.mult, op1=ALU.add))
                links.wait(i)
                nc.vector.tensor_scalar(var_eps[s][:], mean_square[s][:], RMS_EPS, None, ALU.add).then_inc(var_ready[s], 1)
                dve.wait_ge(rstd_ready[s], count(i, 1, 0))
                nc.vector.tensor_scalar(xn[s][:], res[s][:], rstd[s][:], None, ALU.mult).then_inc(xn_ready[s], 1)

            def context_transposed(i, s):
                dve.wait_ge(cT_in_psum[s], count(i, 1, 0))
                nc.vector.tensor_copy(srcT[s][:, :, :, 0, :].rearrange("f c b t -> f (c b) t"),
                                      ps_b[s][:, 0:DIM].rearrange("f (m t) -> f m t", t=SEQ)).then_inc(cT_ready[s], 1)

            def keys(i, s):
                dve.wait_ge(k_in_psum[s], count(i, 1, 0))
                for c in range(DC):
                    for e in range(2):
                        last = nc.vector.tensor_scalar(kT[s][:, c, e, :], ps_a[s][:, c * 2 * P:(c + 1) * 2 * P],
                                                       col("l1_bk", c), parity[:, e:e + 1], ALU.add, ALU.mult)
                last.then_inc(k_ready[s], 1)

            def mask_bias(i, s):
                dve.wait_ge(mask_loaded[s], count(i, 1, 0) * 16 * PER_TILE)
                nc.vector.tensor_scalar(bias[s][:, 0:SEQ], mask[s][:], 0.0, MINUS_INF, ALU.is_equal, ALU.mult).then_inc(bias_ready[s], 1)

            def mask_scores(i, s):
                dve.wait_ge(bias_ready[s], count(i, 1, 0))
                dve.wait_ge(s_in_psum[s], count(i, 1, 0))
                for g in range(4):
                    last = nc.vector.scalar_tensor_tensor(
                        out=probs[s][:, g, :, :], in0=ps_s[:, g, :].rearrange("q (h k) -> q h k", k=2 * SEQ),
                        scalar=scale, in1=bias[s][:].unsqueeze(1).to_broadcast([P, 2 * DC, 2 * SEQ]),
                        op0=ALU.mult, op1=ALU.add)
                last.then_inc(s_masked[s], 1)
                dve.wait_ge(s_masked[s], count(i, 1, 0))
                dve.sem_inc(scores_read, 1)

            def shift_scores(i, s):
                dve.wait_ge(s_masked[s], count(i, 1, 0))
                flat = probs[s][:].rearrange("q g h k -> q (g h) k")
                links.mark(nc.vector.tensor_reduce(row_max[s][:], flat, AX.X, ALU.max))
                links.wait(i)
                nc.vector.tensor_tensor(flat, flat, row_max[s][:].unsqueeze(2).to_broadcast([P, HEADS, 2 * SEQ]),
                                        ALU.subtract).then_inc(shifted[s], 1)

            def probs_transposed(i, s):
                for half in range(2):
                    dve.wait_ge(pT_in_psum[s], count(i, 4, 2 * half + 1))
                    nc.vector.tensor_copy(pT[s][:, 8 * half + 4:8 * half + 8, :], ps_b[s][:].rearrange("k (h q) -> k h q", q=P)
                                          ).then_inc(pT_hi_ready[s], 1)

            def normalise(i, s):
                dve.wait_ge(o_in_psum[s], count(i, 1, 0))
                o = ps_a[s][:, 0:HEADS * (HEAD + 1)].rearrange("q (h d) -> q h d", d=HEAD + 1)
                links.mark(nc.vector.reciprocal(inv_sum[s][:].unsqueeze(2), o[:, :, HEAD:HEAD + 1]))
                links.wait(i)
                nc.vector.tensor_tensor(att[s][:].rearrange("q (h d) -> q h d", d=HEAD), o[:, :, 0:HEAD],
                                        inv_sum[s][:].unsqueeze(2).to_broadcast([P, HEADS, HEAD]), ALU.mult
                                        ).then_inc(att_ready[s], 1)

            def add_residual(i, n, s):
                dve.wait_ge(y_in_psum[s], count(i, 2, n))
                y = ps_a[s][:, 0:DIM]
                if n == 0:
                    dve.wait_ge(res_b_ready[s], count(i, 1, 0))
                    nc.vector.tensor_tensor(res[s][:], y, res_b[s][:], ALU.add).then_inc(res_ready[s], 1)
                    dve.wait_ge(res_ready[s], count(i, 1, 0))
                else:
                    dve.wait_ge(final_b_ready[s], count(i, 1, 0))
                    dve.wait_ge(stored[s], (i + 1) * 16)
                    nc.vector.tensor_tensor(y_out[s][:], y, final_b[s][:], ALU.add).then_inc(y_ready[s], 1)

            dve.wait_ge(set_up, 5)
            skewed(dve, LAG, (mask_bias, context_transposed), (keys,), (mask_scores, shift_scores), (probs_transposed,),
                   (normalise,), (), (lambda i, s: add_residual(i, 0, s), rms_norm), (), (),
                   (lambda i, s: add_residual(i, 1, s),), links=links)

        @block.tensor
        def _(pe):
            def latents(i, s):
                pe.wait_ge(bias_ready[s], count(i, 1, 0))
                pe.wait_ge(x_loaded[s], count(i, 1, 0) * 16)
                for c in range(DC):
                    last = nc.tensor.transpose(ps_a[s][:, c * P:(c + 1) * P], x_tile[s][:, c * P:(c + 1) * P], ident)
                last.then_inc(lT_in_psum[s], 1)

            def normed(i, s):
                pe.wait_ge(xn_ready[s], count(i, 1, 0))
                for c in range(DC):
                    last = nc.tensor.transpose(ps_a[s][:, c * P:(c + 1) * P], xn[s][:, c * P:(c + 1) * P], ident)
                last.then_inc(xT_ready[s], 1)

            def context(i, s):
                pe.wait_ge(c_loaded[s], count(i, 1, 0) * 16)
                for c in range(DC):
                    last = nc.tensor.transpose(ps_b[s][:, c * P:(c + 1) * P], c_tile[s][:, c * P:(c + 1) * P], ident)
                last.then_inc(cT_in_psum[s], 1)

            def project(i, s):
                pe.wait_ge(cT_ready[s], count(i, 1, 0))
                pe.wait_ge(lT_ready[s], count(i, 1, 0))
                for c in range(DC):
                    for k in range(DC):
                        last = nc.tensor.matmul(ps_a[s][:, c * 2 * P:(c + 1) * 2 * P], wk[:, k, c * P:(c + 1) * P],
                                                srcT[s][:, k].rearrange("f b m t -> f (b m t)"),
                                                start=(k == 0), stop=(k == DC - 1))
                last.then_inc(k_in_psum[s], 1)
                for c in range(DC):
                    for k in range(DC):
                        last = nc.tensor.matmul(ps_b[s][:, c * P:(c + 1) * P], wq[:, k, c * P:(c + 1) * P],
                                                srcT[s][:, k, :, 1, :], start=(k == 0), stop=(k == DC - 1))
                last.then_inc(q_in_psum[s], 1)

            def values(i, s):
                for b in range(PER_TILE):
                    for k in range(DC):
                        last = nc.tensor.matmul(ps_b[s][:, b * DIM:(b + 1) * DIM],
                                                srcT[s][:, k, b].rearrange("f m t -> f (m t)"), wv[:, k, :],
                                                start=(k == 0), stop=(k == DC - 1))
                last.then_inc(v_in_psum[s], 1)

            def scores(i, s):
                pe.wait_ge(q_ready[s], count(i, 1, 0))
                pe.wait_ge(k_ready[s], count(i, 1, 0))
                if scores_done.n:
                    scores_done.wait(i)
                scores_done.n += 1
                for g in range(4):
                    rows = slice(32 * g, 32 * g + 32)
                    for c in range(DC):
                        for b in range(PER_TILE):
                            last = nc.tensor.matmul(ps_s[b * SEQ:(b + 1) * SEQ, g, c * 2 * P:(c + 1) * 2 * P],
                                                    qT[s][rows, c, b * SEQ:(b + 1) * SEQ],
                                                    kT[s][rows, c, :, b * 2 * SEQ:(b + 1) * 2 * SEQ], start=True, stop=True)
                last.then_inc(s_in_psum[s], 1)

            def transpose_probs(i, s):
                pe.wait_ge(p_ready[s], count(i, 1, 0))
                pe.wait_ge(v_ready[s], count(i, 1, 0))
                for quarter in range(4):
                    bank = (ps_a, ps_b)[quarter % 2][s]
                    if quarter >= 2:
                        pe.wait_ge((pT_lo_ready, pT_hi_ready)[quarter % 2][s], count(i, 2, 0))
                    for j in range(4):
                        last = nc.tensor.transpose(bank[:, j * P:(j + 1) * P], probs[s][:, quarter, j, :], ident)
                    last.then_inc(pT_in_psum[s], 1)

            def attend(i, s):
                pe.wait_ge(pT_lo_ready[s], count(i, 2, 1))
                pe.wait_ge(pT_hi_ready[s], count(i, 2, 1))
                wide = HEAD + 1
                for g in range(4):
                    for j in range(2 * DC):
                        head = (j // 2) * PAIRS + 2 * g + j % 2
                        for b in range(PER_TILE):
                            last = nc.tensor.matmul(ps_a[s][b * SEQ:(b + 1) * SEQ, head * wide:(head + 1) * wide],
                                                    pT[s][:, 4 * g + j, b * SEQ:(b + 1) * SEQ], v[s][:, b, head, :],
                                                    start=True, stop=True)
                last.then_inc(o_in_psum[s], 1)

            def transpose_attended(i, s):
                pe.wait_ge(att_ready[s], count(i, 1, 0))
                for c in range(DC):
                    last = nc.tensor.transpose(ps_b[s][:, c * P:(c + 1) * P], att[s][:, c * P:(c + 1) * P], ident)
                last.then_inc(aT_in_psum[s], 1)

            def project_out(i, s):
                pe.wait_ge(aT_ready[s], count(i, 1, 0))
                for k in range(DC):
                    last = nc.tensor.matmul(ps_a[s][:, 0:DIM], aT[s][:, k, :], wo[:, k, :],
                                            start=(k == 0), stop=(k == DC - 1))
                last.then_inc(y_in_psum[s], 1)

            def mlp_up(i, s):
                pe.wait_ge(hT_ready[s], count(i, 1, 0))
                for half, bank in enumerate((ps_a[s], ps_b[s])):
                    for c in range(HC // 2):
                        h = half * (HC // 2) + c
                        for k in range(DC):
                            last = nc.tensor.matmul(bank[:, c * P:(c + 1) * P], w1[:, k, h * P:(h + 1) * P], hT[s][:, k, :],
                                                    start=(k == 0), stop=(k == DC - 1))
                    last.then_inc(hid_in_psum[s], 1)

            def mlp_down(i, s):
                for half in range(2):
                    pe.wait_ge(hid_ready[s], count(i, 2, half))
                    for c in range(HC // 2):
                        h = half * (HC // 2) + c
                        last = nc.tensor.matmul(ps_a[s][:, 0:DIM], hidT[s][:, h, :], w2[:, h, :],
                                                start=(h == 0), stop=(h == HC - 1))
                last.then_inc(y_in_psum[s], 1)

            pe.wait_ge(set_up, 5)
            scores_done = Links(scores_read, pe, 2)
            skewed(pe, LAG, (latents, context), (project,), (scores, values), (transpose_probs,), (attend,),
                   (transpose_attended,), (project_out,), (normed,), (mlp_up,), (mlp_down,), links=scores_done)

        running.close()
        cleared(nc, semaphores)


class Normed:

    def __init__(self, nc, sb, sem, x_tile, ps_x, scale_of, bias_of, ident):
        self.nc, self.x_tile, self.ps_x, self.scale_of, self.bias_of, self.ident = nc, x_tile, ps_x, scale_of, bias_of, ident
        self.stats = [sb(f"stats{u}", [P, 6]) for u in range(2)]
        self.pad = [sb(f"pad{u}", [P, 1]) for u in range(2)]
        self.mean_var = [sb(f"mean_var{u}", [P, 2]) for u in range(2)]
        self.var_eps = [sb(f"var_eps{u}", [P, 1]) for u in range(2)]
        self.rstd = [sb(f"rstd{u}", [P, 1]) for u in range(2)]
        self.minus_half = sb("minus_half", [P, 1])
        self.xn = sb("xn", [P, 2, DIM])
        self.hT = sb("hT", [P, DC, 2 * P])
        self.x_loaded = sem("x_loaded")
        self.norm_step = sem("norm_step")
        self.var_ready = sem("var_ready")
        self.rstd_ready = sem("rstd_ready")
        self.xn_ready = sem("xn_ready")
        self.xT_in_psum = sem("xT_in_psum")
        self.hT_ready = sem("hT_ready")

    def variances(self, dve, r):
        nc = self.nc
        dve.wait_ge(self.x_loaded, count(r, 1, 0) * 16)
        for u in range(2):
            nc.vector.bn_stats(self.stats[u][:], self.x_tile[:, u, :]).then_inc(self.norm_step, 1)
        for u in range(2):
            dve.wait_ge(self.norm_step, count(r, 4, u))
            nc.vector.memset(self.pad[u][:], 0.0)
            nc.vector.bn_aggr(self.mean_var[u][:], self.stats[u][:]).then_inc(self.norm_step, 1)
        for u in range(2):
            dve.wait_ge(self.norm_step, count(r, 4, 2 + u))
            nc.vector.tensor_scalar(self.var_eps[u][:], self.mean_var[u][:, 1:2], LN_EPS, None, ALU.add
                                    ).then_inc(self.var_ready, 1)

    def inverse_deviations(self, pool, r):
        for u in range(2):
            pool.wait_ge(self.var_ready, count(r, 2, u))
            self.nc.gpsimd.tensor_tensor(self.rstd[u][:], self.var_eps[u][:], self.minus_half[:], ALU.pow
                                         ).then_inc(self.rstd_ready, 1)

    def normalised(self, dve, r):
        for u in range(2):
            dve.wait_ge(self.rstd_ready, count(r, 2, u))
            self.nc.vector.tensor_scalar(self.xn[:, u, :], self.x_tile[:, u, :], self.mean_var[u][:, 0:1], self.rstd[u][:],
                                         ALU.subtract, ALU.mult).then_inc(self.xn_ready, 1)

    def transposed(self, pe, r):
        for u in range(2):
            pe.wait_ge(self.xn_ready, count(r, 2, u))
            for c in range(DC):
                last = self.nc.tensor.transpose(self.ps_x[:, (c * 2 + u) * P:(c * 2 + u + 1) * P],
                                                self.xn[:, u, c * P:(c + 1) * P], self.ident)
        last.then_inc(self.xT_in_psum, 1)

    def scaled(self, act, r):
        act.wait_ge(self.xT_in_psum, count(r, 1, 0))
        for c in range(DC):
            last = self.nc.scalar.activation(self.hT[:, c, :], self.ps_x[:, c * 2 * P:(c + 1) * 2 * P], ACT.Identity,
                                             bias=self.bias_of(c), scale=self.scale_of(c))
        last.then_inc(self.hT_ready, 1)


def wide_attention(nc, a, x_in, ctx, x_out, w, col, row, ident, prefetch=None):
    with ExitStack() as held:
        semaphores, running = [], ExitStack()

        def sb(name, shape, dtype=F32):
            return held.enter_context(nc.sbuf_tensor(f"l2a{a}_" + name, shape, dtype))

        def sem(name):
            semaphores.append(held.enter_context(nc.semaphore(f"l2a{a}_" + name)))
            return semaphores[-1]

        def bank(name):
            return held.enter_context(nc.psum_tensor(f"l2a{a}_ps_" + name, [P, BANK], F32))

        ROUND = 2 * P
        KEYS = P + 1
        ONES = 2 * HEADS
        scale = WIDE ** -0.5
        wq, wk, wv, wo = (w[f"l2_{n}{a + 1}"] for n in ("wq", "wk", "wv", "wo"))

        x_tile = sb("x_tile", [P, 2, DIM])
        c_tile = sb("c_tile", [P, 2, DIM])
        one = sb("one", [P, 1])
        cT = sb("cT", [P, DC, ROUND])
        qT = sb("qT", [P, ROUND])
        kT = sb("kT", [P, 2, KEYS])
        v = [[sb(f"v{g}{u}", [P, 4 * WIDE]) for u in range(2)] for g in range(2)]
        other_sequence = sb("other_sequence", [P, KEYS])
        probs = [sb(f"probs{u}", [P, KEYS]) for u in range(2)]
        pad = [sb(f"carrier{u}", [P, 1]) for u in range(2)]
        row_max = [sb(f"row_max{u}", [P, 1]) for u in range(2)]
        shift = [sb(f"shift{u}", [P, 1]) for u in range(2)]
        row_sum = [sb(f"row_sum{u}", [P, 1]) for u in range(2)]
        inv_sum = [sb(f"inv_sum{u}", [P, 1]) for u in range(2)]
        learned = [sb(f"learned{u}", [P, P]) for u in range(2)]
        learnedT = sb("learnedT", [P, 2, P])
        pT = sb("pT", [P, 2, P])
        oT = sb("oT", [P, 2, P])
        res_b = sb("res_b", [P, 2, DIM])
        y_out = sb("y_out", [P, 2, DIM])
        value_gap = sb("value_gap", [P, HEADS, ONES + 1])
        gap_out = sb("gap_out", [ONES + 1, DIM])
        ps_q, ps_k, ps_v, ps_s, ps_p, ps_o, ps_y, ps_x = (bank(n) for n in "qkvspoyx")
        norm = Normed(nc, sb, sem, x_tile, ps_x, lambda c: col(f"l2_ln{a}_s", c), lambda c: col(f"l2_ln{a}_b", c), ident)
        hT = norm.hT

        x_loaded, c_loaded, stored = norm.x_loaded, sem("c_loaded"), sem("stored")
        set_up = sem("set_up")
        gap_ready = sem("gap_ready")
        folded_in_psum = sem("folded_in_psum")
        folded_ready = sem("folded_ready")
        vector_step = sem("vector_step")
        cT_in_psum = sem("cT_in_psum")
        cT_ready = sem("cT_ready")
        q_in_psum, q_ready = sem("q_in_psum"), sem("q_ready")
        k_in_psum, k_ready = sem("k_in_psum"), sem("k_ready")
        learned_key_ready = sem("learned_key_ready")
        v_in_psum, v_ready = sem("v_in_psum"), sem("v_ready")
        s_in_psum = sem("s_in_psum")
        shift_ready = sem("shift_ready")
        exp_ready = sem("exp_ready")
        p_ready = sem("p_ready")
        learned_ready = sem("learned_ready")
        pT_in_psum, pT_ready = sem("pT_in_psum"), sem("pT_ready")
        o_in_psum, o_ready = sem("o_in_psum"), sem("o_ready")
        learnedT_in_psum, learnedT_ready = sem("learnedT_in_psum"), sem("learnedT_ready")
        y_in_psum = sem("y_in_psum")
        y_ready = sem("y_ready")
        sums_read = sem("sums_read")
        res_b_ready = sem("res_b_ready")

        def rows_of(dram, first):
            return dram[bass.ds(first, ROUND), :].rearrange("(u p) d -> p u d", p=P)

        def per_head(i, h):
            return count(i, HEADS, h)

        def per_head_tile(i, h, u):
            return count(i, 2 * HEADS, h * 2 + u)

        def value_event(i, g, u):
            return count(i, 8, g * 2 + u)

        def rounds(engine, body):
            with engine.Fori(0, ROUNDS - 1) as i:
                body(i, True)
            body(ROUNDS - 1, False)

        block = running.enter_context(nc.Block())

        @block.sync
        def _(sp):
            sp.dma_start(c_tile[:], rows_of(ctx, 0)).then_inc(c_loaded, 16)
            sp.dma_start(x_tile[:], rows_of(x_in, 0)).then_inc(x_loaded, 16)
            sp.sem_inc(stored, 16)
            if prefetch:
                prefetch(sp)
            with sp.Fori(0, ROUNDS - 1) as i:
                sp.wait_ge(cT_in_psum, count(i, 1, 0))
                sp.nop()
                sp.dma_start(c_tile[:], rows_of(ctx, i * ROUND + ROUND)).then_inc(c_loaded, 16)
                sp.wait_ge(res_b_ready, count(i, 2, 1))
                sp.wait_ge(norm.xn_ready, count(i, 2, 1))
                sp.nop()
                sp.dma_start(x_tile[:], rows_of(x_in, i * ROUND + ROUND)).then_inc(x_loaded, 16)
                sp.wait_ge(y_ready, count(i, 2, 1))
                sp.nop()
                sp.dma_start(rows_of(x_out, i * ROUND), y_out[:]).then_inc(stored, 16)
            sp.wait_ge(y_ready, 2 * ROUNDS)
            sp.dma_start(rows_of(x_out, (ROUNDS - 1) * ROUND), y_out[:]).then_inc(stored, 16)
            sp.wait_ge(stored, 16 * (ROUNDS + 1))

        @block.gpsimd
        def _(pool):
            nc.gpsimd.memset(norm.minus_half[:], -0.5).then_inc(set_up, 1)
            nc.gpsimd.memset(one[:], 1.0).then_inc(set_up, 1)
            nc.gpsimd.memset(value_gap[:], 0.0).then_inc(set_up, 1)
            nc.gpsimd.memset(other_sequence[:], 0.0).then_inc(set_up, 1)
            for u in range(2):
                nc.gpsimd.memset(learned[u][:], 0.0).then_inc(set_up, 1)
            pool.wait_ge(set_up, 6)
            for b in range(2):
                nc.gpsimd.memset(other_sequence[b * SEQ:(b + 1) * SEQ, (1 - b) * SEQ:(2 - b) * SEQ], MINUS_INF).then_inc(set_up, 1)
            pool.wait_ge(set_up, 8)
            for u in range(2):
                nc.gpsimd.memset(learned[u][:, ONES:ONES + 1], 1.0).then_inc(set_up, 1)
            pool.wait_ge(set_up, 10)
            norm.inverse_deviations(pool, 0)

            def learned_key(i, h):
                pool.wait_ge(k_in_psum, per_head(i, h))
                nc.gpsimd.tensor_tensor(kT[:, :, P:KEYS], col(f"l2_bias_k{a + 1}", h).unsqueeze(1).to_broadcast([P, 2, 1]),
                                        one[:].unsqueeze(1).to_broadcast([P, 2, 1]), ALU.mult).then_inc(learned_key_ready, 1)

            def learned_probability(i, h):
                for u in range(2):
                    pool.wait_ge(p_ready, per_head_tile(i, h, u))
                    if h == 0:
                        pool.wait_ge(sums_read, count(i, 1, 0))
                    nc.gpsimd.tensor_tensor(learned[u][:, h:h + 1], probs[u][:, P:KEYS], one[:], ALU.mult).then_inc(learned_ready, 1)

            def body(i, more):
                pool.wait_ge(sums_read, count(i, 1, 0))
                for u in range(2):
                    nc.gpsimd.tensor_tensor(res_b[:, u, :], x_tile[:, u, :], row[f"l2_bo{a + 1}"], ALU.add).then_inc(res_b_ready, 1)
                for h in range(HEADS + 1):
                    if h < HEADS:
                        learned_key(i, h)
                    if h > 0:
                        learned_probability(i, h - 1)
                    if h == HEADS // 2 and more:
                        norm.inverse_deviations(pool, i + 1)

            rounds(pool, body)

        @block.scalar
        def _(act):
            def queries(i, h):
                act.wait_ge(q_in_psum, per_head(i, h))
                nc.scalar.activation(qT[:], ps_q[:, 0:ROUND], ACT.Identity, bias=col(f"l2_bq{a + 1}", h), scale=1.0
                                     ).then_inc(q_ready, 1)

            def values(i, g, u):
                act.wait_ge(v_in_psum, value_event(i, g, u))
                nc.scalar.activation(v[g % 2][u][:], ps_v[:], ACT.Copy).then_inc(v_ready, 1)

            def exponentials(i, h):
                for u in range(2):
                    act.wait_ge(shift_ready, per_head_tile(i, h, u))
                    nc.scalar.activation(probs[u][:], probs[u][:], ACT.Exp, bias=shift[u][:], scale=scale,
                                         accum_out=row_sum[u][:]).then_inc(exp_ready, 1)

            def attended(i, h):
                act.wait_ge(o_in_psum, per_head(i, h))
                nc.scalar.activation(oT[:].rearrange("d u q -> d (u q)"), ps_o[:, 0:ROUND], ACT.Copy).then_inc(o_ready, 1)

            def learned_transposed(i):
                act.wait_ge(learnedT_in_psum, count(i, 1, 0))
                nc.scalar.activation(learnedT[:].rearrange("h u q -> h (u q)"), ps_k[:, 0:ROUND], ACT.Copy
                                     ).then_inc(learnedT_ready, 1)

            def body(i, more):
                for h in range(HEADS + 1):
                    if h > 0:
                        exponentials(i, h - 1)
                    if h < HEADS:
                        queries(i, h)
                        g, r = divmod(h, 4)
                        if r % 2 and g < 3:
                            values(i, g + 1, r // 2)
                    elif more:
                        norm.scaled(act, i + 1)
                    if h > 0:
                        attended(i, h - 1)
                learned_transposed(i)
                if more:
                    for u in range(2):
                        values(i + 1, 0, u)

            norm.scaled(act, 0)
            for u in range(2):
                values(0, 0, u)
            rounds(act, body)

        @block.vector
        def _(dve):
            links = Links(vector_step, dve, L2_VECTOR_LINKS)

            def context(r):
                dve.wait_ge(cT_in_psum, count(r, 1, 0))
                nc.vector.tensor_copy(cT[:].rearrange("f c t -> f (c t)"), ps_v[:]).then_inc(cT_ready, 1)

            def keys(i, h):
                dve.wait_ge(k_in_psum, per_head(i, h))
                nc.vector.tensor_scalar(kT[:, :, 0:P], ps_k[:, 0:ROUND].rearrange("d (u k) -> d u k", u=2),
                                        col(f"l2_bk{a + 1}", h), None, ALU.add).then_inc(k_ready, 1)

            def maxima(i, h):
                dve.wait_ge(s_in_psum, per_head(i, h))
                if h > 0:
                    dve.wait_ge(learned_ready, per_head_tile(i, h - 1, 1))
                for u in range(2):
                    nc.vector.memset(pad[u][:], 0.0)
                    links.mark(nc.vector.tensor_tensor_reduce(
                        out=probs[u][:], in0=ps_s[:, u * KEYS:(u + 1) * KEYS], in1=other_sequence[:], scale=1.0,
                        scalar=MINUS_INF, op0=ALU.add, op1=ALU.max, accum_out=row_max[u][:]))
                for u in range(2):
                    if u == 0:
                        links.wait(i)
                    nc.vector.tensor_scalar(shift[u][:], row_max[u][:], -scale, None, ALU.mult).then_inc(shift_ready, 1)

            def normalise(i, h):
                for u in range(2):
                    dve.wait_ge(exp_ready, per_head_tile(i, h, u))
                    links.mark(nc.vector.reciprocal(inv_sum[u][:], row_sum[u][:]))
                    links.wait(i)
                    nc.vector.tensor_scalar(probs[u][:], probs[u][:], inv_sum[u][:], None, ALU.mult).then_inc(p_ready, 1)

            def probs_transposed(i, h):
                dve.wait_ge(pT_in_psum, per_head(i, h))
                nc.vector.tensor_copy(pT[:].rearrange("k u q -> k (u q)"), ps_p[:, 0:ROUND]).then_inc(pT_ready, 1)

            def add_residual(i):
                dve.wait_ge(y_in_psum, count(i, 1, 0))
                dve.wait_ge(res_b_ready, count(i, 2, 1))
                dve.wait_ge(stored, (i + 1) * 16)
                for u in range(2):
                    last = nc.vector.tensor_tensor(y_out[:, u, :], ps_y[:, u * DIM:(u + 1) * DIM], res_b[:, u, :], ALU.add)
                    last.then_inc(y_ready, 1)
                dve.wait_ge(y_ready, count(i, 2, 1))
                dve.sem_inc(sums_read, 1)

            def body(i, more):
                links.begin()
                for h in range(HEADS + 1):
                    if h > 0:
                        maxima(i, h - 1)
                    if h == HEADS and more:
                        context(i + 1)
                    if h > 0:
                        normalise(i, h - 1)
                    if h < HEADS:
                        keys(i, h)
                    if h > 0:
                        probs_transposed(i, h - 1)
                    if h == HEADS // 2 - 1 and more:
                        dve.wait_ge(norm.xT_in_psum, count(i, 1, 0))
                        norm.variances(dve, i + 1)
                    if h == HEADS // 2 + 1 and more:
                        norm.normalised(dve, i + 1)
                add_residual(i)

            norm.variances(dve, 0)
            norm.normalised(dve, 0)
            context(0)
            dve.wait_ge(set_up, 10)
            gap_columns = value_gap[:].rearrange("p h m -> p (h m)")
            bias_v, bv = (col(f"l2_bias_v{a + 1}", 0, HEADS), col(f"l2_bv{a + 1}", 0, HEADS))
            nc.vector.tensor_tensor(gap_columns[:, 0:(HEADS - 1) * (ONES + 2) + 1:ONES + 2], bias_v, bv, ALU.subtract
                                    ).then_inc(gap_ready, 1)
            nc.vector.tensor_copy(gap_columns[:, ONES:HEADS * (ONES + 1):ONES + 1], bv).then_inc(gap_ready, 1)
            dve.wait_ge(folded_in_psum, 1)
            nc.vector.tensor_copy(gap_out[:], ps_y[0:ONES + 1, 0:DIM]).then_inc(folded_ready, 1)
            dve.sem_inc(sums_read, 1)
            rounds(dve, body)
            links.check()

        @block.tensor
        def _(pe):
            def context(r):
                pe.wait_ge(c_loaded, count(r, 1, 0) * 16)
                for c in range(DC):
                    for u in range(2):
                        last = nc.tensor.transpose(ps_v[:, c * ROUND + u * P:c * ROUND + (u + 1) * P],
                                                   c_tile[:, u, c * P:(c + 1) * P], ident)
                last.then_inc(cT_in_psum, 1)

            def project(ps, weights, h, moving, ready):
                for k in range(DC):
                    last = nc.tensor.matmul(ps[:, 0:ROUND], weights[:, k, h * WIDE:(h + 1) * WIDE], moving[:, k, :],
                                            start=(k == 0), stop=(k == DC - 1))
                last.then_inc(ready, 1)

            def values(i, g, u):
                if g == 0 and u == 0:
                    pe.wait_ge(cT_ready, count(i, 1, 0))
                else:
                    pe.wait_ge(v_ready, value_event(i, g, u) - 1)
                for k in range(DC):
                    last = nc.tensor.matmul(ps_v[:], cT[:, k, u * P:(u + 1) * P],
                                            wv[:, k, g * 4 * WIDE:(g + 1) * 4 * WIDE],
                                            start=(k == 0), stop=(k == DC - 1))
                last.then_inc(v_in_psum, 1)

            def scores(i, h):
                pe.wait_ge(q_ready, per_head(i, h))
                pe.wait_ge(k_ready, per_head(i, h))
                pe.wait_ge(learned_key_ready, per_head(i, h))
                for u in range(2):
                    last = nc.tensor.matmul(ps_s[:, u * KEYS:(u + 1) * KEYS], qT[:, u * P:(u + 1) * P], kT[:, u, :],
                                            start=True, stop=True)
                last.then_inc(s_in_psum, 1)

            def transpose_probs(i, h):
                for u in range(2):
                    pe.wait_ge(p_ready, per_head_tile(i, h, u))
                    last = nc.tensor.transpose(ps_p[:, u * P:(u + 1) * P], probs[u][:, 0:P], ident)
                last.then_inc(pT_in_psum, 1)

            def attend(i, h):
                g, r = divmod(h, 4)
                pe.wait_ge(pT_ready, per_head(i, h))
                if r == 0:
                    pe.wait_ge(v_ready, value_event(i, g, 1))
                for u in range(2):
                    last = nc.tensor.matmul(ps_o[:, u * P:(u + 1) * P], v[g % 2][u][:, r * WIDE:(r + 1) * WIDE],
                                            pT[:, u, :], start=True, stop=True)
                last.then_inc(o_in_psum, 1)

            def project_out(i, h):
                if h == 0:
                    pe.wait_ge(sums_read, count(i, 1, 0))
                pe.wait_ge(o_ready, per_head(i, h))
                for u in range(2):
                    nc.tensor.matmul(ps_y[:, u * DIM:(u + 1) * DIM], oT[:, u, :], wo[:, h, :],
                                     start=(h == 0 and u == 0), stop=False, skip_group_check=True)

            def learned_value(i):
                pe.wait_ge(learned_ready, per_head_tile(i, HEADS - 1, 1))
                for u in range(2):
                    last = nc.tensor.transpose(ps_k[:, u * P:(u + 1) * P], learned[u][:], ident)
                last.then_inc(learnedT_in_psum, 1)

            def add_learned_value(i):
                pe.wait_ge(learnedT_ready, count(i, 1, 0))
                for u in range(2):
                    last = nc.tensor.matmul(ps_y[:, u * DIM:(u + 1) * DIM], learnedT[0:ONES + 1, u, :], gap_out[:],
                                            start=False, stop=True, skip_group_check=True)
                last.then_inc(y_in_psum, 1)

            def body(i, more):
                pe.wait_ge(norm.hT_ready, count(i, 1, 0))
                for h in range(HEADS):
                    project(ps_q, wq, h, hT, q_in_psum)
                    project(ps_k, wk, h, cT, k_in_psum)
                    if h >= 2:
                        project_out(i, h - 2)
                    if h >= 1:
                        transpose_probs(i, h - 1)
                    g, r = divmod(h, 4)
                    if r % 2 and g < 3:
                        values(i, g + 1, r // 2)
                    scores(i, h)
                    if h >= 1:
                        attend(i, h - 1)
                if more:
                    context(i + 1)
                    norm.transposed(pe, i + 1)
                project_out(i, HEADS - 2)
                transpose_probs(i, HEADS - 1)
                if more:
                    values(i + 1, 0, 0)
                attend(i, HEADS - 1)
                learned_value(i)
                if more:
                    values(i + 1, 0, 1)
                project_out(i, HEADS - 1)
                add_learned_value(i)

            context(0)
            norm.transposed(pe, 0)
            for u in range(2):
                values(0, 0, u)
            pe.wait_ge(gap_ready, 2)
            for h in range(HEADS):
                last = nc.tensor.matmul(ps_y[0:ONES + 1, 0:DIM], value_gap[:, h, :], wo[:, h, :], start=(h == 0), stop=(h == HEADS - 1))
            last.then_inc(folded_in_psum, 1)
            pe.wait_ge(folded_ready, 1)
            rounds(pe, body)

        running.close()
        cleared(nc, semaphores)


def wide_mlp(nc, x_in, x_out, w, col, row, ident, prefetch=None):
    with ExitStack() as held:
        semaphores, running = [], ExitStack()

        def sb(name, shape, dtype=F32):
            return held.enter_context(nc.sbuf_tensor("l2m_" + name, shape, dtype))

        def sem(name):
            semaphores.append(held.enter_context(nc.semaphore("l2m_" + name)))
            return semaphores[-1]

        ROUND = 2 * P
        x_tile = sb("x_tile", [P, 2, DIM])
        res_b = sb("res_b", [P, 2, DIM])
        hidT = sb("hidT", [P, HC, ROUND])
        y_out = sb("y_out", [P, 2, DIM])
        ps_hid = [held.enter_context(nc.psum_tensor(f"l2m_ps_hid{j}", [P, BANK], F32)) for j in range(4)]
        ps_y, ps_x = (held.enter_context(nc.psum_tensor("l2m_ps_" + n, [P, BANK], F32)) for n in "yx")
        norm = Normed(nc, sb, sem, x_tile, ps_x, lambda c: col("l2_ln2_s", c), lambda c: col("l2_ln2_b", c), ident)

        x_loaded, stored = norm.x_loaded, sem("stored")
        set_up = sem("set_up")
        hid_in_psum, hid_ready = sem("hid_in_psum"), sem("hid_ready")
        y_in_psum = sem("y_in_psum")
        res_b_ready = sem("res_b_ready")
        y_ready = sem("y_ready")
        sums_read = sem("sums_read")

        def rows_of(dram, first):
            return dram[bass.ds(first, ROUND), :].rearrange("(u p) d -> p u d", p=P)

        def rounds(engine, body):
            with engine.Fori(0, ROUNDS - 1) as i:
                body(i, True)
            body(ROUNDS - 1, False)

        block = running.enter_context(nc.Block())

        @block.sync
        def _(sp):
            sp.dma_start(x_tile[:], rows_of(x_in, 0)).then_inc(x_loaded, 16)
            sp.sem_inc(stored, 16)
            if prefetch:
                prefetch(sp)
            with sp.Fori(0, ROUNDS - 1) as i:
                sp.wait_ge(res_b_ready, count(i, 2, 1))
                sp.wait_ge(norm.xn_ready, count(i, 2, 1))
                sp.nop()
                sp.dma_start(x_tile[:], rows_of(x_in, i * ROUND + ROUND)).then_inc(x_loaded, 16)
                sp.wait_ge(y_ready, count(i, 2, 1))
                sp.nop()
                sp.dma_start(rows_of(x_out, i * ROUND), y_out[:]).then_inc(stored, 16)
            sp.wait_ge(y_ready, 2 * ROUNDS)
            sp.dma_start(rows_of(x_out, (ROUNDS - 1) * ROUND), y_out[:]).then_inc(stored, 16)
            sp.wait_ge(stored, 16 * (ROUNDS + 1))

        @block.gpsimd
        def _(pool):
            nc.gpsimd.memset(norm.minus_half[:], -0.5).then_inc(set_up, 1)
            pool.wait_ge(set_up, 1)
            norm.inverse_deviations(pool, 0)

            def body(i, more):
                pool.wait_ge(sums_read, count(i, 1, 0))
                for u in range(2):
                    nc.gpsimd.tensor_tensor(res_b[:, u, :], x_tile[:, u, :], row["l2_b_fc2"], ALU.add).then_inc(res_b_ready, 1)
                if more:
                    norm.inverse_deviations(pool, i + 1)

            rounds(pool, body)

        @block.scalar
        def _(act):
            def body(i, more):
                for j in range(4):
                    act.wait_ge(hid_in_psum, count(i, 4, j))
                    for c in range(2):
                        last = nc.scalar.activation(hidT[:, 2 * j + c, :], ps_hid[j][:, c * ROUND:(c + 1) * ROUND], ACT.Gelu,
                                                    bias=col("l2_b_fc1", 2 * j + c), scale=1.0)
                    last.then_inc(hid_ready, 1)
                if more:
                    norm.scaled(act, i + 1)

            norm.scaled(act, 0)
            rounds(act, body)

        @block.vector
        def _(dve):
            def add_residual(i):
                dve.wait_ge(y_in_psum, count(i, 1, 0))
                dve.wait_ge(res_b_ready, count(i, 2, 1))
                dve.wait_ge(stored, (i + 1) * 16)
                for u in range(2):
                    nc.vector.tensor_tensor(y_out[:, u, :], ps_y[:, u * DIM:(u + 1) * DIM], res_b[:, u, :], ALU.add
                                            ).then_inc(y_ready, 1)
                dve.wait_ge(y_ready, count(i, 2, 1))
                dve.sem_inc(sums_read, 1)

            def body(i, more):
                if more:
                    dve.wait_ge(norm.xT_in_psum, count(i, 1, 0))
                    norm.variances(dve, i + 1)
                    norm.normalised(dve, i + 1)
                add_residual(i)

            dve.sem_inc(sums_read, 1)
            norm.variances(dve, 0)
            norm.normalised(dve, 0)
            rounds(dve, body)

        @block.tensor
        def _(pe):
            def body(i, more):
                pe.wait_ge(norm.hT_ready, count(i, 1, 0))
                for h in range(HC):
                    for k in range(DC):
                        last = nc.tensor.matmul(ps_hid[h // 2][:, h % 2 * ROUND:(h % 2 + 1) * ROUND],
                                                w["l2_w_fc1"][:, k, h * P:(h + 1) * P], norm.hT[:, k, :],
                                                start=(k == 0), stop=(k == DC - 1))
                    if h % 2:
                        last.then_inc(hid_in_psum, 1)
                pe.wait_ge(sums_read, count(i, 1, 0))
                for h in range(HC):
                    if h % 2 == 0:
                        pe.wait_ge(hid_ready, count(i, 4, h // 2))
                    for u in range(2):
                        last = nc.tensor.matmul(ps_y[:, u * DIM:(u + 1) * DIM], hidT[:, h, u * P:(u + 1) * P],
                                                w["l2_w_fc2"][:, h, :], start=(h == 0 and u == 0),
                                                stop=(h == HC - 1), skip_group_check=True)
                    if h == HC // 2 and more:
                        norm.transposed(pe, i + 1)
                last.then_inc(y_in_psum, 1)

            norm.transposed(pe, 0)
            rounds(pe, body)

        running.close()
        cleared(nc, semaphores)


def recurrent_layer(nc, x_in, ctx, x_out, w, col, ident, select, head_of):
    with ExitStack() as held:
        semaphores, running = [], ExitStack()

        def sb(name, shape, dtype=F32):
            return held.enter_context(nc.sbuf_tensor("l3_" + name, shape, dtype))

        def sem(name):
            semaphores.append(held.enter_context(nc.semaphore("l3_" + name)))
            return semaphores[-1]

        ROUND = 2 * P
        NB = ROUND // SEQ
        ORDER = (0, 2, 1, 3, 4)

        x_tile = sb("x_tile", [P, 2, DIM])
        first_rows = sb("first_rows", [2 * NB, DIM])
        state = sb("state", [P, DC, NB, HEAD8])
        stats = [sb(f"stats{u}", [P, 6]) for u in range(2)]
        pad = [sb(f"pad{u}", [P, 1]) for u in range(2)]
        mean_var = [sb(f"mean_var{u}", [P, 2]) for u in range(2)]
        var_eps = [sb(f"var_eps{u}", [P, 1]) for u in range(2)]
        rstd = [sb(f"rstd{u}", [P, 1]) for u in range(2)]
        minus_half = sb("minus_half", [P, 1])
        one_column = sb("one_column", [P, 1])
        xn = sb("xn", [P, 2, DIM])
        xnT = [sb(f"xnT{n}", [P, DC, NB, 1 + SEQ]) for n in range(2)]
        sxT = sb("sxT", [P, DC, NB, SEQ])
        mixed = sb("mixed", [P, DC, NB, SEQ])
        loraT = sb("loraT", [P, 2, ROUND])
        part = [sb(f"part{j}", [P, DC, NB, SEQ]) for j in range(5)]
        x5 = [sb(f"x5_{j}", [P, DC, ROUND]) for j in range(5)]
        decayT = sb("decayT", [DECAY, ROUND])
        rate = sb("rate", [P, DC, ROUND])
        wT = sb("wT", [P, DC, NB, SEQ])
        kT, vT, rT, gT = (sb(n, [P, DC, ROUND]) for n in ("kT", "vT", "rT", "gT"))
        gate = sb("gate", [P, DC, ROUND])
        rukT = sb("rukT", [P, DC, ROUND])
        s = [sb(f"s{c}", [P, HEAD8, NB, SEQ]) for c in range(DC)]
        ruk = sb("ruk", [P, 2, DC, P // HEAD8])
        att = sb("att", [P, 2, DIM])
        square = sb("square", [P, 2, DIM])
        group = [sb(f"group{n}", [P, 4 * P // HEAD8]) for n in range(4)]
        gated = sb("gated", [P, DC, ROUND])
        res = sb("res", [P, 2, DIM])
        xkT, xrT = sb("xkT", [P, DC, ROUND]), sb("xrT", [P, DC, ROUND])
        kk, kk2 = sb("kk", [P, DC, ROUND]), sb("kk2", [P, DC, ROUND])
        receptance = sb("receptance", [P, 2, DIM])
        part_y = sb("part_y", [P, 2, DIM])
        y_out = sb("y_out", [P, 2, DIM])
        ps_j = [held.enter_context(nc.psum_tensor(f"l3_ps_j{j}", [P, BANK], F32)) for j in range(5)]
        ps_m = [held.enter_context(nc.psum_tensor(f"l3_ps_m{j}", [P, BANK], F32)) for j in range(3)]

        x_loaded, rows_loaded, state_loaded, stored = (sem(n) for n in ("x_loaded", "rows_loaded", "state_loaded", "stored"))
        set_up = sem("set_up")
        vector_step = sem("vector_step")
        scalar_step = sem("scalar_step")
        var_ready, rstd_ready = sem("var_ready"), sem("rstd_ready")
        xn_ready = sem("xn_ready")
        xT_in_psum, xnT_ready = sem("xT_in_psum"), sem("xnT_ready")
        rows_in_psum, rows_ready = sem("rows_in_psum"), sem("rows_ready")
        sx_ready = sem("sx_ready")
        mixed_ready = sem("mixed_ready")
        lora_in_psum, lora_ready = sem("lora_in_psum"), sem("lora_ready")
        mix_in_psum = sem("mix_in_psum")
        part_ready, x5_ready = sem("part_ready"), sem("x5_ready")
        k_in_psum, k_ready = sem("k_in_psum"), sem("k_ready")
        v_in_psum, v_ready = sem("v_in_psum"), sem("v_ready")
        decay_in_psum, decay_ready = sem("decay_in_psum"), sem("decay_ready")
        rate_in_psum, w_ready = sem("rate_in_psum"), sem("w_ready")
        r_in_psum, r_ready = sem("r_in_psum"), sem("r_ready")
        g_in_psum, g_ready = sem("g_in_psum"), sem("g_ready")
        gate_ready = sem("gate_ready")
        start_ready = sem("start_ready")
        spread_in_psum = sem("spread_in_psum")
        addend_ready = sem("addend_ready")
        out_ready = sem("out_ready")
        ruk_ready = sem("ruk_ready")
        att_in_psum = sem("att_in_psum")
        deviation_ready, root_ready = sem("deviation_ready"), sem("root_ready")
        att_ready = sem("att_ready")
        attT_in_psum, attT_ready = sem("attT_in_psum"), sem("attT_ready")
        gated_ready = sem("gated_ready")
        y_in_psum = sem("y_in_psum")
        channel_ready = sem("channel_ready")
        kk_in_psum, kk_ready = sem("kk_in_psum"), sem("kk_ready")
        kk2_ready = sem("kk2_ready")
        rr_in_psum, rr_ready = sem("rr_in_psum"), sem("rr_ready")
        kv_in_psum = sem("kv_in_psum")
        y_ready = sem("y_ready")

        one = lambda i: count(i, 1, 0)

        def rows_of(dram, first):
            return dram[bass.ds(first, ROUND), :].rearrange("(u p) d -> p u d", p=P)

        def flat(t):
            return t.rearrange("p c b t -> p c (b t)")

        ctx_rows = ctx.rearrange("(b r) d -> b (r d)", r=SEQ)

        block = running.enter_context(nc.Block())

        @block.sync
        def _(sp):
            def load_x(b0):
                sp.dma_start(x_tile[:], rows_of(x_in, b0 * SEQ)).then_inc(x_loaded, 16)

            def load_rows(b0):
                for r in range(2):
                    sp.dma_start(first_rows[r * NB:(r + 1) * NB, :], ctx_rows[bass.ds(b0, NB), r * DIM:(r + 1) * DIM]
                                 ).then_inc(rows_loaded, 16)

            def load_state(b0):
                for c in range(DC):
                    first = 2 * DIM + c * P * HEAD8
                    sp.dma_start(state[:, c, :, :], ctx_rows[bass.ds(b0, NB), first:first + P * HEAD8].rearrange(
                        "b (p d) -> p b d", d=HEAD8)).then_inc(state_loaded, 16)

            load_x(0)
            load_rows(0)
            load_state(0)
            sp.sem_inc(stored, 16)
            with sp.Fori(0, ROUNDS - 1) as i:
                sp.wait_ge(rows_in_psum, one(i))
                sp.nop()
                load_rows(i * NB + NB)
                sp.wait_ge(start_ready, one(i))
                sp.nop()
                load_state(i * NB + NB)
                sp.wait_ge(xn_ready, count(i, 4, 2))
                sp.nop()
                load_x(i * NB + NB)
                sp.wait_ge(y_ready, one(i))
                sp.nop()
                sp.dma_start(rows_of(x_out, i * ROUND), y_out[:]).then_inc(stored, 16)
            sp.wait_ge(y_ready, ROUNDS)
            sp.dma_start(rows_of(x_out, (ROUNDS - 1) * ROUND), y_out[:]).then_inc(stored, 16)
            sp.wait_ge(stored, 16 * (ROUNDS + 1))

        @block.gpsimd
        def _(pool):
            nc.gpsimd.memset(minus_half[:], -0.5).then_inc(set_up, 1)
            nc.gpsimd.memset(one_column[:], 1.0).then_inc(set_up, 1)
            nc.gpsimd.memset(wT[:], 0.0).then_inc(set_up, 1)
            pool.wait_ge(set_up, 3)

            def inverse_deviation(i, n, u):
                pool.wait_ge(var_ready, count(i, 4, 2 * n + u))
                nc.gpsimd.tensor_tensor(rstd[u][:], var_eps[u][:], minus_half[:], ALU.pow).then_inc(rstd_ready, 1)

            with pool.Fori(0, ROUNDS) as i:
                for u in range(2):
                    inverse_deviation(i, 0, u)
                pool.wait_ge(state_loaded, one(i) * 16 * DC)
                for c in range(DC):
                    last = nc.gpsimd.tensor_tensor(s[c][:, :, :, 0], state[:, c, :, :].rearrange("p b d -> p d b"),
                                                   one_column[:].unsqueeze(1).to_broadcast([P, HEAD8, NB]), ALU.mult)
                last.then_inc(start_ready, 1)
                for n, j in enumerate(ORDER):
                    pool.wait_ge(part_ready, count(i, 5, n))
                    for c in range(DC):
                        last = nc.gpsimd.tensor_tensor(x5[j][:, c, :].rearrange("p (b t) -> p b t", t=SEQ),
                                                       part[j][:, c, :, :], xnT[0][:, c, :, 1:], ALU.add)
                    last.then_inc(x5_ready, 1)
                for u in range(2):
                    inverse_deviation(i, 1, u)
                pool.wait_ge(kk_ready, one(i))
                nc.gpsimd.tensor_tensor(kk2[:], kk[:], kk[:], ALU.mult).then_inc(kk2_ready, 1)

        @block.scalar
        def _(act):
            links = Links(scalar_step, act, L3_SCALAR_LINKS)

            def normed_transposed(i, n, ps):
                act.wait_ge(xT_in_psum, count(i, 2, n))
                for c in range(DC):
                    last = nc.scalar.activation(xnT[n][:, c, :, 1:], ps[:, c * ROUND:(c + 1) * ROUND].rearrange(
                        "f (b t) -> f b t", t=SEQ), ACT.Identity, bias=col(f"l3_ln{n + 1}_b", c), scale=col(f"l3_ln{n + 1}_w", c))
                last.then_inc(xnT_ready, 1)

            def copied(i, ready, out, ps, done):
                act.wait_ge(ready, one(i))
                nc.scalar.activation(out[:].rearrange("p c t -> p (c t)"), ps[:], ACT.Copy).then_inc(done, 1)

            with act.Fori(0, ROUNDS) as i:
                act.wait_ge(rows_in_psum, one(i))
                for n in range(2):
                    last = nc.scalar.activation(xnT[n][:, :, :, 0], ps_m[1][:, 0:2 * DC * NB].rearrange(
                        "f (c r b) -> f c r b", r=2, b=NB)[:, :, 1 - n, :], ACT.Copy)
                last.then_inc(rows_ready, 1)
                normed_transposed(i, 0, ps_m[0])
                act.wait_ge(lora_in_psum, one(i))
                nc.scalar.activation(loraT[:, 0, :], ps_m[1][:, 0:ROUND], ACT.Tanh)
                nc.scalar.activation(loraT[0:LORA, 1, :], ps_m[1][0:LORA, ROUND:2 * ROUND], ACT.Tanh).then_inc(lora_ready, 1)
                copied(i, k_in_psum, kT, ps_j[0], k_ready)
                copied(i, v_in_psum, vT, ps_j[2], v_ready)
                act.wait_ge(decay_in_psum, one(i))
                nc.scalar.activation(decayT[:], ps_j[1][0:DECAY, 0:ROUND], ACT.Tanh).then_inc(decay_ready, 1)
                copied(i, r_in_psum, rT, ps_j[3], r_ready)
                act.wait_ge(rate_in_psum, one(i))
                for c in range(DC):
                    last = nc.scalar.activation(rate[:, c, :], ps_j[1][:, c * ROUND:(c + 1) * ROUND], ACT.Exp,
                                                bias=col("l3_time_decay", c), scale=1.0)
                links.mark(last)
                links.wait(i)
                for c in range(DC):
                    last = nc.scalar.activation(wT[:, c, :, 1:], rate[:, c, :].rearrange("p (b t) -> p b t", t=SEQ)[:, :, 0:SEQ - 1],
                                                ACT.Exp, scale=-1.0)
                last.then_inc(w_ready, 1)
                act.wait_ge(g_in_psum, one(i))
                nc.scalar.activation(gT[:].rearrange("p c t -> p (c t)"), ps_j[4][:], ACT.Tanh, scale=0.5).then_inc(g_ready, 1)
                act.wait_ge(deviation_ready, one(i))
                nc.scalar.activation(group[3][:], group[2][:], ACT.Sqrt).then_inc(root_ready, 1)
                act.wait_ge(attT_in_psum, one(i))
                for c in range(DC):
                    last = nc.scalar.activation(kk[:, c, :], ps_m[0][:, c * ROUND:(c + 1) * ROUND], ACT.Identity,
                                                bias=col("l3_gn_b", c), scale=col("l3_gn_w", c))
                last.then_inc(attT_ready, 1)
                normed_transposed(i, 1, ps_m[2])
                act.wait_ge(kk_in_psum, one(i))
                nc.scalar.activation(kk[:].rearrange("p c t -> p (c t)"), ps_j[0][:], ACT.Relu).then_inc(kk_ready, 1)
                act.wait_ge(rr_in_psum, one(i))
                nc.scalar.activation(receptance[:].rearrange("p u d -> p (u d)"), ps_j[1][:], ACT.Tanh, scale=0.5).then_inc(rr_ready, 1)
            links.check()

        @block.vector
        def _(dve):
            links = Links(vector_step, dve, L3_VECTOR_LINKS)

            def layer_norm(i, n, u, source):
                links.mark(nc.vector.bn_stats(stats[u][:], source[:, u, :]))
                links.wait(i)
                nc.vector.memset(pad[u][:], 0.0)
                links.mark(nc.vector.bn_aggr(mean_var[u][:], stats[u][:]))
                links.wait(i)
                nc.vector.tensor_scalar(var_eps[u][:], mean_var[u][:, 1:2], LN_EPS, None, ALU.add).then_inc(var_ready, 1)
                dve.wait_ge(rstd_ready, count(i, 4, 2 * n + u))
                nc.vector.tensor_scalar(xn[:, u, :], source[:, u, :], mean_var[u][:, 0:1], rstd[u][:], ALU.subtract, ALU.mult
                                        ).then_inc(xn_ready, 1)

            def shifted(i, n):
                dve.wait_ge(xnT_ready, count(i, 2, n))
                for c in range(DC):
                    last = nc.vector.tensor_tensor(sxT[:, c], xnT[n][:, c, :, 0:SEQ], xnT[n][:, c, :, 1:], ALU.subtract)
                links.mark(last)
                links.wait(i)

            def mix(out, n, amount):
                for c in range(DC):
                    last = nc.vector.scalar_tensor_tensor(out=out[:, c], in0=sxT[:, c], scalar=col(amount, c),
                                                          in1=xnT[n][:, c, :, 1:], op0=ALU.mult, op1=ALU.add)
                return last

            def by_token(t):
                return t.rearrange("p c (b t) -> p c b t", t=SEQ)

            dve.wait_ge(set_up, 3)
            with dve.Fori(0, ROUNDS) as i:
                dve.wait_ge(x_loaded, one(i) * 16)
                for u in range(2):
                    layer_norm(i, 0, u, x_tile)
                shifted(i, 0)
                mix(mixed[:], 0, "l3_maa_x").then_inc(mixed_ready, 1)
                for n, j in enumerate(ORDER):
                    dve.wait_ge(mix_in_psum, count(i, 5, n))
                    for c in range(DC):
                        last = nc.vector.scalar_tensor_tensor(
                            out=part[j][:, c].rearrange("p b t -> p (b t)"), in0=ps_j[j][:, c * ROUND:(c + 1) * ROUND],
                            scalar=col("l3_maa_stack", j * DC + c), in1=sxT[:, c].rearrange("p b t -> p (b t)"),
                            op0=ALU.add, op1=ALU.mult)
                    last.then_inc(part_ready, 1)
                dve.wait_ge(k_ready, one(i))
                dve.wait_ge(r_ready, one(i))
                for c in range(DC):
                    last = nc.vector.scalar_tensor_tensor(out=rukT[:, c, :], in0=rT[:, c, :], scalar=col("l3_faaaa", c),
                                                          in1=kT[:, c, :], op0=ALU.mult, op1=ALU.mult)
                last.then_inc(ruk_ready, 1)
                dve.wait_ge(g_ready, one(i))
                nc.vector.scalar_tensor_tensor(out=gate[:].rearrange("p c t -> p (c t)"), in0=gT[:].rearrange("p c t -> p (c t)"),
                                               scalar=1.0, in1=ps_j[4][:], op0=ALU.add, op1=ALU.mult).then_inc(gate_ready, 1)
                dve.wait_ge(start_ready, one(i))
                dve.wait_ge(w_ready, one(i))
                for c in range(DC):
                    for q in range(HEAD8 // 2):
                        n = c * (HEAD8 // 2) + q
                        dve.wait_ge(spread_in_psum, count(i, 8, n))
                        spread = ps_m[n % 3][:].rearrange("p (d b t) -> p d b t", d=2, t=SEQ)
                        for d in range(2):
                            last = nc.vector.tensor_tensor(s[c][:, 2 * q + d, :, 1:], spread[:, d, :, 0:SEQ - 1],
                                                           by_token(kT[:])[:, c, :, 0:SEQ - 1], ALU.mult)
                        last.then_inc(addend_ready, 1)
                        dve.wait_ge(addend_ready, count(i, 8, n))
                        for d in range(2):
                            run = s[c][:, 2 * q + d].rearrange("p b t -> p (b t)")
                            last = nc.vector.tensor_tensor_scan(run, wT[:, c].rearrange("p b t -> p (b t)"), run, 0.0,
                                                                ALU.mult, ALU.add)
                    links.mark(last)
                    links.wait(i)
                    run = s[c][:].rearrange("p d b t -> p d (b t)")
                    nc.vector.tensor_tensor(run, run, rT[:, c, :].unsqueeze(1).to_broadcast([P, HEAD8, ROUND]), ALU.mult
                                            ).then_inc(out_ready, 1)
                heads = 2 * DIM // HEAD8

                def grouped(t):
                    return t.rearrange("p (h d) -> p h d", d=HEAD8)

                def spread_over_head(t):
                    return t.unsqueeze(2).to_broadcast([P, heads, HEAD8])

                att_flat, sq_flat = (t[:].rearrange("p u d -> p (u d)") for t in (att, square))
                dve.wait_ge(att_in_psum, one(i))
                links.mark(nc.vector.tensor_copy(ruk[:].rearrange("p u c h -> p (u c h)"), ps_j[0][:, 0:heads]))
                links.wait(i)
                links.mark(nc.vector.tensor_tensor(grouped(sq_flat), grouped(ps_j[2][:]),
                                                   spread_over_head(ruk[:].rearrange("p u c h -> p (u c h)")), ALU.mult))
                links.wait(i)
                links.mark(nc.vector.tensor_tensor(att_flat, ps_j[1][:], sq_flat, ALU.add))
                links.wait(i)
                links.mark(nc.vector.tensor_reduce(group[0][:], grouped(att_flat), AX.X, ALU.add))
                links.wait(i)
                links.mark(nc.vector.tensor_scalar(group[1][:], group[0][:], 1.0 / HEAD8, None, ALU.mult))
                links.wait(i)
                links.mark(nc.vector.tensor_tensor(grouped(att_flat), grouped(att_flat), spread_over_head(group[1][:]), ALU.subtract))
                links.wait(i)
                links.mark(nc.vector.tensor_tensor(sq_flat, att_flat, att_flat, ALU.mult))
                links.wait(i)
                links.mark(nc.vector.tensor_reduce(group[0][:], grouped(sq_flat), AX.X, ALU.add))
                links.wait(i)
                nc.vector.tensor_scalar(group[2][:], group[0][:], 1.0 / HEAD8, LN_EPS, ALU.mult, ALU.add).then_inc(deviation_ready, 1)
                dve.wait_ge(root_ready, one(i))
                links.mark(nc.vector.reciprocal(group[1][:], group[3][:]))
                links.wait(i)
                nc.vector.tensor_tensor(grouped(att_flat), grouped(att_flat), spread_over_head(group[1][:]), ALU.mult
                                        ).then_inc(att_ready, 1)
                dve.wait_ge(attT_ready, one(i))
                nc.vector.scalar_tensor_tensor(out=gated[:], in0=kk[:], scalar=0.5, in1=gate[:], op0=ALU.mult, op1=ALU.mult
                                               ).then_inc(gated_ready, 1)
                dve.wait_ge(y_in_psum, one(i))
                links.mark(nc.vector.tensor_tensor(res[:].rearrange("p u d -> p (u d)"), ps_m[1][:],
                                                   x_tile[:].rearrange("p u d -> p (u d)"), ALU.add))
                links.wait(i)
                for u in range(2):
                    layer_norm(i, 1, u, res)
                shifted(i, 1)
                mix(by_token(xkT[:]), 1, "l3_ffn_maa_k").then_inc(channel_ready, 1)
                mix(by_token(xrT[:]), 1, "l3_ffn_maa_r").then_inc(channel_ready, 1)
                dve.wait_ge(rr_ready, one(i))
                dve.wait_ge(kv_in_psum, one(i))
                links.mark(nc.vector.scalar_tensor_tensor(
                    out=part_y[:].rearrange("p u d -> p (u d)"), in0=receptance[:].rearrange("p u d -> p (u d)"), scalar=1.0,
                    in1=ps_j[2][:], op0=ALU.add, op1=ALU.mult))
                links.wait(i)
                dve.wait_ge(stored, one(i) * 16)
                nc.vector.scalar_tensor_tensor(out=y_out[:], in0=part_y[:], scalar=0.5, in1=res[:], op0=ALU.mult, op1=ALU.add
                                               ).then_inc(y_ready, 1)
            links.check()

        @block.tensor
        def _(pe):
            def transposed(ps, tokens, u):
                for c in range(DC):
                    last = nc.tensor.transpose(ps[:, c * ROUND + u * P:c * ROUND + (u + 1) * P], tokens[:, u, c * P:(c + 1) * P], ident)
                return last

            def features_out(ps, weights, moving):
                for c in range(DC):
                    for k in range(DC):
                        last = nc.tensor.matmul(ps[:, c * ROUND:(c + 1) * ROUND], weights[:, k, c * P:(c + 1) * P], moving[:, k, :],
                                                start=(k == 0), stop=(k == DC - 1))
                return last

            def tokens_out(ps, weights, stationary):
                for u in range(2):
                    for k in range(DC):
                        last = nc.tensor.matmul(ps[:, u * DIM:(u + 1) * DIM], stationary[:, k, u * P:(u + 1) * P], weights[:, k, :],
                                                start=(k == 0), stop=(k == DC - 1))
                return last

            with pe.Fori(0, ROUNDS) as i:
                pe.wait_ge(rows_loaded, one(i) * 32)
                for u in range(2):
                    pe.wait_ge(xn_ready, count(i, 4, u))
                    last = transposed(ps_m[0], xn, u)
                last.then_inc(xT_in_psum, 1)
                for c in range(DC):
                    last = nc.tensor.transpose(ps_m[1][:, c * 2 * NB:(c + 1) * 2 * NB], first_rows[:, c * P:(c + 1) * P],
                                               ident[0:2 * NB, 0:2 * NB])
                last.then_inc(rows_in_psum, 1)
                pe.wait_ge(mixed_ready, one(i))
                pe.wait_ge(rows_ready, one(i))
                for k in range(DC):
                    nc.tensor.matmul(ps_m[1][:, 0:ROUND], w["l3_maa_w1"][:, k, 0:P], mixed[:, k].rearrange("p b t -> p (b t)"),
                                     start=(k == 0), stop=(k == DC - 1))
                for k in range(DC):
                    last = nc.tensor.matmul(ps_m[1][0:LORA, ROUND:2 * ROUND], w["l3_maa_w1"][:, k, P:P + LORA],
                                            mixed[:, k].rearrange("p b t -> p (b t)"), start=(k == 0), stop=(k == DC - 1))
                last.then_inc(lora_in_psum, 1)
                pe.wait_ge(lora_ready, one(i))
                for j in ORDER:
                    rows, half = (slice(LORA * j, LORA * (j + 1)), 0) if j < 4 else (slice(0, LORA), 1)
                    for c in range(DC):
                        last = nc.tensor.matmul(ps_j[j][:, c * ROUND:(c + 1) * ROUND], w["l3_maa_w2"][rows, half, c * P:(c + 1) * P],
                                                loraT[rows, half, :], start=True, stop=True)
                    last.then_inc(mix_in_psum, 1)
                x5_at = {j: n for n, j in enumerate(ORDER)}
                for j in (0, 2, 1):
                    pe.wait_ge(x5_ready, count(i, 5, x5_at[j]))
                    if j == 0:
                        features_out(ps_j[0], w["l3_Wk"], x5[0]).then_inc(k_in_psum, 1)
                    if j == 2:
                        features_out(ps_j[2], w["l3_Wv"], x5[2]).then_inc(v_in_psum, 1)
                    if j == 1:
                        for k in range(DC):
                            last = nc.tensor.matmul(ps_j[1][0:DECAY, 0:ROUND], w["l3_decay_w1"][:, k, :], x5[1][:, k, :],
                                                    start=(k == 0), stop=(k == DC - 1))
                        last.then_inc(decay_in_psum, 1)
                pe.wait_ge(x5_ready, count(i, 5, x5_at[3]))
                features_out(ps_j[3], w["l3_Wr"], x5[3]).then_inc(r_in_psum, 1)
                pe.wait_ge(decay_ready, one(i))
                for c in range(DC):
                    last = nc.tensor.matmul(ps_j[1][:, c * ROUND:(c + 1) * ROUND], w["l3_decay_w2"][0:DECAY, 0, c * P:(c + 1) * P],
                                            decayT[:], start=True, stop=True)
                last.then_inc(rate_in_psum, 1)
                pe.wait_ge(x5_ready, count(i, 5, x5_at[4]))
                features_out(ps_j[4], w["l3_Wg"], x5[4]).then_inc(g_in_psum, 1)
                pe.wait_ge(v_ready, one(i))
                for c in range(DC):
                    for q in range(HEAD8 // 2):
                        n = c * (HEAD8 // 2) + q
                        if n >= 3:
                            pe.wait_ge(addend_ready, count(i, 8, n - 3))
                        for d in range(2):
                            last = nc.tensor.matmul(ps_m[n % 3][:, d * ROUND:(d + 1) * ROUND], select[:, 2 * q + d, :],
                                                    vT[:, c, :], start=True, stop=True)
                        last.then_inc(spread_in_psum, 1)
                pe.wait_ge(k_ready, one(i))
                pe.wait_ge(ruk_ready, one(i))
                pe.wait_ge(w_ready, one(i))
                for u in range(2):
                    for c in range(DC):
                        nc.tensor.transpose(ps_j[2][:, u * DIM + c * P:u * DIM + (c + 1) * P], vT[:, c, u * P:(u + 1) * P], ident)
                per_chunk = P // HEAD8
                for u in range(2):
                    for c in range(DC):
                        at = (u * DC + c) * per_chunk
                        nc.tensor.matmul(ps_j[0][:, at:at + per_chunk], rukT[:, c, u * P:(u + 1) * P], head_of, start=True, stop=True)
                for c in range(DC):
                    pe.wait_ge(out_ready, count(i, 2, c))
                    for u in range(2):
                        for d in range(HEAD8):
                            first = u * DIM + c * P + d
                            last = nc.tensor.matmul(ps_j[1][:, first:u * DIM + (c + 1) * P:HEAD8],
                                                    s[c][:, d].rearrange("p b t -> p (b t)")[:, u * P:(u + 1) * P], head_of,
                                                    start=True, stop=True)
                last.then_inc(att_in_psum, 1)
                pe.wait_ge(att_ready, one(i))
                for u in range(2):
                    last = transposed(ps_m[0], att, u)
                last.then_inc(attT_in_psum, 1)
                pe.wait_ge(gated_ready, one(i))
                tokens_out(ps_m[1], w["l3_Wo"], gated).then_inc(y_in_psum, 1)
                for u in range(2):
                    pe.wait_ge(xn_ready, count(i, 4, 2 + u))
                    last = transposed(ps_m[2], xn, u)
                last.then_inc(xT_in_psum, 1)
                pe.wait_ge(channel_ready, count(i, 2, 0))
                features_out(ps_j[0], w["l3_ffn_Wk"], xkT).then_inc(kk_in_psum, 1)
                pe.wait_ge(channel_ready, count(i, 2, 1))
                tokens_out(ps_j[1], w["l3_ffn_Wr"], xrT).then_inc(rr_in_psum, 1)
                pe.wait_ge(kk2_ready, one(i))
                tokens_out(ps_j[2], w["l3_ffn_Wv"], kk2).then_inc(kv_in_psum, 1)

        running.close()
        cleared(nc, semaphores)


LAYER_WEIGHTS = (L0_WEIGHTS, L1_WEIGHTS, L2_WEIGHTS, L3_WEIGHTS)
SHARED = ("l2_wo1", "l2_wo2", "l2_wv1", "l2_wq1", "l2_wk1")
SHARED_COLUMNS = sum(L2_WEIGHTS[n][0] // P * L2_WEIGHTS[n][1] for n in SHARED)


def program(nc, dram, x_out, layers=(0, 1, 2, 3)):
    with ExitStack() as held:
        def sb(name, shape):
            return held.enter_context(nc.sbuf_tensor(name, shape, F32))

        cols = sb("cols", [P, NCOLS])
        rows = sb("rows", [P, NROWS * DIM])
        ident = sb("ident", [P, P])
        parity = sb("parity", [P, 2])
        select = sb("select", [P, HEAD8, P])
        head_of = sb("head_of", [P, P // HEAD8])
        shared = sb("shared", [P, SHARED_COLUMNS])
        col = lambda name, c, n=1: cols[:, COL_AT[name] + c:COL_AT[name] + c + n]
        row = {n: rows[:, k * DIM:(k + 1) * DIM] for k, n in enumerate(ROW_NAMES)}
        between = [nc.dram_tensor(f"between{n}", (BATCH * SEQ, DIM), F32).ap() for n in range(3)]
        inside = [nc.dram_tensor(f"inside{a}", (BATCH * SEQ, DIM), F32).ap() for a in range(2)]
        first_loaded, l0_loaded, l1_loaded, shared_loaded, l2_loaded, l3_loaded = (
            held.enter_context(nc.semaphore(n + "_loaded")) for n in ("first", "l0", "l1", "shared", "l2", "l3"))

        def in_shared(names, shapes):
            w, at = {}, 0
            for n in names:
                k, m = shapes[n]
                w[n] = shared[:, at:at + k // P * m].rearrange("p (k m) -> p k m", m=m)
                at += k // P * m
            return w

        def in_own(stack, names, shapes):
            return {n: stack.enter_context(nc.sbuf_tensor(n, [P, shapes[n][0] // P, shapes[n][1]], F32))[:] for n in names}

        def load(sp, w, loaded):
            for n in w:
                sp.dma_start(w[n], dram[n].rearrange("(k p) m -> p k m", p=P)).then_inc(loaded, 16)

        def wait_for(loaded, count):
            with nc.Block() as block:
                @block.sync
                def _(sp):
                    sp.wait_ge(loaded, 16 * count)

        w_shared = in_shared(SHARED, L2_WEIGHTS)
        with ExitStack() as layers01:
            w1 = in_own(layers01, L1_WEIGHTS, L1_WEIGHTS)
            with ExitStack() as layer0:
                w0 = in_own(layer0, L0_WEIGHTS, L0_WEIGHTS)
                first = ["l0_w_qkv"]
                constants = ((cols, "cols"), (ident, "ident"), (parity, "parity"))
                with nc.Block() as block:
                    @block.sync
                    def _(sp):
                        for tile, name in constants:
                            sp.dma_start(tile[:], dram[name]).then_inc(first_loaded, 16)
                        load(sp, {n: w0[n] for n in first}, first_loaded)
                        sp.dma_start(rows[:], dram["rows"].partition_broadcast(P)).then_inc(first_loaded, 16)
                        sp.wait_ge(first_loaded, 16 * (len(constants) + len(first) + 1))

                def prefetch(sp):
                    load(sp, {n: w0[n] for n in w0 if n not in first}, l0_loaded)
                    load(sp, w1, l1_loaded)
                    load(sp, w_shared, shared_loaded)

                if 0 in layers:
                    decoder_layer(nc, dram["x"], dram["ctx"], dram["self_mask"], dram["cross_mask"],
                                  between[0] if layers[-1] > 0 else x_out, w0, (l0_loaded, 16 * (len(w0) - len(first))),
                                  prefetch, col, row, ident[:], parity)
                else:
                    with nc.Block() as block:
                        @block.sync
                        def _(sp):
                            prefetch(sp)
            wait_for(l1_loaded, len(w1))
            if 1 in layers:
                resampler_layer(nc, between[0] if 0 in layers else dram["x"], dram["ctx"], dram["key_mask"],
                                between[1] if layers[-1] > 1 else x_out, w1, col, row, ident[:], parity)
        wait_for(shared_loaded, len(w_shared))
        with ExitStack() as layer2:
            w2 = in_own(layer2, [n for n in L2_WEIGHTS if n not in SHARED], L2_WEIGHTS)
            if 2 in layers:
                x = between[1] if 1 in layers else dram["x"]
                wide_attention(nc, 0, x, dram["ctx"], inside[0], w_shared | w2, col, row, ident[:],
                               lambda sp: load(sp, w2, l2_loaded))
                wait_for(l2_loaded, len(w2))
                wide_attention(nc, 1, inside[0], dram["ctx"], inside[1], w_shared | w2, col, row, ident[:])
            w3 = in_shared(L3_WEIGHTS, L3_WEIGHTS)

            def prefetch3(sp):
                load(sp, w3, l3_loaded)
                sp.dma_start(select[:], dram["select"]).then_inc(l3_loaded, 16)
                sp.dma_start(head_of[:], dram["head_of"]).then_inc(l3_loaded, 16)

            if 2 in layers:
                wide_mlp(nc, inside[1], between[2] if layers[-1] > 2 else x_out, w2, col, row, ident[:], prefetch3)
            else:
                with nc.Block() as block:
                    @block.sync
                    def _(sp):
                        prefetch3(sp)
        wait_for(l3_loaded, len(w3) + 2)
        if 3 in layers:
            recurrent_layer(nc, between[2] if 2 in layers else dram["x"], dram["ctx"], x_out, w3, col, ident[:], select, head_of[:])


def laid_out(inputs):
    a = {n: np.asarray(x) for n, x in inputs.items()}
    out = {"x": a["x"].reshape(-1, DIM), "ctx": a["ctx_2048"].reshape(-1, DIM),
           "self_mask": a["mask_1x1xSxS2_fc1"].reshape(SEQ, SEQ),
           "cross_mask": a["mask_Bx1xSxS2_ff1"].reshape(-1, SEQ), "key_mask": a["mask_BxS2_ik0"]}
    a["l1_k_b"], a["l1_v_b"] = a["L1_xattn_kv_b"][0::2], a["L1_xattn_kv_b"][1::2]
    out["l1_k_w"], out["l1_v_w"] = a["L1_xattn_kv_w"][:, 0::2], a["L1_xattn_kv_w"][:, 1::2]
    for name in ("Wk", "Wv", "Wr", "Wg", "Wo", "ffn_Wk", "ffn_Wr", "ffn_Wv"):
        out["l3_" + name] = a["L3_xattn_" + name].T
    out["l3_maa_w2"] = np.zeros((2 * P, DIM), np.float32)
    out["l3_maa_w2"][:5 * LORA] = a["L3_xattn_maa_w2"].reshape(5 * LORA, DIM)
    out["l3_decay_w2"] = np.zeros((P, DIM), np.float32)
    out["l3_decay_w2"][:DECAY] = a["L3_xattn_decay_w2"]
    head, within = np.arange(P) // HEAD8, np.arange(P) % HEAD8
    out["select"] = ((head[:, None, None] == head[None, None, :])
                     & (within[:, None, None] == np.arange(HEAD8)[None, :, None])).astype(np.float32)
    out["head_of"] = (head[:, None] == np.arange(P // HEAD8)[None]).astype(np.float32)
    for weights in LAYER_WEIGHTS:
        for name in weights:
            if name not in out:
                out[name] = a["L" + name[1] + "_xattn_" + name[3:]]
    out["cols"] = np.concatenate([a[name].reshape(-1)[first:first + n].reshape(-1, P).T for name, first, n in COLS.values()], 1)
    out["rows"] = np.concatenate([a[name].reshape(-1) for name in ROWS.values()])[None]
    out["ident"] = np.eye(P, dtype=np.float32)
    out["parity"] = (np.arange(P)[:, None] // HEAD % 2 == np.arange(2)[None]).astype(np.float32)
    return {n: np.ascontiguousarray(x) for n, x in out.items()}


def kernel(**inputs):
    import concourse.bacc as bacc
    from concourse.bass_utils import run_bass_kernel_spmd

    nc = bacc.Bacc("TRN2", target_bir_lowering=False, num_devices=1)
    arrays = {f"in_{n}": a for n, a in laid_out(inputs).items()}
    dram = {n[3:]: nc.dram_tensor(n, a.shape, mybir.dt.from_np(a.dtype), kind="ExternalInput").ap() for n, a in arrays.items()}
    out = nc.dram_tensor("out", (BATCH * SEQ, DIM), F32, kind="ExternalOutput").ap()
    program(nc, dram, out)
    result = run_bass_kernel_spmd(nc, [arrays], core_ids=[0])
    return result.results[0]["out"].reshape(BATCH, SEQ, DIM)
```

```python
import numpy as np
from contextlib import ExitStack

import concourse.bass as bass
from concourse import mybir

F32 = mybir.dt.float32
I32 = mybir.dt.int32
ALU = mybir.AluOpType
ACT = mybir.ActivationFunctionType
AX = mybir.AxisListType

BATCH, SEQ, DIM = 32, 64, 256
P = 128
PER_TILE = P // SEQ
TILES = BATCH // PER_TILE
ROUNDS = TILES // 2
DC = DIM // P
HIDDEN = 4 * DIM
HC = HIDDEN // P
HEADS, HEAD = 16, 16
PAIRS = HEADS // 2
MASKED = 10000.0
MINUS_INF = -1.0e30
BANK = 512


class Links:

    def __init__(self, sem, engine, per_round):
        self.sem, self.engine, self.per_round, self.n = sem, engine, per_round, 0
        self.loop_pass = None

    def begin(self, n=0):
        self.n = n

    def mark(self, instruction):
        self.n += 1
        return instruction.then_inc(self.sem, 1)

    def wait(self, i):
        through = i if self.loop_pass is None else self.loop_pass
        self.engine.wait_ge(self.sem, through * self.per_round + self.n)

    def check(self, ahead=0):
        n = self.n - ahead
        assert n == self.per_round, f"links per round: {n}, stated {self.per_round}"


def count(i, per_round, k):
    return i * per_round + k + 1


def skewed(engine, lag, *stages, links=None):
    n = len(stages)

    def in_pass(i):
        if links:
            links.loop_pass = i

    def run(k, i, s):
        for step in stages[k]:
            step(i, s)

    in_pass(0)
    for k in range(lag):
        run(k, 0, 0)
    ahead = links.n if links else 0
    with engine.Fori(0, ROUNDS - 1) as i:
        in_pass(i)
        for k in range(n):
            if k + lag < n:
                run(k + lag, i, 0)
            else:
                run(k + lag - n, i + 1, 0)
            run(k, i, 1)
    if links:
        links.check(ahead)
        links.begin(ahead)
    in_pass(ROUNDS - 1)
    for k in range(n):
        if k + lag < n:
            run(k + lag, ROUNDS - 1, 0)
        run(k, ROUNDS - 1, 1)


def cleared(nc, semaphores):
    with nc.Block() as block:
        @block.sync
        def _(sp):
            for sem in semaphores:
                sp.sem_clear(sem)

LN_EPS = 1e-5

L0_WEIGHTS = {"l0_w_qkv": (DIM, 3 * DIM), "l0_w_ao": (DIM, DIM), "l0_w_q": (DIM, DIM), "l0_w_kv": (DIM, 2 * DIM),
              "l0_w_co": (DIM, DIM), "l0_w1": (DIM, HIDDEN), "l0_w2": (HIDDEN, DIM)}

COLS = {}
for _n in (1, 2, 3):
    COLS[f"l0_ln{_n}_s"] = (f"L0_xattn_ln{_n}_s", 0, DIM)
    COLS[f"l0_ln{_n}_b"] = (f"L0_xattn_ln{_n}_b", 0, DIM)
COLS["l0_bq0"] = ("L0_xattn_b_qkv", 0, DIM)
COLS["l0_bk0"] = ("L0_xattn_b_qkv", DIM, DIM)
COLS["l0_bv0"] = ("L0_xattn_b_qkv", 2 * DIM, DIM)
COLS["l0_bq1"] = ("L0_xattn_b_q", 0, DIM)
COLS["l0_bk1"] = ("L0_xattn_b_kv", 0, DIM)
COLS["l0_bv1"] = ("L0_xattn_b_kv", DIM, DIM)
COLS["l0_b1"] = ("L0_xattn_b1", 0, HIDDEN)
ROWS = {"l0_b_ao": "L0_xattn_b_ao", "l0_b_co": "L0_xattn_b_co", "l0_b2": "L0_xattn_b2"}
RMS_EPS = 1e-6
L1_WEIGHTS = {"l1_q_w": (DIM, DIM), "l1_k_w": (DIM, DIM), "l1_v_w": (DIM, DIM), "l1_out_w": (DIM, DIM),
              "l1_mlp_w1": (DIM, HIDDEN), "l1_mlp_w2": (HIDDEN, DIM)}
COLS["l1_bq"] = ("L1_xattn_q_b", 0, DIM)
COLS["l1_bk"] = ("l1_k_b", 0, DIM)
COLS["l1_bv"] = ("l1_v_b", 0, DIM)
COLS["l1_postnorm_w"] = ("L1_xattn_postnorm_w", 0, DIM)
COLS["l1_b1"] = ("L1_xattn_mlp_b1", 0, HIDDEN)
ROWS["l1_out_b"] = "L1_xattn_out_b"
ROWS["l1_mlp_b2"] = "L1_xattn_mlp_b2"
WIDE = 128
L2_VECTOR_LINKS = HEADS * 4
L2_WEIGHTS = {}
for _a in (1, 2):
    L2_WEIGHTS |= {f"l2_wo{_a}": (HEADS * WIDE, DIM)}
for _a in (1, 2):
    L2_WEIGHTS |= {f"l2_wv{_a}": (DIM, HEADS * WIDE), f"l2_wq{_a}": (DIM, HEADS * WIDE), f"l2_wk{_a}": (DIM, HEADS * WIDE)}
    COLS[f"l2_bq{_a}"] = (f"L2_xattn_bq{_a}", 0, HEADS * WIDE)
    COLS[f"l2_bk{_a}"] = (f"L2_xattn_bk{_a}", 0, HEADS * WIDE)
    COLS[f"l2_bv{_a}"] = (f"L2_xattn_bv{_a}", 0, HEADS * WIDE)
    COLS[f"l2_bias_k{_a}"] = (f"L2_xattn_bias_k{_a}", 0, HEADS * WIDE)
    COLS[f"l2_bias_v{_a}"] = (f"L2_xattn_bias_v{_a}", 0, HEADS * WIDE)
    ROWS[f"l2_bo{_a}"] = f"L2_xattn_bo{_a}"
L2_WEIGHTS |= {"l2_w_fc1": (DIM, HIDDEN), "l2_w_fc2": (HIDDEN, DIM)}
for _n, _name in enumerate(("ln1", "ln2", "ln_mlp")):
    COLS[f"l2_ln{_n}_s"] = (f"L2_xattn_{_name}_scale", 0, DIM)
    COLS[f"l2_ln{_n}_b"] = (f"L2_xattn_{_name}_offset", 0, DIM)
COLS["l2_b_fc1"] = ("L2_xattn_b_fc1", 0, HIDDEN)
ROWS["l2_b_fc2"] = "L2_xattn_b_fc2"
HEAD8 = 8
LORA, DECAY = 32, 64
L3_VECTOR_LINKS = 2 * 19
L3_SCALAR_LINKS = 2
L3_WEIGHTS = {"l3_maa_w1": (DIM, 5 * LORA), "l3_maa_w2": (DIM, DIM), "l3_decay_w1": (DIM, DECAY), "l3_decay_w2": (P, DIM)}
L3_WEIGHTS |= {f"l3_{_n}": (DIM, DIM) for _n in ("Wk", "Wv", "Wr", "Wg", "Wo", "ffn_Wk", "ffn_Wr", "ffn_Wv")}
for _n in (1, 2):
    COLS[f"l3_ln{_n}_w"] = (f"L3_xattn_ln{_n}_w", 0, DIM)
    COLS[f"l3_ln{_n}_b"] = (f"L3_xattn_ln{_n}_b", 0, DIM)
for _n in ("maa_x", "time_decay", "faaaa", "gn_w", "gn_b", "ffn_maa_k", "ffn_maa_r"):
    COLS[f"l3_{_n}"] = (f"L3_xattn_{_n}", 0, DIM)
COLS["l3_maa_stack"] = ("L3_xattn_maa_stack", 0, 5 * DIM)
COL_AT, NCOLS = {}, 0
for _n, (_, _, _length) in COLS.items():
    COL_AT[_n] = NCOLS
    NCOLS += _length // P
ROW_NAMES = list(ROWS)
NROWS = len(ROWS)


def decoder_layer(nc, x_in, ctx, self_mask, cross_mask, x_out, w, weights_in, prefetch, col, row, ident, parity):
    with ExitStack() as held:
        semaphores, running = [], ExitStack()

        def sb(name, shape, dtype=F32):
            return held.enter_context(nc.sbuf_tensor("l0_" + name, shape, dtype))

        def sem(name):
            semaphores.append(held.enter_context(nc.semaphore("l0_" + name)))
            return semaphores[-1]

        x_tile = [sb(f"x_tile{s}", [P, DIM]) for s in range(2)]
        c_tile = [sb(f"c_tile{s}", [P, DIM]) for s in range(2)]
        mask1 = sb("mask1", [P, SEQ])
        mask2 = [sb(f"mask2_{s}", [P, SEQ]) for s in range(2)]
        bias1 = sb("bias1", [P, SEQ])
        bias2 = [sb(f"bias2_{s}", [P, SEQ]) for s in range(2)]
        stats = [sb(f"stats{s}", [P, 6]) for s in range(2)]
        mean_var = [sb(f"mean_var{s}", [P, 2]) for s in range(2)]
        var_eps = [sb(f"var_eps{s}", [P, 1]) for s in range(2)]
        rstd = [sb(f"rstd{s}", [P, 1]) for s in range(2)]
        pad = [sb(f"pad{s}", [P, 1]) for s in range(2)]
        minus_half = sb("minus_half", [P, 1])
        xn = [sb(f"xn{s}", [P, DIM]) for s in range(2)]
        hT = [sb(f"hT{s}", [P, DC, P]) for s in range(2)]
        cT = [sb(f"cT{s}", [P, DC, P]) for s in range(2)]
        qT = [sb(f"qT{s}", [P, DC, P]) for s in range(2)]
        kT = [sb(f"kT{s}", [P, DC, 2, P]) for s in range(2)]
        vp = [sb(f"vp{s}", [P, PER_TILE, PAIRS, 2, HEAD + 1]) for s in range(2)]
        probs = [sb(f"probs{s}", [P, 4, 2 * DC, SEQ]) for s in range(2)]
        row_max = [sb(f"row_max{s}", [P, HEADS]) for s in range(2)]
        pT = [sb(f"pT{s}", [P, PAIRS, P]) for s in range(2)]
        inv_sum = [sb(f"inv_sum{s}", [P, HEADS]) for s in range(2)]
        att = [sb(f"att{s}", [P, DIM]) for s in range(2)]
        aT = [sb(f"aT{s}", [P, DC, P]) for s in range(2)]
        res = [sb(f"res{s}", [P, DIM]) for s in range(2)]
        res_b = [sb(f"res_b{s}", [P, DIM]) for s in range(2)]
        hidT = [sb(f"hidT{s}", [P, HC, P]) for s in range(2)]
        y_out = [sb(f"y_out{s}", [P, DIM]) for s in range(2)]
        ps_s = held.enter_context(nc.psum_tensor("l0_ps_s", [P, 4, BANK], F32))
        ps_a = [held.enter_context(nc.psum_tensor(f"l0_ps_a{s}", [P, BANK], F32)) for s in range(2)]
        ps_b = [held.enter_context(nc.psum_tensor(f"l0_ps_b{s}", [P, BANK], F32)) for s in range(2)]

        x_loaded = [sem(f"x_loaded{s}") for s in range(2)]
        c_loaded = [sem(f"c_loaded{s}") for s in range(2)]
        mask2_loaded = [sem(f"mask2_loaded{s}") for s in range(2)]
        mask1_loaded = sem("mask1_loaded")
        stored = [sem(f"stored{s}") for s in range(2)]
        set_up = sem("set_up")
        scores_read = sem("scores_read")
        vector_set_up = sem("vector_set_up")
        vector_step = sem("vector_step")
        var_ready = [sem(f"var_ready{s}") for s in range(2)]
        rstd_ready = [sem(f"rstd_ready{s}") for s in range(2)]
        xn_ready = [sem(f"xn_ready{s}") for s in range(2)]
        xT_ready = [sem(f"xT_ready{s}") for s in range(2)]
        hT_ready = [sem(f"hT_ready{s}") for s in range(2)]
        cT_in_psum = [sem(f"cT_in_psum{s}") for s in range(2)]
        cT_ready = [sem(f"cT_ready{s}") for s in range(2)]
        k_in_psum = [sem(f"k_in_psum{s}") for s in range(2)]
        v_in_psum = [sem(f"v_in_psum{s}") for s in range(2)]
        q_in_psum = [sem(f"q_in_psum{s}") for s in range(2)]
        q_ready = [sem(f"q_ready{s}") for s in range(2)]
        k_ready = [sem(f"k_ready{s}") for s in range(2)]
        v_ready = [sem(f"v_ready{s}") for s in range(2)]
        s_in_psum = [sem(f"s_in_psum{s}") for s in range(2)]
        s_masked = [sem(f"s_masked{s}") for s in range(2)]
        shifted = [sem(f"shifted{s}") for s in range(2)]
        p_ready = [sem(f"p_ready{s}") for s in range(2)]
        pT_in_psum = [sem(f"pT_in_psum{s}") for s in range(2)]
        pT_lo_ready = [sem(f"pT_lo_ready{s}") for s in range(2)]
        pT_hi_ready = [sem(f"pT_hi_ready{s}") for s in range(2)]
        o_in_psum = [sem(f"o_in_psum{s}") for s in range(2)]
        att_ready = [sem(f"att_ready{s}") for s in range(2)]
        aT_in_psum = [sem(f"aT_in_psum{s}") for s in range(2)]
        aT_ready = [sem(f"aT_ready{s}") for s in range(2)]
        y_in_psum = [sem(f"y_in_psum{s}") for s in range(2)]
        res_ready = [sem(f"res_ready{s}") for s in range(2)]
        res_b_ready = [sem(f"res_b_ready{s}") for s in range(2)]
        y_ready = [sem(f"y_ready{s}") for s in range(2)]
        hid_in_psum = [sem(f"hid_in_psum{s}") for s in range(2)]
        hid_ready = [sem(f"hid_ready{s}") for s in range(2)]

        wq = [w["l0_w_qkv"][:, :, 0:DIM], w["l0_w_q"][:, :, :]]
        wk = [w["l0_w_qkv"][:, :, DIM:2 * DIM], w["l0_w_kv"][:, :, 0:DIM]]
        wv = [w["l0_w_qkv"][:, :, 2 * DIM:3 * DIM], w["l0_w_kv"][:, :, DIM:2 * DIM]]
        wo = [w["l0_w_ao"], w["l0_w_co"]]
        w1, w2 = w["l0_w1"], w["l0_w2"]
        scale = HEAD ** -0.5
        VECTOR_LINKS = 26
        LAG = 6

        block = running.enter_context(nc.Block())

        @block.sync
        def _(sp):
            for b in range(PER_TILE):
                sp.dma_start(mask1[b * SEQ:(b + 1) * SEQ, :], self_mask).then_inc(mask1_loaded, 16)
            for s in range(2):
                sp.dma_start(x_tile[s][:], x_in[bass.ts(s, P), :]).then_inc(x_loaded[s], 16)
                sp.dma_start(c_tile[s][:], ctx[bass.ts(s, P), :]).then_inc(c_loaded[s], 16)
                sp.dma_start(mask2[s][:], cross_mask[bass.ts(s, P), :]).then_inc(mask2_loaded[s], 16)
                sp.sem_inc(stored[s], 16)
            prefetch(sp)

            def store(i, s):
                sp.wait_ge(y_ready[s], count(i, 1, 0))
                sp.nop()
                sp.dma_start(x_out[bass.ds(i * 2 * P + s * P, P), :], y_out[s][:]).then_inc(stored[s], 16)

            with sp.Fori(0, ROUNDS - 1) as i:
                for s in range(2):
                    sp.wait_ge(res_b_ready[s], count(i, 3, 0))
                    sp.wait_ge(xn_ready[s], count(i, 3, 0))
                    sp.nop()
                    sp.dma_start(x_tile[s][:], x_in[bass.ds(i * 2 * P + (s + 2) * P, P), :]).then_inc(x_loaded[s], 16)
                    sp.wait_ge(cT_in_psum[s], count(i, 1, 0))
                    sp.nop()
                    sp.dma_start(c_tile[s][:], ctx[bass.ds(i * 2 * P + (s + 2) * P, P), :]).then_inc(c_loaded[s], 16)
                    sp.wait_ge(s_masked[s], count(i, 2, 1))
                    sp.nop()
                    sp.dma_start(mask2[s][:], cross_mask[bass.ds(i * 2 * P + (s + 2) * P, P), :]).then_inc(mask2_loaded[s], 16)
                    store(i, s)
            for s in range(2):
                store(ROUNDS - 1, s)
            for s in range(2):
                sp.wait_ge(stored[s], 16 * (ROUNDS + 1))

        @block.gpsimd
        def _(pool):
            nc.gpsimd.memset(minus_half[:], -0.5).then_inc(set_up, 1)
            for s in range(2):
                nc.gpsimd.memset(vp[s][:], 0.0).then_inc(set_up, 1)
            pool.wait_ge(set_up, 3)
            for s in range(2):
                for e in range(2):
                    nc.gpsimd.memset(vp[s][e * SEQ:(e + 1) * SEQ, :, :, e, HEAD:HEAD + 1], 1.0).then_inc(set_up, 1)

            def inverse_deviation(i, n, s):
                pool.wait_ge(var_ready[s], count(i, 3, n))
                nc.gpsimd.tensor_tensor(rstd[s][:], var_eps[s][:], minus_half[:], ALU.pow).then_inc(rstd_ready[s], 1)

            def residual_with_bias(n, s, source, bias):
                nc.gpsimd.tensor_tensor(res_b[s][:], source[:], row[bias], ALU.add).then_inc(res_b_ready[s], 1)

            pool.wait_ge(set_up, 7)

            def norm_step(n):
                return lambda i, s: inverse_deviation(i, n, s)

            def residual(n):
                return lambda i, s: residual_with_bias(n, s, x_tile[s] if n == 0 else res[s], ("l0_b_ao", "l0_b_co", "l0_b2")[n])

            skewed(pool, LAG,
                   (norm_step(0),), (residual(0),), (), (), (), (), (), (norm_step(1), residual(1)),
                   (), (), (), (), (), (), (norm_step(2), residual(2)), (), (), ())

        @block.scalar
        def _(act):
            def normed_transposed(i, n, s):
                act.wait_ge(xT_ready[s], count(i, 3, n))
                for c in range(DC):
                    last = nc.scalar.activation(hT[s][:, c, :], ps_a[s][:, c * P:(c + 1) * P], ACT.Identity,
                                                bias=col(f"l0_ln{n + 1}_b", c), scale=col(f"l0_ln{n + 1}_s", c))
                last.then_inc(hT_ready[s], 1)

            def queries(i, a, s):
                act.wait_ge(q_in_psum[s], count(i, 2, a))
                for c in range(DC):
                    last = nc.scalar.activation(qT[s][:, c, :], ps_b[s][:, c * P:(c + 1) * P], ACT.Identity,
                                                bias=col(f"l0_bq{a}", c), scale=1.0)
                last.then_inc(q_ready[s], 1)

            def values(i, a, s):
                act.wait_ge(v_in_psum[s], count(i, 2, a))
                for e in range(2):
                    half = slice(e * SEQ, (e + 1) * SEQ)
                    last = nc.scalar.activation(
                        vp[s][half, :, :, e, 0:HEAD],
                        ps_b[s][half, DIM:2 * DIM].rearrange("k (b h d) -> k b h d", b=PER_TILE, h=PAIRS), ACT.Copy)
                last.then_inc(v_ready[s], 1)

            def exponentials(i, a, s):
                act.wait_ge(shifted[s], count(i, 2, a))
                nc.scalar.activation(probs[s][:], probs[s][:], ACT.Exp).then_inc(p_ready[s], 1)

            def probs_transposed(i, a, s):
                act.wait_ge(pT_in_psum[s], count(i, 4, 2 * a))
                nc.scalar.activation(pT[s][:, 0:PAIRS // 2, :], ps_a[s][:].rearrange("k (h q) -> k h q", q=P),
                                     ACT.Copy).then_inc(pT_lo_ready[s], 1)

            def attended_transposed(i, a, s):
                act.wait_ge(aT_in_psum[s], count(i, 2, a))
                for c in range(DC):
                    last = nc.scalar.activation(aT[s][:, c, :], ps_b[s][:, c * P:(c + 1) * P], ACT.Identity,
                                                bias=col(f"l0_bv{a}", c), scale=1.0)
                last.then_inc(aT_ready[s], 1)

            def hidden(i, s):
                for half, bank in enumerate((ps_a[s], ps_b[s])):
                    act.wait_ge(hid_in_psum[s], count(i, 2, half))
                    for c in range(HC // 2):
                        h = half * (HC // 2) + c
                        last = nc.scalar.activation(hidT[s][:, h, :], bank[:, c * P:(c + 1) * P], ACT.Gelu_apprx_tanh,
                                                    bias=col("l0_b1", h), scale=1.0)
                    last.then_inc(hid_ready[s], 1)

            act.wait_ge(set_up, 7)

            def attention(a):
                of = lambda step: lambda i, s: step(i, a, s)
                return (tuple(map(of, steps)) for steps in (
                    (normed_transposed,), (queries,), (values, exponentials), (probs_transposed,), (), (attended_transposed,), ()))

            skewed(act, LAG,
                   (), *attention(0), *attention(1), (lambda i, s: normed_transposed(i, 2, s),), (hidden,), ())

        @block.vector
        def _(dve):
            links = Links(vector_step, dve, VECTOR_LINKS)

            def layer_norm(i, n, s, source):
                links.mark(nc.vector.bn_stats(stats[s][:], source[:]))
                links.wait(i)
                nc.vector.memset(pad[s][:], 0.0)
                links.mark(nc.vector.bn_aggr(mean_var[s][:], stats[s][:]))
                links.wait(i)
                nc.vector.tensor_scalar(var_eps[s][:], mean_var[s][:, 1:2], LN_EPS, None, ALU.add).then_inc(var_ready[s], 1)
                dve.wait_ge(rstd_ready[s], count(i, 3, n))
                nc.vector.tensor_scalar(xn[s][:], source[:], mean_var[s][:, 0:1], rstd[s][:], ALU.subtract, ALU.mult
                                        ).then_inc(xn_ready[s], 1)

            def context_transposed(i, s):
                dve.wait_ge(cT_in_psum[s], count(i, 1, 0))
                nc.vector.tensor_copy(cT[s][:], ps_b[s][:, 0:DIM].rearrange("f (c t) -> f c t", c=DC)
                                      ).then_inc(cT_ready[s], 1)

            def keys(i, a, s):
                dve.wait_ge(k_in_psum[s], count(i, 2, a))
                for c in range(DC):
                    for e in range(2):
                        last = nc.vector.tensor_scalar(kT[s][:, c, e, :], ps_a[s][:, c * P:(c + 1) * P],
                                                       col(f"l0_bk{a}", c), parity[:, e:e + 1], ALU.add, ALU.mult)
                last.then_inc(k_ready[s], 1)

            def mask_scores(i, a, s):
                mask, bias = (mask1, bias1) if a == 0 else (mask2[s], bias2[s])
                if a == 1:
                    dve.wait_ge(mask2_loaded[s], count(i, 1, 0) * 16)
                    links.mark(nc.vector.tensor_scalar(bias[:], mask[:], 1.0, MASKED, ALU.subtract, ALU.mult))
                dve.wait_ge(s_in_psum[s], count(i, 2, a))
                for g in range(4):
                    last = nc.vector.scalar_tensor_tensor(
                        out=probs[s][:, g, :, :], in0=ps_s[:, g, 0:2 * DC * SEQ].rearrange("q (h k) -> q h k", k=SEQ),
                        scalar=scale, in1=mask[:].unsqueeze(1).to_broadcast([P, 2 * DC, SEQ]),
                        op0=ALU.mult, op1=ALU.mult)
                last.then_inc(s_masked[s], 1)
                dve.wait_ge(s_masked[s], count(i, 2, a))
                dve.sem_inc(scores_read, 1)

            def shift_scores(i, a, s):
                bias = bias1 if a == 0 else bias2[s]
                dve.wait_ge(s_masked[s], count(i, 2, a))
                flat = probs[s][:].rearrange("q g h k -> q (g h) k")
                links.wait(i)
                links.mark(nc.vector.tensor_tensor(flat, flat, bias[:].unsqueeze(1).to_broadcast([P, HEADS, SEQ]), ALU.add))
                links.wait(i)
                links.mark(nc.vector.tensor_reduce(row_max[s][:], flat, AX.X, ALU.max))
                links.wait(i)
                nc.vector.tensor_tensor(flat, flat, row_max[s][:].unsqueeze(2).to_broadcast([P, HEADS, SEQ]),
                                        ALU.subtract).then_inc(shifted[s], 1)

            def probs_transposed(i, a, s):
                dve.wait_ge(pT_in_psum[s], count(i, 4, 2 * a + 1))
                nc.vector.tensor_copy(pT[s][:, PAIRS // 2:, :], ps_b[s][:].rearrange("k (h q) -> k h q", q=P)
                                      ).then_inc(pT_hi_ready[s], 1)

            def normalise(i, a, s):
                dve.wait_ge(o_in_psum[s], count(i, 2, a))
                o = ps_a[s][:, 0:HEADS * (HEAD + 1)].rearrange("q (h d) -> q h d", d=HEAD + 1)
                links.mark(nc.vector.reciprocal(inv_sum[s][:].unsqueeze(2), o[:, :, HEAD:HEAD + 1]))
                links.wait(i)
                nc.vector.tensor_tensor(att[s][:].rearrange("q (h d) -> q h d", d=HEAD), o[:, :, 0:HEAD],
                                        inv_sum[s][:].unsqueeze(2).to_broadcast([P, HEADS, HEAD]), ALU.mult
                                        ).then_inc(att_ready[s], 1)

            def add_residual(i, n, s):
                dve.wait_ge(y_in_psum[s], count(i, 3, n))
                dve.wait_ge(res_b_ready[s], count(i, 3, n))
                y = ps_a[s][:, 0:DIM]
                if n < 2:
                    nc.vector.tensor_tensor(res[s][:], y, res_b[s][:], ALU.add).then_inc(res_ready[s], 1)
                    dve.wait_ge(res_ready[s], count(i, 2, n))
                else:
                    dve.wait_ge(stored[s], (i + 1) * 16)
                    nc.vector.tensor_tensor(y_out[s][:], y, res_b[s][:], ALU.add).then_inc(y_ready[s], 1)

            for b in range(1):
                dve.wait_ge(mask1_loaded, 16 * PER_TILE)
                nc.vector.tensor_scalar(bias1[:], mask1[:], 1.0, MASKED, ALU.subtract, ALU.mult).then_inc(vector_set_up, 1)
                dve.wait_ge(vector_set_up, 1)

            def first_norm(i, s):
                dve.wait_ge(x_loaded[s], count(i, 1, 0) * 16)
                layer_norm(i, 0, s, x_tile[s])

            def attention(a):
                def residual_and_norm(i, a, s):
                    add_residual(i, a, s)
                    layer_norm(i, a + 1, s, res[s])

                of = lambda step: lambda i, s: step(i, a, s)
                return (tuple(map(of, steps)) for steps in (
                    (keys,), (mask_scores, shift_scores), (probs_transposed,), (normalise,), (), (residual_and_norm,)))

            skewed(dve, LAG,
                   (first_norm,), (context_transposed,), *attention(0), (), *attention(1),
                   (), (), (lambda i, s: add_residual(i, 2, s),), links=links)

        @block.tensor
        def _(pe):
            def normed(i, n, s):
                pe.wait_ge(xn_ready[s], count(i, 3, n))
                for c in range(DC):
                    last = nc.tensor.transpose(ps_a[s][:, c * P:(c + 1) * P], xn[s][:, c * P:(c + 1) * P], ident)
                last.then_inc(xT_ready[s], 1)

            def context(i, s):
                pe.wait_ge(c_loaded[s], count(i, 1, 0) * 16)
                for c in range(DC):
                    last = nc.tensor.transpose(ps_b[s][:, c * P:(c + 1) * P], c_tile[s][:, c * P:(c + 1) * P], ident)
                last.then_inc(cT_in_psum[s], 1)

            def project(i, a, s):
                def transposed(bank, weights, moving):
                    for c in range(DC):
                        for k in range(DC):
                            last = nc.tensor.matmul(bank[:, c * P:(c + 1) * P], weights[:, k, c * P:(c + 1) * P],
                                                    moving[:, k, :], start=(k == 0), stop=(k == DC - 1))
                    return last

                source = hT[s] if a == 0 else cT[s]
                pe.wait_ge(hT_ready[s], count(i, 3, a))
                transposed(ps_a[s], wk[a], source).then_inc(k_in_psum[s], 1)
                if a == 0:
                    pe.wait_ge(cT_ready[s], count(i, 1, 0))
                transposed(ps_b[s], wq[a], hT[s]).then_inc(q_in_psum[s], 1)

            def values(i, a, s):
                source = hT[s] if a == 0 else cT[s]
                for b in range(PER_TILE):
                    for e in range(2):
                        for k in range(DC):
                            last = nc.tensor.matmul(
                                ps_b[s][e * SEQ:(e + 1) * SEQ, DIM + b * P:DIM + (b + 1) * P],
                                source[:, k, b * SEQ:(b + 1) * SEQ],
                                wv[a][:, k, :].rearrange("f (h e d) -> f h e d", e=2, d=HEAD)[:, :, e, :],
                                start=(k == 0), stop=(k == DC - 1))
                last.then_inc(v_in_psum[s], 1)

            def scores(i, a, s):
                pe.wait_ge(q_ready[s], count(i, 2, a))
                pe.wait_ge(k_ready[s], count(i, 2, a))
                if scores_done.n:
                    scores_done.wait(i)
                scores_done.n += 1
                for g in range(4):
                    rows = slice(32 * g, 32 * g + 32)
                    for c in range(DC):
                        for b in range(PER_TILE):
                            last = nc.tensor.matmul(ps_s[b * SEQ:(b + 1) * SEQ, g, c * P:(c + 1) * P],
                                                    qT[s][rows, c, b * SEQ:(b + 1) * SEQ],
                                                    kT[s][rows, c, :, b * SEQ:(b + 1) * SEQ], start=True, stop=True)
                last.then_inc(s_in_psum[s], 1)

            def transpose_probs(i, a, s):
                pe.wait_ge(p_ready[s], count(i, 2, a))
                pe.wait_ge(v_ready[s], count(i, 2, a))
                for half, bank in enumerate((ps_a[s], ps_b[s])):
                    for j in range(PAIRS // 2):
                        g, c = divmod(half * (PAIRS // 2) + j, DC)
                        last = nc.tensor.transpose(bank[:, j * P:(j + 1) * P],
                                                   probs[s][:, g, 2 * c:2 * c + 2, :], ident)
                    last.then_inc(pT_in_psum[s], 1)

            def attend(i, a, s):
                pe.wait_ge(pT_lo_ready[s], count(i, 2, a))
                pe.wait_ge(pT_hi_ready[s], count(i, 2, a))
                wide = 2 * (HEAD + 1)
                for j in range(PAIRS):
                    g, c = divmod(j, DC)
                    pair = 4 * c + g
                    for b in range(PER_TILE):
                        last = nc.tensor.matmul(ps_a[s][b * SEQ:(b + 1) * SEQ, pair * wide:(pair + 1) * wide],
                                                pT[s][:, j, b * SEQ:(b + 1) * SEQ], vp[s][:, b, pair, :, :],
                                                start=True, stop=True)
                last.then_inc(o_in_psum[s], 1)

            def transpose_attended(i, a, s):
                pe.wait_ge(att_ready[s], count(i, 2, a))
                for c in range(DC):
                    last = nc.tensor.transpose(ps_b[s][:, c * P:(c + 1) * P], att[s][:, c * P:(c + 1) * P], ident)
                last.then_inc(aT_in_psum[s], 1)

            def project_out(i, a, s):
                pe.wait_ge(*weights_in)
                pe.wait_ge(aT_ready[s], count(i, 2, a))
                for k in range(DC):
                    last = nc.tensor.matmul(ps_a[s][:, 0:DIM], aT[s][:, k, :], wo[a][:, k, :],
                                            start=(k == 0), stop=(k == DC - 1))
                last.then_inc(y_in_psum[s], 1)

            def mlp_up(i, s):
                pe.wait_ge(hT_ready[s], count(i, 3, 2))
                for half, bank in enumerate((ps_a[s], ps_b[s])):
                    for c in range(HC // 2):
                        h = half * (HC // 2) + c
                        for k in range(DC):
                            last = nc.tensor.matmul(bank[:, c * P:(c + 1) * P], w1[:, k, h * P:(h + 1) * P], hT[s][:, k, :],
                                                    start=(k == 0), stop=(k == DC - 1))
                    last.then_inc(hid_in_psum[s], 1)

            def mlp_down(i, s):
                for half in range(2):
                    pe.wait_ge(hid_ready[s], count(i, 2, half))
                    for c in range(HC // 2):
                        h = half * (HC // 2) + c
                        last = nc.tensor.matmul(ps_a[s][:, 0:DIM], hidT[s][:, h, :], w2[:, h, :],
                                                start=(h == 0), stop=(h == HC - 1))
                last.then_inc(y_in_psum[s], 1)

            scores_done = Links(scores_read, pe, 4)
            pe.wait_ge(set_up, 7)

            def attention(a):
                of = lambda step: lambda i, s: step(i, a, s)
                return (tuple(map(of, steps)) for steps in (
                    (project,), (scores, values), (transpose_probs,), (attend,), (transpose_attended,), (project_out,)))

            skewed(pe, LAG,
                   (), (lambda i, s: normed(i, 0, s), context), *attention(0), (lambda i, s: normed(i, 1, s),), *attention(1),
                   (lambda i, s: normed(i, 2, s),), (mlp_up,), (mlp_down,), links=scores_done)

        running.close()
        cleared(nc, semaphores)


def resampler_layer(nc, x_in, ctx, key_mask, x_out, w, col, row, ident, parity):
    with ExitStack() as held:
        semaphores, running = [], ExitStack()

        def sb(name, shape, dtype=F32):
            return held.enter_context(nc.sbuf_tensor("l1_" + name, shape, dtype))

        def sem(name):
            semaphores.append(held.enter_context(nc.semaphore("l1_" + name)))
            return semaphores[-1]

        x_tile = [sb(f"x_tile{s}", [P, DIM]) for s in range(2)]
        c_tile = [sb(f"c_tile{s}", [P, DIM]) for s in range(2)]
        mask = [sb(f"mask{s}", [P, SEQ], I32) for s in range(2)]
        bias = [sb(f"bias{s}", [P, 2 * SEQ]) for s in range(2)]
        stats = [sb(f"stats{s}", [P, 6]) for s in range(2)]
        mean_var = [sb(f"mean_var{s}", [P, 2]) for s in range(2)]
        var_eps = [sb(f"var_eps{s}", [P, 1]) for s in range(2)]
        rstd = [sb(f"rstd{s}", [P, 1]) for s in range(2)]
        pad = [sb(f"pad{s}", [P, 1]) for s in range(2)]
        minus_half = sb("minus_half", [P, 1])
        xn = [sb(f"xn{s}", [P, DIM]) for s in range(2)]
        mean_square = [sb(f"mean_square{s}", [P, 1]) for s in range(2)]
        hT = [sb(f"hT{s}", [P, DC, P]) for s in range(2)]
        srcT = [sb(f"srcT{s}", [P, DC, PER_TILE, 2, SEQ]) for s in range(2)]
        qT = [sb(f"qT{s}", [P, DC, P]) for s in range(2)]
        kT = [sb(f"kT{s}", [P, DC, 2, 2 * P]) for s in range(2)]
        v = [sb(f"v{s}", [P, PER_TILE, HEADS, HEAD + 1]) for s in range(2)]
        probs = [sb(f"probs{s}", [P, 4, 2 * DC, 2 * SEQ]) for s in range(2)]
        row_max = [sb(f"row_max{s}", [P, HEADS]) for s in range(2)]
        pT = [sb(f"pT{s}", [P, HEADS, P]) for s in range(2)]
        inv_sum = [sb(f"inv_sum{s}", [P, HEADS]) for s in range(2)]
        att = [sb(f"att{s}", [P, DIM]) for s in range(2)]
        aT = [sb(f"aT{s}", [P, DC, P]) for s in range(2)]
        res = [sb(f"res{s}", [P, DIM]) for s in range(2)]
        res_b = [sb(f"res_b{s}", [P, DIM]) for s in range(2)]
        final_b = [sb(f"final_b{s}", [P, DIM]) for s in range(2)]
        hidT = [sb(f"hidT{s}", [P, HC, P]) for s in range(2)]
        y_out = [sb(f"y_out{s}", [P, DIM]) for s in range(2)]
        ps_s = held.enter_context(nc.psum_tensor("l1_ps_s", [P, 4, BANK], F32))
        ps_a = [held.enter_context(nc.psum_tensor(f"l1_ps_a{s}", [P, BANK], F32)) for s in range(2)]
        ps_b = [held.enter_context(nc.psum_tensor(f"l1_ps_b{s}", [P, BANK], F32)) for s in range(2)]

        x_loaded = [sem(f"x_loaded{s}") for s in range(2)]
        c_loaded = [sem(f"c_loaded{s}") for s in range(2)]
        mask_loaded = [sem(f"mask_loaded{s}") for s in range(2)]
        stored = [sem(f"stored{s}") for s in range(2)]
        set_up = sem("set_up")
        scores_read = sem("scores_read")
        vector_step = sem("vector_step")
        var_ready = [sem(f"var_ready{s}") for s in range(2)]
        rstd_ready = [sem(f"rstd_ready{s}") for s in range(2)]
        xn_ready = [sem(f"xn_ready{s}") for s in range(2)]
        xT_ready = [sem(f"xT_ready{s}") for s in range(2)]
        hT_ready = [sem(f"hT_ready{s}") for s in range(2)]
        lT_in_psum = [sem(f"lT_in_psum{s}") for s in range(2)]
        lT_ready = [sem(f"lT_ready{s}") for s in range(2)]
        cT_in_psum = [sem(f"cT_in_psum{s}") for s in range(2)]
        cT_ready = [sem(f"cT_ready{s}") for s in range(2)]
        k_in_psum = [sem(f"k_in_psum{s}") for s in range(2)]
        q_in_psum = [sem(f"q_in_psum{s}") for s in range(2)]
        v_in_psum = [sem(f"v_in_psum{s}") for s in range(2)]
        q_ready = [sem(f"q_ready{s}") for s in range(2)]
        k_ready = [sem(f"k_ready{s}") for s in range(2)]
        v_ready = [sem(f"v_ready{s}") for s in range(2)]
        s_in_psum = [sem(f"s_in_psum{s}") for s in range(2)]
        bias_ready = [sem(f"bias_ready{s}") for s in range(2)]
        s_masked = [sem(f"s_masked{s}") for s in range(2)]
        shifted = [sem(f"shifted{s}") for s in range(2)]
        p_ready = [sem(f"p_ready{s}") for s in range(2)]
        pT_in_psum = [sem(f"pT_in_psum{s}") for s in range(2)]
        pT_lo_ready = [sem(f"pT_lo_ready{s}") for s in range(2)]
        pT_hi_ready = [sem(f"pT_hi_ready{s}") for s in range(2)]
        o_in_psum = [sem(f"o_in_psum{s}") for s in range(2)]
        att_ready = [sem(f"att_ready{s}") for s in range(2)]
        aT_in_psum = [sem(f"aT_in_psum{s}") for s in range(2)]
        aT_ready = [sem(f"aT_ready{s}") for s in range(2)]
        y_in_psum = [sem(f"y_in_psum{s}") for s in range(2)]
        res_ready = [sem(f"res_ready{s}") for s in range(2)]
        res_b_ready = [sem(f"res_b_ready{s}") for s in range(2)]
        final_b_ready = [sem(f"final_b_ready{s}") for s in range(2)]
        y_ready = [sem(f"y_ready{s}") for s in range(2)]
        hid_in_psum = [sem(f"hid_in_psum{s}") for s in range(2)]
        hid_ready = [sem(f"hid_ready{s}") for s in range(2)]

        wq, wk, wv, wo = w["l1_q_w"], w["l1_k_w"], w["l1_v_w"], w["l1_out_w"]
        w1, w2 = w["l1_mlp_w1"], w["l1_mlp_w2"]
        scale = 1.0 / HEAD
        VECTOR_LINKS = 10
        LAG = 2

        block = running.enter_context(nc.Block())

        @block.sync
        def _(sp):
            def load_mask(i, t, s):
                for b in range(PER_TILE):
                    sp.dma_start(mask[s][b * SEQ:(b + 1) * SEQ, :],
                                 key_mask[bass.ds(i * 2 * PER_TILE + t * PER_TILE + b, 1), :].partition_broadcast(SEQ)
                                 ).then_inc(mask_loaded[s], 16)

            for s in range(2):
                sp.dma_start(x_tile[s][:], x_in[bass.ts(s, P), :]).then_inc(x_loaded[s], 16)
                sp.dma_start(c_tile[s][:], ctx[bass.ts(s, P), :]).then_inc(c_loaded[s], 16)
                load_mask(0, s, s)
                sp.sem_inc(stored[s], 16)

            def store(i, s):
                sp.wait_ge(y_ready[s], count(i, 1, 0))
                sp.nop()
                sp.dma_start(x_out[bass.ds(i * 2 * P + s * P, P), :], y_out[s][:]).then_inc(stored[s], 16)

            with sp.Fori(0, ROUNDS - 1) as i:
                for s in range(2):
                    sp.wait_ge(final_b_ready[s], count(i, 1, 0))
                    sp.wait_ge(lT_in_psum[s], count(i, 1, 0))
                    sp.nop()
                    sp.dma_start(x_tile[s][:], x_in[bass.ds(i * 2 * P + (s + 2) * P, P), :]).then_inc(x_loaded[s], 16)
                    sp.wait_ge(cT_in_psum[s], count(i, 1, 0))
                    sp.nop()
                    sp.dma_start(c_tile[s][:], ctx[bass.ds(i * 2 * P + (s + 2) * P, P), :]).then_inc(c_loaded[s], 16)
                    sp.wait_ge(s_masked[s], count(i, 1, 0))
                    sp.nop()
                    load_mask(i, s + 2, s)
                    store(i, s)
            for s in range(2):
                store(ROUNDS - 1, s)
            for s in range(2):
                sp.wait_ge(stored[s], 16 * (ROUNDS + 1))

        @block.gpsimd
        def _(pool):
            nc.gpsimd.memset(minus_half[:], -0.5).then_inc(set_up, 1)
            for s in range(2):
                nc.gpsimd.memset(v[s][:, :, :, HEAD:HEAD + 1], 1.0).then_inc(set_up, 1)
                nc.gpsimd.memset(bias[s][:, SEQ:], 0.0).then_inc(set_up, 1)

            pool.wait_ge(set_up, 5)

            def residuals(i, s):
                pool.wait_ge(bias_ready[s], count(i, 1, 0))
                pool.wait_ge(x_loaded[s], count(i, 1, 0) * 16)
                nc.gpsimd.tensor_tensor(res_b[s][:], x_tile[s][:], row["l1_out_b"], ALU.add).then_inc(res_b_ready[s], 1)
                nc.gpsimd.tensor_tensor(final_b[s][:], x_tile[s][:], row["l1_mlp_b2"], ALU.add).then_inc(final_b_ready[s], 1)

            def inverse_root(i, s):
                pool.wait_ge(var_ready[s], count(i, 1, 0))
                nc.gpsimd.tensor_tensor(rstd[s][:], var_eps[s][:], minus_half[:], ALU.pow).then_inc(rstd_ready[s], 1)

            skewed(pool, LAG, (residuals,), (), (), (), (), (), (inverse_root,), (), (), ())

        @block.scalar
        def _(act):
            def latents_transposed(i, s):
                act.wait_ge(lT_in_psum[s], count(i, 1, 0))
                nc.scalar.activation(srcT[s][:, :, :, 1, :].rearrange("f c b t -> f (c b) t"),
                                     ps_a[s][:, 0:DIM].rearrange("f (m t) -> f m t", t=SEQ), ACT.Copy).then_inc(lT_ready[s], 1)

            def normed_transposed(i, s):
                act.wait_ge(xT_ready[s], count(i, 1, 0))
                for c in range(DC):
                    last = nc.scalar.activation(hT[s][:, c, :], ps_a[s][:, c * P:(c + 1) * P], ACT.Identity,
                                                bias=0.0, scale=col("l1_postnorm_w", c))
                last.then_inc(hT_ready[s], 1)

            def queries(i, s):
                act.wait_ge(q_in_psum[s], count(i, 1, 0))
                for c in range(DC):
                    last = nc.scalar.activation(qT[s][:, c, :], ps_b[s][:, c * P:(c + 1) * P], ACT.Identity,
                                                bias=col("l1_bq", c), scale=1.0)
                last.then_inc(q_ready[s], 1)

            def values(i, s):
                act.wait_ge(v_in_psum[s], count(i, 1, 0))
                nc.scalar.activation(v[s][:, :, :, 0:HEAD].rearrange("k b h d -> k (b h) d"),
                                     ps_b[s][:].rearrange("k (m d) -> k m d", d=HEAD), ACT.Copy).then_inc(v_ready[s], 1)

            def exponentials(i, s):
                act.wait_ge(shifted[s], count(i, 1, 0))
                nc.scalar.activation(probs[s][:], probs[s][:], ACT.Exp).then_inc(p_ready[s], 1)

            def probs_transposed(i, s):
                for half in range(2):
                    act.wait_ge(pT_in_psum[s], count(i, 4, 2 * half))
                    nc.scalar.activation(pT[s][:, 8 * half:8 * half + 4, :], ps_a[s][:].rearrange("k (h q) -> k h q", q=P),
                                         ACT.Copy).then_inc(pT_lo_ready[s], 1)

            def attended_transposed(i, s):
                act.wait_ge(aT_in_psum[s], count(i, 1, 0))
                for c in range(DC):
                    last = nc.scalar.activation(aT[s][:, c, :], ps_b[s][:, c * P:(c + 1) * P], ACT.Identity,
                                                bias=col("l1_bv", c), scale=1.0)
                last.then_inc(aT_ready[s], 1)

            def hidden(i, s):
                for half, bank in enumerate((ps_a[s], ps_b[s])):
                    act.wait_ge(hid_in_psum[s], count(i, 2, half))
                    for c in range(HC // 2):
                        h = half * (HC // 2) + c
                        last = nc.scalar.activation(hidT[s][:, h, :], bank[:, c * P:(c + 1) * P], ACT.Gelu_apprx_tanh,
                                                    bias=col("l1_b1", h), scale=1.0)
                    last.then_inc(hid_ready[s], 1)

            act.wait_ge(set_up, 5)
            skewed(act, LAG, (latents_transposed,), (queries,), (values, exponentials), (probs_transposed,), (),
                   (attended_transposed,), (), (normed_transposed,), (hidden,), ())

        @block.vector
        def _(dve):
            links = Links(vector_step, dve, VECTOR_LINKS)

            def rms_norm(i, s):
                links.mark(nc.vector.bn_stats(stats[s][:], res[s][:]))
                links.wait(i)
                nc.vector.memset(pad[s][:], 0.0)
                links.mark(nc.vector.bn_aggr(mean_var[s][:], stats[s][:]))
                links.wait(i)
                links.mark(nc.vector.scalar_tensor_tensor(out=mean_square[s][:], in0=mean_var[s][:, 0:1],
                                                          scalar=mean_var[s][:, 0:1], in1=mean_var[s][:, 1:2],
                                                          op0=ALU.mult, op1=ALU.add))
                links.wait(i)
                nc.vector.tensor_scalar(var_eps[s][:], mean_square[s][:], RMS_EPS, None, ALU.add).then_inc(var_ready[s], 1)
                dve.wait_ge(rstd_ready[s], count(i, 1, 0))
                nc.vector.tensor_scalar(xn[s][:], res[s][:], rstd[s][:], None, ALU.mult).then_inc(xn_ready[s], 1)

            def context_transposed(i, s):
                dve.wait_ge(cT_in_psum[s], count(i, 1, 0))
                nc.vector.tensor_copy(srcT[s][:, :, :, 0, :].rearrange("f c b t -> f (c b) t"),
                                      ps_b[s][:, 0:DIM].rearrange("f (m t) -> f m t", t=SEQ)).then_inc(cT_ready[s], 1)

            def keys(i, s):
                dve.wait_ge(k_in_psum[s], count(i, 1, 0))
                for c in range(DC):
                    for e in range(2):
                        last = nc.vector.tensor_scalar(kT[s][:, c, e, :], ps_a[s][:, c * 2 * P:(c + 1) * 2 * P],
                                                       col("l1_bk", c), parity[:, e:e + 1], ALU.add, ALU.mult)
                last.then_inc(k_ready[s], 1)

            def mask_bias(i, s):
                dve.wait_ge(mask_loaded[s], count(i, 1, 0) * 16 * PER_TILE)
                nc.vector.tensor_scalar(bias[s][:, 0:SEQ], mask[s][:], 0.0, MINUS_INF, ALU.is_equal, ALU.mult).then_inc(bias_ready[s], 1)

            def mask_scores(i, s):
                dve.wait_ge(bias_ready[s], count(i, 1, 0))
                dve.wait_ge(s_in_psum[s], count(i, 1, 0))
                for g in range(4):
                    last = nc.vector.scalar_tensor_tensor(
                        out=probs[s][:, g, :, :], in0=ps_s[:, g, :].rearrange("q (h k) -> q h k", k=2 * SEQ),
                        scalar=scale, in1=bias[s][:].unsqueeze(1).to_broadcast([P, 2 * DC, 2 * SEQ]),
                        op0=ALU.mult, op1=ALU.add)
                last.then_inc(s_masked[s], 1)
                dve.wait_ge(s_masked[s], count(i, 1, 0))
                dve.sem_inc(scores_read, 1)

            def shift_scores(i, s):
                dve.wait_ge(s_masked[s], count(i, 1, 0))
                flat = probs[s][:].rearrange("q g h k -> q (g h) k")
                links.mark(nc.vector.tensor_reduce(row_max[s][:], flat, AX.X, ALU.max))
                links.wait(i)
                nc.vector.tensor_tensor(flat, flat, row_max[s][:].unsqueeze(2).to_broadcast([P, HEADS, 2 * SEQ]),
                                        ALU.subtract).then_inc(shifted[s], 1)

            def probs_transposed(i, s):
                for half in range(2):
                    dve.wait_ge(pT_in_psum[s], count(i, 4, 2 * half + 1))
                    nc.vector.tensor_copy(pT[s][:, 8 * half + 4:8 * half + 8, :], ps_b[s][:].rearrange("k (h q) -> k h q", q=P)
                                          ).then_inc(pT_hi_ready[s], 1)

            def normalise(i, s):
                dve.wait_ge(o_in_psum[s], count(i, 1, 0))
                o = ps_a[s][:, 0:HEADS * (HEAD + 1)].rearrange("q (h d) -> q h d", d=HEAD + 1)
                links.mark(nc.vector.reciprocal(inv_sum[s][:].unsqueeze(2), o[:, :, HEAD:HEAD + 1]))
                links.wait(i)
                nc.vector.tensor_tensor(att[s][:].rearrange("q (h d) -> q h d", d=HEAD), o[:, :, 0:HEAD],
                                        inv_sum[s][:].unsqueeze(2).to_broadcast([P, HEADS, HEAD]), ALU.mult
                                        ).then_inc(att_ready[s], 1)

            def add_residual(i, n, s):
                dve.wait_ge(y_in_psum[s], count(i, 2, n))
                y = ps_a[s][:, 0:DIM]
                if n == 0:
                    dve.wait_ge(res_b_ready[s], count(i, 1, 0))
                    nc.vector.tensor_tensor(res[s][:], y, res_b[s][:], ALU.add).then_inc(res_ready[s], 1)
                    dve.wait_ge(res_ready[s], count(i, 1, 0))
                else:
                    dve.wait_ge(final_b_ready[s], count(i, 1, 0))
                    dve.wait_ge(stored[s], (i + 1) * 16)
                    nc.vector.tensor_tensor(y_out[s][:], y, final_b[s][:], ALU.add).then_inc(y_ready[s], 1)

            dve.wait_ge(set_up, 5)
            skewed(dve, LAG, (mask_bias, context_transposed), (keys,), (mask_scores, shift_scores), (probs_transposed,),
                   (normalise,), (), (lambda i, s: add_residual(i, 0, s), rms_norm), (), (),
                   (lambda i, s: add_residual(i, 1, s),), links=links)

        @block.tensor
        def _(pe):
            def latents(i, s):
                pe.wait_ge(bias_ready[s], count(i, 1, 0))
                pe.wait_ge(x_loaded[s], count(i, 1, 0) * 16)
                for c in range(DC):
                    last = nc.tensor.transpose(ps_a[s][:, c * P:(c + 1) * P], x_tile[s][:, c * P:(c + 1) * P], ident)
                last.then_inc(lT_in_psum[s], 1)

            def normed(i, s):
                pe.wait_ge(xn_ready[s], count(i, 1, 0))
                for c in range(DC):
                    last = nc.tensor.transpose(ps_a[s][:, c * P:(c + 1) * P], xn[s][:, c * P:(c + 1) * P], ident)
                last.then_inc(xT_ready[s], 1)

            def context(i, s):
                pe.wait_ge(c_loaded[s], count(i, 1, 0) * 16)
                for c in range(DC):
                    last = nc.tensor.transpose(ps_b[s][:, c * P:(c + 1) * P], c_tile[s][:, c * P:(c + 1) * P], ident)
                last.then_inc(cT_in_psum[s], 1)

            def project(i, s):
                pe.wait_ge(cT_ready[s], count(i, 1, 0))
                pe.wait_ge(lT_ready[s], count(i, 1, 0))
                for c in range(DC):
                    for k in range(DC):
                        last = nc.tensor.matmul(ps_a[s][:, c * 2 * P:(c + 1) * 2 * P], wk[:, k, c * P:(c + 1) * P],
                                                srcT[s][:, k].rearrange("f b m t -> f (b m t)"),
                                                start=(k == 0), stop=(k == DC - 1))
                last.then_inc(k_in_psum[s], 1)
                for c in range(DC):
                    for k in range(DC):
                        last = nc.tensor.matmul(ps_b[s][:, c * P:(c + 1) * P], wq[:, k, c * P:(c + 1) * P],
                                                srcT[s][:, k, :, 1, :], start=(k == 0), stop=(k == DC - 1))
                last.then_inc(q_in_psum[s], 1)

            def values(i, s):
                for b in range(PER_TILE):
                    for k in range(DC):
                        last = nc.tensor.matmul(ps_b[s][:, b * DIM:(b + 1) * DIM],
                                                srcT[s][:, k, b].rearrange("f m t -> f (m t)"), wv[:, k, :],
                                                start=(k == 0), stop=(k == DC - 1))
                last.then_inc(v_in_psum[s], 1)

            def scores(i, s):
                pe.wait_ge(q_ready[s], count(i, 1, 0))
                pe.wait_ge(k_ready[s], count(i, 1, 0))
                if scores_done.n:
                    scores_done.wait(i)
                scores_done.n += 1
                for g in range(4):
                    rows = slice(32 * g, 32 * g + 32)
                    for c in range(DC):
                        for b in range(PER_TILE):
                            last = nc.tensor.matmul(ps_s[b * SEQ:(b + 1) * SEQ, g, c * 2 * P:(c + 1) * 2 * P],
                                                    qT[s][rows, c, b * SEQ:(b + 1) * SEQ],
                                                    kT[s][rows, c, :, b * 2 * SEQ:(b + 1) * 2 * SEQ], start=True, stop=True)
                last.then_inc(s_in_psum[s], 1)

            def transpose_probs(i, s):
                pe.wait_ge(p_ready[s], count(i, 1, 0))
                pe.wait_ge(v_ready[s], count(i, 1, 0))
                for quarter in range(4):
                    bank = (ps_a, ps_b)[quarter % 2][s]
                    if quarter >= 2:
                        pe.wait_ge((pT_lo_ready, pT_hi_ready)[quarter % 2][s], count(i, 2, 0))
                    for j in range(4):
                        last = nc.tensor.transpose(bank[:, j * P:(j + 1) * P], probs[s][:, quarter, j, :], ident)
                    last.then_inc(pT_in_psum[s], 1)

            def attend(i, s):
                pe.wait_ge(pT_lo_ready[s], count(i, 2, 1))
                pe.wait_ge(pT_hi_ready[s], count(i, 2, 1))
                wide = HEAD + 1
                for g in range(4):
                    for j in range(2 * DC):
                        head = (j // 2) * PAIRS + 2 * g + j % 2
                        for b in range(PER_TILE):
                            last = nc.tensor.matmul(ps_a[s][b * SEQ:(b + 1) * SEQ, head * wide:(head + 1) * wide],
                                                    pT[s][:, 4 * g + j, b * SEQ:(b + 1) * SEQ], v[s][:, b, head, :],
                                                    start=True, stop=True)
                last.then_inc(o_in_psum[s], 1)

            def transpose_attended(i, s):
                pe.wait_ge(att_ready[s], count(i, 1, 0))
                for c in range(DC):
                    last = nc.tensor.transpose(ps_b[s][:, c * P:(c + 1) * P], att[s][:, c * P:(c + 1) * P], ident)
                last.then_inc(aT_in_psum[s], 1)

            def project_out(i, s):
                pe.wait_ge(aT_ready[s], count(i, 1, 0))
                for k in range(DC):
                    last = nc.tensor.matmul(ps_a[s][:, 0:DIM], aT[s][:, k, :], wo[:, k, :],
                                            start=(k == 0), stop=(k == DC - 1))
                last.then_inc(y_in_psum[s], 1)

            def mlp_up(i, s):
                pe.wait_ge(hT_ready[s], count(i, 1, 0))
                for half, bank in enumerate((ps_a[s], ps_b[s])):
                    for c in range(HC // 2):
                        h = half * (HC // 2) + c
                        for k in range(DC):
                            last = nc.tensor.matmul(bank[:, c * P:(c + 1) * P], w1[:, k, h * P:(h + 1) * P], hT[s][:, k, :],
                                                    start=(k == 0), stop=(k == DC - 1))
                    last.then_inc(hid_in_psum[s], 1)

            def mlp_down(i, s):
                for half in range(2):
                    pe.wait_ge(hid_ready[s], count(i, 2, half))
                    for c in range(HC // 2):
                        h = half * (HC // 2) + c
                        last = nc.tensor.matmul(ps_a[s][:, 0:DIM], hidT[s][:, h, :], w2[:, h, :],
                                                start=(h == 0), stop=(h == HC - 1))
                last.then_inc(y_in_psum[s], 1)

            pe.wait_ge(set_up, 5)
            scores_done = Links(scores_read, pe, 2)
            skewed(pe, LAG, (latents, context), (project,), (scores, values), (transpose_probs,), (attend,),
                   (transpose_attended,), (project_out,), (normed,), (mlp_up,), (mlp_down,), links=scores_done)

        running.close()
        cleared(nc, semaphores)


class Normed:

    def __init__(self, nc, sb, sem, x_tile, ps_x, scale_of, bias_of, ident):
        self.nc, self.x_tile, self.ps_x, self.scale_of, self.bias_of, self.ident = nc, x_tile, ps_x, scale_of, bias_of, ident
        self.stats = [sb(f"stats{u}", [P, 6]) for u in range(2)]
        self.pad = [sb(f"pad{u}", [P, 1]) for u in range(2)]
        self.mean_var = [sb(f"mean_var{u}", [P, 2]) for u in range(2)]
        self.var_eps = [sb(f"var_eps{u}", [P, 1]) for u in range(2)]
        self.rstd = [sb(f"rstd{u}", [P, 1]) for u in range(2)]
        self.minus_half = sb("minus_half", [P, 1])
        self.xn = sb("xn", [P, 2, DIM])
        self.hT = sb("hT", [P, DC, 2 * P])
        self.x_loaded = sem("x_loaded")
        self.norm_step = sem("norm_step")
        self.var_ready = sem("var_ready")
        self.rstd_ready = sem("rstd_ready")
        self.xn_ready = sem("xn_ready")
        self.xT_in_psum = sem("xT_in_psum")
        self.hT_ready = sem("hT_ready")

    def variances(self, dve, r):
        nc = self.nc
        dve.wait_ge(self.x_loaded, count(r, 1, 0) * 16)
        for u in range(2):
            nc.vector.bn_stats(self.stats[u][:], self.x_tile[:, u, :]).then_inc(self.norm_step, 1)
        for u in range(2):
            dve.wait_ge(self.norm_step, count(r, 4, u))
            nc.vector.memset(self.pad[u][:], 0.0)
            nc.vector.bn_aggr(self.mean_var[u][:], self.stats[u][:]).then_inc(self.norm_step, 1)
        for u in range(2):
            dve.wait_ge(self.norm_step, count(r, 4, 2 + u))
            nc.vector.tensor_scalar(self.var_eps[u][:], self.mean_var[u][:, 1:2], LN_EPS, None, ALU.add
                                    ).then_inc(self.var_ready, 1)

    def inverse_deviations(self, pool, r):
        for u in range(2):
            pool.wait_ge(self.var_ready, count(r, 2, u))
            self.nc.gpsimd.tensor_tensor(self.rstd[u][:], self.var_eps[u][:], self.minus_half[:], ALU.pow
                                         ).then_inc(self.rstd_ready, 1)

    def normalised(self, dve, r):
        for u in range(2):
            dve.wait_ge(self.rstd_ready, count(r, 2, u))
            self.nc.vector.tensor_scalar(self.xn[:, u, :], self.x_tile[:, u, :], self.mean_var[u][:, 0:1], self.rstd[u][:],
                                         ALU.subtract, ALU.mult).then_inc(self.xn_ready, 1)

    def transposed(self, pe, r):
        for u in range(2):
            pe.wait_ge(self.xn_ready, count(r, 2, u))
            for c in range(DC):
                last = self.nc.tensor.transpose(self.ps_x[:, (c * 2 + u) * P:(c * 2 + u + 1) * P],
                                                self.xn[:, u, c * P:(c + 1) * P], self.ident)
        last.then_inc(self.xT_in_psum, 1)

    def scaled(self, act, r):
        act.wait_ge(self.xT_in_psum, count(r, 1, 0))
        for c in range(DC):
            last = self.nc.scalar.activation(self.hT[:, c, :], self.ps_x[:, c * 2 * P:(c + 1) * 2 * P], ACT.Identity,
                                             bias=self.bias_of(c), scale=self.scale_of(c))
        last.then_inc(self.hT_ready, 1)


def wide_attention(nc, a, x_in, ctx, x_out, w, col, row, ident, prefetch=None):
    with ExitStack() as held:
        semaphores, running = [], ExitStack()

        def sb(name, shape, dtype=F32):
            return held.enter_context(nc.sbuf_tensor(f"l2a{a}_" + name, shape, dtype))

        def sem(name):
            semaphores.append(held.enter_context(nc.semaphore(f"l2a{a}_" + name)))
            return semaphores[-1]

        def bank(name):
            return held.enter_context(nc.psum_tensor(f"l2a{a}_ps_" + name, [P, BANK], F32))

        ROUND = 2 * P
        KEYS = P + 1
        ONES = 2 * HEADS
        scale = WIDE ** -0.5
        wq, wk, wv, wo = (w[f"l2_{n}{a + 1}"] for n in ("wq", "wk", "wv", "wo"))

        x_tile = sb("x_tile", [P, 2, DIM])
        c_tile = sb("c_tile", [P, 2, DIM])
        one = sb("one", [P, 1])
        cT = sb("cT", [P, DC, ROUND])
        qT = sb("qT", [P, ROUND])
        kT = sb("kT", [P, 2, KEYS])
        v = [[sb(f"v{g}{u}", [P, 4 * WIDE]) for u in range(2)] for g in range(2)]
        other_sequence = sb("other_sequence", [P, KEYS])
        probs = [sb(f"probs{u}", [P, KEYS]) for u in range(2)]
        pad = [sb(f"carrier{u}", [P, 1]) for u in range(2)]
        row_max = [sb(f"row_max{u}", [P, 1]) for u in range(2)]
        shift = [sb(f"shift{u}", [P, 1]) for u in range(2)]
        row_sum = [sb(f"row_sum{u}", [P, 1]) for u in range(2)]
        inv_sum = [sb(f"inv_sum{u}", [P, 1]) for u in range(2)]
        learned = [sb(f"learned{u}", [P, P]) for u in range(2)]
        learnedT = sb("learnedT", [P, 2, P])
        pT = sb("pT", [P, 2, P])
        oT = sb("oT", [P, 2, P])
        res_b = sb("res_b", [P, 2, DIM])
        y_out = sb("y_out", [P, 2, DIM])
        value_gap = sb("value_gap", [P, HEADS, ONES + 1])
        gap_out = sb("gap_out", [ONES + 1, DIM])
        ps_q, ps_k, ps_v, ps_s, ps_p, ps_o, ps_y, ps_x = (bank(n) for n in "qkvspoyx")
        norm = Normed(nc, sb, sem, x_tile, ps_x, lambda c: col(f"l2_ln{a}_s", c), lambda c: col(f"l2_ln{a}_b", c), ident)
        hT = norm.hT

        x_loaded, c_loaded, stored = norm.x_loaded, sem("c_loaded"), sem("stored")
        set_up = sem("set_up")
        gap_ready = sem("gap_ready")
        folded_in_psum = sem("folded_in_psum")
        folded_ready = sem("folded_ready")
        vector_step = sem("vector_step")
        cT_in_psum = sem("cT_in_psum")
        cT_ready = sem("cT_ready")
        q_in_psum, q_ready = sem("q_in_psum"), sem("q_ready")
        k_in_psum, k_ready = sem("k_in_psum"), sem("k_ready")
        learned_key_ready = sem("learned_key_ready")
        v_in_psum, v_ready = sem("v_in_psum"), sem("v_ready")
        s_in_psum = sem("s_in_psum")
        shift_ready = sem("shift_ready")
        exp_ready = sem("exp_ready")
        p_ready = sem("p_ready")
        learned_ready = sem("learned_ready")
        pT_in_psum, pT_ready = sem("pT_in_psum"), sem("pT_ready")
        o_in_psum, o_ready = sem("o_in_psum"), sem("o_ready")
        learnedT_in_psum, learnedT_ready = sem("learnedT_in_psum"), sem("learnedT_ready")
        y_in_psum = sem("y_in_psum")
        y_ready = sem("y_ready")
        sums_read = sem("sums_read")
        res_b_ready = sem("res_b_ready")

        def rows_of(dram, first):
            return dram[bass.ds(first, ROUND), :].rearrange("(u p) d -> p u d", p=P)

        def per_head(i, h):
            return count(i, HEADS, h)

        def per_head_tile(i, h, u):
            return count(i, 2 * HEADS, h * 2 + u)

        def value_event(i, g, u):
            return count(i, 8, g * 2 + u)

        def rounds(engine, body):
            with engine.Fori(0, ROUNDS - 1) as i:
                body(i, True)
            body(ROUNDS - 1, False)

        block = running.enter_context(nc.Block())

        @block.sync
        def _(sp):
            sp.dma_start(c_tile[:], rows_of(ctx, 0)).then_inc(c_loaded, 16)
            sp.dma_start(x_tile[:], rows_of(x_in, 0)).then_inc(x_loaded, 16)
            sp.sem_inc(stored, 16)
            if prefetch:
                prefetch(sp)
            with sp.Fori(0, ROUNDS - 1) as i:
                sp.wait_ge(cT_in_psum, count(i, 1, 0))
                sp.nop()
                sp.dma_start(c_tile[:], rows_of(ctx, i * ROUND + ROUND)).then_inc(c_loaded, 16)
                sp.wait_ge(res_b_ready, count(i, 2, 1))
                sp.wait_ge(norm.xn_ready, count(i, 2, 1))
                sp.nop()
                sp.dma_start(x_tile[:], rows_of(x_in, i * ROUND + ROUND)).then_inc(x_loaded, 16)
                sp.wait_ge(y_ready, count(i, 2, 1))
                sp.nop()
                sp.dma_start(rows_of(x_out, i * ROUND), y_out[:]).then_inc(stored, 16)
            sp.wait_ge(y_ready, 2 * ROUNDS)
            sp.dma_start(rows_of(x_out, (ROUNDS - 1) * ROUND), y_out[:]).then_inc(stored, 16)
            sp.wait_ge(stored, 16 * (ROUNDS + 1))

        @block.gpsimd
        def _(pool):
            nc.gpsimd.memset(norm.minus_half[:], -0.5).then_inc(set_up, 1)
            nc.gpsimd.memset(one[:], 1.0).then_inc(set_up, 1)
            nc.gpsimd.memset(value_gap[:], 0.0).then_inc(set_up, 1)
            nc.gpsimd.memset(other_sequence[:], 0.0).then_inc(set_up, 1)
            for u in range(2):
                nc.gpsimd.memset(learned[u][:], 0.0).then_inc(set_up, 1)
            pool.wait_ge(set_up, 6)
            for b in range(2):
                nc.gpsimd.memset(other_sequence[b * SEQ:(b + 1) * SEQ, (1 - b) * SEQ:(2 - b) * SEQ], MINUS_INF).then_inc(set_up, 1)
            pool.wait_ge(set_up, 8)
            for u in range(2):
                nc.gpsimd.memset(learned[u][:, ONES:ONES + 1], 1.0).then_inc(set_up, 1)
            pool.wait_ge(set_up, 10)
            norm.inverse_deviations(pool, 0)

            def learned_key(i, h):
                pool.wait_ge(k_in_psum, per_head(i, h))
                nc.gpsimd.tensor_tensor(kT[:, :, P:KEYS], col(f"l2_bias_k{a + 1}", h).unsqueeze(1).to_broadcast([P, 2, 1]),
                                        one[:].unsqueeze(1).to_broadcast([P, 2, 1]), ALU.mult).then_inc(learned_key_ready, 1)

            def learned_probability(i, h):
                for u in range(2):
                    pool.wait_ge(p_ready, per_head_tile(i, h, u))
                    if h == 0:
                        pool.wait_ge(sums_read, count(i, 1, 0))
                    nc.gpsimd.tensor_tensor(learned[u][:, h:h + 1], probs[u][:, P:KEYS], one[:], ALU.mult).then_inc(learned_ready, 1)

            def body(i, more):
                pool.wait_ge(sums_read, count(i, 1, 0))
                for u in range(2):
                    nc.gpsimd.tensor_tensor(res_b[:, u, :], x_tile[:, u, :], row[f"l2_bo{a + 1}"], ALU.add).then_inc(res_b_ready, 1)
                for h in range(HEADS + 1):
                    if h < HEADS:
                        learned_key(i, h)
                    if h > 0:
                        learned_probability(i, h - 1)
                    if h == HEADS // 2 and more:
                        norm.inverse_deviations(pool, i + 1)

            rounds(pool, body)

        @block.scalar
        def _(act):
            def queries(i, h):
                act.wait_ge(q_in_psum, per_head(i, h))
                nc.scalar.activation(qT[:], ps_q[:, 0:ROUND], ACT.Identity, bias=col(f"l2_bq{a + 1}", h), scale=1.0
                                     ).then_inc(q_ready, 1)

            def values(i, g, u):
                act.wait_ge(v_in_psum, value_event(i, g, u))
                nc.scalar.activation(v[g % 2][u][:], ps_v[:], ACT.Copy).then_inc(v_ready, 1)

            def exponentials(i, h):
                for u in range(2):
                    act.wait_ge(shift_ready, per_head_tile(i, h, u))
                    nc.scalar.activation(probs[u][:], probs[u][:], ACT.Exp, bias=shift[u][:], scale=scale,
                                         accum_out=row_sum[u][:]).then_inc(exp_ready, 1)

            def attended(i, h):
                act.wait_ge(o_in_psum, per_head(i, h))
                nc.scalar.activation(oT[:].rearrange("d u q -> d (u q)"), ps_o[:, 0:ROUND], ACT.Copy).then_inc(o_ready, 1)

            def learned_transposed(i):
                act.wait_ge(learnedT_in_psum, count(i, 1, 0))
                nc.scalar.activation(learnedT[:].rearrange("h u q -> h (u q)"), ps_k[:, 0:ROUND], ACT.Copy
                                     ).then_inc(learnedT_ready, 1)

            def body(i, more):
                for h in range(HEADS + 1):
                    if h > 0:
                        exponentials(i, h - 1)
                    if h < HEADS:
                        queries(i, h)
                        g, r = divmod(h, 4)
                        if r % 2 and g < 3:
                            values(i, g + 1, r // 2)
                    elif more:
                        norm.scaled(act, i + 1)
                    if h > 0:
                        attended(i, h - 1)
                learned_transposed(i)
                if more:
                    for u in range(2):
                        values(i + 1, 0, u)

            norm.scaled(act, 0)
            for u in range(2):
                values(0, 0, u)
            rounds(act, body)

        @block.vector
        def _(dve):
            links = Links(vector_step, dve, L2_VECTOR_LINKS)

            def context(r):
                dve.wait_ge(cT_in_psum, count(r, 1, 0))
                nc.vector.tensor_copy(cT[:].rearrange("f c t -> f (c t)"), ps_v[:]).then_inc(cT_ready, 1)

            def keys(i, h):
                dve.wait_ge(k_in_psum, per_head(i, h))
                nc.vector.tensor_scalar(kT[:, :, 0:P], ps_k[:, 0:ROUND].rearrange("d (u k) -> d u k", u=2),
                                        col(f"l2_bk{a + 1}", h), None, ALU.add).then_inc(k_ready, 1)

            def maxima(i, h):
                dve.wait_ge(s_in_psum, per_head(i, h))
                if h > 0:
                    dve.wait_ge(learned_ready, per_head_tile(i, h - 1, 1))
                for u in range(2):
                    nc.vector.memset(pad[u][:], 0.0)
                    links.mark(nc.vector.tensor_tensor_reduce(
                        out=probs[u][:], in0=ps_s[:, u * KEYS:(u + 1) * KEYS], in1=other_sequence[:], scale=1.0,
                        scalar=MINUS_INF, op0=ALU.add, op1=ALU.max, accum_out=row_max[u][:]))
                for u in range(2):
                    if u == 0:
                        links.wait(i)
                    nc.vector.tensor_scalar(shift[u][:], row_max[u][:], -scale, None, ALU.mult).then_inc(shift_ready, 1)

            def normalise(i, h):
                for u in range(2):
                    dve.wait_ge(exp_ready, per_head_tile(i, h, u))
                    links.mark(nc.vector.reciprocal(inv_sum[u][:], row_sum[u][:]))
                    links.wait(i)
                    nc.vector.tensor_scalar(probs[u][:], probs[u][:], inv_sum[u][:], None, ALU.mult).then_inc(p_ready, 1)

            def probs_transposed(i, h):
                dve.wait_ge(pT_in_psum, per_head(i, h))
                nc.vector.tensor_copy(pT[:].rearrange("k u q -> k (u q)"), ps_p[:, 0:ROUND]).then_inc(pT_ready, 1)

            def add_residual(i):
                dve.wait_ge(y_in_psum, count(i, 1, 0))
                dve.wait_ge(res_b_ready, count(i, 2, 1))
                dve.wait_ge(stored, (i + 1) * 16)
                for u in range(2):
                    last = nc.vector.tensor_tensor(y_out[:, u, :], ps_y[:, u * DIM:(u + 1) * DIM], res_b[:, u, :], ALU.add)
                    last.then_inc(y_ready, 1)
                dve.wait_ge(y_ready, count(i, 2, 1))
                dve.sem_inc(sums_read, 1)

            def body(i, more):
                links.begin()
                for h in range(HEADS + 1):
                    if h > 0:
                        maxima(i, h - 1)
                    if h == HEADS and more:
                        context(i + 1)
                    if h > 0:
                        normalise(i, h - 1)
                    if h < HEADS:
                        keys(i, h)
                    if h > 0:
                        probs_transposed(i, h - 1)
                    if h == HEADS // 2 - 1 and more:
                        dve.wait_ge(norm.xT_in_psum, count(i, 1, 0))
                        norm.variances(dve, i + 1)
                    if h == HEADS // 2 + 1 and more:
                        norm.normalised(dve, i + 1)
                add_residual(i)

            norm.variances(dve, 0)
            norm.normalised(dve, 0)
            context(0)
            dve.wait_ge(set_up, 10)
            gap_columns = value_gap[:].rearrange("p h m -> p (h m)")
            bias_v, bv = (col(f"l2_bias_v{a + 1}", 0, HEADS), col(f"l2_bv{a + 1}", 0, HEADS))
            nc.vector.tensor_tensor(gap_columns[:, 0:(HEADS - 1) * (ONES + 2) + 1:ONES + 2], bias_v, bv, ALU.subtract
                                    ).then_inc(gap_ready, 1)
            nc.vector.tensor_copy(gap_columns[:, ONES:HEADS * (ONES + 1):ONES + 1], bv).then_inc(gap_ready, 1)
            dve.wait_ge(folded_in_psum, 1)
            nc.vector.tensor_copy(gap_out[:], ps_y[0:ONES + 1, 0:DIM]).then_inc(folded_ready, 1)
            dve.sem_inc(sums_read, 1)
            rounds(dve, body)
            links.check()

        @block.tensor
        def _(pe):
            def context(r):
                pe.wait_ge(c_loaded, count(r, 1, 0) * 16)
                for c in range(DC):
                    for u in range(2):
                        last = nc.tensor.transpose(ps_v[:, c * ROUND + u * P:c * ROUND + (u + 1) * P],
                                                   c_tile[:, u, c * P:(c + 1) * P], ident)
                last.then_inc(cT_in_psum, 1)

            def project(ps, weights, h, moving, ready):
                for k in range(DC):
                    last = nc.tensor.matmul(ps[:, 0:ROUND], weights[:, k, h * WIDE:(h + 1) * WIDE], moving[:, k, :],
                                            start=(k == 0), stop=(k == DC - 1))
                last.then_inc(ready, 1)

            def values(i, g, u):
                if g == 0 and u == 0:
                    pe.wait_ge(cT_ready, count(i, 1, 0))
                else:
                    pe.wait_ge(v_ready, value_event(i, g, u) - 1)
                for k in range(DC):
                    last = nc.tensor.matmul(ps_v[:], cT[:, k, u * P:(u + 1) * P],
                                            wv[:, k, g * 4 * WIDE:(g + 1) * 4 * WIDE],
                                            start=(k == 0), stop=(k == DC - 1))
                last.then_inc(v_in_psum, 1)

            def scores(i, h):
                pe.wait_ge(q_ready, per_head(i, h))
                pe.wait_ge(k_ready, per_head(i, h))
                pe.wait_ge(learned_key_ready, per_head(i, h))
                for u in range(2):
                    last = nc.tensor.matmul(ps_s[:, u * KEYS:(u + 1) * KEYS], qT[:, u * P:(u + 1) * P], kT[:, u, :],
                                            start=True, stop=True)
                last.then_inc(s_in_psum, 1)

            def transpose_probs(i, h):
                for u in range(2):
                    pe.wait_ge(p_ready, per_head_tile(i, h, u))
                    last = nc.tensor.transpose(ps_p[:, u * P:(u + 1) * P], probs[u][:, 0:P], ident)
                last.then_inc(pT_in_psum, 1)

            def attend(i, h):
                g, r = divmod(h, 4)
                pe.wait_ge(pT_ready, per_head(i, h))
                if r == 0:
                    pe.wait_ge(v_ready, value_event(i, g, 1))
                for u in range(2):
                    last = nc.tensor.matmul(ps_o[:, u * P:(u + 1) * P], v[g % 2][u][:, r * WIDE:(r + 1) * WIDE],
                                            pT[:, u, :], start=True, stop=True)
                last.then_inc(o_in_psum, 1)

            def project_out(i, h):
                if h == 0:
                    pe.wait_ge(sums_read, count(i, 1, 0))
                pe.wait_ge(o_ready, per_head(i, h))
                for u in range(2):
                    nc.tensor.matmul(ps_y[:, u * DIM:(u + 1) * DIM], oT[:, u, :], wo[:, h, :],
                                     start=(h == 0 and u == 0), stop=False, skip_group_check=True)

            def learned_value(i):
                pe.wait_ge(learned_ready, per_head_tile(i, HEADS - 1, 1))
                for u in range(2):
                    last = nc.tensor.transpose(ps_k[:, u * P:(u + 1) * P], learned[u][:], ident)
                last.then_inc(learnedT_in_psum, 1)

            def add_learned_value(i):
                pe.wait_ge(learnedT_ready, count(i, 1, 0))
                for u in range(2):
                    last = nc.tensor.matmul(ps_y[:, u * DIM:(u + 1) * DIM], learnedT[0:ONES + 1, u, :], gap_out[:],
                                            start=False, stop=True, skip_group_check=True)
                last.then_inc(y_in_psum, 1)

            def body(i, more):
                pe.wait_ge(norm.hT_ready, count(i, 1, 0))
                for h in range(HEADS):
                    project(ps_q, wq, h, hT, q_in_psum)
                    project(ps_k, wk, h, cT, k_in_psum)
                    if h >= 2:
                        project_out(i, h - 2)
                    if h >= 1:
                        transpose_probs(i, h - 1)
                    g, r = divmod(h, 4)
                    if r % 2 and g < 3:
                        values(i, g + 1, r // 2)
                    scores(i, h)
                    if h >= 1:
                        attend(i, h - 1)
                if more:
                    context(i + 1)
                    norm.transposed(pe, i + 1)
                project_out(i, HEADS - 2)
                transpose_probs(i, HEADS - 1)
                if more:
                    values(i + 1, 0, 0)
                attend(i, HEADS - 1)
                learned_value(i)
                if more:
                    values(i + 1, 0, 1)
                project_out(i, HEADS - 1)
                add_learned_value(i)

            context(0)
            norm.transposed(pe, 0)
            for u in range(2):
                values(0, 0, u)
            pe.wait_ge(gap_ready, 2)
            for h in range(HEADS):
                last = nc.tensor.matmul(ps_y[0:ONES + 1, 0:DIM], value_gap[:, h, :], wo[:, h, :], start=(h == 0), stop=(h == HEADS - 1))
            last.then_inc(folded_in_psum, 1)
            pe.wait_ge(folded_ready, 1)
            rounds(pe, body)

        running.close()
        cleared(nc, semaphores)


def wide_mlp(nc, x_in, x_out, w, col, row, ident, prefetch=None):
    with ExitStack() as held:
        semaphores, running = [], ExitStack()

        def sb(name, shape, dtype=F32):
            return held.enter_context(nc.sbuf_tensor("l2m_" + name, shape, dtype))

        def sem(name):
            semaphores.append(held.enter_context(nc.semaphore("l2m_" + name)))
            return semaphores[-1]

        ROUND = 2 * P
        x_tile = sb("x_tile", [P, 2, DIM])
        res_b = sb("res_b", [P, 2, DIM])
        hidT = sb("hidT", [P, HC, ROUND])
        y_out = sb("y_out", [P, 2, DIM])
        ps_hid = [held.enter_context(nc.psum_tensor(f"l2m_ps_hid{j}", [P, BANK], F32)) for j in range(4)]
        ps_y, ps_x = (held.enter_context(nc.psum_tensor("l2m_ps_" + n, [P, BANK], F32)) for n in "yx")
        norm = Normed(nc, sb, sem, x_tile, ps_x, lambda c: col("l2_ln2_s", c), lambda c: col("l2_ln2_b", c), ident)

        x_loaded, stored = norm.x_loaded, sem("stored")
        set_up = sem("set_up")
        hid_in_psum, hid_ready = sem("hid_in_psum"), sem("hid_ready")
        y_in_psum = sem("y_in_psum")
        res_b_ready = sem("res_b_ready")
        y_ready = sem("y_ready")
        sums_read = sem("sums_read")

        def rows_of(dram, first):
            return dram[bass.ds(first, ROUND), :].rearrange("(u p) d -> p u d", p=P)

        def rounds(engine, body):
            with engine.Fori(0, ROUNDS - 1) as i:
                body(i, True)
            body(ROUNDS - 1, False)

        block = running.enter_context(nc.Block())

        @block.sync
        def _(sp):
            sp.dma_start(x_tile[:], rows_of(x_in, 0)).then_inc(x_loaded, 16)
            sp.sem_inc(stored, 16)
            if prefetch:
                prefetch(sp)
            with sp.Fori(0, ROUNDS - 1) as i:
                sp.wait_ge(res_b_ready, count(i, 2, 1))
                sp.wait_ge(norm.xn_ready, count(i, 2, 1))
                sp.nop()
                sp.dma_start(x_tile[:], rows_of(x_in, i * ROUND + ROUND)).then_inc(x_loaded, 16)
                sp.wait_ge(y_ready, count(i, 2, 1))
                sp.nop()
                sp.dma_start(rows_of(x_out, i * ROUND), y_out[:]).then_inc(stored, 16)
            sp.wait_ge(y_ready, 2 * ROUNDS)
            sp.dma_start(rows_of(x_out, (ROUNDS - 1) * ROUND), y_out[:]).then_inc(stored, 16)
            sp.wait_ge(stored, 16 * (ROUNDS + 1))

        @block.gpsimd
        def _(pool):
            nc.gpsimd.memset(norm.minus_half[:], -0.5).then_inc(set_up, 1)
            pool.wait_ge(set_up, 1)
            norm.inverse_deviations(pool, 0)

            def body(i, more):
                pool.wait_ge(sums_read, count(i, 1, 0))
                for u in range(2):
                    nc.gpsimd.tensor_tensor(res_b[:, u, :], x_tile[:, u, :], row["l2_b_fc2"], ALU.add).then_inc(res_b_ready, 1)
                if more:
                    norm.inverse_deviations(pool, i + 1)

            rounds(pool, body)

        @block.scalar
        def _(act):
            def body(i, more):
                for j in range(4):
                    act.wait_ge(hid_in_psum, count(i, 4, j))
                    for c in range(2):
                        last = nc.scalar.activation(hidT[:, 2 * j + c, :], ps_hid[j][:, c * ROUND:(c + 1) * ROUND], ACT.Gelu,
                                                    bias=col("l2_b_fc1", 2 * j + c), scale=1.0)
                    last.then_inc(hid_ready, 1)
                if more:
                    norm.scaled(act, i + 1)

            norm.scaled(act, 0)
            rounds(act, body)

        @block.vector
        def _(dve):
            def add_residual(i):
                dve.wait_ge(y_in_psum, count(i, 1, 0))
                dve.wait_ge(res_b_ready, count(i, 2, 1))
                dve.wait_ge(stored, (i + 1) * 16)
                for u in range(2):
                    nc.vector.tensor_tensor(y_out[:, u, :], ps_y[:, u * DIM:(u + 1) * DIM], res_b[:, u, :], ALU.add
                                            ).then_inc(y_ready, 1)
                dve.wait_ge(y_ready, count(i, 2, 1))
                dve.sem_inc(sums_read, 1)

            def body(i, more):
                if more:
                    dve.wait_ge(norm.xT_in_psum, count(i, 1, 0))
                    norm.variances(dve, i + 1)
                    norm.normalised(dve, i + 1)
                add_residual(i)

            dve.sem_inc(sums_read, 1)
            norm.variances(dve, 0)
            norm.normalised(dve, 0)
            rounds(dve, body)

        @block.tensor
        def _(pe):
            def body(i, more):
                pe.wait_ge(norm.hT_ready, count(i, 1, 0))
                for h in range(HC):
                    for k in range(DC):
                        last = nc.tensor.matmul(ps_hid[h // 2][:, h % 2 * ROUND:(h % 2 + 1) * ROUND],
                                                w["l2_w_fc1"][:, k, h * P:(h + 1) * P], norm.hT[:, k, :],
                                                start=(k == 0), stop=(k == DC - 1))
                    if h % 2:
                        last.then_inc(hid_in_psum, 1)
                pe.wait_ge(sums_read, count(i, 1, 0))
                for h in range(HC):
                    if h % 2 == 0:
                        pe.wait_ge(hid_ready, count(i, 4, h // 2))
                    for u in range(2):
                        last = nc.tensor.matmul(ps_y[:, u * DIM:(u + 1) * DIM], hidT[:, h, u * P:(u + 1) * P],
                                                w["l2_w_fc2"][:, h, :], start=(h == 0 and u == 0),
                                                stop=(h == HC - 1), skip_group_check=True)
                    if h == HC // 2 and more:
                        norm.transposed(pe, i + 1)
                last.then_inc(y_in_psum, 1)

            norm.transposed(pe, 0)
            rounds(pe, body)

        running.close()
        cleared(nc, semaphores)


def recurrent_layer(nc, x_in, ctx, x_out, w, col, ident, select, head_of):
    with ExitStack() as held:
        semaphores, running = [], ExitStack()

        def sb(name, shape, dtype=F32):
            return [held.enter_context(nc.sbuf_tensor(f"l3_{name}{s}", shape, dtype)) for s in range(2)]

        def sem(name):
            semaphores.append(held.enter_context(nc.semaphore("l3_" + name)))
            return semaphores[-1]

        def both(name):
            return [sem(f"{name}{s}") for s in range(2)]

        NB = PER_TILE
        ORDER = (0, 4, 2, 1, 3)
        LAG = 2

        x_tile = sb("x_tile", [P, DIM])
        first_rows = sb("first_rows", [2 * NB, DIM])
        state = sb("state", [P, DC, NB, HEAD8])
        stats = sb("stats", [P, 6])
        pad = sb("pad", [P, 1])
        mean_var = sb("mean_var", [P, 2])
        var_eps = sb("var_eps", [P, 1])
        rstd = sb("rstd", [P, 1])
        minus_half, one_column = (sb(n, [P, 1])[0] for n in ("minus_half", "one_column"))
        xn = sb("xn", [P, DIM])
        xnT = [sb(f"xnT{n}_", [P, DC, NB, 1 + SEQ]) for n in range(2)]
        sxT = sb("sxT", [P, DC, NB, SEQ])
        mixed = sb("mixed", [P, DC, NB, SEQ])
        loraT = sb("loraT", [P, 2, P])
        part = [sb(f"part{j}_", [P, DC, NB, SEQ]) for j in range(5)]
        x5 = [sb(f"x5_{j}_", [P, DC, P]) for j in range(5)]
        decayT = sb("decayT", [DECAY, P])
        rate = sb("rate", [P, DC, P])
        wT = sb("wT", [P, DC, NB, SEQ])
        kT, vT, rT, gT = (sb(n, [P, DC, P]) for n in ("kT", "vT", "rT", "gT"))
        gate = sb("gate", [P, DC, P])
        rukT = sb("rukT", [P, DC, P])
        state_of = [sb(f"s{c}_", [P, HEAD8, NB, SEQ]) for c in range(DC)]
        ruk = sb("ruk", [P, DIM // HEAD8])
        att = sb("att", [P, DIM])
        square = sb("square", [P, DIM])
        group = [sb(f"group{n}_", [P, DIM // HEAD8]) for n in range(4)]
        gated = sb("gated", [P, DC, P])
        res = sb("res", [P, DIM])
        xkT, xrT = sb("xkT", [P, DC, P]), sb("xrT", [P, DC, P])
        kk, kk2 = sb("kk", [P, DC, P]), sb("kk2", [P, DC, P])
        receptance = sb("receptance", [P, DIM])
        part_y = sb("part_y", [P, DIM])
        y_out = sb("y_out", [P, DIM])
        banks = [[held.enter_context(nc.psum_tensor(f"l3_ps{s}_{j}", [P, BANK], F32)) for j in range(4)] for s in range(2)]

        x_loaded, rows_loaded, state_loaded, stored = (both(n) for n in ("x_loaded", "rows_loaded", "state_loaded", "stored"))
        set_up = sem("set_up")
        vector_step = sem("vector_step")
        scalar_step = sem("scalar_step")
        var_ready, rstd_ready = both("var_ready"), both("rstd_ready")
        xn_ready = both("xn_ready")
        xT_in_psum, xnT_ready = both("xT_in_psum"), both("xnT_ready")
        rows_in_psum, rows_ready = both("rows_in_psum"), both("rows_ready")
        mixed_ready = both("mixed_ready")
        lora_in_psum, lora_ready = both("lora_in_psum"), both("lora_ready")
        mix_in_psum = both("mix_in_psum")
        part_ready, x5_ready = both("part_ready"), both("x5_ready")
        k_in_psum, k_ready = both("k_in_psum"), both("k_ready")
        v_in_psum, v_ready = both("v_in_psum"), both("v_ready")
        decay_in_psum, decay_ready = both("decay_in_psum"), both("decay_ready")
        rate_in_psum, w_ready = both("rate_in_psum"), both("w_ready")
        r_in_psum, r_ready = both("r_in_psum"), both("r_ready")
        g_in_psum, g_ready = both("g_in_psum"), both("g_ready")
        gate_ready = both("gate_ready")
        start_ready = both("start_ready")
        spread_in_psum = both("spread_in_psum")
        addend_ready = both("addend_ready")
        out_ready = both("out_ready")
        ruk_ready = both("ruk_ready")
        att_in_psum = both("att_in_psum")
        deviation_ready, root_ready = both("deviation_ready"), both("root_ready")
        att_ready = both("att_ready")
        attT_in_psum, attT_ready = both("attT_in_psum"), both("attT_ready")
        gated_ready = both("gated_ready")
        y_in_psum = both("y_in_psum")
        channel_ready = both("channel_ready")
        kk_in_psum, kk_ready = both("kk_in_psum"), both("kk_ready")
        kk2_ready = both("kk2_ready")
        rr_in_psum, rr_ready = both("rr_in_psum"), both("rr_ready")
        kv_in_psum = both("kv_in_psum")
        y_ready = both("y_ready")

        one = lambda i: count(i, 1, 0)
        WIDE4 = HEAD8 // 2

        def by_token(t):
            return t.rearrange("p c (b t) -> p c b t", t=SEQ)

        def flat(t):
            return t.rearrange("p c t -> p (c t)")

        ctx_rows = ctx.rearrange("(b r) d -> b (r d)", r=SEQ)

        block = running.enter_context(nc.Block())

        @block.sync
        def _(sp):
            def load_x(i, t, s):
                sp.dma_start(x_tile[s][:], x_in[bass.ds(i * 2 * P + t * P, P), :]).then_inc(x_loaded[s], 16)

            def load_rows(i, t, s):
                for r in range(2):
                    sp.dma_start(first_rows[s][r * NB:(r + 1) * NB, :],
                                 ctx_rows[bass.ds(i * 2 * NB + t * NB, NB), r * DIM:(r + 1) * DIM]).then_inc(rows_loaded[s], 16)

            def load_state(i, t, s):
                for c in range(DC):
                    first = 2 * DIM + c * P * HEAD8
                    sp.dma_start(state[s][:, c, :, :], ctx_rows[bass.ds(i * 2 * NB + t * NB, NB), first:first + P * HEAD8].rearrange(
                        "b (p d) -> p b d", d=HEAD8)).then_inc(state_loaded[s], 16)

            def store(i, s):
                sp.wait_ge(y_ready[s], one(i))
                sp.nop()
                sp.dma_start(x_out[bass.ds(i * 2 * P + s * P, P), :], y_out[s][:]).then_inc(stored[s], 16)

            for s in range(2):
                load_x(0, s, s)
                load_rows(0, s, s)
                load_state(0, s, s)
                sp.sem_inc(stored[s], 16)
            with sp.Fori(0, ROUNDS - 1) as i:
                for s in range(2):
                    sp.wait_ge(rows_in_psum[s], one(i))
                    sp.nop()
                    load_rows(i, s + 2, s)
                    sp.wait_ge(start_ready[s], one(i))
                    sp.nop()
                    load_state(i, s + 2, s)
                    sp.wait_ge(xn_ready[s], count(i, 2, 1))
                    sp.nop()
                    load_x(i, s + 2, s)
                    store(i, s)
            for s in range(2):
                store(ROUNDS - 1, s)
            for s in range(2):
                sp.wait_ge(stored[s], 16 * (ROUNDS + 1))

        @block.gpsimd
        def _(pool):
            nc.gpsimd.memset(minus_half[:], -0.5).then_inc(set_up, 1)
            nc.gpsimd.memset(one_column[:], 1.0).then_inc(set_up, 1)
            for s in range(2):
                nc.gpsimd.memset(wT[s][:], 0.0).then_inc(set_up, 1)
            pool.wait_ge(set_up, 4)

            def inverse_deviation(n):
                def step(i, s):
                    pool.wait_ge(var_ready[s], count(i, 2, n))
                    nc.gpsimd.tensor_tensor(rstd[s][:], var_eps[s][:], minus_half[:], ALU.pow).then_inc(rstd_ready[s], 1)
                return step

            def start(i, s):
                pool.wait_ge(state_loaded[s], one(i) * 16 * DC)
                for c in range(DC):
                    last = nc.gpsimd.tensor_tensor(state_of[c][s][:, :, :, 0], state[s][:, c, :, :].rearrange("p b d -> p d b"),
                                                   one_column[:].unsqueeze(1).to_broadcast([P, HEAD8, NB]), ALU.mult)
                last.then_inc(start_ready[s], 1)

            def mixes(i, s):
                for n, j in enumerate(ORDER):
                    pool.wait_ge(part_ready[s], count(i, 5, n))
                    for c in range(DC):
                        last = nc.gpsimd.tensor_tensor(by_token(x5[j][s][:])[:, c], part[j][s][:, c, :, :],
                                                       xnT[0][s][:, c, :, 1:], ALU.add)
                    last.then_inc(x5_ready[s], 1)

            def squares(i, s):
                pool.wait_ge(kk_ready[s], one(i))
                nc.gpsimd.tensor_tensor(kk2[s][:], kk[s][:], kk[s][:], ALU.mult).then_inc(kk2_ready[s], 1)

            skewed(pool, LAG, (inverse_deviation(0), start), (), (), (mixes,), (), (), (), (), (),
                   (inverse_deviation(1),), (), (squares,), ())

        @block.scalar
        def _(act):
            links = Links(scalar_step, act, L3_SCALAR_LINKS)

            def given_rows(i, s):
                act.wait_ge(rows_in_psum[s], one(i))
                for n in range(2):
                    last = nc.scalar.activation(xnT[n][s][:, :, :, 0], banks[s][1][:, 0:2 * DC * NB].rearrange(
                        "f (c r b) -> f c r b", r=2, b=NB)[:, :, 1 - n, :], ACT.Copy)
                last.then_inc(rows_ready[s], 1)

            def normed_transposed(n):
                def step(i, s):
                    act.wait_ge(xT_in_psum[s], count(i, 2, n))
                    for c in range(DC):
                        last = nc.scalar.activation(xnT[n][s][:, c, :, 1:], banks[s][0][:, c * P:(c + 1) * P].rearrange(
                            "f (b t) -> f b t", t=SEQ), ACT.Identity, bias=col(f"l3_ln{n + 1}_b", c), scale=col(f"l3_ln{n + 1}_w", c))
                    last.then_inc(xnT_ready[s], 1)
                return step

            def copied(i, s, arrived, out, ps, done):
                act.wait_ge(arrived[s], one(i))
                nc.scalar.activation(flat(out[s][:]), ps, ACT.Copy).then_inc(done[s], 1)

            def lora(i, s):
                act.wait_ge(lora_in_psum[s], one(i))
                nc.scalar.activation(loraT[s][:, 0, :], banks[s][1][:, 0:P], ACT.Tanh)
                nc.scalar.activation(loraT[s][0:LORA, 1, :], banks[s][1][0:LORA, P:2 * P], ACT.Tanh).then_inc(lora_ready[s], 1)

            def projected(i, s):
                copied(i, s, k_in_psum, kT, banks[s][0][:, 0:DIM], k_ready)
                copied(i, s, v_in_psum, vT, banks[s][2][:, 0:DIM], v_ready)
                act.wait_ge(decay_in_psum[s], one(i))
                nc.scalar.activation(decayT[s][:], banks[s][1][0:DECAY, 0:P], ACT.Tanh).then_inc(decay_ready[s], 1)
                copied(i, s, r_in_psum, rT, banks[s][3][:, 0:DIM], r_ready)

            def decay_and_gate(i, s):
                act.wait_ge(rate_in_psum[s], one(i))
                for c in range(DC):
                    last = nc.scalar.activation(rate[s][:, c, :], banks[s][1][:, c * P:(c + 1) * P], ACT.Exp,
                                                bias=col("l3_time_decay", c), scale=1.0)
                links.mark(last)
                links.wait(i)
                nc.scalar.activation(wT[s][:, :, :, 1:].rearrange("p c b t -> p (c b) t"),
                                     rate[s][:].rearrange("p c (b t) -> p (c b) t", t=SEQ)[:, :, 0:SEQ - 1],
                                     ACT.Exp, scale=-1.0).then_inc(w_ready[s], 1)
                act.wait_ge(g_in_psum[s], one(i))
                nc.scalar.activation(flat(gT[s][:]), banks[s][0][:, DIM:2 * DIM], ACT.Tanh, scale=0.5).then_inc(g_ready[s], 1)

            def root(i, s):
                act.wait_ge(deviation_ready[s], one(i))
                nc.scalar.activation(group[3][s][:], group[2][s][:], ACT.Sqrt).then_inc(root_ready[s], 1)

            def attended_transposed(i, s):
                act.wait_ge(attT_in_psum[s], one(i))
                for c in range(DC):
                    last = nc.scalar.activation(kk[s][:, c, :], banks[s][2][:, c * P:(c + 1) * P], ACT.Identity,
                                                bias=col("l3_gn_b", c), scale=col("l3_gn_w", c))
                last.then_inc(attT_ready[s], 1)

            def channel(i, s):
                act.wait_ge(kk_in_psum[s], one(i))
                nc.scalar.activation(flat(kk[s][:]), banks[s][1][:, 0:DIM], ACT.Relu).then_inc(kk_ready[s], 1)
                act.wait_ge(rr_in_psum[s], one(i))
                nc.scalar.activation(receptance[s][:], banks[s][2][:, 0:DIM], ACT.Tanh, scale=0.5).then_inc(rr_ready[s], 1)

            skewed(act, LAG, (), (given_rows, normed_transposed(0)), (lora,), (), (projected,), (decay_and_gate,), (), (root,),
                   (attended_transposed,), (), (normed_transposed(1),), (channel,), (), links=links)

        @block.vector
        def _(dve):
            links = Links(vector_step, dve, L3_VECTOR_LINKS)

            def layer_norm(i, n, s, source):
                links.mark(nc.vector.bn_stats(stats[s][:], source[s][:]))
                links.wait(i)
                nc.vector.memset(pad[s][:], 0.0)
                links.mark(nc.vector.bn_aggr(mean_var[s][:], stats[s][:]))
                links.wait(i)
                nc.vector.tensor_scalar(var_eps[s][:], mean_var[s][:, 1:2], LN_EPS, None, ALU.add).then_inc(var_ready[s], 1)
                dve.wait_ge(rstd_ready[s], count(i, 2, n))
                nc.vector.tensor_scalar(xn[s][:], source[s][:], mean_var[s][:, 0:1], rstd[s][:], ALU.subtract, ALU.mult
                                        ).then_inc(xn_ready[s], 1)

            def shifted(i, n, s):
                dve.wait_ge(xnT_ready[s], count(i, 2, n))
                rows = xnT[n][s][:].rearrange("p c b t -> p (c b) t")
                links.mark(nc.vector.tensor_tensor(sxT[s][:].rearrange("p c b t -> p (c b) t"), rows[:, :, 0:SEQ], rows[:, :, 1:],
                                                   ALU.subtract))
                links.wait(i)

            def mix(out, n, s, amount):
                for c in range(DC):
                    last = nc.vector.scalar_tensor_tensor(out=out[:, c], in0=sxT[s][:, c], scalar=col(amount, c),
                                                          in1=xnT[n][s][:, c, :, 1:], op0=ALU.mult, op1=ALU.add)
                return last

            def first_norm(i, s):
                dve.wait_ge(x_loaded[s], one(i) * 16)
                layer_norm(i, 0, s, x_tile)

            def first_mix(i, s):
                shifted(i, 0, s)
                dve.wait_ge(rows_ready[s], one(i))
                mix(mixed[s][:], 0, s, "l3_maa_x").then_inc(mixed_ready[s], 1)

            def mixes(i, s):
                for n, j in enumerate(ORDER):
                    at = DIM if j == 4 else 0
                    dve.wait_ge(mix_in_psum[s], count(i, 5, n))
                    for c in range(DC):
                        last = nc.vector.scalar_tensor_tensor(
                            out=part[j][s][:, c].rearrange("p b t -> p (b t)"), in0=banks[s][j % 4][:, at + c * P:at + (c + 1) * P],
                            scalar=col("l3_maa_stack", j * DC + c), in1=sxT[s][:, c].rearrange("p b t -> p (b t)"),
                            op0=ALU.add, op1=ALU.mult)
                    last.then_inc(part_ready[s], 1)

            def own_token_and_gate(i, s):
                dve.wait_ge(k_ready[s], one(i))
                dve.wait_ge(r_ready[s], one(i))
                for c in range(DC):
                    last = nc.vector.scalar_tensor_tensor(out=rukT[s][:, c, :], in0=rT[s][:, c, :], scalar=col("l3_faaaa", c),
                                                          in1=kT[s][:, c, :], op0=ALU.mult, op1=ALU.mult)
                last.then_inc(ruk_ready[s], 1)
                dve.wait_ge(g_ready[s], one(i))
                nc.vector.scalar_tensor_tensor(out=flat(gate[s][:]), in0=flat(gT[s][:]), scalar=1.0,
                                               in1=banks[s][0][:, DIM:2 * DIM], op0=ALU.add, op1=ALU.mult).then_inc(gate_ready[s], 1)

            def scans(i, s):
                dve.wait_ge(start_ready[s], one(i))
                dve.wait_ge(w_ready[s], one(i))
                for c in range(DC):
                    for q in range(2):
                        n = 2 * c + q
                        dve.wait_ge(spread_in_psum[s], count(i, 4, n))
                        spread = banks[s][2 + q][:].rearrange("p (d b t) -> p d b t", d=WIDE4, t=SEQ)
                        for b in range(NB):
                            last = nc.vector.tensor_tensor(
                                state_of[c][s][:, WIDE4 * q:WIDE4 * (q + 1), b, 1:], spread[:, :, b, 0:SEQ - 1],
                                kT[s][:, c, b * SEQ:(b + 1) * SEQ - 1].unsqueeze(1).to_broadcast([P, WIDE4, SEQ - 1]), ALU.mult)
                        last.then_inc(addend_ready[s], 1)
                        dve.wait_ge(addend_ready[s], count(i, 4, n))
                        for d in range(WIDE4 * q, WIDE4 * (q + 1)):
                            run = state_of[c][s][:, d].rearrange("p b t -> p (b t)")
                            last = nc.vector.tensor_tensor_scan(run, wT[s][:, c].rearrange("p b t -> p (b t)"), run, 0.0,
                                                                ALU.mult, ALU.add)
                    links.mark(last)
                    links.wait(i)
                    run = state_of[c][s][:].rearrange("p d b t -> p d (b t)")
                    nc.vector.tensor_tensor(run, run, rT[s][:, c, :].unsqueeze(1).to_broadcast([P, HEAD8, P]), ALU.mult
                                            ).then_inc(out_ready[s], 1)

            def head_norm(i, s):
                heads = DIM // HEAD8

                def grouped(t):
                    return t.rearrange("p (h d) -> p h d", d=HEAD8)

                def spread_over_head(t):
                    return t.unsqueeze(2).to_broadcast([P, heads, HEAD8])

                own, sq = att[s][:], square[s][:]
                dve.wait_ge(att_in_psum[s], one(i))
                links.mark(nc.vector.tensor_copy(ruk[s][:], banks[s][0][:, DIM:DIM + heads]))
                links.wait(i)
                links.mark(nc.vector.tensor_tensor(grouped(sq), grouped(banks[s][0][:, 0:DIM]), spread_over_head(ruk[s][:]), ALU.mult))
                links.wait(i)
                links.mark(nc.vector.tensor_tensor(own, banks[s][1][:, 0:DIM], sq, ALU.add))
                links.wait(i)
                links.mark(nc.vector.tensor_reduce(group[0][s][:], grouped(own), AX.X, ALU.add))
                links.wait(i)
                links.mark(nc.vector.tensor_scalar(group[1][s][:], group[0][s][:], 1.0 / HEAD8, None, ALU.mult))
                links.wait(i)
                links.mark(nc.vector.tensor_tensor(grouped(own), grouped(own), spread_over_head(group[1][s][:]), ALU.subtract))
                links.wait(i)
                links.mark(nc.vector.tensor_tensor(sq, own, own, ALU.mult))
                links.wait(i)
                links.mark(nc.vector.tensor_reduce(group[0][s][:], grouped(sq), AX.X, ALU.add))
                links.wait(i)
                nc.vector.tensor_scalar(group[2][s][:], group[0][s][:], 1.0 / HEAD8, LN_EPS, ALU.mult, ALU.add).then_inc(deviation_ready[s], 1)
                dve.wait_ge(root_ready[s], one(i))
                links.mark(nc.vector.reciprocal(group[1][s][:], group[3][s][:]))
                links.wait(i)
                nc.vector.tensor_tensor(grouped(own), grouped(own), spread_over_head(group[1][s][:]), ALU.mult
                                        ).then_inc(att_ready[s], 1)

            def gated_output(i, s):
                dve.wait_ge(attT_ready[s], one(i))
                nc.vector.scalar_tensor_tensor(out=gated[s][:], in0=kk[s][:], scalar=0.5, in1=gate[s][:], op0=ALU.mult, op1=ALU.mult
                                               ).then_inc(gated_ready[s], 1)

            def residual_and_norm(i, s):
                dve.wait_ge(y_in_psum[s], one(i))
                links.mark(nc.vector.tensor_tensor(res[s][:], banks[s][3][:, 0:DIM], x_tile[s][:], ALU.add))
                links.wait(i)
                layer_norm(i, 1, s, res)

            def channel_mixes(i, s):
                shifted(i, 1, s)
                mix(by_token(xkT[s][:]), 1, s, "l3_ffn_maa_k").then_inc(channel_ready[s], 1)
                mix(by_token(xrT[s][:]), 1, s, "l3_ffn_maa_r").then_inc(channel_ready[s], 1)

            def output(i, s):
                dve.wait_ge(rr_ready[s], one(i))
                dve.wait_ge(kv_in_psum[s], one(i))
                links.mark(nc.vector.scalar_tensor_tensor(out=part_y[s][:], in0=receptance[s][:], scalar=1.0,
                                                          in1=banks[s][3][:, 0:DIM], op0=ALU.add, op1=ALU.mult))
                links.wait(i)
                dve.wait_ge(stored[s], one(i) * 16)
                nc.vector.scalar_tensor_tensor(out=y_out[s][:], in0=part_y[s][:], scalar=0.5, in1=res[s][:], op0=ALU.mult, op1=ALU.add
                                               ).then_inc(y_ready[s], 1)

            dve.wait_ge(set_up, 4)
            skewed(dve, LAG, (first_norm,), (first_mix,), (), (mixes,), (), (own_token_and_gate,), (scans,), (head_norm,),
                   (gated_output,), (residual_and_norm,), (channel_mixes,), (), (output,), links=links)

        @block.tensor
        def _(pe):
            def transposed(ps, tokens):
                for c in range(DC):
                    last = nc.tensor.transpose(ps[:, c * P:(c + 1) * P], tokens[:, c * P:(c + 1) * P], ident)
                return last

            def features_out(ps, at, weights, moving):
                for c in range(DC):
                    for k in range(DC):
                        last = nc.tensor.matmul(ps[:, at + c * P:at + (c + 1) * P], weights[:, k, c * P:(c + 1) * P], moving[:, k, :],
                                                start=(k == 0), stop=(k == DC - 1))
                return last

            def tokens_out(ps, weights, stationary):
                for k in range(DC):
                    last = nc.tensor.matmul(ps[:, 0:DIM], stationary[:, k, :], weights[:, k, :], start=(k == 0), stop=(k == DC - 1))
                return last

            def normed(i, s):
                pe.wait_ge(xn_ready[s], count(i, 2, 0))
                pe.wait_ge(rows_loaded[s], one(i) * 32)
                transposed(banks[s][0], xn[s]).then_inc(xT_in_psum[s], 1)
                for c in range(DC):
                    last = nc.tensor.transpose(banks[s][1][:, c * 2 * NB:(c + 1) * 2 * NB], first_rows[s][:, c * P:(c + 1) * P],
                                               ident[0:2 * NB, 0:2 * NB])
                last.then_inc(rows_in_psum[s], 1)

            def lora(i, s):
                pe.wait_ge(mixed_ready[s], one(i))
                pe.wait_ge(rows_ready[s], one(i))
                for k in range(DC):
                    nc.tensor.matmul(banks[s][1][:, 0:P], w["l3_maa_w1"][:, k, 0:P], mixed[s][:, k].rearrange("p b t -> p (b t)"),
                                     start=(k == 0), stop=(k == DC - 1))
                for k in range(DC):
                    last = nc.tensor.matmul(banks[s][1][0:LORA, P:2 * P], w["l3_maa_w1"][:, k, P:P + LORA],
                                            mixed[s][:, k].rearrange("p b t -> p (b t)"), start=(k == 0), stop=(k == DC - 1))
                last.then_inc(lora_in_psum[s], 1)

            def mixes(i, s):
                pe.wait_ge(lora_ready[s], one(i))
                for pair in ((0, 4), (2,), (1,), (3,)):
                    for j in pair:
                        rows, half = (slice(LORA * j, LORA * (j + 1)), 0) if j < 4 else (slice(0, LORA), 1)
                        at = DIM if j == 4 else 0
                        for c in range(DC):
                            last = nc.tensor.matmul(banks[s][j % 4][:, at + c * P:at + (c + 1) * P],
                                                    w["l3_maa_w2"][rows, half, c * P:(c + 1) * P],
                                                    loraT[s][rows, half, :], start=True, stop=True)
                    last.then_inc(mix_in_psum[s], len(pair))

            def projections(i, s):
                x5_at = {j: n for n, j in enumerate(ORDER)}
                pe.wait_ge(x5_ready[s], count(i, 5, x5_at[4]))
                features_out(banks[s][0], 0, w["l3_Wk"], x5[0][s]).then_inc(k_in_psum[s], 1)
                pe.wait_ge(x5_ready[s], count(i, 5, x5_at[2]))
                features_out(banks[s][2], 0, w["l3_Wv"], x5[2][s]).then_inc(v_in_psum[s], 1)
                pe.wait_ge(x5_ready[s], count(i, 5, x5_at[1]))
                for k in range(DC):
                    last = nc.tensor.matmul(banks[s][1][0:DECAY, 0:P], w["l3_decay_w1"][:, k, :], x5[1][s][:, k, :],
                                            start=(k == 0), stop=(k == DC - 1))
                last.then_inc(decay_in_psum[s], 1)
                pe.wait_ge(x5_ready[s], count(i, 5, x5_at[3]))
                features_out(banks[s][3], 0, w["l3_Wr"], x5[3][s]).then_inc(r_in_psum[s], 1)

            def rate_and_gate(i, s):
                pe.wait_ge(decay_ready[s], one(i))
                for c in range(DC):
                    last = nc.tensor.matmul(banks[s][1][:, c * P:(c + 1) * P], w["l3_decay_w2"][0:DECAY, 0, c * P:(c + 1) * P],
                                            decayT[s][:], start=True, stop=True)
                last.then_inc(rate_in_psum[s], 1)
                pe.wait_ge(k_ready[s], one(i))
                features_out(banks[s][0], DIM, w["l3_Wg"], x5[4][s]).then_inc(g_in_psum[s], 1)

            def spreads(i, s):
                pe.wait_ge(v_ready[s], one(i))
                pe.wait_ge(r_ready[s], one(i))
                for c in range(DC):
                    for q in range(2):
                        n = 2 * c + q
                        if n >= 2:
                            pe.wait_ge(addend_ready[s], count(i, 4, n - 2))
                        for d in range(WIDE4):
                            last = nc.tensor.matmul(banks[s][2 + q][:, d * P:(d + 1) * P], select[:, WIDE4 * q + d, :],
                                                    vT[s][:, c, :], start=True, stop=True)
                        last.then_inc(spread_in_psum[s], 1)
                    if c == 0:
                        own_value(i, s)

            def own_value(i, s):
                pe.wait_ge(gate_ready[s], one(i))
                pe.wait_ge(ruk_ready[s], one(i))
                transposed(banks[s][0], flat(vT[s][:]))
                per_chunk = P // HEAD8
                for c in range(DC):
                    nc.tensor.matmul(banks[s][0][:, DIM + c * per_chunk:DIM + (c + 1) * per_chunk], rukT[s][:, c, :], head_of,
                                     start=True, stop=True)

            def outputs(i, s):
                pe.wait_ge(w_ready[s], one(i))
                for c in range(DC):
                    pe.wait_ge(out_ready[s], count(i, 2, c))
                    for d in range(HEAD8):
                        first = c * P + d
                        last = nc.tensor.matmul(banks[s][1][:, first:(c + 1) * P:HEAD8],
                                                state_of[c][s][:, d].rearrange("p b t -> p (b t)"), head_of, start=True, stop=True)
                last.then_inc(att_in_psum[s], 1)

            def attended(i, s):
                pe.wait_ge(att_ready[s], one(i))
                transposed(banks[s][2], att[s]).then_inc(attT_in_psum[s], 1)

            def project_out(i, s):
                pe.wait_ge(gated_ready[s], one(i))
                tokens_out(banks[s][3], w["l3_Wo"], gated[s]).then_inc(y_in_psum[s], 1)

            def normed_again(i, s):
                pe.wait_ge(xn_ready[s], count(i, 2, 1))
                transposed(banks[s][0], xn[s]).then_inc(xT_in_psum[s], 1)

            def channel(i, s):
                pe.wait_ge(channel_ready[s], count(i, 2, 0))
                features_out(banks[s][1], 0, w["l3_ffn_Wk"], xkT[s]).then_inc(kk_in_psum[s], 1)
                pe.wait_ge(channel_ready[s], count(i, 2, 1))
                tokens_out(banks[s][2], w["l3_ffn_Wr"], xrT[s]).then_inc(rr_in_psum[s], 1)

            def channel_out(i, s):
                pe.wait_ge(kk2_ready[s], one(i))
                tokens_out(banks[s][3], w["l3_ffn_Wv"], kk2[s]).then_inc(kv_in_psum[s], 1)

            skewed(pe, LAG, (), (normed,), (lora,), (mixes,), (projections,), (rate_and_gate,), (spreads,), (outputs,),
                   (attended,), (project_out,), (normed_again,), (channel,), (channel_out,))

        running.close()
        cleared(nc, semaphores)


LAYER_WEIGHTS = (L0_WEIGHTS, L1_WEIGHTS, L2_WEIGHTS, L3_WEIGHTS)
SHARED = ("l2_wo1", "l2_wo2", "l2_wv1", "l2_wq1", "l2_wk1")
SHARED_COLUMNS = sum(L2_WEIGHTS[n][0] // P * L2_WEIGHTS[n][1] for n in SHARED)


def program(nc, dram, x_out, layers=(0, 1, 2, 3)):
    with ExitStack() as held:
        def sb(name, shape):
            return held.enter_context(nc.sbuf_tensor(name, shape, F32))

        cols = sb("cols", [P, NCOLS])
        rows = sb("rows", [P, NROWS * DIM])
        ident = sb("ident", [P, P])
        parity = sb("parity", [P, 2])
        select = sb("select", [P, HEAD8, P])
        head_of = sb("head_of", [P, P // HEAD8])
        shared = sb("shared", [P, SHARED_COLUMNS])
        col = lambda name, c, n=1: cols[:, COL_AT[name] + c:COL_AT[name] + c + n]
        row = {n: rows[:, k * DIM:(k + 1) * DIM] for k, n in enumerate(ROW_NAMES)}
        between = [nc.dram_tensor(f"between{n}", (BATCH * SEQ, DIM), F32).ap() for n in range(3)]
        inside = [nc.dram_tensor(f"inside{a}", (BATCH * SEQ, DIM), F32).ap() for a in range(2)]
        first_loaded, l0_loaded, l1_loaded, shared_loaded, l2_loaded, l3_loaded = (
            held.enter_context(nc.semaphore(n + "_loaded")) for n in ("first", "l0", "l1", "shared", "l2", "l3"))

        def in_shared(names, shapes):
            w, at = {}, 0
            for n in names:
                k, m = shapes[n]
                w[n] = shared[:, at:at + k // P * m].rearrange("p (k m) -> p k m", m=m)
                at += k // P * m
            return w

        def in_own(stack, names, shapes):
            return {n: stack.enter_context(nc.sbuf_tensor(n, [P, shapes[n][0] // P, shapes[n][1]], F32))[:] for n in names}

        def load(sp, w, loaded):
            for n in w:
                sp.dma_start(w[n], dram[n].rearrange("(k p) m -> p k m", p=P)).then_inc(loaded, 16)

        def wait_for(loaded, count):
            with nc.Block() as block:
                @block.sync
                def _(sp):
                    sp.wait_ge(loaded, 16 * count)

        w_shared = in_shared(SHARED, L2_WEIGHTS)
        with ExitStack() as layers01:
            w1 = in_own(layers01, L1_WEIGHTS, L1_WEIGHTS)
            with ExitStack() as layer0:
                w0 = in_own(layer0, L0_WEIGHTS, L0_WEIGHTS)
                first = ["l0_w_qkv"]
                constants = ((cols, "cols"), (ident, "ident"), (parity, "parity"))
                with nc.Block() as block:
                    @block.sync
                    def _(sp):
                        for tile, name in constants:
                            sp.dma_start(tile[:], dram[name]).then_inc(first_loaded, 16)
                        load(sp, {n: w0[n] for n in first}, first_loaded)
                        sp.dma_start(rows[:], dram["rows"].partition_broadcast(P)).then_inc(first_loaded, 16)
                        sp.wait_ge(first_loaded, 16 * (len(constants) + len(first) + 1))

                def prefetch(sp):
                    load(sp, {n: w0[n] for n in w0 if n not in first}, l0_loaded)
                    load(sp, w1, l1_loaded)
                    load(sp, w_shared, shared_loaded)

                if 0 in layers:
                    decoder_layer(nc, dram["x"], dram["ctx"], dram["self_mask"], dram["cross_mask"],
                                  between[0] if layers[-1] > 0 else x_out, w0, (l0_loaded, 16 * (len(w0) - len(first))),
                                  prefetch, col, row, ident[:], parity)
                else:
                    with nc.Block() as block:
                        @block.sync
                        def _(sp):
                            prefetch(sp)
            wait_for(l1_loaded, len(w1))
            if 1 in layers:
                resampler_layer(nc, between[0] if 0 in layers else dram["x"], dram["ctx"], dram["key_mask"],
                                between[1] if layers[-1] > 1 else x_out, w1, col, row, ident[:], parity)
        wait_for(shared_loaded, len(w_shared))
        with ExitStack() as layer2:
            w2 = in_own(layer2, [n for n in L2_WEIGHTS if n not in SHARED], L2_WEIGHTS)
            if 2 in layers:
                x = between[1] if 1 in layers else dram["x"]
                wide_attention(nc, 0, x, dram["ctx"], inside[0], w_shared | w2, col, row, ident[:],
                               lambda sp: load(sp, w2, l2_loaded))
                wait_for(l2_loaded, len(w2))
                wide_attention(nc, 1, inside[0], dram["ctx"], inside[1], w_shared | w2, col, row, ident[:])
            w3 = in_shared(L3_WEIGHTS, L3_WEIGHTS)

            def prefetch3(sp):
                load(sp, w3, l3_loaded)
                sp.dma_start(select[:], dram["select"]).then_inc(l3_loaded, 16)
                sp.dma_start(head_of[:], dram["head_of"]).then_inc(l3_loaded, 16)

            if 2 in layers:
                wide_mlp(nc, inside[1], between[2] if layers[-1] > 2 else x_out, w2, col, row, ident[:], prefetch3)
            else:
                with nc.Block() as block:
                    @block.sync
                    def _(sp):
                        prefetch3(sp)
        wait_for(l3_loaded, len(w3) + 2)
        if 3 in layers:
            recurrent_layer(nc, between[2] if 2 in layers else dram["x"], dram["ctx"], x_out, w3, col, ident[:], select, head_of[:])


def laid_out(inputs):
    a = {n: np.asarray(x) for n, x in inputs.items()}
    out = {"x": a["x"].reshape(-1, DIM), "ctx": a["ctx_2048"].reshape(-1, DIM),
           "self_mask": a["mask_1x1xSxS2_fc1"].reshape(SEQ, SEQ),
           "cross_mask": a["mask_Bx1xSxS2_ff1"].reshape(-1, SEQ), "key_mask": a["mask_BxS2_ik0"]}
    a["l1_k_b"], a["l1_v_b"] = a["L1_xattn_kv_b"][0::2], a["L1_xattn_kv_b"][1::2]
    out["l1_k_w"], out["l1_v_w"] = a["L1_xattn_kv_w"][:, 0::2], a["L1_xattn_kv_w"][:, 1::2]
    for name in ("Wk", "Wv", "Wr", "Wg", "Wo", "ffn_Wk", "ffn_Wr", "ffn_Wv"):
        out["l3_" + name] = a["L3_xattn_" + name].T
    out["l3_maa_w2"] = np.zeros((2 * P, DIM), np.float32)
    out["l3_maa_w2"][:5 * LORA] = a["L3_xattn_maa_w2"].reshape(5 * LORA, DIM)
    out["l3_decay_w2"] = np.zeros((P, DIM), np.float32)
    out["l3_decay_w2"][:DECAY] = a["L3_xattn_decay_w2"]
    head, within = np.arange(P) // HEAD8, np.arange(P) % HEAD8
    out["select"] = ((head[:, None, None] == head[None, None, :])
                     & (within[:, None, None] == np.arange(HEAD8)[None, :, None])).astype(np.float32)
    out["head_of"] = (head[:, None] == np.arange(P // HEAD8)[None]).astype(np.float32)
    for weights in LAYER_WEIGHTS:
        for name in weights:
            if name not in out:
                out[name] = a["L" + name[1] + "_xattn_" + name[3:]]
    out["cols"] = np.concatenate([a[name].reshape(-1)[first:first + n].reshape(-1, P).T for name, first, n in COLS.values()], 1)
    out["rows"] = np.concatenate([a[name].reshape(-1) for name in ROWS.values()])[None]
    out["ident"] = np.eye(P, dtype=np.float32)
    out["parity"] = (np.arange(P)[:, None] // HEAD % 2 == np.arange(2)[None]).astype(np.float32)
    return {n: np.ascontiguousarray(x) for n, x in out.items()}


def kernel(**inputs):
    import concourse.bacc as bacc
    from concourse.bass_utils import run_bass_kernel_spmd

    nc = bacc.Bacc("TRN2", target_bir_lowering=False, num_devices=1)
    arrays = {f"in_{n}": a for n, a in laid_out(inputs).items()}
    dram = {n[3:]: nc.dram_tensor(n, a.shape, mybir.dt.from_np(a.dtype), kind="ExternalInput").ap() for n, a in arrays.items()}
    out = nc.dram_tensor("out", (BATCH * SEQ, DIM), F32, kind="ExternalOutput").ap()
    program(nc, dram, out)
    result = run_bass_kernel_spmd(nc, [arrays], core_ids=[0])
    return result.results[0]["out"].reshape(BATCH, SEQ, DIM)
```
